# Optimizing a Trainium2 kernel written in Bass

```python
import numpy as np
import jax
import jax.numpy as jnp

def _softmax(x, axis=-1):
    return jax.nn.softmax(x, axis=axis)

def _gelu(x):
    return jax.nn.gelu(x, approximate=True)

def _silu(x):
    return jax.nn.silu(x)

def _sigmoid(x):
    return jax.nn.sigmoid(x)

def _layernorm(x, axis=-1, eps=1e-05):
    m = jnp.mean(x, axis=axis, keepdims=True)
    v = jnp.var(x, axis=axis, keepdims=True)
    return (x - m) / jnp.sqrt(v + eps)

def _scatter_add(tgt, idx, src, axis=0):
    return tgt.at[idx].add(src)

def _segment_sum(src, seg, n):
    return jax.ops.segment_sum(src, seg, n)
kernel_name = 'mk_conv_attn_hybrid_d4_conv_nhwc768_r4_0b7201'

def setup_inputs(seed: int=0):
    np.random.seed(seed)
    _w = jnp.asarray

    def _rec_inputs():
        import jax
        import jax.numpy as jnp
        _gk = jax.random.key(seed)
        x = -0.0001538 + 1 * jax.random.normal(jax.random.fold_in(_gk, 1), (32, 16, 16, 192), jnp.float32)
        return x
    x = _rec_inputs()

    def _L0_conv_setup():
        import jax, jax.numpy as jnp
        import numpy as np
        D_MODEL = 192
        R = 48
        D_INNER = 96
        D_STATE = 16
        D_CONV = 4
        DT_RANK = 12
        LN_EPS = 1e-05

        def _mamba(xs, in_proj_w, conv_w, conv_b, x_proj_w, dt_proj_w, dt_proj_b, A_log, D_ssm, out_proj_w):
            B, L, _ = xs.shape
            xz = xs @ in_proj_w.T
            xi, z = (xz[..., :D_INNER], xz[..., D_INNER:])
            xp = jnp.pad(xi, ((0, 0), (D_CONV - 1, 0), (0, 0)))
            conv = conv_b
            for k in range(D_CONV):
                conv = conv + xp[:, k:k + L, :] * conv_w[:, k]
            u = jax.nn.silu(conv)
            x_dbl = u @ x_proj_w.T
            dt = x_dbl[..., :DT_RANK]
            Bm = x_dbl[..., DT_RANK:DT_RANK + D_STATE]
            Cm = x_dbl[..., DT_RANK + D_STATE:]
            delta = jax.nn.softplus(dt @ dt_proj_w.T + dt_proj_b)
            A = -jnp.exp(A_log)
            dA = jnp.exp(delta[..., None] * A)
            dBu = (delta * u)[..., None] * Bm[:, :, None, :]

            def step(h, ins):
                dA_t, dBu_t, C_t = ins
                h = dA_t * h + dBu_t
                y_t = jnp.einsum('bdn,bn->bd', h, C_t)
                return (h, y_t)
            h0 = jnp.zeros((B, D_INNER, D_STATE), xs.dtype)
            _, ys = jax.lax.scan(step, h0, (dA.transpose(1, 0, 2, 3), dBu.transpose(1, 0, 2, 3), Cm.transpose(1, 0, 2)))
            y = ys.transpose(1, 0, 2) + u * D_ssm
            y = y * jax.nn.silu(z)
            return y @ out_proj_w.T
        key = jax.random.key(seed)
        ks = jax.random.split(key, 12)

        def n(k, shape, s=0.02):
            return jax.random.normal(k, shape, jnp.float32) * s
        return {'x': jax.random.normal(ks[0], (32, 16, 16, D_MODEL), jnp.float32), 'down_w': n(ks[1], (R, D_MODEL)), 'up_w': n(ks[2], (D_MODEL, R)), 'in_proj_w': n(ks[3], (2 * D_INNER, R)), 'conv_w': n(ks[4], (D_INNER, D_CONV), 0.2), 'conv_b': n(ks[5], (D_INNER,), 0.02), 'x_proj_w': n(ks[6], (DT_RANK + 2 * D_STATE, D_INNER)), 'dt_proj_w': n(ks[7], (D_INNER, DT_RANK), 0.1), 'dt_proj_b': n(ks[8], (D_INNER,), 0.5), 'A_log': jnp.log(jnp.broadcast_to(jnp.arange(1, D_STATE + 1, dtype=jnp.float32), (D_INNER, D_STATE))), 'D_ssm': jnp.ones((D_INNER,), jnp.float32), 'out_proj_w': n(ks[9], (R, D_INNER)), 'ln_g': jnp.ones((R,), jnp.float32), 'ln_b': jnp.zeros((R,), jnp.float32), 'b': 2}
    _L0_conv_all = _L0_conv_setup()
    _L0_conv_in = {k: v for k, v in _L0_conv_all.items() if k in ('down_w', 'up_w', 'in_proj_w', 'conv_w', 'conv_b', 'x_proj_w', 'dt_proj_w', 'dt_proj_b', 'A_log', 'D_ssm', 'out_proj_w', 'ln_g', 'ln_b')}
    del _L0_conv_all

    def _L1_conv_setup():
        import jax, jax.numpy as jnp
        import numpy as np
        HIDDEN_SIZE = 192
        NUM_BLOCKS = 8
        BLOCK_SIZE = HIDDEN_SIZE // NUM_BLOCKS
        HSF = 1
        LAMBDA = 0.01
        FRAC = 1.0
        SCALE = 0.02

        def softshrink(v, lambd):
            return jnp.sign(v) * jnp.maximum(jnp.abs(v) - lambd, 0.0)
        key = jax.random.key(seed)
        k = jax.random.split(key, 5)
        x = jax.random.normal(k[0], (1, 64, 64, HIDDEN_SIZE), dtype=jnp.float32)
        w1 = SCALE * jax.random.normal(k[1], (2, NUM_BLOCKS, BLOCK_SIZE, BLOCK_SIZE * HSF), dtype=jnp.float32)
        b1 = SCALE * jax.random.normal(k[2], (2, NUM_BLOCKS, BLOCK_SIZE * HSF), dtype=jnp.float32)
        w2 = SCALE * jax.random.normal(k[3], (2, NUM_BLOCKS, BLOCK_SIZE * HSF, BLOCK_SIZE), dtype=jnp.float32)
        b2 = SCALE * jax.random.normal(k[4], (2, NUM_BLOCKS, BLOCK_SIZE), dtype=jnp.float32)
        return {'x': x, 'w1': w1, 'b1': b1, 'w2': w2, 'b2': b2}
    _L1_conv_all = _L1_conv_setup()
    _L1_conv_in = {k: v for k, v in _L1_conv_all.items() if k in ('w1', 'b1', 'w2', 'b2')}
    del _L1_conv_all

    def _L2_attn_setup():
        import jax, jax.numpy as jnp
        import numpy as np
        import itertools
        B, T, C, H = (2, 128, 192, 12)
        HS = C // H
        M = 8
        MIN_SIZE, MAX_SIZE = (2, 3)
        TEMP = 1.0
        ALPHA = 1.0
        SIGN = 1.0
        NEG = -1e+30
        COMBS = [np.array(list(itertools.combinations(range(M), s)), dtype=np.int32) for s in range(MIN_SIZE - 1, MAX_SIZE)]

        def _token(i, q_i, k, v):
            Tn = k.shape[0]
            sim = k @ q_i
            sim = jnp.where(jnp.arange(Tn) <= i, sim, -jnp.inf)
            _, top_idx = jax.lax.top_k(sim, M)
            n_cand = jnp.minimum(M, i + 1)
            slot_valid = jnp.arange(M) < n_cand
            slot_is_i = (top_idx == i) & slot_valid
            scores, outs, valids = ([], [], [])
            for comb in COMBS:
                slots = jnp.asarray(comb)
                nc, s = comb.shape
                valid = slot_valid[slots].all(axis=1) & ~slot_is_i[slots].any(axis=1)
                idx = jnp.concatenate([jnp.full((nc, 1), i, dtype=top_idx.dtype), top_idx[slots]], axis=1)
                K = k[idx]
                V = v[idx]
                gram = jnp.einsum('cnd,cmd->cnm', K, K)
                det = jnp.linalg.det(gram)
                log_det = jnp.log(jnp.where(valid, det, 1.0) + 1e-06)
                score = SIGN * log_det / float(s + 1) ** ALPHA
                dot = jnp.einsum('cnd,d->cn', K, q_i) / HS ** 0.5
                w = jax.nn.softmax(dot, axis=1)
                out_s = jnp.einsum('cn,cnd->cd', w, V)
                scores.append(jnp.where(valid, score, NEG))
                outs.append(out_s)
                valids.append(valid)
            scores = jnp.concatenate(scores)
            outs = jnp.concatenate(outs, axis=0)
            has_valid = jnp.concatenate(valids).any()
            probs = jax.nn.softmax(scores / TEMP)
            best = jnp.argmax(probs)
            y_st = outs[best]
            y_soft = probs @ outs
            y = y_st + jax.lax.stop_gradient(y_soft - y_st)
            return jnp.where(has_valid, y, v[i])

        def _dpp_head(q, k, v):
            return jax.vmap(lambda i, qi: _token(i, qi, k, v))(jnp.arange(q.shape[0]), q)

        def _forward(x, W_attn, b_attn, W_proj, b_proj):
            Bx, Tx, Cx = x.shape
            qkv = x @ W_attn.T + b_attn
            q, k, v = jnp.split(qkv, 3, axis=2)

            def heads(t):
                return t.reshape(Bx, Tx, H, HS).transpose(0, 2, 1, 3).reshape(Bx * H, Tx, HS)
            y = jax.vmap(_dpp_head)(heads(q), heads(k), heads(v))
            y = y.reshape(Bx, H, Tx, HS).transpose(0, 2, 1, 3).reshape(Bx, Tx, Cx)
            return y @ W_proj.T + b_proj
        key = jax.random.key(seed)
        k1, k2, k3, k4, k5 = jax.random.split(key, 5)
        return {'x': jax.random.normal(k1, (B, T, C), dtype=jnp.float32), 'W_attn': jax.random.normal(k2, (3 * C, C), dtype=jnp.float32) * 0.02, 'b_attn': jax.random.normal(k3, (3 * C,), dtype=jnp.float32) * 0.02, 'W_proj': jax.random.normal(k4, (C, C), dtype=jnp.float32) * 0.02, 'b_proj': jax.random.normal(k5, (C,), dtype=jnp.float32) * 0.02}
    _L2_attn_all = _L2_attn_setup()
    _L2_attn_in = {k: v for k, v in _L2_attn_all.items() if k in ('W_attn', 'b_attn', 'W_proj', 'b_proj')}
    del _L2_attn_all

    def _L2_ffn_setup():
        import jax, jax.numpy as jnp
        import numpy as np
        ALPHA = 1.702
        LIMIT = 7.0
        TOP_K = 2
        B, S, H, E, I = (2, 256, 192, 8, 192)
        key = jax.random.key(seed)
        ks = jax.random.split(key, 7)
        scale = 0.02
        return {'hidden_states': jax.random.normal(ks[0], (B, S, H), dtype=jnp.float32), 'Wr': jax.random.normal(ks[1], (H, E), dtype=jnp.float32) * scale, 'br': jax.random.normal(ks[2], (E,), dtype=jnp.float32) * scale, 'Wgu': jax.random.normal(ks[3], (E, H, 2 * I), dtype=jnp.float32) * scale, 'bgu': jax.random.normal(ks[4], (E, 2 * I), dtype=jnp.float32) * scale, 'Wd': jax.random.normal(ks[5], (E, I, H), dtype=jnp.float32) * scale, 'bd': jax.random.normal(ks[6], (E, H), dtype=jnp.float32) * scale}
    _L2_ffn_all = _L2_ffn_setup()
    _L2_ffn_in = {k: v for k, v in _L2_ffn_all.items() if k in ('Wr', 'br', 'Wgu', 'bgu', 'Wd', 'bd')}
    del _L2_ffn_all

    def _L3_attn_setup():
        import jax, jax.numpy as jnp
        import numpy as np
        B, N, M, D = (32, 64, 8, 192)
        key = jax.random.key(seed)
        ks = jax.random.split(key, 6)
        w_scale = D ** (-0.5)
        return {'x': jax.random.normal(ks[0], (B, N, D), dtype=jnp.float32), 'memory': jax.random.normal(ks[1], (M, D), dtype=jnp.float32) * 0.02, 'Wq': jax.random.normal(ks[2], (D, D), dtype=jnp.float32) * w_scale, 'bq': jnp.zeros((D,), dtype=jnp.float32), 'Wk': jax.random.normal(ks[3], (D, D), dtype=jnp.float32) * w_scale, 'bk': jnp.zeros((D,), dtype=jnp.float32), 'Wv': jax.random.normal(ks[4], (D, D), dtype=jnp.float32) * w_scale, 'bv': jnp.zeros((D,), dtype=jnp.float32), 'Wo': jax.random.normal(ks[5], (D, D), dtype=jnp.float32) * w_scale, 'bo': jnp.zeros((D,), dtype=jnp.float32)}
    _L3_attn_all = _L3_attn_setup()
    _L3_attn_in = {k: v for k, v in _L3_attn_all.items() if k in ('memory', 'Wq', 'bq', 'Wk', 'bk', 'Wv', 'bv', 'Wo', 'bo')}
    del _L3_attn_all

    def _L3_ffn_setup():
        import jax, jax.numpy as jnp
        import numpy as np
        TOP_K = 2
        key = jax.random.key(seed)
        ks = jax.random.split(key, 5)
        B, T, C, H, E = (4, 256, 192, 768, 8)
        x = jax.random.normal(ks[0], (B, T, C), dtype=jnp.float32)
        Wg = jax.random.normal(ks[1], (C, E), dtype=jnp.float32) * 0.02
        W1 = jax.random.normal(ks[2], (E, C, H), dtype=jnp.float32) * (1.0 / np.sqrt(C))
        b1 = jnp.zeros((E, H), dtype=jnp.float32)
        W2 = jax.random.normal(ks[3], (E, H, C), dtype=jnp.float32) * (1.0 / np.sqrt(H))
        b2 = jnp.zeros((E, C), dtype=jnp.float32)
        return {'x': x, 'Wg': Wg, 'W1': W1, 'b1': b1, 'W2': W2, 'b2': b2}
    _L3_ffn_all = _L3_ffn_setup()
    _L3_ffn_in = {k: v for k, v in _L3_ffn_all.items() if k in ('Wg', 'W1', 'b1', 'W2', 'b2')}
    del _L3_ffn_all
    return {'x': x, 'L0_conv_down_w': _L0_conv_in['down_w'], 'L0_conv_up_w': _L0_conv_in['up_w'], 'L0_conv_in_proj_w': _L0_conv_in['in_proj_w'], 'L0_conv_conv_w': _L0_conv_in['conv_w'], 'L0_conv_conv_b': _L0_conv_in['conv_b'], 'L0_conv_x_proj_w': _L0_conv_in['x_proj_w'], 'L0_conv_dt_proj_w': _L0_conv_in['dt_proj_w'], 'L0_conv_dt_proj_b': _L0_conv_in['dt_proj_b'], 'L0_conv_A_log': _L0_conv_in['A_log'], 'L0_conv_D_ssm': _L0_conv_in['D_ssm'], 'L0_conv_out_proj_w': _L0_conv_in['out_proj_w'], 'L0_conv_ln_g': _L0_conv_in['ln_g'], 'L0_conv_ln_b': _L0_conv_in['ln_b'], 'L1_conv_w1': _L1_conv_in['w1'], 'L1_conv_b1': _L1_conv_in['b1'], 'L1_conv_w2': _L1_conv_in['w2'], 'L1_conv_b2': _L1_conv_in['b2'], 'L2_attn_W_attn': _L2_attn_in['W_attn'], 'L2_attn_b_attn': _L2_attn_in['b_attn'], 'L2_attn_W_proj': _L2_attn_in['W_proj'], 'L2_attn_b_proj': _L2_attn_in['b_proj'], 'L2_ffn_Wr': _L2_ffn_in['Wr'], 'L2_ffn_br': _L2_ffn_in['br'], 'L2_ffn_Wgu': _L2_ffn_in['Wgu'], 'L2_ffn_bgu': _L2_ffn_in['bgu'], 'L2_ffn_Wd': _L2_ffn_in['Wd'], 'L2_ffn_bd': _L2_ffn_in['bd'], 'L3_attn_memory': _L3_attn_in['memory'], 'L3_attn_Wq': _L3_attn_in['Wq'], 'L3_attn_bq': _L3_attn_in['bq'], 'L3_attn_Wk': _L3_attn_in['Wk'], 'L3_attn_bk': _L3_attn_in['bk'], 'L3_attn_Wv': _L3_attn_in['Wv'], 'L3_attn_bv': _L3_attn_in['bv'], 'L3_attn_Wo': _L3_attn_in['Wo'], 'L3_attn_bo': _L3_attn_in['bo'], 'L3_ffn_Wg': _L3_ffn_in['Wg'], 'L3_ffn_W1': _L3_ffn_in['W1'], 'L3_ffn_b1': _L3_ffn_in['b1'], 'L3_ffn_W2': _L3_ffn_in['W2'], 'L3_ffn_b2': _L3_ffn_in['b2']}

def reference(x, L0_conv_down_w, L0_conv_up_w, L0_conv_in_proj_w, L0_conv_conv_w, L0_conv_conv_b, L0_conv_x_proj_w, L0_conv_dt_proj_w, L0_conv_dt_proj_b, L0_conv_A_log, L0_conv_D_ssm, L0_conv_out_proj_w, L0_conv_ln_g, L0_conv_ln_b, L1_conv_w1, L1_conv_b1, L1_conv_w2, L1_conv_b2, L2_attn_W_attn, L2_attn_b_attn, L2_attn_W_proj, L2_attn_b_proj, L2_ffn_Wr, L2_ffn_br, L2_ffn_Wgu, L2_ffn_bgu, L2_ffn_Wd, L2_ffn_bd, L3_attn_memory, L3_attn_Wq, L3_attn_bq, L3_attn_Wk, L3_attn_bk, L3_attn_Wv, L3_attn_bv, L3_attn_Wo, L3_attn_bo, L3_ffn_Wg, L3_ffn_W1, L3_ffn_b1, L3_ffn_W2, L3_ffn_b2):
    import jax
    import jax.numpy as jnp

    def _L0_conv_ref(x, down_w, up_w, in_proj_w, conv_w, conv_b, x_proj_w, dt_proj_w, dt_proj_b, A_log, D_ssm, out_proj_w, ln_g, ln_b, b):
        import jax, jax.numpy as jnp
        import numpy as np
        D_MODEL = 192
        R = 48
        D_INNER = 96
        D_STATE = 16
        D_CONV = 4
        DT_RANK = 12
        LN_EPS = 1e-05

        def _mamba(xs, in_proj_w, conv_w, conv_b, x_proj_w, dt_proj_w, dt_proj_b, A_log, D_ssm, out_proj_w):
            B, L, _ = xs.shape
            xz = xs @ in_proj_w.T
            xi, z = (xz[..., :D_INNER], xz[..., D_INNER:])
            xp = jnp.pad(xi, ((0, 0), (D_CONV - 1, 0), (0, 0)))
            conv = conv_b
            for k in range(D_CONV):
                conv = conv + xp[:, k:k + L, :] * conv_w[:, k]
            u = jax.nn.silu(conv)
            x_dbl = u @ x_proj_w.T
            dt = x_dbl[..., :DT_RANK]
            Bm = x_dbl[..., DT_RANK:DT_RANK + D_STATE]
            Cm = x_dbl[..., DT_RANK + D_STATE:]
            delta = jax.nn.softplus(dt @ dt_proj_w.T + dt_proj_b)
            A = -jnp.exp(A_log)
            dA = jnp.exp(delta[..., None] * A)
            dBu = (delta * u)[..., None] * Bm[:, :, None, :]

            def step(h, ins):
                dA_t, dBu_t, C_t = ins
                h = dA_t * h + dBu_t
                y_t = jnp.einsum('bdn,bn->bd', h, C_t)
                return (h, y_t)
            h0 = jnp.zeros((B, D_INNER, D_STATE), xs.dtype)
            _, ys = jax.lax.scan(step, h0, (dA.transpose(1, 0, 2, 3), dBu.transpose(1, 0, 2, 3), Cm.transpose(1, 0, 2)))
            y = ys.transpose(1, 0, 2) + u * D_ssm
            y = y * jax.nn.silu(z)
            return y @ out_proj_w.T
        bd, h, w, _ = x.shape
        d = bd // b
        shortcut = x
        xd = x @ down_w.T
        xs = xd.reshape(b, d * h * w, R)
        m = _mamba(xs, in_proj_w, conv_w, conv_b, x_proj_w, dt_proj_w, dt_proj_b, A_log, D_ssm, out_proj_w)
        mu = m.mean(-1, keepdims=True)
        var = ((m - mu) ** 2).mean(-1, keepdims=True)
        m = (m - mu) * jax.lax.rsqrt(var + LN_EPS) * ln_g + ln_b
        m = jax.nn.gelu(m, approximate=False)
        m = m.reshape(bd, h, w, R)
        return shortcut + m @ up_w.T

    def _L1_conv_ref(x, w1, b1, w2, b2):
        import jax, jax.numpy as jnp
        import numpy as np
        HIDDEN_SIZE = 192
        NUM_BLOCKS = 8
        BLOCK_SIZE = HIDDEN_SIZE // NUM_BLOCKS
        HSF = 1
        LAMBDA = 0.01
        FRAC = 1.0
        SCALE = 0.02

        def softshrink(v, lambd):
            return jnp.sign(v) * jnp.maximum(jnp.abs(v) - lambd, 0.0)
        bias = x
        dtype = x.dtype
        B, H, W, C = x.shape
        Wc = W // 2 + 1
        xf = jnp.fft.rfft2(x.astype(jnp.float32), axes=(1, 2), norm='ortho')
        xr = xf.real.reshape(B, H, Wc, NUM_BLOCKS, BLOCK_SIZE)
        xi = xf.imag.reshape(B, H, Wc, NUM_BLOCKS, BLOCK_SIZE)
        total_modes = H // 2 + 1
        kept = int(total_modes * FRAC)
        ymask = (jnp.arange(H) >= total_modes - kept) & (jnp.arange(H) < total_modes + kept)
        xmask = jnp.arange(Wc) < kept
        mask = (ymask[:, None] & xmask[None, :]).astype(jnp.float32)[None, :, :, None, None]
        o1r = jax.nn.relu(jnp.einsum('nyxbi,bio->nyxbo', xr, w1[0]) - jnp.einsum('nyxbi,bio->nyxbo', xi, w1[1]) + b1[0]) * mask
        o1i = jax.nn.relu(jnp.einsum('nyxbi,bio->nyxbo', xi, w1[0]) + jnp.einsum('nyxbi,bio->nyxbo', xr, w1[1]) + b1[1]) * mask
        o2r = (jnp.einsum('nyxbi,bio->nyxbo', o1r, w2[0]) - jnp.einsum('nyxbi,bio->nyxbo', o1i, w2[1]) + b2[0]) * mask
        o2i = (jnp.einsum('nyxbi,bio->nyxbo', o1i, w2[0]) + jnp.einsum('nyxbi,bio->nyxbo', o1r, w2[1]) + b2[1]) * mask
        o2r = softshrink(o2r, LAMBDA)
        o2i = softshrink(o2i, LAMBDA)
        xc = (o2r + 1j * o2i).reshape(B, H, Wc, C)
        out = jnp.fft.irfft2(xc, s=(H, W), axes=(1, 2), norm='ortho').astype(dtype)
        return out + bias

    def _L2_attn_ref(x, W_attn, b_attn, W_proj, b_proj):
        import jax, jax.numpy as jnp
        import numpy as np
        import itertools
        B, T, C, H = (2, 128, 192, 12)
        HS = C // H
        M = 8
        MIN_SIZE, MAX_SIZE = (2, 3)
        TEMP = 1.0
        ALPHA = 1.0
        SIGN = 1.0
        NEG = -1e+30
        COMBS = [np.array(list(itertools.combinations(range(M), s)), dtype=np.int32) for s in range(MIN_SIZE - 1, MAX_SIZE)]

        def _token(i, q_i, k, v):
            Tn = k.shape[0]
            sim = k @ q_i
            sim = jnp.where(jnp.arange(Tn) <= i, sim, -jnp.inf)
            _, top_idx = jax.lax.top_k(sim, M)
            n_cand = jnp.minimum(M, i + 1)
            slot_valid = jnp.arange(M) < n_cand
            slot_is_i = (top_idx == i) & slot_valid
            scores, outs, valids = ([], [], [])
            for comb in COMBS:
                slots = jnp.asarray(comb)
                nc, s = comb.shape
                valid = slot_valid[slots].all(axis=1) & ~slot_is_i[slots].any(axis=1)
                idx = jnp.concatenate([jnp.full((nc, 1), i, dtype=top_idx.dtype), top_idx[slots]], axis=1)
                K = k[idx]
                V = v[idx]
                gram = jnp.einsum('cnd,cmd->cnm', K, K)
                det = jnp.linalg.det(gram)
                log_det = jnp.log(jnp.where(valid, det, 1.0) + 1e-06)
                score = SIGN * log_det / float(s + 1) ** ALPHA
                dot = jnp.einsum('cnd,d->cn', K, q_i) / HS ** 0.5
                w = jax.nn.softmax(dot, axis=1)
                out_s = jnp.einsum('cn,cnd->cd', w, V)
                scores.append(jnp.where(valid, score, NEG))
                outs.append(out_s)
                valids.append(valid)
            scores = jnp.concatenate(scores)
            outs = jnp.concatenate(outs, axis=0)
            has_valid = jnp.concatenate(valids).any()
            probs = jax.nn.softmax(scores / TEMP)
            best = jnp.argmax(probs)
            y_st = outs[best]
            y_soft = probs @ outs
            y = y_st + jax.lax.stop_gradient(y_soft - y_st)
            return jnp.where(has_valid, y, v[i])

        def _dpp_head(q, k, v):
            return jax.vmap(lambda i, qi: _token(i, qi, k, v))(jnp.arange(q.shape[0]), q)

        def _forward(x, W_attn, b_attn, W_proj, b_proj):
            Bx, Tx, Cx = x.shape
            qkv = x @ W_attn.T + b_attn
            q, k, v = jnp.split(qkv, 3, axis=2)

            def heads(t):
                return t.reshape(Bx, Tx, H, HS).transpose(0, 2, 1, 3).reshape(Bx * H, Tx, HS)
            y = jax.vmap(_dpp_head)(heads(q), heads(k), heads(v))
            y = y.reshape(Bx, H, Tx, HS).transpose(0, 2, 1, 3).reshape(Bx, Tx, Cx)
            return y @ W_proj.T + b_proj
        return _forward(x, W_attn, b_attn, W_proj, b_proj)

    def _L2_ffn_ref(hidden_states, Wr, br, Wgu, bgu, Wd, bd):
        import jax, jax.numpy as jnp
        import numpy as np
        ALPHA = 1.702
        LIMIT = 7.0
        TOP_K = 2
        B, S, H, E, I = (2, 256, 192, 8, 192)
        logits = jnp.einsum('bsh,he->bse', hidden_states, Wr) + br
        topk_vals, topk_idx = jax.lax.top_k(logits, TOP_K)
        router_scores = jax.nn.softmax(topk_vals, axis=-1)
        gu = jnp.einsum('bsh,ehf->bsef', hidden_states, Wgu) + bgu
        gu = jnp.minimum(gu, LIMIT)
        gate = gu[..., :I]
        up = jnp.maximum(gu[..., I:], -LIMIT)
        glu = gate * jax.nn.sigmoid(gate * ALPHA)
        activated = (up + 1.0) * glu
        down = jnp.einsum('bsei,eih->bseh', activated, Wd) + bd
        sel = jnp.take_along_axis(down, topk_idx[..., None], axis=2)
        output = jnp.sum(sel * router_scores[..., None], axis=2)
        return output

    def _L3_attn_ref(x, memory, Wq, bq, Wk, bk, Wv, bv, Wo, bo):
        import jax, jax.numpy as jnp
        import numpy as np
        B, N, M, D = (32, 64, 8, 192)
        b, n, d = x.shape
        m = memory.shape[0]
        t = n + m
        scaling = d ** (-0.5)
        cat = jnp.concatenate([x, jnp.broadcast_to(memory[None], (b, m, d))], axis=1)
        q = cat @ Wq + bq
        k = cat @ Wk + bk
        v = cat @ Wv + bv
        att = jax.nn.softmax(jnp.einsum('bqd,bkd->bqk', q, k) * scaling, axis=-1)
        row_mask = (jnp.arange(t) < n).astype(att.dtype)[None, :, None]
        att = att * row_mask
        head_out = jnp.einsum('bqk,bkd->bqd', att, v)
        attended = head_out @ Wo + bo
        return attended[:, :n, :]

    def _L3_ffn_ref(x, Wg, W1, b1, W2, b2):
        import jax, jax.numpy as jnp
        import numpy as np
        TOP_K = 2
        E = Wg.shape[-1]
        logits = jnp.einsum('btc,ce->bte', x, Wg)
        probs = jax.nn.softmax(logits, axis=-1)
        top_vals, top_idx = jax.lax.top_k(probs, TOP_K)
        gates = (jax.nn.one_hot(top_idx, E, dtype=probs.dtype) * top_vals[..., None]).sum(-2)
        h = jax.nn.relu(jnp.einsum('btc,ech->bteh', x, W1) + b1)
        y = jnp.einsum('bteh,ehc->btec', h, W2) + b2
        out = jnp.einsum('bte,btec->btc', gates, y)
        return out

    def _gn(v, G=32, eps=1e-05):
        B_, H_, W_, C_ = v.shape
        g = v.reshape(B_, H_, W_, G, C_ // G)
        m = jnp.mean(g, axis=(1, 2, 4), keepdims=True)
        s = jnp.var(g, axis=(1, 2, 4), keepdims=True)
        return ((g - m) / jnp.sqrt(s + eps)).reshape(v.shape)

    def _ln_c(v, eps=1e-06):
        m = jnp.mean(v, axis=-1, keepdims=True)
        s = jnp.var(v, axis=-1, keepdims=True)
        return (v - m) / jnp.sqrt(s + eps)

    def _ln_t(v, eps=1e-05):
        m = jnp.mean(v, axis=-1, keepdims=True)
        s = jnp.var(v, axis=-1, keepdims=True)
        return (v - m) / jnp.sqrt(s + eps)

    def _to_tokens(v):
        B_, H_, W_, C_ = v.shape
        return v.reshape(B_, H_ * W_, C_)

    def _from_tokens(t, like):
        return t.reshape(like.shape)
    x = _L0_conv_ref(x, L0_conv_down_w, L0_conv_up_w, L0_conv_in_proj_w, L0_conv_conv_w, L0_conv_conv_b, L0_conv_x_proj_w, L0_conv_dt_proj_w, L0_conv_dt_proj_b, L0_conv_A_log, L0_conv_D_ssm, L0_conv_out_proj_w, L0_conv_ln_g, L0_conv_ln_b, 2)
    x = _L1_conv_ref(x, L1_conv_w1, L1_conv_b1, L1_conv_w2, L1_conv_b2)
    t = _to_tokens(x)
    t = t + _L2_attn_ref(_ln_t(t), L2_attn_W_attn, L2_attn_b_attn, L2_attn_W_proj, L2_attn_b_proj)
    t = t + _L2_ffn_ref(_ln_t(t), L2_ffn_Wr, L2_ffn_br, L2_ffn_Wgu, L2_ffn_bgu, L2_ffn_Wd, L2_ffn_bd)
    t = t + _L3_attn_ref(_ln_t(t), L3_attn_memory, L3_attn_Wq, L3_attn_bq, L3_attn_Wk, L3_attn_bk, L3_attn_Wv, L3_attn_bv, L3_attn_Wo, L3_attn_bo)
    t = t + _L3_ffn_ref(_ln_t(t), L3_ffn_Wg, L3_ffn_W1, L3_ffn_b1, L3_ffn_W2, L3_ffn_b2)
    x = _from_tokens(t, x)
    return x

_drawn_inputs = setup_inputs


def setup_inputs(seed=0):
    import zlib

    import numpy as np

    out = dict(_drawn_inputs(seed))
    spreads = {'L0_conv_D_ssm': (1.0, 0.6),
     'L0_conv_ln_g': (1.0, 0.6),
     'L0_conv_ln_b': (0.0, 0.308),
     'L3_attn_bq': (0.0, 0.403),
     'L3_attn_bk': (0.0, 2.0),
     'L3_attn_bv': (0.0, 0.1),
     'L3_attn_bo': (0.0, 0.1),
     'L3_ffn_b1': (0.0, 0.491),
     'L3_ffn_b2': (0.0, 0.345)}
    factors = {'L0_conv_down_w': 8.0,
     'L0_conv_in_proj_w': 8.0,
     'L0_conv_conv_w': 8.0,
     'L0_conv_conv_b': 22.11,
     'L0_conv_x_proj_w': 8.0,
     'L0_conv_dt_proj_w': 8.0,
     'L0_conv_dt_proj_b': 8.0,
     'L0_conv_A_log': 8.0,
     'L0_conv_out_proj_w': 8.0,
     'L1_conv_w1': 3.847,
     'L1_conv_b1': 8.0,
     'L1_conv_w2': 3.591,
     'L2_attn_b_attn': 4.002,
     'L2_ffn_br': 4.243,
     'L2_ffn_bgu': 7.481,
     'L3_attn_memory': 64.0}
    for name, (base, spread) in spreads.items():
        noise = np.random.default_rng([zlib.crc32(name.encode()), seed]).standard_normal(out[name].shape)
        drawn = base * np.exp(spread * noise) if base else spread * noise
        out[name] = jnp.asarray(drawn.astype(out[name].dtype))
    for name, factor in factors.items():
        out[name] = (out[name] * factor).astype(out[name].dtype)
    return out
```

```python
import numpy as np
import concourse.bass as bass
from concourse import mybir
from contextlib import ExitStack

F32 = mybir.dt.float32
BF16 = mybir.dt.bfloat16
ALU = mybir.AluOpType
ACT = mybir.ActivationFunctionType
AX = mybir.AxisListType

P = 128
B, HH, WW, C = 32, 16, 16, 192
T = HH * WW
TOK = B * T
TILES = TOK // P
HC = C // 2
EPS = 1e-5
E = 8


def counted(n):
    return n + 1


class Chain:

    def __init__(self, eng, sem, per=0, it=None):
        self.eng, self.sem, self.n, self.base = eng, sem, 0, (it * per if it is not None else 0)
        self.per = per

    def link(self, ins):
        self.n += 1
        ins.then_inc(self.sem, 1)
        self.eng.wait_ge(self.sem, self.base + self.n)

    def close(self):
        assert not self.per or self.n == self.per, (self.n, self.per)


class Mem:

    def __init__(self, nc, ctx, tag):
        self.nc, self.ctx, self.tag, self.sems = nc, ctx, tag, []

    def sb(self, name, shape, dt=F32):
        return self.ctx.enter_context(self.nc.sbuf_tensor(f"{self.tag}_{name}", shape, dt))

    def ps(self, name, shape, dt=F32):
        return self.ctx.enter_context(self.nc.psum_tensor(f"{self.tag}_{name}", shape, dt))

    def sem(self, name):
        self.sems.append(self.ctx.enter_context(self.nc.semaphore(f"{self.tag}_{name}")))
        return self.sems[-1]

    def clear(self):
        with self.nc.Block() as block:
            @block.gpsimd
            def _(pool):
                for s in self.sems:
                    pool.sem_clear(s)


def rstd_steps_act(nc, act, var_ready, half_log, moments, y0, eps_col):
    nc.scalar.activation(y0[:, 0, :], moments[:, :, 1], ACT.Ln, bias=eps_col).then_inc(half_log, 1)
    act.wait_ge(half_log, 1)
    nc.scalar.activation(y0[:, 1, :], y0[:, 0, :], ACT.Exp, scale=-0.5).then_inc(half_log, 1)


def rstd_steps_dve(nc, dve, chain, half_log, moments, y0, rstd, shift):
    dve.wait_ge(half_log, 2)
    chain.link(nc.vector.tensor_tensor(y0[:, 2, :], y0[:, 1, :], y0[:, 1, :], ALU.mult))
    chain.link(nc.vector.scalar_tensor_tensor(out=y0[:, 3, :], in0=moments[:, :, 1], scalar=EPS,
                                              in1=y0[:, 2, :], op0=ALU.add, op1=ALU.mult))
    chain.link(nc.vector.tensor_scalar(y0[:, 2, :], y0[:, 3, :], -0.5, 1.5, ALU.mult, ALU.add))
    chain.link(nc.vector.tensor_tensor(rstd[:, :], y0[:, 2, :], y0[:, 1, :], ALU.mult))
    return nc.vector.scalar_tensor_tensor(out=shift[:, :], in0=moments[:, :, 0], scalar=-1.0, in1=rstd[:, :],
                                          op0=ALU.mult, op1=ALU.mult)


def normalise(nc, xn, x_res, rstd, shift, tile):
    for t in range(2):
        at = bass.ds(tile + t, 1)
        ins = nc.scalar.activation(xn[:, t, :], x_res[:, at, :].rearrange("p a c -> p (a c)"), ACT.Identity,
                                   bias=shift[:, at], scale=rstd[:, at])
    return ins


def hold(eng, held):
    eng.sem_inc(held, 1)


def top2_select(nc, chain, held, val, m8, work, sel, ones8):
    v2 = m8[:, :, 1:2].broadcast_to([P, 2, E])
    gt, eq, cum, cnt = (work[:, k, :, :] for k in range(4))
    for t in range(2):
        hold(chain.eng, held)
        chain.link(nc.vector.max(m8[:, t, :], val[:, t, :]))
    chain.link(nc.vector.tensor_tensor(gt, val, v2, ALU.is_gt))
    chain.link(nc.vector.tensor_tensor(eq, val, v2, ALU.is_equal))
    chain.link(nc.vector.tensor_reduce(cnt[:, :, 0:1], gt, AX.X, ALU.add))
    for t in range(2):
        chain.link(nc.vector.tensor_tensor_scan(cum[:, t, :], ones8, eq[:, t, :], 0.0, ALU.mult, ALU.add))
    chain.link(nc.vector.tensor_tensor(cum, cum, cnt[:, :, 0:1].broadcast_to([P, 2, E]), ALU.add))
    chain.link(nc.vector.tensor_scalar(cum, cum, 2.5, None, ALU.is_lt))
    chain.link(nc.vector.tensor_tensor(eq, eq, cum, ALU.mult))
    chain.link(nc.vector.tensor_tensor(sel, eq, gt, ALU.add))


def x_pair(x_res, n):
    return x_res[:, bass.ds(2 * n, 2), :]


def pipelined(eng, first, rest, count=B):
    first(0, 0)
    with eng.Fori(0, count // 2 - 1) as it:
        rest(it * 2, 0, lambda: first(it * 2 + 1, 1))
        rest(it * 2 + 1, 1, lambda: first(it * 2 + 2, 0))
    rest(count - 2, 0, lambda: first(count - 1, 1))
    rest(count - 1, 1, lambda: None)


def tile_of(x_res, n, t):
    return x_res[:, bass.ds(n * 2 + t, 1), :].rearrange("p a c -> p (a c)")


def moe_relu_phase(nc, x_res, moments, consts, w):
    H = 768
    MC = H // P
    HB = MC // 2
    RING = 4
    with ExitStack() as ctx:
        m = Mem(nc, ctx, "l3f")
        w1 = m.sb("w1", [HC, 2, E, H])
        w2 = m.sb("w2", [P, MC, E, C])
        b1 = m.sb("b1", [P, E, MC])
        b2 = m.sb("b2", [E, C])
        wg = m.sb("wg", [HC, 2, E])
        rstd = m.sb("rstd", [P, TILES])
        shift = m.sb("shift", [P, TILES])
        y0 = m.sb("guess", [P, 4, TILES])
        xn = m.sb("xn", [P, 2, 2, C])
        tT = m.sb("tT", [HC, 2, 2, T])
        hT = m.sb("hT", [P, 2, MC, T])
        m8 = m.sb("m8", [P, 2, 8])
        work = m.sb("work", [P, 6, 2, E])
        gates = m.sb("gates", [P, 2, 2, E])
        gT = m.sb("gT", [E, 2, P])
        small = m.sb("small", [P, 4, 2])
        h_ps = [m.ps(f"h{k}", [P, 2, T]) for k in range(RING)]
        y_ps = [m.ps(f"y{k}", [P, 512]) for k in range(2)]
        tp = m.ps("tp", [P, 512])
        lg = m.ps("lg", [P, 512])
        tp_ps = tp[0:HC, :].rearrange("p (h t) -> p h t", h=2)
        lg_ps = lg[:, 0:2 * E].rearrange("p (t e) -> p t e", t=2)
        gt_ps = lg[0:E, 0:2 * P].rearrange("p (t k) -> p t k", t=2)

        weights_in = m.sem("weights_in")
        half_log = m.sem("half_log")
        dve_chain0 = m.sem("dve_chain0")
        rstd_ready = m.sem("rstd_ready")
        xn_ready = m.sem("xn_ready")
        tp_ready = m.sem("tp_ready")
        tT_ready = m.sem("tT_ready")
        logits_ready = m.sem("logits_ready")
        shifted = m.sem("shifted")
        exp_ready = m.sem("exp_ready")
        gates_ready = m.sem("gates_ready")
        gatesT_ps = m.sem("gatesT_ps")
        gatesT = m.sem("gatesT")
        h_ready = m.sem("h_ready")
        relu_done = m.sem("relu_done")
        y_ready = m.sem("y_ready")
        y_used = m.sem("y_used")
        gate_chain = m.sem("gate_chain")
        sum_chain = m.sem("sum_chain")
        dve_held = m.sem("dve_held")
        act_held = m.sem("act_held")

        with nc.Block() as block:
            @block.sync
            def _(sp):
                sp.dma_start(wg[:, :, :], w["wg"]).then_inc(weights_in, 16)
                sp.dma_start(b1[:, :, :], w["b1"]).then_inc(weights_in, 16)
                sp.dma_start(b2[:, :], w["b2"]).then_inc(weights_in, 16)
                sp.dma_start(w1[:, :, :, :], w["w1"]).then_inc(weights_in, 16)
                sp.dma_start(w2[:, :, :, :], w["w2"]).then_inc(weights_in, 16)

            @block.scalar
            def _(act):
                for s in (xn_ready, tT_ready, exp_ready, relu_done, gatesT):
                    act.sem_inc(s, 1)
                rstd_steps_act(nc, act, None, half_log, moments, y0, consts["eps"])
                act.wait_ge(rstd_ready, 1)
                act.wait_ge(weights_in, 80)
                hold(act, act_held)

                def normal(n, u):
                    normalise(nc, xn[:, u, :, :], x_res, rstd, shift, n * 2).then_inc(xn_ready, 1)
                    act.wait_ge(tp_ready, counted(n + 1))
                    nc.scalar.copy(tT[:, u, :, :], tp_ps).then_inc(tT_ready, 1)

                def gate(n, u):
                    act.wait_ge(shifted, counted(n + 1))
                    nc.scalar.activation(work[:, 5, :, :], work[:, 4, :, :], ACT.Exp).then_inc(exp_ready, 1)

                def first(n, u):
                    normal(n, u)
                    gate(n, u)

                def rest(n, u, nxt):
                    for e in range(E):
                        if e == 4:
                            nxt()
                        if e >= 2:
                            act.wait_ge(y_ready, counted(n * (E + 1) + (e - 1)))
                        else:
                            act.wait_ge(y_ready, counted(n * (E + 1)))
                        for c in range(MC):
                            q = e * HB + c // 2
                            if c % 2 == 0:
                                act.wait_ge(h_ready, counted(n * (E * HB) + (q + 1)))
                            ins = nc.scalar.activation(hT[:, e % 2, c, :], h_ps[q % RING][:, c % 2, :], ACT.Relu,
                                                       bias=b1[:, e, c:c + 1])
                            if c % 2:
                                ins.then_inc(relu_done, 1)
                        if e == 1:
                            act.wait_ge(gatesT_ps, counted(n + 1))
                            nc.scalar.copy(gT[:, :, :], gt_ps).then_inc(gatesT, 1)

                pipelined(act, first, rest)

            @block.vector
            def _(dve):
                chain0 = Chain(dve, dve_chain0)
                rstd_steps_dve(nc, dve, chain0, half_log, moments, y0, rstd, shift).then_inc(rstd_ready, 1)
                for s in (shifted, gates_ready, y_used):
                    dve.sem_inc(s, 1)

                def first(n, u):
                    chain = Chain(dve, gate_chain, 4 + 11, n)
                    link = chain.link
                    dve.wait_ge(logits_ready, counted(n + 1))
                    link(nc.vector.tensor_reduce(small[:, 0, :], lg_ps, AX.X, ALU.max))
                    nc.vector.tensor_tensor(work[:, 4, :, :], lg_ps,
                                            small[:, 0, :].unsqueeze(2).broadcast_to([P, 2, E]),
                                            ALU.subtract).then_inc(shifted, 1)
                    dve.wait_ge(exp_ready, counted(n + 1))
                    ex = work[:, 5, :, :]
                    link(nc.vector.tensor_reduce(small[:, 1, :], ex, AX.X, ALU.add))
                    link(nc.vector.reciprocal(small[:, 2, :], small[:, 1, :]))
                    link(nc.vector.tensor_tensor(ex, ex, small[:, 2, :].unsqueeze(2).broadcast_to([P, 2, E]),
                                                 ALU.mult))
                    top2_select(nc, chain, dve_held, ex, m8, work, gates[:, u, :, :], consts["ones8"])
                    nc.vector.tensor_tensor(gates[:, u, :, :], gates[:, u, :, :], ex, ALU.mult).then_inc(gates_ready, 1)
                    chain.close()

                def rest(n, u, nxt):
                    chain = Chain(dve, sum_chain, 2 * (E + 1), n)
                    dve.wait_ge(gates_ready, counted(n + 1))
                    for e in range(E + 1):
                        if e == 3:
                            nxt()
                        dve.wait_ge(y_ready, counted(n * (E + 1) + (e + 1)))
                        for t in range(2):
                            xt = tile_of(x_res, n, t)
                            yt = y_ps[(u + e) % 2][:, t * C:(t + 1) * C]
                            if e < E:
                                ins = nc.vector.scalar_tensor_tensor(out=xt, in0=yt, scalar=gates[:, u, t, e:e + 1],
                                                                     in1=xt, op0=ALU.mult, op1=ALU.add)
                            else:
                                ins = nc.vector.tensor_tensor(xt, yt, xt, ALU.add)
                            chain.link(ins)
                        dve.sem_inc(y_used, 1)
                    chain.close()

                pipelined(dve, first, rest)

            @block.tensor
            def _(pe):
                for s in (tp_ready, logits_ready, h_ready, y_ready, gatesT_ps):
                    pe.sem_inc(s, 1)
                pe.wait_ge(weights_in, 80)

                def first(n, u):
                    pe.wait_ge(xn_ready, counted(n + 1))
                    for h in range(2):
                        for t in range(2):
                            ins = nc.tensor.transpose(tp_ps[:, h, t * P:(t + 1) * P],
                                                      xn[:, u, t, h * HC:(h + 1) * HC], consts["ident"])
                    ins.then_inc(tp_ready, 1)
                    pe.wait_ge(tT_ready, counted(n + 1))
                    pe.wait_ge(gatesT, counted(n))
                    for t in range(2):
                        for h in range(2):
                            ins = nc.tensor.matmul(lg_ps[:, t, :], tT[:, u, h, t * P:(t + 1) * P], wg[:, h, :],
                                                   start=h == 0, stop=h == 1)
                    ins.then_inc(logits_ready, 1)

                def rest(n, u, nxt):
                    def y_bank(e):
                        if u == 0 and e == 0:
                            pe.wait_ge(y_used, counted(n * (E + 1)))
                        else:
                            pe.wait_ge(y_used, counted(n * (E + 1) + (e - 1)))
                        return y_ps[(u + e) % 2]

                    def second(e):
                        pe.wait_ge(relu_done, counted(n * (E * HB) + (e + 1) * HB))
                        y = y_bank(e)
                        for t in range(2):
                            for c in range(MC):
                                ins = nc.tensor.matmul(y[:, t * C:(t + 1) * C], hT[:, e % 2, c, t * P:(t + 1) * P],
                                                       w2[:, c, e, :], start=c == 0, stop=c == MC - 1)
                        ins.then_inc(y_ready, 1)

                    for e in range(E):
                        if e == 4:
                            nxt()
                        for c in range(MC):
                            q = e * HB + c // 2
                            if c % 2 == 0:
                                if q >= RING:
                                    pe.wait_ge(relu_done, counted(n * (E * HB) + (q - RING + 1)))
                                else:
                                    pe.wait_ge(relu_done, counted(n * (E * HB)))
                            for h in range(2):
                                ins = nc.tensor.matmul(h_ps[q % RING][:, c % 2, :], w1[:, h, e, c * P:(c + 1) * P],
                                                       tT[:, u, h, :], start=h == 0, stop=h == 1)
                            if c % 2:
                                ins.then_inc(h_ready, 1)
                        if e == 0:
                            pe.wait_ge(gates_ready, counted(n + 1))
                            for t in range(2):
                                ins = nc.tensor.transpose(gt_ps[:, t, :], gates[:, u, t, :], consts["ident"])
                            ins.then_inc(gatesT_ps, 1)
                        if e:
                            second(e - 1)
                    second(E - 1)
                    pe.wait_ge(gatesT, counted(n + 1))
                    y = y_bank(E)
                    for t in range(2):
                        ins = nc.tensor.matmul(y[:, t * C:(t + 1) * C], gT[:, t, :], b2[:, :], start=True, stop=True)
                    ins.then_inc(y_ready, 1)

                pipelined(pe, first, rest)
        m.clear()


def moe_glu_phase(nc, x_res, moments, consts, w):
    LIMIT = 7.0
    ALPHA = 1.702
    with ExitStack() as ctx:
        m = Mem(nc, ctx, "l2f")
        wgu = m.sb("wgu", [HC, 2, E, 4 * HC])
        wd = m.sb("wd", [HC, 2, E, C])
        bgu = m.sb("bgu", [HC, E, 4])
        bd = m.sb("bd", [E, C])
        wr = m.sb("wr", [HC, 2, E])
        br = m.sb("br", [P, E])
        rstd = m.sb("rstd", [P, TILES])
        shift = m.sb("shift", [P, TILES])
        y0 = m.sb("guess", [P, 4, TILES])
        xn = m.sb("xn", [P, 2, 2, C])
        tT = m.sb("tT", [HC, 2, 2, T])
        gate_in = m.sb("gate_in", [HC, 2, 2, T])
        up_in = m.sb("up_in", [HC, 2, 2, T])
        sig = m.sb("sig", [HC, 2, 2, T])
        aT = m.sb("aT", [HC, 2, 2, T])
        m8 = m.sb("m8", [P, 2, 8])
        work = m.sb("work", [P, 6, 2, E])
        logit = m.sb("logit", [P, 2, E])
        gates = m.sb("gates", [P, 2, 2, E])
        gT = m.sb("gT", [E, 2, P])
        small = m.sb("small", [P, 4, 2])
        gate_ps = [m.ps(f"gate{k}", [HC, 2, T]) for k in range(2)]
        up_ps = [m.ps(f"up{k}", [HC, 2, T]) for k in range(2)]
        y_ps = [m.ps(f"y{k}", [P, 512]) for k in range(2)]
        tp = m.ps("tp", [P, 512])
        lg = m.ps("lg", [P, 512])
        tp_ps = tp[0:HC, :].rearrange("p (h t) -> p h t", h=2)
        lg_ps = lg[:, 0:2 * E].rearrange("p (t e) -> p t e", t=2)
        gt_ps = lg[0:E, 0:2 * P].rearrange("p (t k) -> p t k", t=2)

        weights_in = m.sem("weights_in")
        half_log = m.sem("half_log")
        dve_chain0 = m.sem("dve_chain0")
        rstd_ready = m.sem("rstd_ready")
        xn_ready = m.sem("xn_ready")
        tp_ready = m.sem("tp_ready")
        tT_ready = m.sem("tT_ready")
        logits_ready = m.sem("logits_ready")
        shifted = m.sem("shifted")
        share_ready = m.sem("share_ready")
        gates_ready = m.sem("gates_ready")
        gatesT_ps = m.sem("gatesT_ps")
        gatesT = m.sem("gatesT")
        gate_ready = m.sem("gate_ready")
        up_ready = m.sem("up_ready")
        gate_clipped = m.sem("gate_clipped")
        up_clipped = m.sem("up_clipped")
        sig_ready = m.sem("sig_ready")
        glu_ready = m.sem("glu_ready")
        aT_ready = m.sem("aT_ready")
        y_ready = m.sem("y_ready")
        y_used = m.sem("y_used")
        gate_chain = m.sem("gate_chain")
        sum_chain = m.sem("sum_chain")
        clip_chain = m.sem("clip_chain")
        dve_held = m.sem("dve_held")
        act_held = m.sem("act_held")

        with nc.Block() as block:
            @block.sync
            def _(sp):
                sp.dma_start(wr[:, :, :], w["wr"]).then_inc(weights_in, 16)
                sp.dma_start(br[:, :], w["br"].partition_broadcast(P)).then_inc(weights_in, 16)
                sp.dma_start(bgu[:, :, :], w["bgu"]).then_inc(weights_in, 16)
                sp.dma_start(bd[:, :], w["bd"]).then_inc(weights_in, 16)
                sp.dma_start(wgu[:, :, :, :], w["wgu"]).then_inc(weights_in, 16)
                sp.dma_start(wd[:, :, :, :], w["wd"]).then_inc(weights_in, 16)

            @block.scalar
            def _(act):
                for s in (xn_ready, tT_ready, share_ready, sig_ready, gatesT):
                    act.sem_inc(s, 1)
                rstd_steps_act(nc, act, None, half_log, moments, y0, consts["eps"])
                act.wait_ge(rstd_ready, 1)
                hold(act, act_held)

                def first(n, u):
                    normalise(nc, xn[:, u, :, :], x_res, rstd, shift, n * 2).then_inc(xn_ready, 1)
                    act.wait_ge(tp_ready, counted(n + 1))
                    nc.scalar.copy(tT[:, u, :, :], tp_ps).then_inc(tT_ready, 1)
                    act.wait_ge(shifted, counted(n + 1))
                    nc.scalar.activation(work[:, 5, :, :], work[:, 4, :, :], ACT.Sigmoid).then_inc(share_ready, 1)

                def rest(n, u, nxt):
                    for e in range(E):
                        if e == 4:
                            nxt()
                        act.wait_ge(gate_clipped, counted(n * E + (e + 1)))
                        nc.scalar.activation(sig[:, e % 2, :, :], gate_in[:, e % 2, :, :], ACT.Sigmoid,
                                             scale=ALPHA).then_inc(sig_ready, 1)
                        if e == 1:
                            act.wait_ge(gatesT_ps, counted(n + 1))
                            nc.scalar.copy(gT[:, :, :], gt_ps).then_inc(gatesT, 1)

                pipelined(act, first, rest)

            @block.gpsimd
            def _(pool):
                for s in (glu_ready, aT_ready):
                    pool.sem_inc(s, 1)
                with pool.Fori(0, B) as n:
                    for e in range(E):
                        k = n * E + e
                        pool.wait_ge(sig_ready, counted(k + 1))
                        nc.gpsimd.tensor_tensor(sig[:, e % 2, :, :], gate_in[:, e % 2, :, :], sig[:, e % 2, :, :],
                                                ALU.mult).then_inc(glu_ready, 1)
                        pool.wait_ge(glu_ready, counted(k + 1))
                        pool.wait_ge(up_clipped, counted(k + 1))
                        pool.wait_ge(y_ready, counted(n * (E + 1) + max(e - 1, 0)))
                        nc.gpsimd.tensor_tensor(aT[:, e % 2, :, :], up_in[:, e % 2, :, :], sig[:, e % 2, :, :],
                                                ALU.mult).then_inc(aT_ready, 1)

            @block.vector
            def _(dve):
                chain0 = Chain(dve, dve_chain0)
                rstd_steps_dve(nc, dve, chain0, half_log, moments, y0, rstd, shift).then_inc(rstd_ready, 1)
                for s in (shifted, gates_ready, y_used, gate_clipped, up_clipped):
                    dve.sem_inc(s, 1)
                dve.wait_ge(weights_in, 96)

                def first(n, u):
                    chain = Chain(dve, gate_chain, 2 + 11, n)
                    link = chain.link
                    dve.wait_ge(logits_ready, counted(n + 1))
                    link(nc.vector.tensor_tensor(logit[:, :, :], lg_ps, br[:, :].unsqueeze(1).broadcast_to([P, 2, E]),
                                                 ALU.add))
                    top2_select(nc, chain, dve_held, logit[:, :, :], m8, work, gates[:, u, :, :], consts["ones8"])
                    link(nc.vector.tensor_tensor(small[:, 0, :], m8[:, :, 0], m8[:, :, 1], ALU.add))
                    nc.vector.scalar_tensor_tensor(out=work[:, 4, :, :], in0=logit[:, :, :], scalar=2.0,
                                                   in1=small[:, 0, :].unsqueeze(2).broadcast_to([P, 2, E]),
                                                   op0=ALU.mult, op1=ALU.subtract).then_inc(shifted, 1)
                    dve.wait_ge(share_ready, counted(n + 1))
                    nc.vector.tensor_tensor(gates[:, u, :, :], gates[:, u, :, :], work[:, 5, :, :],
                                            ALU.mult).then_inc(gates_ready, 1)
                    chain.close()

                def rest(n, u, nxt):
                    chain = Chain(dve, sum_chain, 2 * (E + 1), n)
                    clip = Chain(dve, clip_chain, 2 * E, n)
                    dve.wait_ge(gates_ready, counted(n + 1))

                    def add_up(e):
                        dve.wait_ge(y_ready, counted(n * (E + 1) + (e + 1)))
                        for t in range(2):
                            xt = tile_of(x_res, n, t)
                            yt = y_ps[(u + e) % 2][:, t * C:(t + 1) * C]
                            if e < E:
                                ins = nc.vector.scalar_tensor_tensor(out=xt, in0=yt, scalar=gates[:, u, t, e:e + 1],
                                                                     in1=xt, op0=ALU.mult, op1=ALU.add)
                            else:
                                ins = nc.vector.tensor_tensor(xt, yt, xt, ALU.add)
                            chain.link(ins)
                        dve.sem_inc(y_used, 1)

                    for e in range(E):
                        if e == 4:
                            nxt()
                        k = n * E + e
                        if e:
                            dve.wait_ge(aT_ready, counted(k - 1))
                        else:
                            dve.wait_ge(aT_ready, counted(k))
                        dve.wait_ge(gate_ready, counted(k + 1))
                        for c in range(2):
                            ins = nc.vector.tensor_scalar(gate_in[:, e % 2, c, :], gate_ps[e % 2][:, c, :],
                                                          bgu[:, e, c:c + 1], LIMIT, ALU.add, ALU.min)
                        ins.then_inc(gate_clipped, 1)
                        dve.wait_ge(up_ready, counted(k + 1))
                        for c in range(2):
                            clip.link(nc.vector.tensor_scalar(up_in[:, e % 2, c, :], up_ps[e % 2][:, c, :],
                                                              bgu[:, e, 2 + c:3 + c], LIMIT, ALU.add, ALU.min))
                        nc.vector.tensor_scalar(up_in[:, e % 2, :, :], up_in[:, e % 2, :, :], -LIMIT, 1.0,
                                                ALU.max, ALU.add).then_inc(up_clipped, 1)
                        if e:
                            add_up(e - 1)
                    add_up(E - 1)
                    add_up(E)
                    chain.close()
                    clip.close()

                pipelined(dve, first, rest)

            @block.tensor
            def _(pe):
                for s in (tp_ready, logits_ready, gate_ready, up_ready, y_ready, gatesT_ps):
                    pe.sem_inc(s, 1)
                pe.wait_ge(weights_in, 96)

                def first(n, u):
                    pe.wait_ge(xn_ready, counted(n + 1))
                    for h in range(2):
                        for t in range(2):
                            ins = nc.tensor.transpose(tp_ps[:, h, t * P:(t + 1) * P],
                                                      xn[:, u, t, h * HC:(h + 1) * HC], consts["ident"])
                    ins.then_inc(tp_ready, 1)
                    pe.wait_ge(tT_ready, counted(n + 1))
                    pe.wait_ge(gatesT, counted(n))
                    for t in range(2):
                        for h in range(2):
                            ins = nc.tensor.matmul(lg_ps[:, t, :], tT[:, u, h, t * P:(t + 1) * P], wr[:, h, :],
                                                   start=h == 0, stop=h == 1)
                    ins.then_inc(logits_ready, 1)

                def rest(n, u, nxt):
                    def y_bank(e):
                        if u == 0 and e == 0:
                            pe.wait_ge(y_used, counted(n * (E + 1)))
                        else:
                            pe.wait_ge(y_used, counted(n * (E + 1) + (e - 1)))
                        return y_ps[(u + e) % 2]

                    def second(e):
                        pe.wait_ge(aT_ready, counted(n * E + (e + 1)))
                        y = y_bank(e)
                        for t in range(2):
                            for h in range(2):
                                ins = nc.tensor.matmul(y[:, t * C:(t + 1) * C], aT[:, e % 2, h, t * P:(t + 1) * P],
                                                       wd[:, h, e, :], start=h == 0, stop=h == 1)
                        ins.then_inc(y_ready, 1)

                    for e in range(E):
                        if e == 4:
                            nxt()
                        k = n * E + e
                        for ps, free, ready, c0 in ((gate_ps, gate_clipped, gate_ready, 0),
                                                    (up_ps, up_clipped, up_ready, 2)):
                            pe.wait_ge(free, counted(k - 1) if e else counted(k))
                            for c in range(2):
                                for h in range(2):
                                    ins = nc.tensor.matmul(ps[e % 2][:, c, :],
                                                           wgu[:, h, e, (c0 + c) * HC:(c0 + c + 1) * HC],
                                                           tT[:, u, h, :], start=h == 0, stop=h == 1)
                            ins.then_inc(ready, 1)
                        if e == 0:
                            pe.wait_ge(gates_ready, counted(n + 1))
                            for t in range(2):
                                ins = nc.tensor.transpose(gt_ps[:, t, :], gates[:, u, t, :], consts["ident"])
                            ins.then_inc(gatesT_ps, 1)
                        if e:
                            second(e - 1)
                    second(E - 1)
                    pe.wait_ge(gatesT, counted(n + 1))
                    y = y_bank(E)
                    for t in range(2):
                        ins = nc.tensor.matmul(y[:, t * C:(t + 1) * C], gT[:, t, :], bd[:, :], start=True, stop=True)
                    ins.then_inc(y_ready, 1)

                pipelined(pe, first, rest)
        m.clear()


def memory_attention_phase(nc, x_res, moments, consts, w):
    M = 8
    SCALE = float(C) ** -0.5
    with ExitStack() as ctx:
        m = Mem(nc, ctx, "l3a")
        wq = m.sb("wq", [HC, 2, C])
        wk = m.sb("wk", [HC, 2, C])
        wv = m.sb("wv", [HC, 2, C])
        wo = m.sb("wo", [HC, 2, C])
        memT = m.sb("memT", [HC, 2, M])
        bq = m.sb("bq", [HC, 2])
        bk = m.sb("bk", [HC, 2])
        bv = m.sb("bv", [P, C])
        bo = m.sb("bo", [P, C])
        rstd = m.sb("rstd", [P, TILES])
        shift = m.sb("shift", [P, TILES])
        y0 = m.sb("guess", [P, 4, TILES])
        xn = m.sb("xn", [P, 2, 2, C])
        tT = m.sb("tT", [HC, 2, 2, T])
        qT = m.sb("qT", [HC, 2, 2, T])
        kT = [m.sb(f"kT{k}", [HC, 2, T + M]) for k in range(2)]
        v = m.sb("v", [P, 2, 2, C])
        vm = m.sb("vm", [M, C])
        top = m.sb("top", [P, 2, 2])
        sums = m.sb("sums", [P, 2, 2])
        probs = m.sb("probs", [P, 2, T + M])
        pT = m.sb("pT", [P, 2, T])
        pmT = m.sb("pmT", [M, T])
        oT = m.sb("oT", [HC, 2, T])
        tp = m.ps("tp", [P, 512])
        q_ps = m.ps("q", [HC, 2, T])
        k_ps = m.ps("k", [HC, 2, T])
        v_ps = m.ps("v_ps", [P, 512])
        s_ps = [m.ps(f"s{t}", [P, 512]) for t in range(2)]
        pT_ps = m.ps("pT_ps", [P, 2, T])
        pmT_ps = m.ps("pmT_ps", [P, 512])
        tp_ps = tp[0:HC, :].rearrange("p (h t) -> p h t", h=2)
        o_ps = q_ps
        y_ps = pmT_ps

        weights_in = m.sem("weights_in")
        half_log = m.sem("half_log")
        dve_chain0 = m.sem("dve_chain0")
        rstd_ready = m.sem("rstd_ready")
        xn_ready = m.sem("xn_ready")
        tp_ready = m.sem("tp_ready")
        tT_ready = m.sem("tT_ready")
        mem_ps = m.sem("mem_ps")
        mem_ready = m.sem("mem_ready")
        q_ready = m.sem("q_ready")
        k_ready = m.sem("k_ready")
        v_ready = m.sem("v_ready")
        qT_ready = m.sem("qT_ready")
        kT_ready = m.sem("kT_ready")
        vb_ready = m.sem("vb_ready")
        scores_ready = m.sem("scores_ready")
        max_ready = m.sem("max_ready")
        probs_ready = m.sem("probs_ready")
        pT_psum = m.sem("pT_psum")
        pT_ready = m.sem("pT_ready")
        pmT_ready = m.sem("pmT_ready")
        o_ready = m.sem("o_ready")
        oT_ready = m.sem("oT_ready")
        y_ready = m.sem("y_ready")
        y_used = m.sem("y_used")
        dve_chain = m.sem("dve_chain")
        act_held = m.sem("act_held")

        with nc.Block() as block:
            @block.sync
            def _(sp):
                for dst, src in ((memT[:, :, :], w["memT"]), (wk[:, :, :], w["wk"]), (wv[:, :, :], w["wv"]),
                                 (wq[:, :, :], w["wq"]), (wo[:, :, :], w["wo"]), (bq[:, :], w["bq"]),
                                 (bk[:, :], w["bk"]), (bv[:, :], w["bv"].partition_broadcast(P)),
                                 (bo[:, :], w["bo"].partition_broadcast(P))):
                    sp.dma_start(dst, src).then_inc(weights_in, 16)

            @block.scalar
            def _(act):
                for s in (xn_ready, tT_ready, qT_ready, kT_ready, probs_ready, oT_ready):
                    act.sem_inc(s, 1)
                rstd_steps_act(nc, act, None, half_log, moments, y0, consts["eps"])
                act.wait_ge(weights_in, 9 * 16)
                act.wait_ge(mem_ps, 1)
                for k in range(2):
                    for h in range(2):
                        nc.scalar.activation(kT[k][:, h, T:T + M], k_ps[:, h, 0:M], ACT.Identity,
                                             bias=bk[:, h:h + 1]).then_inc(mem_ready, 1)
                act.wait_ge(rstd_ready, 1)
                hold(act, act_held)

                def first(n, u):
                    normalise(nc, xn[:, u, :, :], x_res, rstd, shift, n * 2).then_inc(xn_ready, 1)
                    act.wait_ge(tp_ready, counted(n + 1))
                    nc.scalar.copy(tT[:, u, :, :], tp_ps).then_inc(tT_ready, 1)
                    act.wait_ge(q_ready, counted(n + 1))
                    for h in range(2):
                        ins = nc.scalar.activation(qT[:, u, h, :], q_ps[:, h, :], ACT.Identity, bias=bq[:, h:h + 1])
                    ins.then_inc(qT_ready, 1)
                    act.wait_ge(k_ready, counted(n + 1))
                    for h in range(2):
                        ins = nc.scalar.activation(kT[u][:, h, 0:T], k_ps[:, h, :], ACT.Identity, bias=bk[:, h:h + 1])
                    ins.then_inc(kT_ready, 1)

                def rest(n, u, nxt):
                    for t in range(2):
                        act.wait_ge(max_ready, counted(n * 2 + (t + 1)))
                        nc.scalar.activation(probs[:, t, :], s_ps[t][:, 0:T + M], ACT.Exp, bias=top[:, t, 1:2],
                                             scale=SCALE, accum_out=sums[:, t, 0:1]).then_inc(probs_ready, 1)
                    nxt()
                    act.wait_ge(o_ready, counted(n + 1))
                    nc.scalar.copy(oT[:, :, :], o_ps[:, :, :]).then_inc(oT_ready, 1)

                pipelined(act, first, rest)

            @block.vector
            def _(dve):
                chain0 = Chain(dve, dve_chain0)
                rstd_steps_dve(nc, dve, chain0, half_log, moments, y0, rstd, shift).then_inc(rstd_ready, 1)
                for s in (vb_ready, max_ready, pT_ready, pmT_ready, y_used):
                    dve.sem_inc(s, 1)
                dve.wait_ge(weights_in, 9 * 16)
                dve.wait_ge(mem_ps, 2)
                nc.vector.tensor_tensor(vm[:, :], v_ps[0:M, 0:C], bv[0:M, :], ALU.add).then_inc(mem_ready, 1)

                def first(n, u):
                    dve.wait_ge(v_ready, counted(n + 1))
                    nc.vector.tensor_tensor(v[:, u, :, :], v_ps[:, 0:2 * C].rearrange("p (t c) -> p t c", t=2),
                                            bv[:, :].unsqueeze(1).broadcast_to([P, 2, C]), ALU.add).then_inc(vb_ready, 1)

                def rest(n, u, nxt):
                    chain = Chain(dve, dve_chain, 2 + 1 + 4, n)
                    link = chain.link
                    for t in range(2):
                        dve.wait_ge(scores_ready, counted(n * 2 + (t + 1)))
                        link(nc.vector.tensor_reduce(top[:, t, 0:1], s_ps[t][:, 0:T + M], AX.X, ALU.max))
                        nc.vector.tensor_scalar(top[:, t, 1:2], top[:, t, 0:1], -SCALE, None,
                                                ALU.mult).then_inc(max_ready, 1)
                    nxt()
                    dve.wait_ge(pT_psum, counted(n + 1))
                    nc.vector.tensor_copy(pT[:, :, :], pT_ps[:, :, :]).then_inc(pT_ready, 1)
                    nc.vector.tensor_copy(pmT[:, :], pmT_ps[0:M, 0:T]).then_inc(pmT_ready, 1)
                    link(nc.vector.reciprocal(sums[:, :, 1], sums[:, :, 0]))
                    dve.wait_ge(y_ready, counted(n + 1))
                    for t in range(2):
                        xt = tile_of(x_res, n, t)
                        link(nc.vector.scalar_tensor_tensor(out=xt, in0=y_ps[:, t * C:(t + 1) * C],
                                                            scalar=sums[:, t, 1:2], in1=xt, op0=ALU.mult, op1=ALU.add))
                    for t in range(2):
                        xt = tile_of(x_res, n, t)
                        link(nc.vector.tensor_tensor(xt, xt, bo[:, :], ALU.add))
                    dve.sem_inc(y_used, 1)
                    chain.close()

                pipelined(dve, first, rest)

            @block.tensor
            def _(pe):
                for s in (tp_ready, q_ready, k_ready, v_ready, scores_ready, pT_psum, o_ready, y_ready):
                    pe.sem_inc(s, 1)
                pe.wait_ge(weights_in, 9 * 16)
                for ho in range(2):
                    for h in range(2):
                        ins = nc.tensor.matmul(k_ps[:, ho, 0:M], wk[:, h, ho * HC:(ho + 1) * HC], memT[:, h, :],
                                               start=h == 0, stop=h == 1)
                ins.then_inc(mem_ps, 1)
                for h in range(2):
                    ins = nc.tensor.matmul(v_ps[0:M, 0:C], memT[:, h, :], wv[:, h, :], start=h == 0, stop=h == 1)
                ins.then_inc(mem_ps, 1)
                pe.wait_ge(mem_ready, 5)

                def first(n, u):
                    pe.wait_ge(xn_ready, counted(n + 1))
                    for h in range(2):
                        for t in range(2):
                            ins = nc.tensor.transpose(tp_ps[:, h, t * P:(t + 1) * P],
                                                      xn[:, u, t, h * HC:(h + 1) * HC], consts["ident"])
                    ins.then_inc(tp_ready, 1)
                    pe.wait_ge(tT_ready, counted(n + 1))
                    for ps, wx, ready, free in ((q_ps, wq, q_ready, oT_ready), (k_ps, wk, k_ready, kT_ready)):
                        if free is oT_ready:
                            pe.wait_ge(free, counted(n) if isinstance(n, int) and n == 0 else counted(n - 1))
                        else:
                            pe.wait_ge(free, counted(n))
                        for ho in range(2):
                            for h in range(2):
                                ins = nc.tensor.matmul(ps[:, ho, :], wx[:, h, ho * HC:(ho + 1) * HC], tT[:, u, h, :],
                                                       start=h == 0, stop=h == 1)
                        ins.then_inc(ready, 1)
                    pe.wait_ge(vb_ready, counted(n))
                    for t in range(2):
                        for h in range(2):
                            ins = nc.tensor.matmul(v_ps[:, t * C:(t + 1) * C], tT[:, u, h, t * P:(t + 1) * P],
                                                   wv[:, h, :], start=h == 0, stop=h == 1)
                    ins.then_inc(v_ready, 1)

                def rest(n, u, nxt):
                    pe.wait_ge(qT_ready, counted(n + 1))
                    pe.wait_ge(kT_ready, counted(n + 1))
                    for t in range(2):
                        pe.wait_ge(probs_ready, counted(n * 2))
                        for h in range(2):
                            ins = nc.tensor.matmul(s_ps[t][:, 0:T + M], qT[:, u, h, t * P:(t + 1) * P], kT[u][:, h, :],
                                                   start=h == 0, stop=h == 1)
                        ins.then_inc(scores_ready, 1)
                    nxt()
                    pe.wait_ge(pT_ready, counted(n))
                    pe.wait_ge(y_used, counted(n))
                    for t in range(2):
                        pe.wait_ge(probs_ready, counted(n * 2 + (t + 1)))
                        for j in range(2):
                            nc.tensor.transpose(pT_ps[:, j, t * P:(t + 1) * P], probs[:, t, j * P:(j + 1) * P],
                                                consts["ident"])
                        ins = nc.tensor.transpose(pmT_ps[0:M, t * P:(t + 1) * P], probs[:, t, T:T + M], consts["ident"])
                    ins.then_inc(pT_psum, 1)
                    pe.wait_ge(pT_ready, counted(n + 1))
                    pe.wait_ge(pmT_ready, counted(n + 1))
                    pe.wait_ge(vb_ready, counted(n + 1))
                    pe.wait_ge(qT_ready, counted(n + 2) if not (isinstance(n, int) and n == B - 1) else counted(B))
                    for h in range(2):
                        for j in range(2):
                            nc.tensor.matmul(o_ps[:, h, :], v[:, u, j, h * HC:(h + 1) * HC], pT[:, j, :],
                                             start=j == 0, stop=False)
                        ins = nc.tensor.matmul(o_ps[:, h, :], vm[:, h * HC:(h + 1) * HC], pmT[:, :],
                                               start=False, stop=True)
                    ins.then_inc(o_ready, 1)
                    pe.wait_ge(oT_ready, counted(n + 1))
                    for t in range(2):
                        for h in range(2):
                            ins = nc.tensor.matmul(y_ps[:, t * C:(t + 1) * C], oT[:, h, t * P:(t + 1) * P], wo[:, h, :],
                                                   start=h == 0, stop=h == 1)
                    ins.then_inc(y_ready, 1)

                pipelined(pe, first, rest)
        m.clear()


def fourier_phase(nc, x_res, moments, consts, w):
    MODES = HH * (WW // 2 + 1)
    MH = MODES // 2
    LAMBDA = 0.01
    with ExitStack() as ctx:
        m = Mem(nc, ctx, "l1")
        dft = m.sb("dft", [P, 2, 2 * MODES])
        idft = m.sb("idft", [MH, 2, 2, T])
        w1 = m.sb("w1", [HC, 3, 2, HC])
        w2 = m.sb("w2", [HC, 2, 3, HC])
        b1 = m.sb("b1", [HC, 2, 2])
        b2 = m.sb("b2", [MH, 2, 2, HC])
        xs = m.sb("xs", [P, 2, 2, C])
        spec = m.sb("spec", [HC, 2, 2, 2 * MODES])
        o1 = m.sb("o1", [HC, 2, 2 * MODES])
        o2 = m.sb("o2", [MH, 2, 2, 2, HC])
        clip = m.sb("clip", [MH, 2, 2, 2, HC])
        o3 = m.sb("o3", [MH, 2, 2, 2, HC])
        spec_ps = [m.ps(f"spec{h}", [P, 512]) for h in range(2)]
        o1_ps = [m.ps(f"o1_{h}", [P, 512]) for h in range(2)]
        o2_ps = [m.ps(f"o2_{h}", [P, 512]) for h in range(2)]
        y_ps = m.ps("y", [P, 512])

        weights_in = m.sem("weights_in")
        negated = m.sem("negated")
        xs_ready = m.sem("xs_ready")
        spec_psum = m.sem("spec_psum")
        spec_ready = m.sem("spec_ready")
        o1_psum = m.sem("o1_psum")
        o1_ready = m.sem("o1_ready")
        o2_psum = m.sem("o2_psum")
        biased = m.sem("biased")
        clipped = m.sem("clipped")
        o3_ready = m.sem("o3_ready")
        y_ready = m.sem("y_ready")
        y_used = m.sem("y_used")

        with nc.Block() as block:
            @block.sync
            def _(sp):
                for dst, src in ((dft[:, :, :], w["dft"]), (w1[:, 0:2, :, :], w["w1"]), (w2[:, :, 1:3, :], w["w2"]),
                                 (b1[:, :, :], w["b1"]), (b2[:, :, :, :], w["b2"].partition_broadcast(MH)),
                                 (idft[:, :, :, :], w["idft"])):
                    sp.dma_start(dst, src).then_inc(weights_in, 16)

            @block.scalar
            def _(act):
                for s in (xs_ready, spec_ready, o1_ready):
                    act.sem_inc(s, 1)
                act.wait_ge(weights_in, 6 * 16)

                def first(n, u):
                    nc.scalar.copy(xs[:, u, :, :], x_res[:, bass.ds(n * 2, 2), :]).then_inc(xs_ready, 1)
                    for h in range(2):
                        act.wait_ge(spec_psum, counted(n * 2 + (h + 1)))
                        nc.scalar.copy(spec[:, u, h, :], spec_ps[h][0:HC, 0:2 * MODES]).then_inc(spec_ready, 1)

                def rest(n, u, nxt):
                    for h in range(2):
                        act.wait_ge(o1_psum, counted(n * 2 + (h + 1)))
                        for ri in range(2):
                            at = slice(ri * MODES, (ri + 1) * MODES)
                            ins = nc.scalar.activation(o1[:, h, at], o1_ps[h][0:HC, at], ACT.Relu,
                                                       bias=b1[:, h, ri:ri + 1])
                        ins.then_inc(o1_ready, 1)
                    nxt()

                pipelined(act, first, rest)

            @block.gpsimd
            def _(pool):
                pool.sem_inc(o3_ready, 1)
                with pool.Fori(0, B) as n:
                    pool.wait_ge(clipped, counted(n * 2 + 2))
                    pool.wait_ge(y_ready, counted(n))
                    nc.gpsimd.tensor_tensor(o3[:, :, :, :, :], o2[:, :, :, :, :], clip[:, :, :, :, :],
                                            ALU.subtract).then_inc(o3_ready, 1)

            @block.vector
            def _(dve):
                for s in (biased, clipped, y_used):
                    dve.sem_inc(s, 1)
                dve.wait_ge(weights_in, 6 * 16)
                nc.vector.tensor_scalar(w1[:, 2, :, :], w1[:, 1, :, :], -1.0, None, ALU.mult).then_inc(negated, 1)
                nc.vector.tensor_scalar(w2[:, :, 0, :], w2[:, :, 2, :], -1.0, None, ALU.mult).then_inc(negated, 1)

                def first(n, u):
                    pass

                def rest(n, u, nxt):
                    dve.wait_ge(o3_ready, counted(n))
                    for q in range(2):
                        dve.wait_ge(o2_psum, counted(n * 2 + (q + 1)))
                        nc.vector.tensor_tensor(o2[:, q, :, :, :],
                                                o2_ps[q][0:MH, 0:2 * C].rearrange("p (h r c) -> p h r c", h=2, r=2),
                                                b2[:, :, :, :], ALU.add).then_inc(biased, 1)
                        dve.wait_ge(biased, counted(n * 2 + (q + 1)))
                        nc.vector.tensor_scalar(clip[:, q, :, :, :], o2[:, q, :, :, :], LAMBDA, -LAMBDA,
                                                ALU.min, ALU.max).then_inc(clipped, 1)
                    dve.wait_ge(y_ready, counted(n + 1))
                    xt = x_res[:, bass.ds(n * 2, 2), :]
                    nc.vector.tensor_tensor(xt, y_ps[:, 0:2 * C].rearrange("p (t c) -> p t c", t=2), xt,
                                            ALU.add).then_inc(y_used, 1)

                pipelined(dve, first, rest)

            @block.tensor
            def _(pe):
                for s in (spec_psum, o1_psum, o2_psum, y_ready):
                    pe.sem_inc(s, 1)
                pe.wait_ge(weights_in, 6 * 16)
                pe.wait_ge(negated, 2)

                def first(n, u):
                    pe.wait_ge(xs_ready, counted(n + 1))
                    for h in range(2):
                        pe.wait_ge(spec_ready, counted(n * 2 + (h + 1) - 2) if h else counted(n * 2))
                        for t in range(2):
                            ins = nc.tensor.matmul(spec_ps[h][0:HC, 0:2 * MODES], xs[:, u, t, h * HC:(h + 1) * HC],
                                                   dft[:, t, :], start=t == 0, stop=t == 1)
                        ins.then_inc(spec_psum, 1)

                def rest(n, u, nxt):
                    re, im = slice(0, MODES), slice(MODES, 2 * MODES)
                    for h in range(2):
                        pe.wait_ge(spec_ready, counted(n * 2 + (h + 1)))
                        pe.wait_ge(o1_ready, counted(n * 2))
                        o = o1_ps[h][0:HC, :]
                        s = spec[:, u, h, :]
                        nc.tensor.matmul(o[:, 0:2 * MODES], w1[:, 0, h, :], s, start=True, stop=False,
                                         skip_group_check=True)
                        nc.tensor.matmul(o[:, re], w1[:, 2, h, :], s[:, im], start=False, stop=False,
                                         skip_group_check=True)
                        nc.tensor.matmul(o[:, im], w1[:, 1, h, :], s[:, re], start=False, stop=True,
                                         skip_group_check=True).then_inc(o1_psum, 1)
                    nxt()
                    pe.wait_ge(o1_ready, counted(n * 2 + 2))
                    for q in range(2):
                        pe.wait_ge(biased, counted(n * 2))
                        for h in range(2):
                            o = o2_ps[q][0:MH, h * C:(h + 1) * C]
                            for ri in range(2):
                                rhs = w2[:, h, 1:3, :] if ri == 0 else w2[:, h, 0:2, :]
                                lhs = o1[:, h, ri * MODES + q * MH:ri * MODES + (q + 1) * MH]
                                ins = nc.tensor.matmul(o, lhs, rhs, start=ri == 0, stop=ri == 1)
                        ins.then_inc(o2_psum, 1)
                    pe.wait_ge(o3_ready, counted(n + 1))
                    pe.wait_ge(y_used, counted(n))
                    for t in range(2):
                        for k in range(4):
                            q, ri = k // 2, k % 2
                            ins = nc.tensor.matmul(y_ps[:, t * C:(t + 1) * C], idft[:, q, ri, t * P:(t + 1) * P],
                                                   o3[:, q, :, ri, :], start=k == 0, stop=k == 3)
                    ins.then_inc(y_ready, 1)

                pipelined(pe, first, rest)
        m.clear()


def mamba_phase(nc, x_res, moments, consts, w):
    R, DI, NS, DC, DTR = 48, 96, 16, 4, 12
    CH = 512
    CHUNKS = TOK // CH
    CT = CH // P
    ATANH = [2.0 / (2 * k + 1) for k in range(8)]
    DG = P // NS
    G = DI // DG
    with ExitStack() as ctx:
        m = Mem(nc, ctx, "l0")
        down = m.sb("down", [HC, 2, R])
        inp = m.sb("inp", [R, 2 * DI])
        convw = m.sb("convw", [DI, DC])
        cols = m.sb("cols", [DI, 3])
        xdt = m.sb("xdt", [DI, DTR])
        xb = m.sb("xb", [DI, 2, DG, NS])
        dtw = m.sb("dtw", [DTR, DI])
        a_col = m.sb("a_col", [P, G])
        sel = m.sb("sel", [DI, G, P])
        selT = m.sb("selT", [P, G, DI])
        outp = m.sb("outp", [DI, R])
        up = m.sb("up", [R, C])
        ln_g = m.sb("ln_g", [P, R])
        ln_b = m.sb("ln_b", [P, R])
        keep = m.sb("keep", [P, CHUNKS])
        xT = m.sb("xT", [HC, 2, 2, CH])
        xsT = m.sb("xsT", [R, CH])
        xi = m.sb("xi", [DI, 2, DC - 1 + CH])
        conv = m.sb("conv", [DI, 2, CH])
        u_sb = m.sb("u", [DI, 2, CH])
        zs = m.sb("zs", [DI, 2, CH])
        dt_sb = m.sb("dt", [DTR, CH])
        bc = m.sb("bc", [P, 2, 2, CH])
        sp_a = m.sb("sp_a", [DI, 6, CH])
        delta = m.sb("delta", [DI, 2, CH])
        du = m.sb("du", [DI, 2, CH])
        dA = m.sb("dA", [P, 2, CH])
        dBu = m.sb("dBu", [P, 2, CH])
        hs = m.sb("hs", [P, 2, CH])
        hc = m.sb("hc", [P, 2, CH])
        state = m.sb("state", [P, 1, G])
        yy = m.sb("yy", [DI, 2, CH])
        mm = m.sb("mm", [P, 2, CT, R])
        mg = m.sb("mg", [P, CT, R])
        mT = m.sb("mT", [R, CH])
        bns = m.sb("bns", [P, CT, 6])
        mom = m.sb("mom", [P, CT, 2])
        sm = m.sb("sm", [P, 6, CT])
        one = m.sb("one", [P, 1])
        drep_ps = [m.ps(f"drep{k}", [P, CH]) for k in range(2)]
        urep_ps = [m.ps(f"urep{k}", [P, CH]) for k in range(2)]
        y_ps = m.ps("y", [DI, CH])
        g_ps = [m.ps(f"g{k}", [P, CH]) for k in range(3)]

        weights_in = m.sem("weights_in")
        setup = m.sem("setup")
        xT_in = m.sem("xT_in")
        front_ps = m.sem("front_ps")
        front_sb = m.sem("front_sb")
        act_front = m.sem("act_front")
        conv_ready = m.sem("conv_ready")
        silu_ready = m.sem("silu_ready")
        ea_ready = m.sem("ea_ready")
        soft_ready = m.sem("soft_ready")
        delta_ready = m.sem("delta_ready")
        du_ready = m.sem("du_ready")
        drep_ready = m.sem("drep_ready")
        urep_ready = m.sem("urep_ready")
        dA_ready = m.sem("dA_ready")
        dBu_ready = m.sem("dBu_ready")
        scan_ready = m.sem("scan_ready")
        state_ready = m.sem("state_ready")
        hc_ready = m.sem("hc_ready")
        hc_used = m.sem("hc_used")
        y_gated = m.sem("y_gated")
        m_ready = m.sem("m_ready")
        var_ready = m.sem("var_ready")
        guess_ready = m.sem("guess_ready")
        ln_ready = m.sem("ln_ready")
        gelu_ready = m.sem("gelu_ready")
        mT_ps = m.sem("mT_ps")
        mT_ready = m.sem("mT_ready")
        up_ready = m.sem("up_ready")
        x_added = m.sem("x_added")
        conv_chain = m.sem("conv_chain")
        tail_chain = m.sem("tail_chain")
        act_chain = m.sem("act_chain")
        act_held = m.sem("act_held")
        dve_held = m.sem("dve_held")
        pe_held = m.sem("pe_held")
        sp_held = m.sem("sp_held")

        loads = ((down[:, :, :], w["down"]), (inp[:, :], w["inp"]), (convw[:, :], w["convw"]), (cols[:, :], w["cols"]),
                 (xdt[:, :], w["xdt"]), (xb[:, :, :, :], w["xb"]), (dtw[:, :], w["dtw"]), (a_col[:, :], w["alog"]),
                 (sel[:, :, :], w["sel"]), (selT[:, :, :], w["selT"]), (outp[:, :], w["outp"]), (up[:, :], w["up"]),
                 (ln_g[:, :], w["lng"].partition_broadcast(P)), (ln_b[:, :], w["lnb"].partition_broadcast(P)),
                 (keep[:, :], w["keep"].partition_broadcast(P)))
        FRONT = 5

        with nc.Block() as block:
            @block.sync
            def _(sp):
                for dst, src in loads:
                    sp.dma_start(dst, src).then_inc(weights_in, 16)

                def load(n, u):
                    sp.dma_start(xT[:, u, :, :], w["xT"][:, :, bass.ds(n * CH, CH)]).then_inc(xT_in, 16)

                load(0, 0)
                sp.wait_ge(xT_in, 16)
                load(1, 1)
                sp.wait_ge(xT_in, 32)
                with sp.Fori(0, CHUNKS // 2 - 1) as it:
                    for u in range(2):
                        sp.wait_ge(front_ps, counted(it * 14 + (7 * u + 1)))
                        hold(sp, sp_held)
                        load(it * 2 + (2 + u), u)
                        sp.wait_ge(xT_in, it * 32 + (48 + 16 * u))
                        hold(sp, sp_held)

            @block.scalar
            def _(act):
                act.wait_ge(weights_in, len(loads) * 16)
                nc.scalar.activation(a_col[:, :], a_col[:, :], ACT.Exp).then_inc(setup, 1)
                for s in (act_front, silu_ready, ea_ready, soft_ready, dA_ready, guess_ready, gelu_ready, mT_ready,
                          state_ready):
                    act.sem_inc(s, 1)
                act.wait_ge(setup, 4)
                hold(act, act_held)

                def first(n, u):
                    def bank(k):
                        act.wait_ge(front_ps, counted(n * 7 + (k + 1)))
                    bank(0)
                    nc.scalar.copy(xsT[:, :], g_ps[0][0:R, :]).then_inc(act_front, 1)
                    bank(1)
                    nc.scalar.copy(xi[:, u, DC - 1:], g_ps[1][0:DI, :]).then_inc(act_front, 1)
                    bank(2)
                    nc.scalar.activation(zs[:, u, :], g_ps[2][0:DI, :], ACT.Silu).then_inc(act_front, 1)
                    act.wait_ge(conv_ready, counted(n + 1))
                    nc.scalar.activation(u_sb[:, u, :], conv[:, 1, :], ACT.Silu).then_inc(silu_ready, 1)
                    bank(3)
                    nc.scalar.copy(dt_sb[:, :], g_ps[0][0:DTR, :]).then_inc(act_front, 1)
                    for k in range(2):
                        bank(4 + k)
                        nc.scalar.copy(bc[:, u, k, :], g_ps[1 + k][:, :]).then_inc(act_front, 1)
                    bank(6)
                    chain = Chain(act, act_chain, 2, n)
                    nc.scalar.activation(sp_a[:, 0, :], g_ps[0][0:DI, :], ACT.Identity,
                                         bias=cols[:, 1:2]).then_inc(act_front, 1)
                    act.wait_ge(act_front, counted(n * 7 + 7))
                    chain.link(nc.scalar.activation(sp_a[:, 1, :], sp_a[:, 0, :], ACT.Abs))
                    chain.link(nc.scalar.activation(sp_a[:, 2, :], sp_a[:, 1, :], ACT.Exp, scale=-1.0))
                    act.sem_inc(soft_ready, 1)
                    chain.close()

                def rest(n, u, nxt):
                    for g in range(G):
                        if g == G // 2:
                            nxt()
                        k = n * G + g
                        act.wait_ge(drep_ready, counted(k + 1))
                        act.wait_ge(scan_ready, counted(k - 1) if g else counted(k))
                        nc.scalar.activation(dA[:, g % 2, :], drep_ps[g % 2][:, :], ACT.Exp,
                                             scale=a_col[:, g:g + 1]).then_inc(dA_ready, 1)
                    act.wait_ge(var_ready, counted(n + 1))
                    nc.scalar.activation(sm[:, 0, :], mom[:, :, 1], ACT.Ln, bias=consts["eps"]).then_inc(ea_ready, 1)
                    act.wait_ge(ea_ready, counted(n + 1))
                    nc.scalar.activation(sm[:, 1, :], sm[:, 0, :], ACT.Exp, scale=-0.5).then_inc(guess_ready, 1)
                    act.wait_ge(ln_ready, counted(n + 1))
                    nc.scalar.activation(mg[:, :, :], mm[:, 0, :, :], ACT.Gelu).then_inc(gelu_ready, 1)
                    act.wait_ge(mT_ps, counted(n + 1))
                    nc.scalar.copy(mT[:, :], g_ps[1][0:R, :]).then_inc(mT_ready, 1)

                pipelined(act, first, rest, CHUNKS)

            @block.gpsimd
            def _(pool):
                pool.sem_inc(hc_ready, 1)
                pool.sem_inc(du_ready, 1)

                def first(n, u):
                    pool.wait_ge(delta_ready, counted(n + 1))
                    nc.gpsimd.tensor_tensor(du[:, u, :], delta[:, u, :], u_sb[:, u, :], ALU.mult).then_inc(du_ready, 1)

                def rest(n, u, nxt):
                    for g in range(G):
                        if g == G // 2 + 1:
                            nxt()
                        k = n * G + g
                        pool.wait_ge(scan_ready, counted(k + 1))
                        pool.wait_ge(hc_used, counted(k - 1) if g else counted(k))
                        nc.gpsimd.tensor_tensor(hc[:, g % 2, :], hs[:, g % 2, :], bc[:, u, 1, :],
                                                ALU.mult).then_inc(hc_ready, 1)

                pipelined(pool, first, rest, CHUNKS)

            @block.vector
            def _(dve):
                for s in (front_sb, conv_ready, delta_ready, dBu_ready, scan_ready, y_gated, var_ready, ln_ready,
                          x_added):
                    dve.sem_inc(s, 1)
                dve.wait_ge(setup, 1)
                nc.vector.tensor_scalar(a_col[:, :], a_col[:, :], -1.0, None, ALU.mult).then_inc(setup, 1)
                nc.vector.memset(xi[:, :, :], 0.0).then_inc(setup, 1)
                nc.vector.memset(one[:, :], 1.0)
                nc.vector.memset(state[:, :, :], 0.0).then_inc(setup, 1)
                dve.wait_ge(setup, 4)

                def first(n, u):
                    chain = Chain(dve, conv_chain, 1 + DC + 4 + len(ATANH), n)
                    chain.link(nc.vector.tensor_scalar(xi[:, u, 0:DC - 1], xi[:, 1 - u, CH:CH + DC - 1],
                                                       keep[0:DI, bass.ds(n, 1)], None, ALU.mult))
                    dve.wait_ge(act_front, counted(n * 7 + 2))
                    chain.link(nc.vector.tensor_scalar(conv[:, 0, :], xi[:, u, 0:CH], convw[:, 0:1], cols[:, 0:1],
                                                       ALU.mult, ALU.add))
                    for k in range(1, DC):
                        chain.link(nc.vector.scalar_tensor_tensor(out=conv[:, k % 2, :], in0=xi[:, u, k:k + CH],
                                                                  scalar=convw[:, k:k + 1], in1=conv[:, (k + 1) % 2, :],
                                                                  op0=ALU.mult, op1=ALU.add))
                    dve.sem_inc(conv_ready, 1)
                    dve.wait_ge(soft_ready, counted(n + 1))
                    v, a, wexp, s, q, acc = (sp_a[:, k, :] for k in range(6))
                    chain.link(nc.vector.tensor_scalar(a, wexp, 2.0, None, ALU.add))
                    chain.link(nc.vector.reciprocal(s, a))
                    chain.link(nc.vector.tensor_tensor(s, s, wexp, ALU.mult))
                    chain.link(nc.vector.tensor_tensor(q, s, s, ALU.mult))
                    chain.link(nc.vector.tensor_scalar(acc, q, ATANH[-1], None, ALU.mult))
                    for c in ATANH[-2:0:-1]:
                        chain.link(nc.vector.scalar_tensor_tensor(out=acc, in0=acc, scalar=c, in1=q, op0=ALU.add,
                                                                  op1=ALU.mult))
                    chain.link(nc.vector.scalar_tensor_tensor(out=acc, in0=acc, scalar=ATANH[0], in1=s, op0=ALU.add,
                                                              op1=ALU.mult))
                    nc.vector.scalar_tensor_tensor(out=delta[:, u, :], in0=v, scalar=0.0,
                                                   in1=acc, op0=ALU.max, op1=ALU.add).then_inc(delta_ready, 1)
                    chain.close()

                def rest(n, u, nxt):
                    chain = Chain(dve, tail_chain, G + 1 + 2 * CT + 1 + 6, n)
                    for g in range(G):
                        if g == G // 2:
                            nxt()
                        k = n * G + g
                        dve.wait_ge(urep_ready, counted(k + 1))
                        nc.vector.tensor_tensor(dBu[:, g % 2, :], urep_ps[g % 2][:, :], bc[:, u, 0, :],
                                                ALU.mult).then_inc(dBu_ready, 1)
                        chain.link(nc.vector.tensor_scalar(state[:, 0, g:g + 1], state[:, 0, g:g + 1],
                                                           keep[:, bass.ds(n, 1)], None, ALU.mult))
                        dve.wait_ge(dBu_ready, counted(k + 1))
                        dve.wait_ge(dA_ready, counted(k + 1))
                        dve.wait_ge(hc_ready, counted(k - 1) if g else counted(k))
                        nc.vector.tensor_tensor_scan(hs[:, g % 2, :], dA[:, g % 2, :], dBu[:, g % 2, :],
                                                     state[:, 0, g:g + 1], ALU.mult, ALU.add).then_inc(scan_ready, 1)
                        dve.wait_ge(scan_ready, counted(k + 1))
                        nc.vector.tensor_copy(state[:, 0, g:g + 1], hs[:, g % 2, CH - 1:CH]).then_inc(state_ready, 1)
                        dve.wait_ge(state_ready, counted(k + 1))
                    dve.wait_ge(hc_used, counted(n * G + G))
                    chain.link(nc.vector.scalar_tensor_tensor(out=yy[:, 0, :], in0=u_sb[:, u, :], scalar=cols[:, 2:3],
                                                              in1=y_ps[:, :], op0=ALU.mult, op1=ALU.add))
                    nc.vector.tensor_tensor(yy[:, 1, :], yy[:, 0, :], zs[:, u, :], ALU.mult).then_inc(y_gated, 1)
                    dve.wait_ge(m_ready, counted(n + 1))
                    m_ps = g_ps[0][:, 0:CT * R].rearrange("p (t r) -> p t r", t=CT)
                    for t in range(CT):
                        hold(dve, dve_held)
                        chain.link(nc.vector.bn_stats(bns[:, t, :], m_ps[:, t, :]))
                    for t in range(CT):
                        hold(dve, dve_held)
                        chain.link(nc.vector.bn_aggr(mom[:, t, :], bns[:, t, :]))
                    dve.sem_inc(var_ready, 1)
                    chain.link(nc.vector.tensor_tensor(mm[:, 0, :, :], m_ps,
                                                       mom[:, :, 0:1].broadcast_to([P, CT, R]), ALU.subtract))
                    dve.wait_ge(guess_ready, counted(n + 1))
                    y = sm[:, 1, :]
                    chain.link(nc.vector.tensor_tensor(sm[:, 2, :], y, y, ALU.mult))
                    chain.link(nc.vector.scalar_tensor_tensor(out=sm[:, 3, :], in0=mom[:, :, 1], scalar=EPS,
                                                              in1=sm[:, 2, :], op0=ALU.add, op1=ALU.mult))
                    chain.link(nc.vector.tensor_scalar(sm[:, 4, :], sm[:, 3, :], -0.5, 1.5, ALU.mult, ALU.add))
                    chain.link(nc.vector.tensor_tensor(sm[:, 5, :], sm[:, 4, :], y, ALU.mult))
                    chain.link(nc.vector.tensor_tensor(mm[:, 1, :, :], mm[:, 0, :, :],
                                                       sm[:, 5, :].unsqueeze(2).broadcast_to([P, CT, R]), ALU.mult))
                    chain.link(nc.vector.tensor_tensor(mm[:, 1, :, :], mm[:, 1, :, :],
                                                       ln_g[:, :].unsqueeze(1).broadcast_to([P, CT, R]), ALU.mult))
                    nc.vector.tensor_tensor(mm[:, 0, :, :], mm[:, 1, :, :],
                                            ln_b[:, :].unsqueeze(1).broadcast_to([P, CT, R]),
                                            ALU.add).then_inc(ln_ready, 1)
                    for k in range(2):
                        dve.wait_ge(up_ready, counted(n * 2 + (k + 1)))
                        xt = x_res[:, bass.ds(n * CT + 2 * k, 2), :]
                        u_ps = (g_ps[2], g_ps[0])[k]
                        nc.vector.tensor_tensor(xt, u_ps[:, 0:2 * C].rearrange("p (t c) -> p t c", t=2), xt,
                                                ALU.add).then_inc(x_added, 1)
                    chain.close()

                pipelined(dve, first, rest, CHUNKS)

            @block.tensor
            def _(pe):
                for s in (front_ps, drep_ready, urep_ready, hc_used, m_ready, mT_ps, up_ready):
                    pe.sem_inc(s, 1)
                pe.wait_ge(weights_in, len(loads) * 16)

                def first(n, u):
                    pe.wait_ge(xT_in, n * 16 + 16)
                    if isinstance(n, int) and n == 0:
                        pass
                    else:
                        pe.wait_ge(x_added, counted(n * 2 - 2))
                    for h in range(2):
                        ins = nc.tensor.matmul(g_ps[0][0:R, :], down[:, h, :], xT[:, u, h, :], start=h == 0, stop=h == 1)
                    ins.then_inc(front_ps, 1)
                    pe.wait_ge(act_front, counted(n * 7 + 1))
                    for k in range(2):
                        nc.tensor.matmul(g_ps[1 + k][0:DI, :], inp[:, k * DI:(k + 1) * DI], xsT[:, :], start=True,
                                         stop=True).then_inc(front_ps, 1)
                    pe.wait_ge(act_front, counted(n * 7 + 3))
                    pe.wait_ge(silu_ready, counted(n + 1))
                    nc.tensor.matmul(g_ps[0][0:DTR, :], xdt[:, :], u_sb[:, u, :], start=True,
                                     stop=True).then_inc(front_ps, 1)
                    for k in range(2):
                        nc.tensor.matmul(g_ps[1 + k][:, :], xb[:, k, :, :], u_sb[:, u, :], start=True,
                                         stop=True).then_inc(front_ps, 1)
                    pe.wait_ge(act_front, counted(n * 7 + 4))
                    nc.tensor.matmul(g_ps[0][0:DI, :], dtw[:, :], dt_sb[:, :], start=True,
                                     stop=True).then_inc(front_ps, 1)

                def rest(n, u, nxt):
                    pe.wait_ge(delta_ready, counted(n + 1))
                    pe.wait_ge(du_ready, counted(n + 1))
                    pe.wait_ge(y_gated, counted(n))

                    def add_states(g):
                        pe.wait_ge(hc_ready, counted(n * G + (g + 1)))
                        nc.tensor.matmul(y_ps[:, :], selT[:, g, :], hc[:, g % 2, :], start=g == 0,
                                         stop=g == G - 1).then_inc(hc_used, 1)

                    for g in range(G):
                        if g == G // 2 + 1:
                            nxt()
                        k = n * G + g
                        pe.wait_ge(dA_ready, counted(k - 1) if g else counted(k))
                        nc.tensor.matmul(drep_ps[g % 2][:, :], sel[:, g, :], delta[:, u, :], start=True,
                                         stop=True).then_inc(drep_ready, 1)
                        pe.wait_ge(dBu_ready, counted(k - 1) if g else counted(k))
                        nc.tensor.matmul(urep_ps[g % 2][:, :], sel[:, g, :], du[:, u, :], start=True,
                                         stop=True).then_inc(urep_ready, 1)
                        if g:
                            add_states(g - 1)
                    add_states(G - 1)
                    pe.wait_ge(act_front, counted(n * 7 + 14) if not (isinstance(n, int) and n == CHUNKS - 1)
                               else counted(CHUNKS * 7))
                    pe.wait_ge(y_gated, counted(n + 1))
                    for t in range(CT):
                        ins = nc.tensor.matmul(g_ps[0][:, t * R:(t + 1) * R], yy[:, 1, t * P:(t + 1) * P], outp[:, :],
                                               start=True, stop=True)
                    ins.then_inc(m_ready, 1)
                    pe.wait_ge(gelu_ready, counted(n + 1))
                    hold(pe, pe_held)
                    for t in range(CT):
                        ins = nc.tensor.transpose(g_ps[1][0:R, t * P:(t + 1) * P], mg[:, t, :], consts["ident"])
                    ins.then_inc(mT_ps, 1)
                    pe.wait_ge(mT_ready, counted(n + 1))
                    for k in range(2):
                        for t in range(2):
                            at = 2 * k + t
                            ins = nc.tensor.matmul((g_ps[2], g_ps[0])[k][:, t * C:(t + 1) * C],
                                                   mT[:, at * P:(at + 1) * P], up[:, :], start=True, stop=True)
                        ins.then_inc(up_ready, 1)

                pipelined(pe, first, rest, CHUNKS)
        m.clear()


HEADS, HS, SLOTS = 12, 16, 8
FEAT = 2 * HS + 2
EXT = 12
PAIRS = HEADS // 2
STEPS = 2 * PAIRS
BIG, HUGE = 1.0e38, 3.4e38


def wrapped(ap, shift, depth):
    dims = [list(x) for x in ap.ap]
    step = dims[-1][0]
    return bass.AP(tensor=ap.tensor, offset=ap.offset + shift * step, ap=dims[:-1] + [[step, depth], [step, 8]])


def dpp_attention_phase(nc, x_res, moments, consts, w):
    RD = 4
    NCOMB = (1 + RD) * SLOTS
    with ExitStack() as ctx:
        m = Mem(nc, ctx, "l2a")
        wqk = m.sb("wqk", [HC, 2, 8, HC])
        wtok = m.sb("wtok", [HC, 2, 3 * C])
        bqk = m.sb("bqk", [HC, 8])
        btok = m.sb("btok", [1, 3 * C])
        wp = m.sb("wp", [HC, 2, C])
        bp = m.sb("bp", [P, C])
        thr = m.sb("thr", [P, 2 * P])
        ident_bf = m.sb("ident_bf", [P, P], BF16)
        mask_bf = m.sb("mask_bf", [P, P], BF16)
        tri_bf = m.sb("tri_bf", [P, P], BF16)
        ones_bf = m.sb("ones_bf", [P, P], BF16)
        ones_row = m.sb("ones_row", [1, P])
        weight_of = m.sb("weight_of", [P, 2, NCOMB])
        rstd = m.sb("rstd", [P, TILES])
        shift = m.sb("shift", [P, TILES])
        guess = m.sb("guess", [P, 4, TILES])
        xn = m.sb("xn", [P, 2, C])
        tT = m.sb("tT", [HC, 2, T])
        qkT = m.sb("qkT", [HC, 2, 8, T])
        q_tok = m.sb("q_tok", [P, 2, 2, 2, C])
        feat = m.sb("feat", [P, 2, 2, HEADS, FEAT])
        rest_buf = m.sb("rest_f", [P, 2 * HEADS * FEAT])
        rest_f = rest_buf[:, :].rearrange("p (t h f) -> p t h f", t=2, h=HEADS)
        feat3 = m.sb("feat3", [P, 2, 2, 3, HEADS, FEAT], BF16)
        square = rest_buf[:, 0:4 * HEADS * HS].rearrange("p (k t h d) -> p k t h d", k=2, t=2, h=HEADS)
        own = m.sb("own", [P, 2, 2, HEADS])
        top8 = m.sb("top8", [P, 2, 2, 8])
        marked = m.sb("marked", [P, 2, 2 * P])
        chosen = m.sb("chosen", [P, 2, 2, 2 * P], BF16)
        chosenT = m.sb("chosenT", [P, 2, 2, 2, P], BF16)
        code = m.sb("code", [P, 2, 2, 2, P], BF16)
        onehot = m.sb("onehot", [P, SLOTS, 2, 2, P], BF16)
        keys = m.sb("keys", [P, 2, HEADS, EXT, HS])
        values = m.sb("values", [P, 2, HEADS, SLOTS, HS])
        facts = m.sb("facts", [P, 2, HEADS, EXT, 2])
        prod = m.sb("prod", [P, 2, 2, RD * SLOTS + 2 * EXT, HS])
        dots = m.sb("dots", [P, 2, HEADS, RD * SLOTS + 2 * EXT])
        sv = m.sb("sv", [P, 3, HEADS, EXT])
        det = m.sb("det", [P, HEADS, 1 + RD, SLOTS])
        sc = m.sb("sc", [P, HEADS, 1 + RD, SLOTS])
        veto = m.sb("veto", [P, HEADS, 1 + RD, SLOTS])
        mx = m.sb("mx", [P, HEADS, 1 + RD, SLOTS])
        ex = m.sb("ex", [P, 3, HEADS, 1 + RD, SLOTS])
        shared = m.sb("shared", [P, HEADS * SLOTS * HS])
        pw = shared[:, 0:3 * HEADS * RD * SLOTS].rearrange("p (k h d a) -> p k h d a", k=3, h=HEADS, d=RD)
        z = shared[:, 0:3 * HEADS * NCOMB].rearrange("p (k h d a) -> p k h d a", k=3, h=HEADS, d=1 + RD)
        pv = shared[:, :].rearrange("p (h a d) -> p h a d", h=HEADS, a=SLOTS)
        hd = m.sb("hd", [P, 6, HEADS])
        alpha = m.sb("alpha", [P, HEADS, SLOTS])
        spread = m.sb("spread", [P, HEADS, EXT])
        y = m.sb("y", [P, 2, C])
        yT = m.sb("yT", [HC, 2, P])

        s_ps = [m.ps(f"s{k}", [P, 512]) for k in range(2)]
        mt_ps = m.ps("mt", [P, 2, 2, P])
        code_psum = m.ps("code_psum", [P, 2, 2, P])
        g_ps = [m.ps(f"g{k}", [P, 512]) for k in range(2)]
        a_ps = [m.ps(f"a{k}", [P, 512]) for k in range(2)]

        names = """weights_in half_log dve_chain0 rstd_ready const_ready xn_ready a_psum a_sb
            rest_ready mid_ready split_ready square_ready own_ready scores_ready marked_ready chosen_ready
            chosenT_psum chosenT_ready code_in_psum code_ready onehot_ready gathered kv_ready prod_ready
            dots_ready det_ready log_ready shifted probs_ready diff_ready exp_ready denom_ready inv_ready
            alpha_ready pv_ready y_ready yT_psum yT_ready proj_ready x_added act_chain max_chain
            score_chain dve_held act_held pe_held pool_held""".split()
        S = {name: m.sem(name) for name in names}
        loads = ((wqk[:, :, :, :], w["wqk"]), (wtok[:, :, :], w["wtok"]), (bqk[:, :], w["bqk"]),
                 (btok[:, :], w["btok"].unsqueeze(0)), (wp[:, :, :], w["wp"]),
                 (bp[:, :], w["bp"].partition_broadcast(P)), (y[:, 0, 0:P], w["mask"]), (thr[:, :], w["thr"]),
                 (y[:, 1, 0:P], w["tri"]), (weight_of[:, :, :], w["comb"].partition_broadcast(P)))
        LOADED = len(loads) * 16

        def first_head(i):
            return 6 * (i % PAIRS // 3) + i % 3

        def keys_of(t):
            return (t + 1) * P

        def steps(eng, body):
            def image(n, u, first=False, last=False):
                for i in range(STEPS):
                    def back(lag, i=i):
                        if i >= lag:
                            return n, u, i - lag
                        return None if first else (n - 1, 1 - u, i - lag + STEPS)
                    body(n, u, i, back, last)
            image(0, 0, first=True)
            with eng.Fori(0, B // 2 - 1) as it:
                image(it * 2 + 1, 1)
                image(it * 2 + 2, 0)
            image(B - 1, 1, last=True)
            for i in range(STEPS, STEPS + 7):
                def back(lag, i=i):
                    return (B - 1, 1, i - lag) if 0 <= i - lag < STEPS else None
                body(B, 0, i - STEPS, back, True)

        FRONT, SCORE0, SCORE1, OUT0, OUT1 = 6, 9, 3, 11, 5

        def around(n, u, i, back, last, front, score, out):
            if i == SCORE1 and back(SCORE1 + 1):
                score(back(SCORE1 + 1)[0], back(SCORE1 + 1)[1], 1)
            if i == OUT1 and back(OUT1 + 1):
                out(back(OUT1 + 1)[0], back(OUT1 + 1)[1], 1)
            if isinstance(n, int) and n == B:
                return
            if i == FRONT and not last:
                front(n + 1, 1 - u)
            if i == SCORE0:
                score(n, u, 0)
            if i == OUT0:
                out(n, u, 0)

        def count_of(step):
            n, u, i = step
            return n * STEPS + i

        with nc.Block() as block:
            @block.sync
            def _(sp):
                for dst, src in loads:
                    sp.dma_start(dst, src).then_inc(S["weights_in"], 16)

            @block.scalar
            def _(act):
                for name in ("xn_ready a_sb mid_ready chosenT_ready code_ready kv_ready log_ready "
                             "probs_ready exp_ready inv_ready yT_ready").split():
                    act.sem_inc(S[name], 1)
                rstd_steps_act(nc, act, None, S["half_log"], moments, guess, consts["eps"])
                act.wait_ge(S["weights_in"], LOADED)
                act.wait_ge(S["const_ready"], 1)
                act.wait_ge(S["rstd_ready"], 1)
                hold(act, S["act_held"])

                def front(n, u):
                    def bank(k):
                        act.wait_ge(S["a_psum"], counted(n * 8 + (k + 1)))
                        return a_ps[k % 2]
                    if not (isinstance(n, int) and n == 0):
                        act.wait_ge(S["prod_ready"], counted(n * STEPS - STEPS))
                        act.wait_ge(S["y_ready"], counted(n * 2 - 2))
                        hold(act, S["act_held"])
                    normalise(nc, xn[:, :, :], x_res, rstd, shift, n * 2).then_inc(S["xn_ready"], 1)
                    b = bank(0)
                    nc.scalar.copy(tT[:, :, :], b[0:HC, :].rearrange("p (h t) -> p h t", h=2)).then_inc(S["a_sb"], 1)
                    for k in range(4):
                        b = bank(1 + k)
                        for j in range(2):
                            ins = nc.scalar.activation(qkT[:, u, 2 * k + j, :], b[0:HC, j * T:(j + 1) * T],
                                                       ACT.Identity, bias=bqk[:, 2 * k + j:2 * k + j + 1])
                        ins.then_inc(S["a_sb"], 1)
                    for t in range(2):
                        b = bank(5 + 2 * t)
                        nc.scalar.copy(q_tok[:, u, t, :, :], b[:, 0:2 * C].rearrange("p (k c) -> p k c", k=2))
                        nc.scalar.copy(feat[:, u, t, :, 0:HS],
                                       b[:, C:2 * C].rearrange("p (h d) -> p h d", h=HEADS)).then_inc(S["a_sb"], 1)
                        if t == 0:
                            b = bank(6)
                            for tt in range(2):
                                ins = nc.scalar.copy(feat[:, u, tt, :, HS:2 * HS],
                                                     b[:, tt * C:(tt + 1) * C].rearrange("p (h d) -> p h d", h=HEADS))
                            ins.then_inc(S["a_sb"], 1)
                    act.wait_ge(S["own_ready"], counted(n + 1))
                    nc.scalar.copy(feat3[:, u, :, 0, :, :], feat[:, u, :, :, :]).then_inc(S["mid_ready"], 1)
                    act.wait_ge(S["rest_ready"], counted(n + 1))
                    nc.scalar.copy(feat3[:, u, :, 1, :, :], rest_f[:, :, :, :]).then_inc(S["mid_ready"], 1)

                def score(n, u, t):
                    r = n * 2 + t
                    act.wait_ge(S["det_ready"], counted(r + 1))
                    nc.scalar.activation(sc[:, :, :, :], det[:, :, :, :], ACT.Ln,
                                         bias=consts["eps6"]).then_inc(S["log_ready"], 1)
                    act.wait_ge(S["diff_ready"], counted(r + 1))
                    nc.scalar.activation(ex[:, :, :, :, :], ex[:, :, :, :, :], ACT.Exp,
                                         scale=0.25).then_inc(S["exp_ready"], 1)
                    act.wait_ge(S["denom_ready"], counted(r + 1))
                    nc.scalar.activation(z[:, 1, :, :, :], z[:, 0, :, :, :], ACT.Ln).then_inc(S["act_chain"], 1)
                    act.wait_ge(S["act_chain"], r + 1)
                    nc.scalar.activation(z[:, 1, :, :, :], z[:, 1, :, :, :], ACT.Exp,
                                         scale=-1.0).then_inc(S["inv_ready"], 1)
                    act.wait_ge(S["shifted"], counted(r + 1))
                    nc.scalar.activation(sc[:, :, :, :], sc[:, :, :, :], ACT.Exp).then_inc(S["probs_ready"], 1)

                def out(n, u, t):
                    act.wait_ge(S["yT_psum"], counted(n * 2 + (t + 1)))
                    nc.scalar.copy(yT[:, :, :], a_ps[0][0:HC, 0:2 * P].rearrange("p (h t) -> p h t", h=2)
                                   ).then_inc(S["yT_ready"], 1)

                def body(n, u, i, back, last):
                    s = back(1)
                    if s:
                        q, t = count_of(s), s[2] // PAIRS
                        act.wait_ge(S["chosenT_psum"], counted(q + 1))
                        act.wait_ge(S["code_in_psum"], counted(q - 1) if not (isinstance(q, int) and q < 2) else 1)
                        nc.scalar.copy(chosenT[:, s[2] % 2, 0:t + 1, :, :],
                                       mt_ps[:, 0:t + 1, :, :]).then_inc(S["chosenT_ready"], 1)
                    s = back(3)
                    if s:
                        q, t = count_of(s), s[2] // PAIRS
                        if s[2] % PAIRS == 0:
                            act.wait_ge(S["y_ready"], counted(s[0] * 2 + t - 1) if not (isinstance(s[0], int) and s[0] == 0)
                                        else 1)
                        for j in range(2):
                            act.wait_ge(S["gathered"], counted(q * 2 + (j + 1)))
                            src = g_ps[j][:, 0:SLOTS * FEAT].rearrange("p (a f) -> p a f", a=SLOTS)
                            h = first_head(s[2]) + 3 * j
                            nc.scalar.copy(keys[:, t, h, 0:SLOTS, :], src[:, :, 0:HS])
                            nc.scalar.copy(keys[:, t, h, SLOTS:EXT, :], src[:, 0:EXT - SLOTS, 0:HS])
                            nc.scalar.copy(values[:, t, h, :, :], src[:, :, HS:2 * HS])
                            nc.scalar.copy(facts[:, t, h, 0:SLOTS, :], src[:, :, 2 * HS:])
                            ins = nc.scalar.copy(facts[:, t, h, SLOTS:EXT, :], src[:, 0:EXT - SLOTS, 2 * HS:])
                        ins.then_inc(S["kv_ready"], 1)
                    s = back(1)
                    if s:
                        q, t = count_of(s), s[2] // PAIRS
                        act.wait_ge(S["code_in_psum"], counted(q + 1))
                        act.wait_ge(S["onehot_ready"], counted(q - 1) if not (isinstance(q, int) and q < 2) else 1)
                        nc.scalar.copy(code[:, s[2] % 2, 0:t + 1, :, :],
                                       code_psum[:, 0:t + 1, :, :]).then_inc(S["code_ready"], 1)
                    around(n, u, i, back, last, front, score, out)

                front(0, 0)
                steps(act, body)

            @block.gpsimd
            def _(pool):
                for name in ("rest_ready split_ready square_ready prod_ready pv_ready").split():
                    pool.sem_inc(S[name], 1)

                def front(n, u):
                    pool.wait_ge(S["a_sb"], counted(n * 8 + 8))
                    key = feat[:, u, :, :, 0:HS]
                    nc.gpsimd.tensor_tensor(square[:, 0, :, :, :], key, key, ALU.mult)
                    for t in range(2):
                        ins = nc.gpsimd.tensor_tensor(square[:, 1, t, :, :], feat[:, u, t, :, 0:HS],
                                                      q_tok[:, u, t, 0, :].rearrange("p (h d) -> p h d", h=HEADS),
                                                      ALU.mult)
                    ins.then_inc(S["square_ready"], 1)
                    pool.wait_ge(S["mid_ready"], counted(n * 2 + 1))
                    nc.gpsimd.tensor_tensor(rest_f[:, :, :, :], feat[:, u, :, :, :], feat3[:, u, :, 0, :, :],
                                            ALU.subtract).then_inc(S["rest_ready"], 1)
                    pool.wait_ge(S["mid_ready"], counted(n * 2 + 2))
                    nc.gpsimd.tensor_tensor(feat3[:, u, :, 2, :, :], rest_f[:, :, :, :], feat3[:, u, :, 1, :, :],
                                            ALU.subtract).then_inc(S["split_ready"], 1)

                def score(n, u, t):
                    r = n * 2 + t
                    pool.wait_ge(S["alpha_ready"], counted(r + 1))
                    for h in range(0, HEADS, 4):
                        ins = nc.gpsimd.tensor_tensor(pv[:, h:h + 4, :, :], values[:, t, h:h + 4, :, :],
                                                      alpha[:, h:h + 4, :].unsqueeze(3).broadcast_to([P, 4, SLOTS, HS]),
                                                      ALU.mult)
                    ins.then_inc(S["pv_ready"], 1)

                def body(n, u, i, back, last):
                    s = back(3)
                    if s:
                        q, t = count_of(s), s[2] // PAIRS
                        pool.wait_ge(S["kv_ready"], counted(q + 1))
                        pool.wait_ge(S["dots_ready"], counted(q - 1) if not (isinstance(q, int) and q < 2) else 1)
                        for j in range(2):
                            h = first_head(s[2]) + 3 * j
                            key = keys[:, t, h, :, :]
                            lo = key[:, 0:SLOTS, :].unsqueeze(1).broadcast_to([P, RD, SLOTS, HS])
                            dims = [list(x) for x in key.ap]
                            hi = bass.AP(tensor=key.tensor, offset=key.offset + HS,
                                         ap=[dims[0], [HS, RD], [HS, SLOTS], [1, HS]])
                            nc.gpsimd.tensor_tensor(
                                prod[:, s[2] % 2, j, 0:RD * SLOTS, :].rearrange("p (d a) f -> p d a f", d=RD),
                                lo, hi, ALU.mult)
                            mine = q_tok[:, s[1], t, :, h * HS:(h + 1) * HS]
                            ins = nc.gpsimd.tensor_tensor(
                                prod[:, s[2] % 2, j, RD * SLOTS:, :].rearrange("p (k a) f -> p k a f", k=2),
                                key.unsqueeze(1).broadcast_to([P, 2, EXT, HS]),
                                mine.unsqueeze(2).broadcast_to([P, 2, EXT, HS]), ALU.mult)
                        ins.then_inc(S["prod_ready"], 1)
                    around(n, u, i, back, last, front, score, lambda *a: None)

                front(0, 0)
                steps(pool, body)

            @block.vector
            def _(dve):
                for name in ("own_ready chosen_ready marked_ready onehot_ready dots_ready det_ready shifted diff_ready "
                             "denom_ready alpha_ready y_ready x_added").split():
                    dve.sem_inc(S[name], 1)
                chain0 = Chain(dve, S["dve_chain0"])
                rstd_steps_dve(nc, dve, chain0, S["half_log"], moments, guess, rstd, shift).then_inc(S["rstd_ready"], 1)
                dve.wait_ge(S["weights_in"], LOADED)
                nc.vector.tensor_copy(ident_bf[:, :], consts["ident"])
                nc.vector.tensor_copy(mask_bf[:, :], y[:, 0, 0:P])
                nc.vector.tensor_copy(tri_bf[:, :], y[:, 1, 0:P])
                nc.vector.memset(ones_bf[:, :], 1.0)
                nc.vector.memset(ones_row[:, :], 1.0)
                nc.vector.memset(feat[:, :, :, :, 2 * HS:2 * HS + 1], 1.0)
                nc.vector.memset(sv[:, :, :, :], 0.0).then_inc(S["const_ready"], 1)
                dve.wait_ge(S["const_ready"], 1)

                def front(n, u):
                    dve.wait_ge(S["square_ready"], counted(n + 1))
                    nc.vector.tensor_reduce(feat[:, u, :, :, 2 * HS + 1], square[:, 0, :, :, :], AX.X, ALU.add)
                    nc.vector.tensor_reduce(own[:, u, :, :], square[:, 1, :, :, :], AX.X, ALU.add
                                            ).then_inc(S["own_ready"], 1)

                def score(n, u, t):
                    r = n * 2 + t
                    chain = Chain(dve, S["score_chain"], 53, r)
                    link = chain.link
                    H = HEADS

                    def tt(out, a, b, op):
                        link(nc.vector.tensor_tensor(out, a, b, op))

                    gram = dots[:, t, :, 0:RD * SLOTS]
                    sim = dots[:, t, :, RD * SLOTS:RD * SLOTS + EXT]
                    cross = dots[:, t, :, RD * SLOTS + EXT:]
                    norm = facts[:, t, :, :, 1]
                    there = facts[:, t, :, :, 0]
                    mine = feat[:, u, t, :, 2 * HS + 1]
                    self_sim = own[:, u, t, :]
                    det2, cross2 = sv[:, 0, :, :], sv[:, 1, :, :]
                    flat = lambda x: x.rearrange("p h d a -> p (h d a)")
                    per_head = lambda x, k: x.rearrange("p h d a -> p h (d a)")
                    over = lambda x, k: x.unsqueeze(2).broadcast_to([P, H, k])
                    A = lambda x: x[:, :, 0:SLOTS].unsqueeze(2).broadcast_to([P, H, RD, SLOTS])
                    Bx = lambda x: wrapped(x, 1, RD)
                    w0, w1, w2 = (pw[:, k, :, :, :] for k in range(3))

                    dve.wait_ge(S["dots_ready"], counted(n * STEPS + (t + 1) * PAIRS))
                    tt(sv[:, 2, :, :], norm, over(mine, EXT), ALU.mult)
                    tt(cross2, cross, cross, ALU.mult)
                    tt(det2, sv[:, 2, :, :], cross2, ALU.subtract)
                    link(nc.vector.tensor_copy(det[:, :, 0, :], det2[:, :, 0:SLOTS]))
                    tt(w0, A(cross), Bx(cross), ALU.mult)
                    tt(per_head(w1, 0), gram, over(mine, RD * SLOTS), ALU.mult)
                    link(nc.vector.scalar_tensor_tensor(out=flat(w2), in0=flat(w0), scalar=2.0, in1=flat(w1),
                                                        op0=ALU.mult, op1=ALU.subtract))
                    tt(per_head(w0, 0), per_head(w2, 0), gram, ALU.mult)
                    tt(w1, A(det2), Bx(norm), ALU.mult)
                    tt(flat(w0), flat(w0), flat(w1), ALU.add)
                    tt(w1, A(norm), Bx(cross2), ALU.mult)
                    tt(det[:, :, 1:, :], w0, w1, ALU.subtract)
                    dve.sem_inc(S["det_ready"], 1)
                    tt(w2, A(there), Bx(there), ALU.mult)
                    link(nc.vector.tensor_scalar(veto[:, :, 1:, :], w2, 1e30, -1e30, ALU.mult, ALU.add))
                    link(nc.vector.tensor_scalar(veto[:, :, 0, :], there[:, :, 0:SLOTS], 1e30, -1e30, ALU.mult, ALU.add))
                    tt(mx[:, :, 1:, :], A(sim), Bx(sim), ALU.max)
                    link(nc.vector.tensor_copy(mx[:, :, 0, :], sim[:, :, 0:SLOTS]))
                    tt(per_head(mx[:, :, :, :], 0), per_head(mx[:, :, :, :], 0), over(self_sim, NCOMB), ALU.max)
                    tt(per_head(ex[:, 0, :, :, :], 0), over(self_sim, NCOMB), per_head(mx[:, :, :, :], 0), ALU.subtract)
                    tt(ex[:, 1, :, :, :], sim[:, :, 0:SLOTS].unsqueeze(2).broadcast_to([P, H, 1 + RD, SLOTS]),
                       mx[:, :, :, :], ALU.subtract)
                    tt(ex[:, 2, :, 1:, :], Bx(sim), mx[:, :, 1:, :], ALU.subtract)
                    link(nc.vector.memset(ex[:, 2, :, 0, :], -1e30))
                    dve.sem_inc(S["diff_ready"], 1)
                    dve.wait_ge(S["log_ready"], counted(r + 1))
                    cw = weight_of[:, 0, :].unsqueeze(1).broadcast_to([P, H, NCOMB])
                    cn = weight_of[:, 1, :].unsqueeze(1).broadcast_to([P, H, NCOMB])
                    scp = per_head(sc[:, :, :, :], 0)
                    tt(scp, scp, cw, ALU.mult)
                    tt(flat(sc[:, :, :, :]), flat(sc[:, :, :, :]), flat(veto[:, :, :, :]), ALU.add)
                    tt(scp, scp, cn, ALU.add)
                    link(nc.vector.tensor_reduce(hd[:, 0, :], scp, AX.X, ALU.max))
                    dve.wait_ge(S["exp_ready"], counted(r + 1))
                    zf = lambda k: flat(z[:, k, :, :, :])
                    ef = lambda k: flat(ex[:, k, :, :, :])
                    tt(zf(0), ef(0), ef(1), ALU.add)
                    nc.vector.tensor_tensor(zf(0), zf(0), ef(2), ALU.add).then_inc(S["denom_ready"], 1)
                    tt(scp, scp, over(hd[:, 0, :], NCOMB), ALU.subtract)
                    dve.sem_inc(S["shifted"], 1)
                    dve.wait_ge(S["inv_ready"], counted(r + 1))
                    tt(zf(2), zf(0), zf(1), ALU.mult)
                    link(nc.vector.scalar_tensor_tensor(out=zf(2), in0=zf(2), scalar=2.0, in1=zf(1),
                                                        op0=ALU.subtract, op1=ALU.mult))
                    dve.wait_ge(S["probs_ready"], counted(r + 1))
                    link(nc.vector.tensor_reduce(hd[:, 1, :], scp, AX.X, ALU.add))
                    link(nc.vector.reciprocal(hd[:, 2, :], hd[:, 1, :]))
                    tt(zf(2), zf(2), flat(sc[:, :, :, :]), ALU.mult)
                    for k in range(3):
                        link(nc.vector.tensor_tensor(ef(k), ef(k), zf(2), ALU.mult))
                    link(nc.vector.tensor_reduce(hd[:, 3, :], per_head(ex[:, 0, :, :, :], 0), AX.X, ALU.add))
                    link(nc.vector.tensor_reduce(alpha[:, :, :], ex[:, 1, :, :, :].rearrange("p h d a -> p h a d"),
                                                 AX.X, ALU.add))
                    link(nc.vector.memset(spread[:, :, :], 0.0))
                    for dd in range(1, RD + 1):
                        tt(spread[:, :, dd:dd + SLOTS], spread[:, :, dd:dd + SLOTS], ex[:, 2, :, dd, :], ALU.add)
                    tt(alpha[:, :, :], alpha[:, :, :], spread[:, :, 0:SLOTS], ALU.add)
                    tt(alpha[:, :, 0:EXT - SLOTS], alpha[:, :, 0:EXT - SLOTS], spread[:, :, SLOTS:], ALU.add)
                    link(nc.vector.scalar_tensor_tensor(out=hd[:, 4, :], in0=hd[:, 3, :], scalar=-1.0, in1=hd[:, 2, :],
                                                        op0=ALU.mult, op1=ALU.mult))
                    link(nc.vector.tensor_scalar(hd[:, 2, :], hd[:, 2, :], -1.0, None, ALU.mult))
                    tt(alpha[:, :, :], alpha[:, :, :], over(hd[:, 2, :], SLOTS), ALU.mult)
                    dve.sem_inc(S["alpha_ready"], 1)
                    link(nc.vector.scalar_tensor_tensor(out=hd[:, 5, :], in0=hd[:, 4, :], scalar=1.0,
                                                        in1=there[:, :, 0], op0=ALU.subtract, op1=ALU.mult))
                    link(nc.vector.tensor_scalar(hd[:, 5, :], hd[:, 5, :], 1.0, None, ALU.add))
                    y3 = y[:, t, :].rearrange("p (h d) -> p h d", h=H)
                    dve.wait_ge(S["pv_ready"], counted(r + 1))
                    link(nc.vector.tensor_reduce(y3, pv[:, :, :, :].rearrange("p h a d -> p h d a"), AX.X, ALU.add))
                    v_own = pv[:, :, 0, :]
                    tt(v_own, feat[:, u, t, :, HS:2 * HS], hd[:, 5, :].unsqueeze(2).broadcast_to([P, H, HS]), ALU.mult)
                    tt(y3, y3, v_own, ALU.add)
                    dve.sem_inc(S["y_ready"], 1)
                    chain.close()

                def out(n, u, t):
                    r = n * 2 + t
                    dve.wait_ge(S["proj_ready"], counted(r + 1))
                    xt = tile_of(x_res, n, t)
                    nc.vector.tensor_tensor(xt, a_ps[1][:, 0:C], xt, ALU.add).then_inc(S["x_added"], 1)
                    dve.wait_ge(S["x_added"], counted(r * 2 + 1))
                    nc.vector.tensor_tensor(xt, xt, bp[:, :], ALU.add).then_inc(S["x_added"], 1)

                def body(n, u, i, back, last):
                    if not (isinstance(n, int) and n == B):
                        q, t = count_of((n, u, i)), i // PAIRS
                        nk = keys_of(t)
                        dve.wait_ge(S["scores_ready"], counted(q + 1))
                        hold(dve, S["dve_held"])
                        for j in range(2):
                            ins = nc.vector.max(top8[:, i % 2, j, :], s_ps[i % 2][:, j * nk:(j + 1) * nk])
                            ins.then_inc(S["max_chain"], 1)
                        for j in range(2):
                            dve.wait_ge(S["max_chain"], q * 2 + (j + 1))
                            hold(dve, S["dve_held"])
                            ins = nc.vector.match_replace(marked[:, j, 0:nk], top8[:, i % 2, j, :],
                                                          s_ps[i % 2][:, j * nk:(j + 1) * nk], HUGE * 0.9)
                        ins.then_inc(S["marked_ready"], 1)
                        dve.wait_ge(S["marked_ready"], counted(q + 1))
                        dve.wait_ge(S["chosenT_psum"], counted(q - 1) if not (isinstance(q, int) and q < 2) else 1)
                        nc.vector.tensor_tensor(chosen[:, i % 2, :, 0:nk], marked[:, :, 0:nk],
                                                thr[:, 2 * P - nk:2 * P].unsqueeze(1).broadcast_to([P, 2, nk]),
                                                ALU.is_ge).then_inc(S["chosen_ready"], 1)
                    s = back(2)
                    if s:
                        q, t = count_of(s), s[2] // PAIRS
                        dve.wait_ge(S["code_ready"], counted(q + 1))
                        dve.wait_ge(S["gathered"], counted(q * 2))
                        for a in range(SLOTS):
                            ins = nc.vector.tensor_scalar(onehot[:, a, 0:t + 1, :, :],
                                                          code[:, s[2] % 2, 0:t + 1, :, :], float(64 + 1 + a), None,
                                                          ALU.is_equal)
                        ins.then_inc(S["onehot_ready"], 1)
                    s = back(4)
                    if s:
                        q, t = count_of(s), s[2] // PAIRS
                        dve.wait_ge(S["prod_ready"], counted(q + 1))
                        h = first_head(s[2])
                        nc.vector.tensor_reduce(dots[:, t, h:h + 4:3, :], prod[:, s[2] % 2, :, :, :], AX.X,
                                                ALU.add).then_inc(S["dots_ready"], 1)
                    around(n, u, i, back, last, front, score, out)

                front(0, 0)
                steps(dve, body)

            @block.tensor
            def _(pe):
                for name in ("a_psum scores_ready chosenT_psum code_in_psum gathered yT_psum proj_ready").split():
                    pe.sem_inc(S[name], 1)
                pe.wait_ge(S["weights_in"], LOADED)
                pe.wait_ge(S["const_ready"], 1)

                def front(n, u):
                    def free(k):
                        pe.wait_ge(S["a_sb"], counted(n * 8 + k))
                    pe.wait_ge(S["xn_ready"], counted(n + 1))
                    first = isinstance(n, int) and n == 0
                    pe.wait_ge(S["yT_ready"], counted(0) if first else counted(n * 2 - 2))
                    pe.wait_ge(S["x_added"], counted(0) if first else counted(n * 4 - 4))
                    pe.wait_ge(S["a_sb"], counted(n * 8))
                    for h in range(2):
                        for t in range(2):
                            ins = nc.tensor.transpose(a_ps[0][0:HC, (2 * h + t) * P:(2 * h + t + 1) * P],
                                                      xn[:, t, h * HC:(h + 1) * HC], consts["ident"])
                    ins.then_inc(S["a_psum"], 1)
                    for k in range(4):
                        free(max(k, 1))
                        for j in range(2):
                            for h in range(2):
                                ins = nc.tensor.matmul(a_ps[(1 + k) % 2][0:HC, j * T:(j + 1) * T],
                                                       wqk[:, h, 2 * k + j, :], tT[:, h, :], start=h == 0, stop=h == 1)
                        ins.then_inc(S["a_psum"], 1)

                    def token_major(k, regions):
                        free(k - 1)
                        for at, t, c0, c1 in regions:
                            o = a_ps[k % 2][:, at:at + c1 - c0]
                            for h in range(2):
                                nc.tensor.matmul(o, tT[:, h, t * P:(t + 1) * P], wtok[:, h, c0:c1], start=h == 0,
                                                 stop=False)
                            ins = nc.tensor.matmul(o, ones_row[:, :], btok[:, c0:c1], start=False, stop=True)
                        ins.then_inc(S["a_psum"], 1)

                    token_major(5, [(0, 0, 0, 2 * C)])
                    token_major(6, [(0, 0, 2 * C, 3 * C), (C, 1, 2 * C, 3 * C)])
                    token_major(7, [(0, 1, 0, 2 * C)])

                def out(n, u, t):
                    r = n * 2 + t
                    pe.wait_ge(S["y_ready"], counted(r + 1))
                    pe.wait_ge(S["a_sb"], counted(B * 8) if isinstance(n, int) and n == B - 1 else counted(n * 8 + 16))
                    hold(pe, S["pe_held"])
                    for h in range(2):
                        ins = nc.tensor.transpose(a_ps[0][0:HC, h * P:(h + 1) * P], y[:, t, h * HC:(h + 1) * HC],
                                                  consts["ident"])
                    ins.then_inc(S["yT_psum"], 1)
                    pe.wait_ge(S["yT_ready"], counted(r + 1))
                    pe.wait_ge(S["x_added"], counted(r * 2))
                    for h in range(2):
                        ins = nc.tensor.matmul(a_ps[1][:, 0:C], yT[:, h, :], wp[:, h, :], start=h == 0, stop=h == 1)
                    ins.then_inc(S["proj_ready"], 1)

                def body(n, u, i, back, last):
                    if not (isinstance(n, int) and n == B):
                        q, t = count_of((n, u, i)), i // PAIRS
                        nk = keys_of(t)
                        if i == 0:
                            pe.wait_ge(S["a_sb"], counted(n * 8 + 8))
                        pe.wait_ge(S["marked_ready"], counted(q - 1) if not (isinstance(q, int) and q < 2) else 1)
                        for j in range(2):
                            h = first_head(i) + 3 * j
                            rows = slice(32 * (h % 3), 32 * (h % 3) + 32)
                            o = s_ps[i % 2][:, j * nk:(j + 1) * nk]
                            nc.tensor.matmul(o, qkT[rows, u, h // 3, t * P:(t + 1) * P], qkT[rows, u, 4 + h // 3, 0:nk],
                                             start=True, stop=False, skip_group_check=True)
                            ins = nc.tensor.matmul(o[:, nk - P:nk], ident_bf[:, :], mask_bf[:, :], start=False,
                                                   stop=True, skip_group_check=True)
                        ins.then_inc(S["scores_ready"], 1)
                    s = back(1)
                    if s:
                        q, t = count_of(s), s[2] // PAIRS
                        pe.wait_ge(S["chosen_ready"], counted(q + 1))
                        pe.wait_ge(S["chosenT_ready"], counted(q))
                        for kt in range(t + 1):
                            for j in range(2):
                                ins = nc.tensor.matmul(mt_ps[:, kt, j, :], chosen[:, s[2] % 2, j, kt * P:(kt + 1) * P],
                                                       ident_bf[:, :], start=True, stop=True)
                        ins.then_inc(S["chosenT_psum"], 1)
                    s = back(3)
                    if s:
                        q, t = count_of(s), s[2] // PAIRS
                        if s[2] == 0:
                            pe.wait_ge(S["split_ready"], counted(s[0] + 1))
                        pe.wait_ge(S["onehot_ready"], counted(q + 1))
                        pe.wait_ge(S["kv_ready"], counted(q))
                        for j in range(2):
                            h = first_head(s[2]) + 3 * j
                            for a in range(SLOTS):
                                for kt in range(t + 1):
                                    for part in range(3):
                                        ins = nc.tensor.matmul(g_ps[j][:, a * FEAT:(a + 1) * FEAT],
                                                               onehot[:, a, kt, j, :],
                                                               feat3[:, s[1], kt, part, h, :],
                                                               start=kt == 0 and part == 0, stop=kt == t and part == 2)
                            ins.then_inc(S["gathered"], 1)
                    s = back(1)
                    if s:
                        q, t = count_of(s), s[2] // PAIRS
                        pe.wait_ge(S["chosenT_ready"], counted(q + 1))
                        pe.wait_ge(S["code_ready"], counted(q))
                        for kt in range(t + 1):
                            o = code_psum[:, kt, :, :]
                            ins = nc.tensor.matmul(o, tri_bf[:, :], chosenT[:, s[2] % 2, kt, :, :], start=True,
                                                   stop=kt == 0)
                            if kt:
                                ins = nc.tensor.matmul(o, ones_bf[:, :], chosenT[:, s[2] % 2, 0, :, :], start=False,
                                                       stop=True)
                        ins.then_inc(S["code_in_psum"], 1)
                    around(n, u, i, back, last, front, lambda *a: None, out)

                front(0, 0)
                steps(pe, body)
        m.clear()


def host_layouts(inputs):
    a = {k: np.asarray(v) for k, v in inputs.items()}
    lay = {}

    def halves(m):
        return np.ascontiguousarray(m.reshape(2, HC, -1).transpose(1, 0, 2))

    lay["x"] = np.ascontiguousarray(a["x"].reshape(TILES, P, C).transpose(1, 0, 2))
    lay["l3f_wg"] = halves(a["L3_ffn_Wg"])
    lay["l3f_w1"] = np.ascontiguousarray(a["L3_ffn_W1"].reshape(E, 2, HC, 768).transpose(2, 1, 0, 3))
    lay["l3f_w2"] = np.ascontiguousarray(a["L3_ffn_W2"].reshape(E, 6, P, C).transpose(2, 1, 0, 3))
    lay["l3f_b1"] = np.ascontiguousarray(a["L3_ffn_b1"].reshape(E, 6, P).transpose(2, 0, 1))
    lay["l0_xT"] = np.ascontiguousarray(a["x"].reshape(TOK, 2, HC).transpose(2, 1, 0))
    lay["l0_down"] = halves(a["L0_conv_down_w"].T)
    lay["l0_inp"] = np.ascontiguousarray(a["L0_conv_in_proj_w"].T)
    lay["l0_convw"] = a["L0_conv_conv_w"]
    lay["l0_cols"] = np.ascontiguousarray(np.stack([a["L0_conv_conv_b"], a["L0_conv_dt_proj_b"],
                                                    a["L0_conv_D_ssm"]], axis=1))
    xp = a["L0_conv_x_proj_w"]
    lay["l0_xdt"] = np.ascontiguousarray(xp[0:12].T)
    lay["l0_xb"] = np.ascontiguousarray(np.broadcast_to(xp[12:44].T.reshape(96, 2, 1, 16), (96, 2, 8, 16)))
    lay["l0_dtw"] = np.ascontiguousarray(a["L0_conv_dt_proj_w"].T)
    lay["l0_alog"] = np.ascontiguousarray(a["L0_conv_A_log"].reshape(12, P).T)
    sel = np.zeros((96, 12, P), np.float32)
    for row in range(96):
        sel[row, row // 8, (row % 8) * 16:(row % 8 + 1) * 16] = 1.0
    lay["l0_sel"] = sel
    lay["l0_selT"] = np.ascontiguousarray(sel.transpose(2, 1, 0))
    lay["l0_outp"] = np.ascontiguousarray(a["L0_conv_out_proj_w"].T)
    lay["l0_up"] = np.ascontiguousarray(a["L0_conv_up_w"].T)
    lay["l0_lng"] = a["L0_conv_ln_g"]
    lay["l0_lnb"] = a["L0_conv_ln_b"]
    keep = np.ones(16, np.float32)
    keep[0] = keep[8] = 0.0
    lay["l0_keep"] = keep
    wa, ba = a["L2_attn_W_attn"], a["L2_attn_b_attn"]
    wqk, bqk = np.zeros((HC, 2, 8, 3, 32), np.float32), np.zeros((HC, 8), np.float32)
    for part in range(2):
        wpart = wa[part * C:(part + 1) * C].reshape(4, 3, 16, 2, HC)
        wqk[:, :, 4 * part:4 * part + 4, :, 0:16] = wpart.transpose(4, 3, 0, 1, 2)
        bqk.reshape(3, 32, 8)[:, 0:16, 4 * part:4 * part + 4] = \
            ba[part * C:(part + 1) * C].reshape(4, 3, 16).transpose(1, 2, 0)
    lay["l2a_wqk"] = wqk.reshape(HC, 2, 8, HC)
    lay["l2a_bqk"] = bqk
    lay["l2a_wtok"] = halves(wa.T)
    lay["l2a_btok"] = ba
    lay["l2a_wp"] = halves(a["L2_attn_W_proj"].T)
    lay["l2a_bp"] = a["L2_attn_b_proj"]
    row, col = np.arange(P)[:, None], np.arange(P)[None, :]
    lay["l2a_mask"] = np.where(col > row, -1e30, 0.0).astype(np.float32)
    lay["l2a_thr"] = np.concatenate([np.full((P, P), BIG), np.where(col < row, BIG, HUGE)], axis=1).astype(np.float32)
    lay["l2a_tri"] = (np.where(row <= col, 1.0, 0.0) + 64.0 * (row == col)).astype(np.float32)
    comb = np.zeros((2, 5, SLOTS), np.float32)
    comb[0, 0], comb[0, 1:] = 1.0 / 2.0, 1.0 / 3.0
    comb[1, 4, 4:] = -1e30
    lay["l2a_comb"] = comb.reshape(2, 5 * SLOTS)
    ky, kx = np.meshgrid(np.arange(HH), np.arange(WW // 2 + 1), indexing="ij")
    yy, xx = np.meshgrid(np.arange(HH), np.arange(WW), indexing="ij")
    turn = 2 * np.pi * (np.outer(yy.ravel(), ky.ravel()) + np.outer(xx.ravel(), kx.ravel())) / HH
    dft = np.concatenate([np.cos(turn), -np.sin(turn)], axis=1) / HH
    lay["l1_dft"] = np.ascontiguousarray(dft.reshape(2, P, 288).transpose(1, 0, 2)).astype(np.float32)
    twice = np.where((kx.ravel() == 0) | (kx.ravel() == WW // 2), 1.0, 2.0)[:, None]
    idft = np.stack([np.cos(turn).T * twice, -np.sin(turn).T * twice], axis=0) / HH
    lay["l1_idft"] = np.ascontiguousarray(idft.reshape(2, 2, 72, T).transpose(2, 1, 0, 3)).astype(np.float32)
    for name in ("w1", "w2"):
        full = np.zeros((HC, 2, 2, HC), np.float32)
        for blk in range(8):
            at = slice((blk % 4) * 24, (blk % 4 + 1) * 24)
            full[at, :, blk // 4, at] = a["L1_conv_" + name][:, blk].transpose(1, 0, 2)
        lay["l1_" + name] = full
    lay["l1_w2"] = np.ascontiguousarray(lay["l1_w2"].transpose(0, 2, 1, 3))
    lay["l1_b1"] = np.ascontiguousarray(a["L1_conv_b1"].reshape(2, 2, HC).transpose(2, 1, 0))
    lay["l1_b2"] = np.ascontiguousarray(a["L1_conv_b2"].reshape(2, 2, HC).transpose(1, 0, 2))
    for name in ("q", "k", "v", "o"):
        lay["l3a_w" + name] = halves(a["L3_attn_W" + name])
    lay["l3a_memT"] = halves(a["L3_attn_memory"].T)
    lay["l3a_bq"] = np.ascontiguousarray(a["L3_attn_bq"].reshape(2, HC).T)
    lay["l3a_bk"] = np.ascontiguousarray(a["L3_attn_bk"].reshape(2, HC).T)
    lay["l3a_bv"] = a["L3_attn_bv"]
    lay["l3a_bo"] = a["L3_attn_bo"]
    lay["l2f_wr"] = halves(a["L2_ffn_Wr"])
    lay["l2f_br"] = a["L2_ffn_br"]
    lay["l2f_wgu"] = np.ascontiguousarray(a["L2_ffn_Wgu"].reshape(E, 2, HC, 2 * C).transpose(2, 1, 0, 3))
    lay["l2f_wd"] = np.ascontiguousarray(a["L2_ffn_Wd"].reshape(E, 2, HC, C).transpose(2, 1, 0, 3))
    lay["l2f_bgu"] = np.ascontiguousarray(a["L2_ffn_bgu"].reshape(E, 4, HC).transpose(2, 0, 1))
    lay["l2f_bd"] = a["L2_ffn_bd"]
    lay["l3f_b2"] = a["L3_ffn_b2"]
    lay["ident"] = np.eye(P, dtype=np.float32)
    return lay


def moments_phase(nc, x_res, moments, tag):
    with ExitStack() as ctx:
        m = Mem(nc, ctx, tag + "_mom")
        stats = m.sb("stats", [P, TILES, 6])
        stats_ready = m.sem("stats_ready")
        with nc.Block() as block:
            @block.vector
            def _(dve):
                for t in range(TILES):
                    nc.vector.bn_stats(stats[:, t, :], x_res[:, t, :]).then_inc(stats_ready, 1)
                for t in range(TILES):
                    dve.wait_ge(stats_ready, t + 1)
                    nc.vector.bn_aggr(moments[:, t, :], stats[:, t, :])
        m.clear()


def build(nc, d, out, phases=("l0", "l1", "l2a", "l2f", "l3a", "l3f")):
    with ExitStack() as ctx:
        m = Mem(nc, ctx, "main")
        x_res = m.sb("x_res", [P, TILES, C])
        moments = m.sb("moments", [P, TILES, 2])
        ident = m.sb("ident", [P, P])
        ones8 = m.sb("ones8", [P, E])
        eps = m.sb("eps", [P, 1])
        eps6 = m.sb("eps6", [P, 1])
        x_in = m.sem("x_in")
        const_in = m.sem("const_in")
        x_out = m.sem("x_out")
        consts = {"ident": ident[:, :], "ones8": ones8[:, :], "eps": eps[:, :], "eps6": eps6[:, :]}
        with nc.Block() as block:
            @block.sync
            def _(sp):
                sp.dma_start(ident[:, :], d["ident"]).then_inc(const_in, 16)
                sp.dma_start(x_res[:, :, :], d["x"]).then_inc(x_in, 16)
                sp.wait_ge(const_in, 16)
                sp.wait_ge(x_in, 16)

            @block.vector
            def _(dve):
                nc.vector.memset(ones8[:, :], 1.0)
                nc.vector.memset(eps[:, :], EPS)
                nc.vector.memset(eps6[:, :], 1e-6)
        w = {}
        for k, v in d.items():
            if "_" in k:
                tag, name = k.split("_", 1)
                w.setdefault(tag, {})[name] = v
        PH = {"l2a": lambda: dpp_attention_phase(nc, x_res, moments, consts, w["l2a"]),
              "l1": lambda: fourier_phase(nc, x_res, moments, consts, w["l1"]),
              "l0": lambda: mamba_phase(nc, x_res, moments, consts, w["l0"]),
              "l3a": lambda: memory_attention_phase(nc, x_res, moments, consts, w["l3a"]),
              "l2f": lambda: moe_glu_phase(nc, x_res, moments, consts, w["l2f"]),
              "l3f": lambda: moe_relu_phase(nc, x_res, moments, consts, w["l3f"])}
        for ph in phases:
            if ph not in ("l0", "l1"):
                moments_phase(nc, x_res, moments, ph)
            PH[ph]()
        with nc.Block() as block:
            @block.sync
            def _(sp):
                sp.dma_start(out, x_res[:, :, :]).then_inc(x_out, 16)
                sp.wait_ge(x_out, 16)


def kernel(**inputs):
    import concourse.bacc as _bacc
    from concourse.bass_utils import run_bass_kernel_spmd as _run

    nc = _bacc.Bacc("TRN2", target_bir_lowering=False, num_devices=1)
    arrays, d = {}, {}
    for name, a in host_layouts(inputs).items():
        arrays[f"in_{name}"] = a
        d[name] = nc.dram_tensor(f"in_{name}", a.shape, mybir.dt.from_np(a.dtype), kind="ExternalInput").ap()
    out = nc.dram_tensor("out_x", (P, TILES, C), F32, kind="ExternalOutput").ap()
    build(nc, d, out)
    r = _run(nc, [arrays], core_ids=[0])
    got = r.results[0]["out_x"]
    return np.ascontiguousarray(got.transpose(1, 0, 2)).reshape(B, HH, WW, C)
```

```python
import numpy as np
import concourse.bass as bass
from concourse import mybir
from contextlib import ExitStack

F32 = mybir.dt.float32
BF16 = mybir.dt.bfloat16
U32 = mybir.dt.uint32
I32 = mybir.dt.int32
ALU = mybir.AluOpType
ACT = mybir.ActivationFunctionType
AX = mybir.AxisListType

P = 128
B, HH, WW, C = 32, 16, 16, 192
T = HH * WW
TOK = B * T
TILES = TOK // P
HC = C // 2
EPS = 1e-5
E = 8
ETOK = 2 * P
ETILES = 2 * TOK // ETOK + E


def counted(n):
    return n + 1


class Chain:

    def __init__(self, eng, sem, per=0, it=None):
        self.eng, self.sem, self.n, self.base = eng, sem, 0, (it * per if it is not None else 0)
        self.per = per

    def link(self, ins):
        self.n += 1
        ins.then_inc(self.sem, 1)
        self.eng.wait_ge(self.sem, self.base + self.n)

    def send(self, ins):
        self.n += 1
        ins.then_inc(self.sem, 1)

    def close(self):
        assert not self.per or self.n == self.per, (self.n, self.per)


class Mem:

    def __init__(self, nc, ctx, tag):
        self.nc, self.ctx, self.tag, self.sems = nc, ctx, tag, []

    def sb(self, name, shape, dt=F32):
        return self.ctx.enter_context(self.nc.sbuf_tensor(f"{self.tag}_{name}", shape, dt))

    def ps(self, name, shape, dt=F32):
        return self.ctx.enter_context(self.nc.psum_tensor(f"{self.tag}_{name}", shape, dt))

    def sem(self, name):
        self.sems.append(self.ctx.enter_context(self.nc.semaphore(f"{self.tag}_{name}")))
        return self.sems[-1]

    def clear(self):
        with self.nc.Block() as block:
            @block.gpsimd
            def _(pool):
                for s in self.sems:
                    pool.sem_clear(s)


def rstd_steps_act(nc, act, var_ready, half_log, moments, y0, eps_col):
    nc.scalar.activation(y0[:, 0, :], moments[:, :, 1], ACT.Ln, bias=eps_col).then_inc(half_log, 1)
    act.wait_ge(half_log, 1)
    nc.scalar.activation(y0[:, 1, :], y0[:, 0, :], ACT.Exp, scale=-0.5).then_inc(half_log, 1)


def rstd_steps_dve(nc, dve, chain, half_log, moments, y0, rstd, shift):
    dve.wait_ge(half_log, 2)
    chain.link(nc.vector.tensor_tensor(y0[:, 2, :], y0[:, 1, :], y0[:, 1, :], ALU.mult))
    chain.link(nc.vector.scalar_tensor_tensor(out=y0[:, 3, :], in0=moments[:, :, 1], scalar=EPS,
                                              in1=y0[:, 2, :], op0=ALU.add, op1=ALU.mult))
    chain.link(nc.vector.tensor_scalar(y0[:, 2, :], y0[:, 3, :], -0.5, 1.5, ALU.mult, ALU.add))
    chain.link(nc.vector.tensor_tensor(rstd[:, :], y0[:, 2, :], y0[:, 1, :], ALU.mult))
    return nc.vector.scalar_tensor_tensor(out=shift[:, :], in0=moments[:, :, 0], scalar=-1.0, in1=rstd[:, :],
                                          op0=ALU.mult, op1=ALU.mult)


def normalise(nc, xn, x_res, rstd, shift, tile):
    for t in range(2):
        at = bass.ds(tile + t, 1)
        ins = nc.scalar.activation(xn[:, t, :], x_res[:, at, :].rearrange("p a c -> p (a c)"), ACT.Identity,
                                   bias=shift[:, at], scale=rstd[:, at])
    return ins


def hold(eng, held):
    eng.sem_inc(held, 1)


def top2_select(nc, chain, held, val, m8, work, sel, ones8):
    v2 = m8[:, :, 1:2].broadcast_to([P, 2, E])
    gt, eq, cum, cnt = (work[:, k, :, :] for k in range(4))
    for t in range(2):
        hold(chain.eng, held)
        chain.link(nc.vector.max(m8[:, t, :], val[:, t, :]))
    chain.link(nc.vector.tensor_tensor(gt, val, v2, ALU.is_gt))
    chain.link(nc.vector.tensor_tensor(eq, val, v2, ALU.is_equal))
    chain.link(nc.vector.tensor_reduce(cnt[:, :, 0:1], gt, AX.X, ALU.add))
    for t in range(2):
        chain.link(nc.vector.tensor_tensor_scan(cum[:, t, :], ones8, eq[:, t, :], 0.0, ALU.mult, ALU.add))
    chain.link(nc.vector.tensor_tensor(cum, cum, cnt[:, :, 0:1].broadcast_to([P, 2, E]), ALU.add))
    chain.link(nc.vector.tensor_scalar(cum, cum, 2.5, None, ALU.is_lt))
    chain.link(nc.vector.tensor_tensor(eq, eq, cum, ALU.mult))
    chain.link(nc.vector.tensor_tensor(sel, eq, gt, ALU.add))


def x_pair(x_res, n):
    return x_res[:, bass.ds(2 * n, 2), :]


def pipelined(eng, first, rest, count=B):
    first(0, 0)
    with eng.Fori(0, count // 2 - 1) as it:
        rest(it * 2, 0, lambda: first(it * 2 + 1, 1))
        rest(it * 2 + 1, 1, lambda: first(it * 2 + 2, 0))
    rest(count - 2, 0, lambda: first(count - 1, 1))
    rest(count - 1, 1, lambda: None)


def tile_of(x_res, n, t):
    return x_res[:, bass.ds(n * 2 + t, 1), :].rearrange("p a c -> p (a c)")


def rounds(eng, tile):
    tile(0, 0)
    tile(0, 1)
    with eng.Fori(1, ETILES // 2) as r:
        for u in range(2):
            tile(r, u)


def ring_rounds(eng, ring, tile):
    for k in range(ring):
        tile(0, k)
    with eng.Fori(1, TILES // ring) as r:
        for k in range(ring):
            tile(r, k)


def first_round(r):
    return isinstance(r, int) and r == 0


def route(nc, x_res, moments, consts, w, norm, plan, tag, from_probabilities):
    with ExitStack() as ctx:
        m = Mem(nc, ctx, tag + "_route")
        wr = m.sb("wr", [HC, 2, E])
        br = m.sb("br", [P, E])
        y0 = m.sb("guess", [P, 4, TILES])
        xn = m.sb("xn", [P, 2, 2, C])
        tT = m.sb("tT", [HC, 2, 2, T])
        val = m.sb("val", [P, TILES, E])
        soft = m.sb("soft", [P, TILES, E])
        key = m.sb("key", [P, TILES, E])
        one_hot = m.sb("one_hot", [P, 2, TILES, E])
        sel = m.sb("sel", [P, TILES, E])
        col = m.sb("col", [P, 4, TILES])
        tot = m.sb("tot", [P, E, TILES])
        incl = m.sb("incl", [P, E, TILES])
        over = m.sb("over", [P, E, TOK // ETOK])
        counts = m.sb("counts", [P, 4, E])
        after = m.sb("after", [P, ETILES, E])
        row_f = m.sb("row_f", [P, 2, TILES])
        owner = m.sb("owner", [P, ETILES])
        ones = m.sb("ones", [P, P])[:, :]
        tri = m.sb("tri", [P, P])[:, :]
        rev = m.sb("rev", [P, E])[:, :]
        floor = m.sb("floor", [P, TOK // ETOK])[:, :]
        index = m.sb("index", [P, ETILES])[:, :]
        tp = [m.ps(f"tp{k}", [P, 512]) for k in range(2)]
        lg = m.ps("lg", [P, TILES, E])
        before = m.ps("before", [P, TILES, E])
        total = m.ps("total", [P, TILES, E])

        router_in = m.sem("router_in")
        tables_in = m.sem("tables_in")
        ones_ready = m.sem("ones_ready")
        half_log = m.sem("half_log")
        steps = m.sem("steps")
        norm_ready = m.sem("norm_ready")
        xn_ready = m.sem("xn_ready")
        tp_ready = m.sem("tp_ready")
        tT_ready = m.sem("tT_ready")
        logits_ready = m.sem("logits_ready")
        soft_in = m.sem("soft_in")
        soft_ready = m.sem("soft_ready")
        sel_ready = m.sem("sel_ready")
        counted_ready = m.sem("counted_ready")
        act_held = m.sem("act_held")

        with nc.Block() as block:
            @block.sync
            def _(sp):
                sp.dma_start(wr[:, :, :], w["wr"]).then_inc(router_in, 16)
                if not from_probabilities:
                    sp.dma_start(br[:, :], w["br"].partition_broadcast(P)).then_inc(router_in, 16)
                sp.dma_start(tri, consts["moe"][0]).then_inc(tables_in, 16)
                for place, source in zip((rev, floor, index), consts["moe"][1:]):
                    sp.dma_start(place, source.partition_broadcast(P)).then_inc(tables_in, 16)
                sp.wait_ge(consts["zeroed"], 16)
                for place, source in norm["weights"]:
                    sp.dma_start(place, source).then_inc(norm["weights_in"], 16)

            @block.scalar
            def _(act):
                act.sem_inc(xn_ready, 1)
                rstd_steps_act(nc, act, None, half_log, moments, y0, consts["eps"])
                act.wait_ge(norm_ready, 1)
                hold(act, act_held)

                def image(n, u):
                    act.wait_ge(tp_ready, counted(n))
                    normalise(nc, xn[:, u, :, :], x_res, norm["rstd"], norm["shift"], n * 2).then_inc(xn_ready, 1)

                with act.Fori(0, B // 2) as it:
                    image(it * 2, 0)
                    image(it * 2 + 1, 1)
                act.wait_ge(soft_in, 1)
                nc.scalar.activation(soft[:, :, :] if from_probabilities else col[:, 2, :],
                                     soft[:, :, :] if from_probabilities else col[:, 2, :],
                                     ACT.Exp if from_probabilities else ACT.Sigmoid).then_inc(soft_ready, 1)

            @block.tensor
            def _(pe):
                pe.sem_inc(tp_ready, 2)
                pe.sem_inc(logits_ready, 1)
                pe.wait_ge(router_in, 16 if from_probabilities else 32)

                def first(n, u):
                    pe.wait_ge(xn_ready, counted(n + 1))
                    pe.wait_ge(tT_ready, counted(n))
                    for h in range(2):
                        for t in range(2):
                            ins = nc.tensor.transpose(tp[u][0:HC, (2 * h + t) * P:(2 * h + t + 1) * P],
                                                      xn[:, u, t, h * HC:(h + 1) * HC], consts["ident"])
                    ins.then_inc(tp_ready, 1)

                def rest(n, u, nxt):
                    nxt()
                    pe.wait_ge(tT_ready, counted(n + 2))
                    for t in range(2):
                        for h in range(2):
                            ins = nc.tensor.matmul(lg[:, bass.ds(n * 2 + t, 1), :].rearrange("p a e -> p (a e)"),
                                                   tT[:, u, h, t * P:(t + 1) * P], wr[:, h, :],
                                                   start=h == 0, stop=h == 1)
                    ins.then_inc(logits_ready, 1)

                pipelined(pe, first, rest)
                pe.wait_ge(sel_ready, 1)
                pe.wait_ge(tables_in, 64)
                pe.wait_ge(ones_ready, 1)
                chosen = sel[:, :, :].rearrange("p t e -> p (t e)")
                nc.tensor.matmul(before[:, :, :].rearrange("p t e -> p (t e)"), tri, chosen, start=True, stop=True)
                nc.tensor.matmul(total[:, :, :].rearrange("p t e -> p (t e)"), ones, chosen,
                                 start=True, stop=True).then_inc(counted_ready, 1)

            @block.vector
            def _(dve):
                chain = Chain(dve, steps)
                link = chain.link
                dve.sem_inc(tT_ready, 2)
                nc.vector.memset(ones, 1.0).then_inc(ones_ready, 1)
                dve.wait_ge(ones_ready, 1)
                dve.wait_ge(tables_in, 64)
                rstd_steps_dve(nc, dve, chain, half_log, moments, y0, norm["rstd"],
                               norm["shift"]).then_inc(norm_ready, 1)

                def image(n, u):
                    dve.wait_ge(tp_ready, counted(n + 2))
                    dve.wait_ge(logits_ready, counted(n - 1) if not (isinstance(n, int) and n < 2) else 1)
                    nc.vector.tensor_copy(tT[:, u, :, :].rearrange("p h t -> p (h t)"),
                                          tp[u][0:HC, :]).then_inc(tT_ready, 1)

                image(0, 0)
                image(1, 1)
                with dve.Fori(0, B // 2 - 1) as it:
                    image(it * 2 + 2, 0)
                    image(it * 2 + 3, 1)
                dve.wait_ge(logits_ready, counted(B))

                def over_experts(c):
                    return c.unsqueeze(2).broadcast_to([P, TILES, E])

                def of_expert(r):
                    return r.unsqueeze(1).broadcast_to([P, TILES, E])

                if from_probabilities:
                    link(nc.vector.tensor_reduce(col[:, 0, :], lg[:, :, :], AX.X, ALU.max))
                    nc.vector.tensor_tensor(soft[:, :, :], lg[:, :, :], over_experts(col[:, 0, :]),
                                            ALU.subtract).then_inc(soft_in, 1)
                    dve.wait_ge(soft_ready, 1)
                    link(nc.vector.tensor_reduce(col[:, 1, :], soft[:, :, :], AX.X, ALU.add))
                    link(nc.vector.reciprocal(col[:, 2, :], col[:, 1, :]))
                    link(nc.vector.tensor_tensor(val[:, :, :], soft[:, :, :], over_experts(col[:, 2, :]), ALU.mult))
                    best = [plan["gates"][:, k, :] for k in range(2)]
                else:
                    dve.wait_ge(router_in, 32)
                    link(nc.vector.tensor_tensor(val[:, :, :], lg[:, :, :], of_expert(br[:, :]), ALU.add))
                    best = [col[:, k, :] for k in range(2)]
                for k in range(2):
                    hot = one_hot[:, k, :, :]
                    link(nc.vector.tensor_reduce(best[k], val[:, :, :], AX.X, ALU.max))
                    link(nc.vector.tensor_tensor(key[:, :, :], val[:, :, :], over_experts(best[k]), ALU.is_equal))
                    link(nc.vector.tensor_tensor(key[:, :, :], key[:, :, :], of_expert(rev), ALU.mult))
                    link(nc.vector.tensor_reduce(col[:, 3, :], key[:, :, :], AX.X, ALU.max))
                    link(nc.vector.tensor_tensor(hot, key[:, :, :], over_experts(col[:, 3, :]), ALU.is_equal))
                    if k == 0:
                        link(nc.vector.scalar_tensor_tensor(
                            out=val[:, :, :].rearrange("p t e -> p (t e)"), in0=hot.rearrange("p t e -> p (t e)"),
                            scalar=-1e30, in1=val[:, :, :].rearrange("p t e -> p (t e)"), op0=ALU.mult, op1=ALU.add))
                nc.vector.tensor_tensor(sel[:, :, :], one_hot[:, 0, :, :], one_hot[:, 1, :, :],
                                        ALU.add).then_inc(sel_ready, 1)
                if not from_probabilities:
                    nc.vector.tensor_tensor(col[:, 2, :], best[0], best[1], ALU.subtract).then_inc(soft_in, 1)
                    dve.wait_ge(soft_ready, 1)
                    link(nc.vector.tensor_copy(plan["gates"][:, 0, :], col[:, 2, :]))
                    link(nc.vector.tensor_scalar(plan["gates"][:, 1, :], col[:, 2, :], -1.0, 1.0, ALU.mult, ALU.add))
                dve.wait_ge(counted_ready, 1)
                link(nc.vector.tensor_copy(tot[:, :, :], total[:, :, :].rearrange("p t e -> p e t")))
                for e in range(E):
                    ins = nc.vector.tensor_tensor_scan(incl[:, e, :], ones[:, 0:TILES], tot[:, e, :], 0.0,
                                                       ALU.mult, ALU.add)
                link(ins)
                shape = [P, E, TOK // ETOK]
                link(nc.vector.tensor_tensor(over[:, :, :], incl[:, :, TILES - 1:TILES].broadcast_to(shape),
                                             floor.unsqueeze(1).broadcast_to(shape), ALU.is_gt))
                link(nc.vector.tensor_reduce(counts[:, 0, :], over[:, :, :], AX.X, ALU.add))
                link(nc.vector.tensor_tensor_scan(counts[:, 1, :], ones[:, 0:E], counts[:, 0, :], 0.0,
                                                  ALU.mult, ALU.add))
                link(nc.vector.tensor_tensor(after[:, :, :],
                                             index.unsqueeze(2).broadcast_to([P, ETILES, E]),
                                             counts[:, 1, :].unsqueeze(1).broadcast_to([P, ETILES, E]), ALU.is_ge))
                link(nc.vector.tensor_reduce(owner[:, :], after[:, :, :], AX.X, ALU.add))
                link(nc.vector.tensor_scalar(plan["expert"][:, :], owner[:, :], float(E - 1), None, ALU.min))
                link(nc.vector.tensor_tensor(counts[:, 2, :], counts[:, 1, :], counts[:, 0, :], ALU.subtract))
                link(nc.vector.tensor_scalar(counts[:, 3, :], counts[:, 2, :], float(ETOK), None, ALU.mult))
                link(nc.vector.tensor_tensor(incl[:, :, :], incl[:, :, :], tot[:, :, :], ALU.subtract))
                link(nc.vector.tensor_tensor(incl[:, :, :], incl[:, :, :],
                                             counts[:, 3, :].unsqueeze(2).broadcast_to([P, E, TILES]), ALU.add))
                link(nc.vector.tensor_tensor(val[:, :, :], before[:, :, :],
                                             incl[:, :, :].rearrange("p e t -> p t e"), ALU.add))
                for k in range(2):
                    link(nc.vector.tensor_tensor(key[:, :, :], val[:, :, :], one_hot[:, k, :, :], ALU.mult))
                    link(nc.vector.tensor_reduce(row_f[:, k, :], key[:, :, :], AX.X, ALU.add))
                link(nc.vector.tensor_copy(plan["rows"][:, :, :], row_f[:, :, :]))
        m.clear()


def dispatch(nc, x_res, norm, plan, rows_dram, tag):
    RING = 4
    with ExitStack() as ctx:
        m = Mem(nc, ctx, tag + "_dispatch")
        xn = m.sb("xn", [P, RING, C])
        at = m.sb("at", [P, RING, 2], U32)
        xn_ready = m.sem("xn_ready")
        at_ready = m.sem("at_ready")
        act_held = m.sem("act_held")
        pool_held = m.sem("pool_held")
        written = [m.sem(f"written{k}") for k in range(RING)]
        with nc.Block() as block:
            @block.scalar
            def _(act):
                def tile(r, k):
                    if not first_round(r):
                        act.wait_ge(written[k], r * 32)
                        hold(act, act_held)
                    at_tile = bass.ds(r * RING + k, 1)
                    nc.scalar.activation(xn[:, k, :], x_res[:, at_tile, :].rearrange("p a c -> p (a c)"),
                                         ACT.Identity, bias=norm["shift"][:, at_tile],
                                         scale=norm["rstd"][:, at_tile]).then_inc(xn_ready, 1)

                ring_rounds(act, RING, tile)

            @block.gpsimd
            def _(pool):
                def tile(r, k):
                    if not first_round(r):
                        pool.wait_ge(written[k], r * 32)
                        hold(pool, pool_held)
                    nc.gpsimd.tensor_copy(at[:, k, :], plan["rows"][:, :, bass.ds(r * RING + k, 1)]
                                          .rearrange("p c a -> p (c a)")).then_inc(at_ready, 1)
                    pool.wait_ge(xn_ready, r * RING + k + 1)
                    pool.wait_ge(at_ready, r * RING + k + 1)
                    hold(pool, pool_held)
                    for c in range(2):
                        pool.indirect_dma_start(rows_dram, bass.IndirectOffsetOnAxis(ap=at[:, k, c:c + 1], axis=0),
                                                xn[:, k, :], None).then_inc(written[k], 16)

                ring_rounds(pool, RING, tile)
                for k in range(RING):
                    pool.wait_ge(written[k], TILES // RING * 32)
        m.clear()


def combine(nc, x_res, plan, rows_dram, tag):
    RING = 4
    with ExitStack() as ctx:
        m = Mem(nc, ctx, tag + "_combine")
        y = m.sb("y", [P, RING, 2, C])
        at = m.sb("at", [P, RING, 2], U32)
        at_ready = m.sem("at_ready")
        half = m.sem("half")
        added = m.sem("added")
        pool_held = m.sem("pool_held")
        gathered = [m.sem(f"gathered{k}") for k in range(RING)]
        with nc.Block() as block:
            @block.gpsimd
            def _(pool):
                def tile(n, k, peeled):
                    if not peeled:
                        pool.wait_ge(added, n - RING + 1)
                        hold(pool, pool_held)
                    nc.gpsimd.tensor_copy(at[:, k, :], plan["rows"][:, :, bass.ds(n, 1)].rearrange("p c a -> p (c a)")
                                          ).then_inc(at_ready, 1)
                    pool.wait_ge(at_ready, n + 1)
                    hold(pool, pool_held)
                    for c in range(2):
                        pool.indirect_dma_start(y[:, k, c, :], None, rows_dram,
                                                bass.IndirectOffsetOnAxis(ap=at[:, k, c:c + 1], axis=0)
                                                ).then_inc(gathered[k], 16)

                for k in range(RING):
                    tile(k, k, True)
                with pool.Fori(1, TILES // RING) as it:
                    for k in range(RING):
                        tile(it * RING + k, k, False)

            @block.vector
            def _(dve):
                with dve.Fori(0, TILES // RING) as it:
                    for k in range(RING):
                        n = it * RING + k
                        xt = x_res[:, bass.ds(n, 1), :].rearrange("p a c -> p (a c)")
                        dve.wait_ge(gathered[k], it * 32 + 32)
                        nc.vector.scalar_tensor_tensor(out=xt, in0=y[:, k, 0, :],
                                                       scalar=plan["gates"][:, 0, bass.ds(n, 1)],
                                                       in1=xt, op0=ALU.mult, op1=ALU.add).then_inc(half, 1)
                        dve.wait_ge(half, n + 1)
                        nc.vector.scalar_tensor_tensor(out=xt, in0=y[:, k, 1, :],
                                                       scalar=plan["gates"][:, 1, bass.ds(n, 1)],
                                                       in1=xt, op0=ALU.mult, op1=ALU.add).then_inc(added, 1)
        m.clear()


def moe_buffers(nc, m):
    norm = {"rstd": m.sb("rstd", [P, TILES])[:, :], "shift": m.sb("shift", [P, TILES])[:, :]}
    plan = {"gates": m.sb("gates", [P, 2, TILES]), "rows": m.sb("rows", [P, 2, TILES], U32),
            "expert": m.sb("expert", [P, ETILES], I32)}
    return norm, plan


def owner_of(eng, plan, j):
    return eng.value_load(plan["expert"][0:1, bass.ds(j, 1)], min_val=0, max_val=E - 1)


def rows_of(rows, r, u):
    return rows.rearrange("(j t p) c -> p (j t) c", p=P, t=2)[:, bass.ds((r * 2 + u) * 2, 2), :]


def load_rows(sp, rows_in, xg, xg_in, tp_ready):
    for u in range(2):
        sp.dma_start(xg[:, u, :, :], rows_of(rows_in, 0, u)).then_inc(xg_in[u], 16)
    with sp.Fori(1, ETILES // 2) as r:
        for u in range(2):
            sp.wait_ge(tp_ready, r * 2 + u - 1)
            sp.dma_start(xg[:, u, :, :], rows_of(rows_in, r, u)).then_inc(xg_in[u], 16)


def store_rows(pool, held, rows_out, ys, ys_out, ys_ready, r, u):
    pool.wait_ge(ys_ready, r * 2 + u + 1)
    hold(pool, held)
    pool.dma_start(rows_of(rows_out, r, u), ys[:, u, :, :]).then_inc(ys_out[u], 16)


def turn_rows(nc, tp, rows, ident):
    for h in range(2):
        for t in range(2):
            ins = nc.tensor.transpose(tp[0:HC, (2 * h + t) * P:(2 * h + t + 1) * P],
                                      rows[:, t, h * HC:(h + 1) * HC], ident)
    return ins


def expert_order(pe, turn, first_layer, second_layer):
    last = ETILES // 2 - 1
    turn(0, 0)
    first_layer(0, 0)
    turn(0, 1)
    first_layer(0, 1)
    turn(1, 0)
    second_layer(0, 0)
    with pe.Fori(1, last) as r:
        first_layer(r, 0)
        turn(r, 1)
        second_layer(r - 1, 1)
        first_layer(r, 1)
        turn(r + 1, 0)
        second_layer(r, 0)
    first_layer(last, 0)
    turn(last, 1)
    second_layer(last - 1, 1)
    first_layer(last, 1)
    second_layer(last, 0)
    second_layer(last, 1)


def moe_relu_phase(nc, x_res, moments, consts, w):
    H = 768
    MC = H // P
    HB = MC // 2
    rows_in, rows_out = consts["rows_in"], consts["rows_out"]
    with ExitStack() as ctx:
        m = Mem(nc, ctx, "l3f")
        w1 = m.sb("w1", [HC, 2, E, H])
        w2 = m.sb("w2", [P, MC, E, C])
        b1 = m.sb("b1", [P, E, MC])
        b2 = m.sb("b2", [P, E, C])
        norm, plan = moe_buffers(nc, m)
        weights_in = m.sem("weights_in")
        norm["weights_in"] = weights_in
        norm["weights"] = [(b1[:, :, :], w["b1"]), (b2[:, :, :], w["b2"].partition_broadcast(P)),
                           (w1[:, :, :, :], w["w1"]), (w2[:, :, :, :], w["w2"])]
        route(nc, x_res, moments, consts, w, norm, plan, "l3f", True)
        dispatch(nc, x_res, norm, plan, rows_in, "l3f")

        xg = m.sb("xg", [P, 2, 2, C])
        tT = m.sb("tT", [HC, 2, 2, ETOK])
        w1_own = m.sb("w1_own", [HC, 2, 2, H])
        hT = m.sb("hT", [P, 2, MC, ETOK])
        ys = m.sb("ys", [P, 2, 2, C])
        pctx = ctx.enter_context(ExitStack())
        pm = Mem(nc, pctx, "l3f_expert")
        h_ps = [pm.ps(f"h{k}", [P, 2, ETOK]) for k in range(HB)]
        y_ps = [pm.ps(f"y{k}", [P, 512]) for k in range(2)]
        tp = [pm.ps(f"tp{k}", [P, 512]) for k in range(2)]
        xg_in = [m.sem(f"xg_in{k}") for k in range(2)]
        ys_out = [m.sem(f"ys_out{k}") for k in range(2)]
        tp_ready = m.sem("tp_ready")
        tT_ready = m.sem("tT_ready")
        w1_ready = m.sem("w1_ready")
        h_ready = m.sem("h_ready")
        relu_done = m.sem("relu_done")
        y_ready = m.sem("y_ready")
        ys_ready = m.sem("ys_ready")
        act_held = m.sem("act_held")
        pool_held = m.sem("pool_held")
        dve_held = m.sem("dve_held")
        LAST = ETILES // 2 - 1

        with nc.Block() as block:
            @block.sync
            def _(sp):
                load_rows(sp, rows_in, xg, xg_in, tp_ready)

            @block.gpsimd
            def _(pool):
                rounds(pool, lambda r, u: store_rows(pool, pool_held, rows_out, ys, ys_out, ys_ready, r, u))
                for u in range(2):
                    pool.wait_ge(ys_out[u], ETILES // 2 * 16)

            @block.tensor
            def _(pe):
                pe.wait_ge(weights_in, 64)

                def turn(r, u):
                    pe.wait_ge(xg_in[u], r * 16 + 16)
                    turn_rows(nc, tp[u], xg[:, u, :, :], consts["ident"]).then_inc(tp_ready, 1)

                def first_layer(r, u):
                    j = r * 2 + u
                    pe.wait_ge(tT_ready, j + 1)
                    pe.wait_ge(w1_ready, j + 1)
                    for b in range(HB):
                        if not (u == 0 and first_round(r)):
                            pe.wait_ge(relu_done, j * HB - HB + b + 1)
                        for c in (2 * b, 2 * b + 1):
                            for h in range(2):
                                ins = nc.tensor.matmul(h_ps[b][:, c % 2, :], w1_own[:, u, h, c * P:(c + 1) * P],
                                                       tT[:, u, h, :], start=h == 0, stop=h == 1)
                        ins.then_inc(h_ready, 1)

                def second_layer(r, u):
                    j = r * 2 + u
                    e = owner_of(pe, plan, j)
                    pe.wait_ge(relu_done, j * HB + HB)
                    if not first_round(r):
                        pe.wait_ge(ys_ready, j - 1)
                    for t in range(2):
                        for c in range(MC):
                            ins = nc.tensor.matmul(y_ps[u][:, t * C:(t + 1) * C], hT[:, u, c, t * P:(t + 1) * P],
                                                   w2[:, c, bass.ds(e, 1), :].rearrange("p a c -> p (a c)"),
                                                   start=c == 0, stop=c == MC - 1)
                    ins.then_inc(y_ready, 1)

                expert_order(pe, turn, first_layer, second_layer)

            @block.scalar
            def _(act):
                def tile(r, u):
                    j = r * 2 + u
                    e = owner_of(act, plan, j)
                    if not first_round(r):
                        act.wait_ge(h_ready, j * HB - HB)
                    act.wait_ge(tp_ready, j + 1)
                    nc.scalar.copy(tT[:, u, :, :].rearrange("p h t -> p (h t)"), tp[u][0:HC, :]).then_inc(tT_ready, 1)
                    if not first_round(r):
                        act.wait_ge(y_ready, j - 1)
                    for c in range(MC):
                        if c % 2 == 0:
                            act.wait_ge(h_ready, j * HB + c // 2 + 1)
                            hold(act, act_held)
                        ins = nc.scalar.activation(hT[:, u, c, :], h_ps[c // 2][:, c % 2, :], ACT.Relu,
                                                   bias=b1[:, bass.ds(e, 1), c:c + 1].rearrange("p a c -> p (a c)"))
                        if c % 2:
                            ins.then_inc(relu_done, 1)

                rounds(act, tile)

            @block.vector
            def _(dve):
                dve.wait_ge(weights_in, 64)

                def own_weights(r, u):
                    j = r * 2 + u
                    e = owner_of(dve, plan, j)
                    if not first_round(r):
                        dve.wait_ge(h_ready, j * HB - HB)
                        hold(dve, dve_held)
                    nc.vector.tensor_copy(w1_own[:, u, :, :],
                                          w1[:, :, bass.ds(e, 1), :].rearrange("p h a f -> p h (a f)")
                                          ).then_inc(w1_ready, 1)

                def finish(r, u):
                    j = r * 2 + u
                    e = owner_of(dve, plan, j)
                    if not first_round(r):
                        dve.wait_ge(ys_out[u], r * 16)
                    dve.wait_ge(y_ready, j + 1)
                    nc.vector.tensor_tensor(ys[:, u, :, :], y_ps[u][:, 0:2 * C].rearrange("p (t c) -> p t c", t=2),
                                            b2[:, bass.ds(e, 1), :].broadcast_to([P, 2, C]),
                                            ALU.add).then_inc(ys_ready, 1)

                own_weights(0, 0)
                own_weights(0, 1)
                own_weights(1, 0)
                own_weights(1, 1)
                finish(0, 0)
                with dve.Fori(1, LAST) as r:
                    own_weights(r + 1, 0)
                    finish(r - 1, 1)
                    own_weights(r + 1, 1)
                    finish(r, 0)
                finish(LAST - 1, 1)
                finish(LAST, 0)
                finish(LAST, 1)
        pctx.close()
        combine(nc, x_res, plan, rows_out, "l3f")
        m.clear()


def moe_glu_phase(nc, x_res, moments, consts, w):
    LIMIT = 7.0
    ALPHA = 1.702
    rows_in, rows_out = consts["rows_in"], consts["rows_out"]
    with ExitStack() as ctx:
        m = Mem(nc, ctx, "l2f")
        wgu = m.sb("wgu", [HC, 2, E, 4 * HC])
        wd = m.sb("wd", [HC, 2, E, C])
        bgu = m.sb("bgu", [HC, E, 4])
        bd = m.sb("bd", [P, E, C])
        norm, plan = moe_buffers(nc, m)
        weights_in = m.sem("weights_in")
        norm["weights_in"] = weights_in
        norm["weights"] = [(bgu[:, :, :], w["bgu"]), (bd[:, :, :], w["bd"].partition_broadcast(P)),
                           (wgu[:, :, :, :], w["wgu"]), (wd[:, :, :, :], w["wd"])]
        route(nc, x_res, moments, consts, w, norm, plan, "l2f", False)
        dispatch(nc, x_res, norm, plan, rows_in, "l2f")

        xg = m.sb("xg", [P, 2, 2, C])
        tT = m.sb("tT", [HC, 2, 2, ETOK])
        wgu_own = m.sb("wgu_own", [HC, 2, 2, 4 * HC])
        gate_in = m.sb("gate_in", [HC, 2, 2, ETOK])
        up_in = m.sb("up_in", [HC, 2, 2, ETOK])
        silu = m.sb("silu", [HC, 2, 2, ETOK])
        aT = m.sb("aT", [HC, 2, 2, ETOK])
        ys = m.sb("ys", [P, 2, 2, C])
        pctx = ctx.enter_context(ExitStack())
        pm = Mem(nc, pctx, "l2f_expert")
        gate_ps = [pm.ps(f"gate{k}", [HC, 2, ETOK]) for k in range(2)]
        up_ps = [pm.ps(f"up{k}", [HC, 2, ETOK]) for k in range(2)]
        y_ps = [pm.ps(f"y{k}", [P, 512]) for k in range(2)]
        tp = [pm.ps(f"tp{k}", [P, 512]) for k in range(2)]
        xg_in = [m.sem(f"xg_in{k}") for k in range(2)]
        ys_out = [m.sem(f"ys_out{k}") for k in range(2)]
        tp_ready = m.sem("tp_ready")
        tT_ready = m.sem("tT_ready")
        own_ready = m.sem("own_ready")
        gate_ready = m.sem("gate_ready")
        up_ready = m.sem("up_ready")
        gate_clipped = m.sem("gate_clipped")
        up_half = m.sem("up_half")
        up_clipped = m.sem("up_clipped")
        silu_ready = m.sem("silu_ready")
        aT_ready = m.sem("aT_ready")
        y_ready = m.sem("y_ready")
        ys_ready = m.sem("ys_ready")
        pool_held = m.sem("pool_held")
        LAST = ETILES // 2 - 1

        with nc.Block() as block:
            @block.sync
            def _(sp):
                load_rows(sp, rows_in, xg, xg_in, tp_ready)

            @block.tensor
            def _(pe):
                pe.wait_ge(weights_in, 64)

                def turn(r, u):
                    pe.wait_ge(xg_in[u], r * 16 + 16)
                    turn_rows(nc, tp[u], xg[:, u, :, :], consts["ident"]).then_inc(tp_ready, 1)

                def first_layer(r, u):
                    j = r * 2 + u
                    pe.wait_ge(tT_ready, j + 1)
                    pe.wait_ge(own_ready, j + 1)
                    for ps, free, ready, c0 in ((gate_ps, gate_clipped, gate_ready, 0),
                                                (up_ps, up_half, up_ready, 2)):
                        if not first_round(r):
                            pe.wait_ge(free, j - 1)
                        for c in range(2):
                            for h in range(2):
                                ins = nc.tensor.matmul(ps[u][:, c, :],
                                                       wgu_own[:, u, h, (c0 + c) * HC:(c0 + c + 1) * HC],
                                                       tT[:, u, h, :], start=h == 0, stop=h == 1)
                        ins.then_inc(ready, 1)

                def second_layer(r, u):
                    j = r * 2 + u
                    e = owner_of(pe, plan, j)
                    pe.wait_ge(aT_ready, j + 1)
                    if not first_round(r):
                        pe.wait_ge(ys_ready, j - 1)
                    for t in range(2):
                        for h in range(2):
                            ins = nc.tensor.matmul(y_ps[u][:, t * C:(t + 1) * C], aT[:, u, h, t * P:(t + 1) * P],
                                                   wd[:, h, bass.ds(e, 1), :].rearrange("p a c -> p (a c)"),
                                                   start=h == 0, stop=h == 1)
                    ins.then_inc(y_ready, 1)

                expert_order(pe, turn, first_layer, second_layer)

            @block.scalar
            def _(act):
                def turned(r, u):
                    j = r * 2 + u
                    if not first_round(r):
                        act.wait_ge(up_ready, j - 1)
                    act.wait_ge(tp_ready, j + 1)
                    nc.scalar.copy(tT[:, u, :, :].rearrange("p h t -> p (h t)"), tp[u][0:HC, :]).then_inc(tT_ready, 1)

                def silu_of(r, u):
                    j = r * 2 + u
                    if not first_round(r):
                        act.wait_ge(aT_ready, j - 1)
                    act.wait_ge(gate_clipped, j + 1)
                    nc.scalar.activation(silu[:, u, :, :], gate_in[:, u, :, :], ACT.Silu,
                                         scale=ALPHA).then_inc(silu_ready, 1)

                turned(0, 0)
                turned(0, 1)
                silu_of(0, 0)
                with act.Fori(1, LAST + 1) as r:
                    turned(r, 0)
                    silu_of(r - 1, 1)
                    turned(r, 1)
                    silu_of(r, 0)
                silu_of(LAST, 1)

            @block.gpsimd
            def _(pool):
                def own_weights(r, u):
                    e = owner_of(pool, plan, r * 2 + u)
                    if not first_round(r):
                        pool.wait_ge(up_ready, r * 2 + u - 1)
                        hold(pool, pool_held)
                    nc.gpsimd.tensor_copy(wgu_own[:, u, :, :],
                                          wgu[:, :, bass.ds(e, 1), :].rearrange("p h a f -> p h (a f)")
                                          ).then_inc(own_ready, 1)

                def store(r, u):
                    store_rows(pool, pool_held, rows_out, ys, ys_out, ys_ready, r, u)

                pool.wait_ge(weights_in, 64)
                own_weights(0, 0)
                own_weights(0, 1)
                own_weights(1, 0)
                own_weights(1, 1)
                store(0, 0)
                with pool.Fori(1, LAST) as r:
                    own_weights(r + 1, 0)
                    store(r - 1, 1)
                    own_weights(r + 1, 1)
                    store(r, 0)
                store(LAST - 1, 1)
                store(LAST, 0)
                store(LAST, 1)
                for u in range(2):
                    pool.wait_ge(ys_out[u], ETILES // 2 * 16)

            @block.vector
            def _(dve):
                dve.wait_ge(weights_in, 64)

                def clip(r, u):
                    j = r * 2 + u
                    e = owner_of(dve, plan, j)
                    if not first_round(r):
                        dve.wait_ge(silu_ready, j - 1)
                        dve.wait_ge(aT_ready, j - 1)
                    dve.wait_ge(gate_ready, j + 1)
                    for c in range(2):
                        ins = nc.vector.tensor_scalar(gate_in[:, u, c, :], gate_ps[u][:, c, :],
                                                      bgu[:, bass.ds(e, 1), c:c + 1].rearrange("p a c -> p (a c)"),
                                                      LIMIT, ALU.add, ALU.min)
                    ins.then_inc(gate_clipped, 1)
                    dve.wait_ge(up_ready, j + 1)
                    for c in range(2):
                        ins = nc.vector.tensor_scalar(up_in[:, u, c, :], up_ps[u][:, c, :],
                                                      bgu[:, bass.ds(e, 1), 2 + c:3 + c].rearrange("p a c -> p (a c)"),
                                                      LIMIT, ALU.add, ALU.min)
                    ins.then_inc(up_half, 1)
                    dve.wait_ge(up_half, j + 1)
                    nc.vector.tensor_scalar(up_in[:, u, :, :], up_in[:, u, :, :], -LIMIT, 1.0,
                                            ALU.max, ALU.add).then_inc(up_clipped, 1)

                    dve.wait_ge(silu_ready, j + 1)
                    dve.wait_ge(up_clipped, j + 1)
                    if not first_round(r):
                        dve.wait_ge(y_ready, j - 1)
                    nc.vector.scalar_tensor_tensor(out=aT[:, u, :, :], in0=silu[:, u, :, :], scalar=1.0 / ALPHA,
                                                   in1=up_in[:, u, :, :], op0=ALU.mult,
                                                   op1=ALU.mult).then_inc(aT_ready, 1)

                def finish(r, u):
                    j = r * 2 + u
                    e = owner_of(dve, plan, j)
                    if not first_round(r):
                        dve.wait_ge(ys_out[u], r * 16)
                    dve.wait_ge(y_ready, j + 1)
                    nc.vector.tensor_tensor(ys[:, u, :, :], y_ps[u][:, 0:2 * C].rearrange("p (t c) -> p t c", t=2),
                                            bd[:, bass.ds(e, 1), :].broadcast_to([P, 2, C]),
                                            ALU.add).then_inc(ys_ready, 1)

                clip(0, 0)
                clip(0, 1)
                finish(0, 0)
                with dve.Fori(1, LAST + 1) as r:
                    clip(r, 0)
                    finish(r - 1, 1)
                    clip(r, 1)
                    finish(r, 0)
                finish(LAST, 1)
        pctx.close()
        combine(nc, x_res, plan, rows_out, "l2f")
        m.clear()


def memory_attention_phase(nc, x_res, moments, consts, w):
    M = 8
    SCALE = float(C) ** -0.5
    with ExitStack() as ctx:
        m = Mem(nc, ctx, "l3a")
        wq = m.sb("wq", [HC, 2, C])
        wk = m.sb("wk", [HC, 2, C])
        wv = m.sb("wv", [HC, 2, C])
        wo = m.sb("wo", [HC, 2, C])
        memT = m.sb("memT", [HC, 2, M])
        bq = m.sb("bq", [HC, 2])
        bk = m.sb("bk", [HC, 2])
        bv = m.sb("bv", [P, C])
        bo = m.sb("bo", [P, C])
        rstd = m.sb("rstd", [P, TILES])
        shift = m.sb("shift", [P, TILES])
        y0 = m.sb("guess", [P, 4, TILES])
        xn = m.sb("xn", [P, 2, 2, C])
        tT = m.sb("tT", [HC, 2, 2, T])
        qT = m.sb("qT", [HC, 2, 2, T])
        kT = [m.sb(f"kT{k}", [HC, 2, T + M]) for k in range(2)]
        v = m.sb("v", [P, 2, 2, C])
        vm = m.sb("vm", [M, C])
        top = m.sb("top", [P, 2, 2])
        sums = m.sb("sums", [P, 2, 2])
        probs = m.sb("probs", [P, 2, T + M])
        pT = m.sb("pT", [P, 2, T])
        pmT = m.sb("pmT", [M, T])
        oT = m.sb("oT", [HC, 2, T])
        tp = m.ps("tp", [P, 512])
        q_ps = m.ps("q", [HC, 2, T])
        k_ps = m.ps("k", [HC, 2, T])
        v_ps = m.ps("v_ps", [P, 512])
        s_ps = [m.ps(f"s{t}", [P, 512]) for t in range(2)]
        pT_ps = m.ps("pT_ps", [P, 2, T])
        pmT_ps = m.ps("pmT_ps", [P, 512])
        tp_ps = tp[0:HC, :].rearrange("p (h t) -> p h t", h=2)
        o_ps = q_ps
        y_ps = pmT_ps

        weights_in = m.sem("weights_in")
        half_log = m.sem("half_log")
        dve_chain0 = m.sem("dve_chain0")
        rstd_ready = m.sem("rstd_ready")
        xn_ready = m.sem("xn_ready")
        tp_ready = m.sem("tp_ready")
        tT_ready = m.sem("tT_ready")
        mem_ps = m.sem("mem_ps")
        mem_ready = m.sem("mem_ready")
        q_ready = m.sem("q_ready")
        k_ready = m.sem("k_ready")
        v_ready = m.sem("v_ready")
        qT_ready = m.sem("qT_ready")
        kT_ready = m.sem("kT_ready")
        vb_ready = m.sem("vb_ready")
        scores_ready = m.sem("scores_ready")
        max_ready = m.sem("max_ready")
        probs_ready = m.sem("probs_ready")
        pT_psum = m.sem("pT_psum")
        pT_ready = m.sem("pT_ready")
        pmT_ready = m.sem("pmT_ready")
        o_ready = m.sem("o_ready")
        oT_ready = m.sem("oT_ready")
        y_ready = m.sem("y_ready")
        y_used = m.sem("y_used")
        dve_chain = m.sem("dve_chain")
        act_held = m.sem("act_held")

        with nc.Block() as block:
            @block.sync
            def _(sp):
                for dst, src in ((memT[:, :, :], w["memT"]), (wk[:, :, :], w["wk"]), (wv[:, :, :], w["wv"]),
                                 (wq[:, :, :], w["wq"]), (wo[:, :, :], w["wo"]), (bq[:, :], w["bq"]),
                                 (bk[:, :], w["bk"]), (bv[:, :], w["bv"].partition_broadcast(P)),
                                 (bo[:, :], w["bo"].partition_broadcast(P))):
                    sp.dma_start(dst, src).then_inc(weights_in, 16)

            @block.scalar
            def _(act):
                for s in (xn_ready, tT_ready, qT_ready, kT_ready, probs_ready, oT_ready):
                    act.sem_inc(s, 1)
                rstd_steps_act(nc, act, None, half_log, moments, y0, consts["eps"])
                act.wait_ge(weights_in, 9 * 16)
                act.wait_ge(mem_ps, 1)
                for k in range(2):
                    for h in range(2):
                        nc.scalar.activation(kT[k][:, h, T:T + M], k_ps[:, h, 0:M], ACT.Identity,
                                             bias=bk[:, h:h + 1]).then_inc(mem_ready, 1)
                act.wait_ge(rstd_ready, 1)
                hold(act, act_held)

                def first(n, u):
                    normalise(nc, xn[:, u, :, :], x_res, rstd, shift, n * 2).then_inc(xn_ready, 1)
                    act.wait_ge(tp_ready, counted(n + 1))
                    nc.scalar.copy(tT[:, u, :, :], tp_ps).then_inc(tT_ready, 1)
                    act.wait_ge(q_ready, counted(n + 1))
                    for h in range(2):
                        ins = nc.scalar.activation(qT[:, u, h, :], q_ps[:, h, :], ACT.Identity, bias=bq[:, h:h + 1])
                    ins.then_inc(qT_ready, 1)
                    act.wait_ge(k_ready, counted(n + 1))
                    for h in range(2):
                        ins = nc.scalar.activation(kT[u][:, h, 0:T], k_ps[:, h, :], ACT.Identity, bias=bk[:, h:h + 1])
                    ins.then_inc(kT_ready, 1)

                def rest(n, u, nxt):
                    for t in range(2):
                        act.wait_ge(max_ready, counted(n * 2 + (t + 1)))
                        nc.scalar.activation(probs[:, t, :], s_ps[t][:, 0:T + M], ACT.Exp, bias=top[:, t, 1:2],
                                             scale=SCALE, accum_out=sums[:, t, 0:1]).then_inc(probs_ready, 1)
                    nxt()
                    act.wait_ge(o_ready, counted(n + 1))
                    nc.scalar.copy(oT[:, :, :], o_ps[:, :, :]).then_inc(oT_ready, 1)

                pipelined(act, first, rest)

            @block.vector
            def _(dve):
                chain0 = Chain(dve, dve_chain0)
                rstd_steps_dve(nc, dve, chain0, half_log, moments, y0, rstd, shift).then_inc(rstd_ready, 1)
                for s in (vb_ready, max_ready, pT_ready, pmT_ready, y_used):
                    dve.sem_inc(s, 1)
                dve.wait_ge(weights_in, 9 * 16)
                dve.wait_ge(mem_ps, 2)
                nc.vector.tensor_tensor(vm[:, :], v_ps[0:M, 0:C], bv[0:M, :], ALU.add).then_inc(mem_ready, 1)

                def first(n, u):
                    dve.wait_ge(v_ready, counted(n + 1))
                    nc.vector.tensor_tensor(v[:, u, :, :], v_ps[:, 0:2 * C].rearrange("p (t c) -> p t c", t=2),
                                            bv[:, :].unsqueeze(1).broadcast_to([P, 2, C]), ALU.add).then_inc(vb_ready, 1)

                def rest(n, u, nxt):
                    chain = Chain(dve, dve_chain, 2 + 1 + 4, n)
                    link = chain.link
                    for t in range(2):
                        dve.wait_ge(scores_ready, counted(n * 2 + (t + 1)))
                        link(nc.vector.tensor_reduce(top[:, t, 0:1], s_ps[t][:, 0:T + M], AX.X, ALU.max))
                        nc.vector.tensor_scalar(top[:, t, 1:2], top[:, t, 0:1], -SCALE, None,
                                                ALU.mult).then_inc(max_ready, 1)
                    nxt()
                    dve.wait_ge(pT_psum, counted(n + 1))
                    nc.vector.tensor_copy(pT[:, :, :], pT_ps[:, :, :]).then_inc(pT_ready, 1)
                    nc.vector.tensor_copy(pmT[:, :], pmT_ps[0:M, 0:T]).then_inc(pmT_ready, 1)
                    link(nc.vector.reciprocal(sums[:, :, 1], sums[:, :, 0]))
                    dve.wait_ge(y_ready, counted(n + 1))
                    for t in range(2):
                        xt = tile_of(x_res, n, t)
                        link(nc.vector.scalar_tensor_tensor(out=xt, in0=y_ps[:, t * C:(t + 1) * C],
                                                            scalar=sums[:, t, 1:2], in1=xt, op0=ALU.mult, op1=ALU.add))
                    for t in range(2):
                        xt = tile_of(x_res, n, t)
                        link(nc.vector.tensor_tensor(xt, xt, bo[:, :], ALU.add))
                    dve.sem_inc(y_used, 1)
                    chain.close()

                pipelined(dve, first, rest)

            @block.tensor
            def _(pe):
                for s in (tp_ready, q_ready, k_ready, v_ready, scores_ready, pT_psum, o_ready, y_ready):
                    pe.sem_inc(s, 1)
                pe.wait_ge(weights_in, 9 * 16)
                for ho in range(2):
                    for h in range(2):
                        ins = nc.tensor.matmul(k_ps[:, ho, 0:M], wk[:, h, ho * HC:(ho + 1) * HC], memT[:, h, :],
                                               start=h == 0, stop=h == 1)
                ins.then_inc(mem_ps, 1)
                for h in range(2):
                    ins = nc.tensor.matmul(v_ps[0:M, 0:C], memT[:, h, :], wv[:, h, :], start=h == 0, stop=h == 1)
                ins.then_inc(mem_ps, 1)
                pe.wait_ge(mem_ready, 5)

                def first(n, u):
                    pe.wait_ge(xn_ready, counted(n + 1))
                    for h in range(2):
                        for t in range(2):
                            ins = nc.tensor.transpose(tp_ps[:, h, t * P:(t + 1) * P],
                                                      xn[:, u, t, h * HC:(h + 1) * HC], consts["ident"])
                    ins.then_inc(tp_ready, 1)
                    pe.wait_ge(tT_ready, counted(n + 1))
                    for ps, wx, ready, free in ((q_ps, wq, q_ready, oT_ready), (k_ps, wk, k_ready, kT_ready)):
                        if free is oT_ready:
                            pe.wait_ge(free, counted(n) if isinstance(n, int) and n == 0 else counted(n - 1))
                        else:
                            pe.wait_ge(free, counted(n))
                        for ho in range(2):
                            for h in range(2):
                                ins = nc.tensor.matmul(ps[:, ho, :], wx[:, h, ho * HC:(ho + 1) * HC], tT[:, u, h, :],
                                                       start=h == 0, stop=h == 1)
                        ins.then_inc(ready, 1)
                    pe.wait_ge(vb_ready, counted(n))
                    for t in range(2):
                        for h in range(2):
                            ins = nc.tensor.matmul(v_ps[:, t * C:(t + 1) * C], tT[:, u, h, t * P:(t + 1) * P],
                                                   wv[:, h, :], start=h == 0, stop=h == 1)
                    ins.then_inc(v_ready, 1)

                def rest(n, u, nxt):
                    pe.wait_ge(qT_ready, counted(n + 1))
                    pe.wait_ge(kT_ready, counted(n + 1))
                    for t in range(2):
                        pe.wait_ge(probs_ready, counted(n * 2))
                        for h in range(2):
                            ins = nc.tensor.matmul(s_ps[t][:, 0:T + M], qT[:, u, h, t * P:(t + 1) * P], kT[u][:, h, :],
                                                   start=h == 0, stop=h == 1)
                        ins.then_inc(scores_ready, 1)
                    nxt()
                    pe.wait_ge(pT_ready, counted(n))
                    pe.wait_ge(y_used, counted(n))
                    for t in range(2):
                        pe.wait_ge(probs_ready, counted(n * 2 + (t + 1)))
                        for j in range(2):
                            nc.tensor.transpose(pT_ps[:, j, t * P:(t + 1) * P], probs[:, t, j * P:(j + 1) * P],
                                                consts["ident"])
                        ins = nc.tensor.transpose(pmT_ps[0:M, t * P:(t + 1) * P], probs[:, t, T:T + M], consts["ident"])
                    ins.then_inc(pT_psum, 1)
                    pe.wait_ge(pT_ready, counted(n + 1))
                    pe.wait_ge(pmT_ready, counted(n + 1))
                    pe.wait_ge(vb_ready, counted(n + 1))
                    pe.wait_ge(qT_ready, counted(n + 2) if not (isinstance(n, int) and n == B - 1) else counted(B))
                    for h in range(2):
                        for j in range(2):
                            nc.tensor.matmul(o_ps[:, h, :], v[:, u, j, h * HC:(h + 1) * HC], pT[:, j, :],
                                             start=j == 0, stop=False)
                        ins = nc.tensor.matmul(o_ps[:, h, :], vm[:, h * HC:(h + 1) * HC], pmT[:, :],
                                               start=False, stop=True)
                    ins.then_inc(o_ready, 1)
                    pe.wait_ge(oT_ready, counted(n + 1))
                    for t in range(2):
                        for h in range(2):
                            ins = nc.tensor.matmul(y_ps[:, t * C:(t + 1) * C], oT[:, h, t * P:(t + 1) * P], wo[:, h, :],
                                                   start=h == 0, stop=h == 1)
                    ins.then_inc(y_ready, 1)

                pipelined(pe, first, rest)
        m.clear()


def fourier_phase(nc, x_res, moments, consts, w):
    MODES = HH * (WW // 2 + 1)
    MH = MODES // 2
    LAMBDA = 0.01
    with ExitStack() as ctx:
        m = Mem(nc, ctx, "l1")
        dft = m.sb("dft", [P, 2, 2 * MODES])
        idft = m.sb("idft", [MH, 2, 2, T])
        w1 = m.sb("w1", [HC, 3, 2, HC])
        w2 = m.sb("w2", [HC, 2, 3, HC])
        b1 = m.sb("b1", [HC, 2, 2])
        b2 = m.sb("b2", [MH, 2, 2, HC])
        xs = m.sb("xs", [P, 2, 2, C])
        spec = m.sb("spec", [HC, 2, 2, 2 * MODES])
        o1 = m.sb("o1", [HC, 2, 2 * MODES])
        o2 = m.sb("o2", [MH, 2, 2, 2, HC])
        clip = m.sb("clip", [MH, 2, 2, 2, HC])
        o3 = m.sb("o3", [MH, 2, 2, 2, HC])
        spec_ps = [m.ps(f"spec{h}", [P, 512]) for h in range(2)]
        o1_ps = [m.ps(f"o1_{h}", [P, 512]) for h in range(2)]
        o2_ps = [m.ps(f"o2_{h}", [P, 512]) for h in range(2)]
        y_ps = m.ps("y", [P, 512])

        weights_in = m.sem("weights_in")
        negated = m.sem("negated")
        xs_ready = m.sem("xs_ready")
        spec_psum = m.sem("spec_psum")
        spec_ready = m.sem("spec_ready")
        o1_psum = m.sem("o1_psum")
        o1_ready = m.sem("o1_ready")
        o2_psum = m.sem("o2_psum")
        biased = m.sem("biased")
        clipped = m.sem("clipped")
        o3_ready = m.sem("o3_ready")
        y_ready = m.sem("y_ready")
        y_used = m.sem("y_used")

        with nc.Block() as block:
            @block.sync
            def _(sp):
                for dst, src in ((dft[:, :, :], w["dft"]), (w1[:, 0:2, :, :], w["w1"]), (w2[:, :, 1:3, :], w["w2"]),
                                 (b1[:, :, :], w["b1"]), (b2[:, :, :, :], w["b2"].partition_broadcast(MH)),
                                 (idft[:, :, :, :], w["idft"])):
                    sp.dma_start(dst, src).then_inc(weights_in, 16)

            @block.scalar
            def _(act):
                for s in (xs_ready, spec_ready, o1_ready):
                    act.sem_inc(s, 1)
                act.wait_ge(weights_in, 6 * 16)

                def first(n, u):
                    nc.scalar.copy(xs[:, u, :, :], x_res[:, bass.ds(n * 2, 2), :]).then_inc(xs_ready, 1)
                    for h in range(2):
                        act.wait_ge(spec_psum, counted(n * 2 + (h + 1)))
                        nc.scalar.copy(spec[:, u, h, :], spec_ps[h][0:HC, 0:2 * MODES]).then_inc(spec_ready, 1)

                def rest(n, u, nxt):
                    for h in range(2):
                        act.wait_ge(o1_psum, counted(n * 2 + (h + 1)))
                        for ri in range(2):
                            at = slice(ri * MODES, (ri + 1) * MODES)
                            ins = nc.scalar.activation(o1[:, h, at], o1_ps[h][0:HC, at], ACT.Relu,
                                                       bias=b1[:, h, ri:ri + 1])
                        ins.then_inc(o1_ready, 1)
                    nxt()

                pipelined(act, first, rest)

            @block.gpsimd
            def _(pool):
                pool.sem_inc(o3_ready, 1)
                with pool.Fori(0, B) as n:
                    pool.wait_ge(clipped, counted(n * 2 + 2))
                    pool.wait_ge(y_ready, counted(n))
                    nc.gpsimd.tensor_tensor(o3[:, :, :, :, :], o2[:, :, :, :, :], clip[:, :, :, :, :],
                                            ALU.subtract).then_inc(o3_ready, 1)

            @block.vector
            def _(dve):
                for s in (biased, clipped, y_used):
                    dve.sem_inc(s, 1)
                dve.wait_ge(weights_in, 6 * 16)
                nc.vector.tensor_scalar(w1[:, 2, :, :], w1[:, 1, :, :], -1.0, None, ALU.mult).then_inc(negated, 1)
                nc.vector.tensor_scalar(w2[:, :, 0, :], w2[:, :, 2, :], -1.0, None, ALU.mult).then_inc(negated, 1)

                def first(n, u):
                    pass

                def rest(n, u, nxt):
                    dve.wait_ge(o3_ready, counted(n))
                    for q in range(2):
                        dve.wait_ge(o2_psum, counted(n * 2 + (q + 1)))
                        nc.vector.tensor_tensor(o2[:, q, :, :, :],
                                                o2_ps[q][0:MH, 0:2 * C].rearrange("p (h r c) -> p h r c", h=2, r=2),
                                                b2[:, :, :, :], ALU.add).then_inc(biased, 1)
                        dve.wait_ge(biased, counted(n * 2 + (q + 1)))
                        nc.vector.tensor_scalar(clip[:, q, :, :, :], o2[:, q, :, :, :], LAMBDA, -LAMBDA,
                                                ALU.min, ALU.max).then_inc(clipped, 1)
                    dve.wait_ge(y_ready, counted(n + 1))
                    xt = x_res[:, bass.ds(n * 2, 2), :]
                    nc.vector.tensor_tensor(xt, y_ps[:, 0:2 * C].rearrange("p (t c) -> p t c", t=2), xt,
                                            ALU.add).then_inc(y_used, 1)

                pipelined(dve, first, rest)

            @block.tensor
            def _(pe):
                for s in (spec_psum, o1_psum, o2_psum, y_ready):
                    pe.sem_inc(s, 1)
                pe.wait_ge(weights_in, 6 * 16)
                pe.wait_ge(negated, 2)

                def first(n, u):
                    pe.wait_ge(xs_ready, counted(n + 1))
                    for h in range(2):
                        pe.wait_ge(spec_ready, counted(n * 2 + (h + 1) - 2) if h else counted(n * 2))
                        for t in range(2):
                            ins = nc.tensor.matmul(spec_ps[h][0:HC, 0:2 * MODES], xs[:, u, t, h * HC:(h + 1) * HC],
                                                   dft[:, t, :], start=t == 0, stop=t == 1)
                        ins.then_inc(spec_psum, 1)

                def rest(n, u, nxt):
                    re, im = slice(0, MODES), slice(MODES, 2 * MODES)
                    for h in range(2):
                        pe.wait_ge(spec_ready, counted(n * 2 + (h + 1)))
                        pe.wait_ge(o1_ready, counted(n * 2))
                        o = o1_ps[h][0:HC, :]
                        s = spec[:, u, h, :]
                        nc.tensor.matmul(o[:, 0:2 * MODES], w1[:, 0, h, :], s, start=True, stop=False,
                                         skip_group_check=True)
                        nc.tensor.matmul(o[:, re], w1[:, 2, h, :], s[:, im], start=False, stop=False,
                                         skip_group_check=True)
                        nc.tensor.matmul(o[:, im], w1[:, 1, h, :], s[:, re], start=False, stop=True,
                                         skip_group_check=True).then_inc(o1_psum, 1)
                    nxt()
                    pe.wait_ge(o1_ready, counted(n * 2 + 2))
                    for q in range(2):
                        pe.wait_ge(biased, counted(n * 2))
                        for h in range(2):
                            o = o2_ps[q][0:MH, h * C:(h + 1) * C]
                            for ri in range(2):
                                rhs = w2[:, h, 1:3, :] if ri == 0 else w2[:, h, 0:2, :]
                                lhs = o1[:, h, ri * MODES + q * MH:ri * MODES + (q + 1) * MH]
                                ins = nc.tensor.matmul(o, lhs, rhs, start=ri == 0, stop=ri == 1)
                        ins.then_inc(o2_psum, 1)
                    pe.wait_ge(o3_ready, counted(n + 1))
                    pe.wait_ge(y_used, counted(n))
                    for t in range(2):
                        for k in range(4):
                            q, ri = k // 2, k % 2
                            ins = nc.tensor.matmul(y_ps[:, t * C:(t + 1) * C], idft[:, q, ri, t * P:(t + 1) * P],
                                                   o3[:, q, :, ri, :], start=k == 0, stop=k == 3)
                    ins.then_inc(y_ready, 1)

                pipelined(pe, first, rest)
        m.clear()


def mamba_phase(nc, x_res, moments, consts, w):
    R, DI, NS, DC, DTR = 48, 96, 16, 4, 12
    CH = 512
    CHUNKS = TOK // CH
    CT = CH // P
    ATANH = [2.0 / (2 * k + 1) for k in range(8)]
    DG = P // NS
    G = DI // DG
    with ExitStack() as ctx:
        m = Mem(nc, ctx, "l0")
        down = m.sb("down", [HC, 2, R])
        inp = m.sb("inp", [R, 2 * DI])
        convw = m.sb("convw", [DI, DC])
        cols = m.sb("cols", [DI, 3])
        xdt = m.sb("xdt", [DI, DTR])
        xb = m.sb("xb", [DI, 2, DG, NS])
        dtw = m.sb("dtw", [DTR, DI])
        a_col = m.sb("a_col", [P, G])
        sel = m.sb("sel", [DI, G, P])
        selT = m.sb("selT", [P, G, DI])
        outp = m.sb("outp", [DI, R])
        up = m.sb("up", [R, C])
        ln_g = m.sb("ln_g", [P, R])
        ln_b = m.sb("ln_b", [P, R])
        keep = m.sb("keep", [P, CHUNKS])
        xT = m.sb("xT", [HC, 2, 2, CH])
        xsT = m.sb("xsT", [R, CH])
        xi = m.sb("xi", [DI, 2, DC - 1 + CH])
        conv = m.sb("conv", [DI, 2, CH])
        u_sb = m.sb("u", [DI, 2, CH])
        zs = m.sb("zs", [DI, 2, CH])
        dt_sb = m.sb("dt", [DTR, CH])
        bc = m.sb("bc", [P, 2, 2, CH])
        sp_a = m.sb("sp_a", [DI, 6, CH])
        delta = m.sb("delta", [DI, 2, CH])
        du = m.sb("du", [DI, 2, CH])
        dA = m.sb("dA", [P, 2, CH])
        dBu = m.sb("dBu", [P, 2, CH])
        hs = m.sb("hs", [P, 2, CH])
        hc = m.sb("hc", [P, 2, CH])
        state = m.sb("state", [P, 1, G])
        yy = m.sb("yy", [DI, 2, CH])
        mm = m.sb("mm", [P, 2, CT, R])
        mg = m.sb("mg", [P, CT, R])
        mT = m.sb("mT", [R, CH])
        bns = m.sb("bns", [P, CT, 6])
        mom = m.sb("mom", [P, CT, 2])
        sm = m.sb("sm", [P, 6, CT])
        one = m.sb("one", [P, 1])
        drep_ps = [m.ps(f"drep{k}", [P, CH]) for k in range(2)]
        urep_ps = [m.ps(f"urep{k}", [P, CH]) for k in range(2)]
        y_ps = m.ps("y", [DI, CH])
        g_ps = [m.ps(f"g{k}", [P, CH]) for k in range(3)]

        weights_in = m.sem("weights_in")
        setup = m.sem("setup")
        xT_in = m.sem("xT_in")
        front_ps = m.sem("front_ps")
        front_sb = m.sem("front_sb")
        act_front = m.sem("act_front")
        conv_ready = m.sem("conv_ready")
        silu_ready = m.sem("silu_ready")
        ea_ready = m.sem("ea_ready")
        soft_ready = m.sem("soft_ready")
        delta_ready = m.sem("delta_ready")
        du_ready = m.sem("du_ready")
        drep_ready = m.sem("drep_ready")
        urep_ready = m.sem("urep_ready")
        dA_ready = m.sem("dA_ready")
        dBu_ready = m.sem("dBu_ready")
        scan_ready = m.sem("scan_ready")
        state_ready = m.sem("state_ready")
        hc_ready = m.sem("hc_ready")
        hc_used = m.sem("hc_used")
        y_gated = m.sem("y_gated")
        m_ready = m.sem("m_ready")
        var_ready = m.sem("var_ready")
        guess_ready = m.sem("guess_ready")
        ln_ready = m.sem("ln_ready")
        gelu_ready = m.sem("gelu_ready")
        mT_ps = m.sem("mT_ps")
        mT_ready = m.sem("mT_ready")
        up_ready = m.sem("up_ready")
        x_added = m.sem("x_added")
        conv_chain = m.sem("conv_chain")
        tail_chain = m.sem("tail_chain")
        act_chain = m.sem("act_chain")
        act_held = m.sem("act_held")
        dve_held = m.sem("dve_held")
        pe_held = m.sem("pe_held")
        sp_held = m.sem("sp_held")

        loads = ((down[:, :, :], w["down"]), (inp[:, :], w["inp"]), (convw[:, :], w["convw"]), (cols[:, :], w["cols"]),
                 (xdt[:, :], w["xdt"]), (xb[:, :, :, :], w["xb"]), (dtw[:, :], w["dtw"]), (a_col[:, :], w["alog"]),
                 (sel[:, :, :], w["sel"]), (selT[:, :, :], w["selT"]), (outp[:, :], w["outp"]), (up[:, :], w["up"]),
                 (ln_g[:, :], w["lng"].partition_broadcast(P)), (ln_b[:, :], w["lnb"].partition_broadcast(P)),
                 (keep[:, :], w["keep"].partition_broadcast(P)))
        FRONT = 5

        with nc.Block() as block:
            @block.sync
            def _(sp):
                for dst, src in loads:
                    sp.dma_start(dst, src).then_inc(weights_in, 16)

                def load(n, u):
                    sp.dma_start(xT[:, u, :, :], w["xT"][:, :, bass.ds(n * CH, CH)]).then_inc(xT_in, 16)

                load(0, 0)
                sp.wait_ge(xT_in, 16)
                load(1, 1)
                sp.wait_ge(xT_in, 32)
                with sp.Fori(0, CHUNKS // 2 - 1) as it:
                    for u in range(2):
                        sp.wait_ge(front_ps, counted(it * 14 + (7 * u + 1)))
                        hold(sp, sp_held)
                        load(it * 2 + (2 + u), u)
                        sp.wait_ge(xT_in, it * 32 + (48 + 16 * u))
                        hold(sp, sp_held)

            @block.scalar
            def _(act):
                act.wait_ge(weights_in, len(loads) * 16)
                nc.scalar.activation(a_col[:, :], a_col[:, :], ACT.Exp).then_inc(setup, 1)
                for s in (act_front, silu_ready, ea_ready, soft_ready, dA_ready, guess_ready, gelu_ready, mT_ready,
                          state_ready):
                    act.sem_inc(s, 1)
                act.wait_ge(setup, 4)
                hold(act, act_held)

                def first(n, u):
                    def bank(k):
                        act.wait_ge(front_ps, counted(n * 7 + (k + 1)))
                    bank(0)
                    nc.scalar.copy(xsT[:, :], g_ps[0][0:R, :]).then_inc(act_front, 1)
                    bank(1)
                    nc.scalar.copy(xi[:, u, DC - 1:], g_ps[1][0:DI, :]).then_inc(act_front, 1)
                    bank(2)
                    nc.scalar.activation(zs[:, u, :], g_ps[2][0:DI, :], ACT.Silu).then_inc(act_front, 1)
                    act.wait_ge(conv_ready, counted(n + 1))
                    nc.scalar.activation(u_sb[:, u, :], conv[:, 1, :], ACT.Silu).then_inc(silu_ready, 1)
                    bank(3)
                    nc.scalar.copy(dt_sb[:, :], g_ps[0][0:DTR, :]).then_inc(act_front, 1)
                    for k in range(2):
                        bank(4 + k)
                        nc.scalar.copy(bc[:, u, k, :], g_ps[1 + k][:, :]).then_inc(act_front, 1)
                    bank(6)
                    chain = Chain(act, act_chain, 2, n)
                    nc.scalar.activation(sp_a[:, 0, :], g_ps[0][0:DI, :], ACT.Identity,
                                         bias=cols[:, 1:2]).then_inc(act_front, 1)
                    act.wait_ge(act_front, counted(n * 7 + 7))
                    chain.link(nc.scalar.activation(sp_a[:, 1, :], sp_a[:, 0, :], ACT.Abs))
                    chain.link(nc.scalar.activation(sp_a[:, 2, :], sp_a[:, 1, :], ACT.Exp, scale=-1.0))
                    act.sem_inc(soft_ready, 1)
                    chain.close()

                def rest(n, u, nxt):
                    for g in range(G):
                        if g == G // 2:
                            nxt()
                        k = n * G + g
                        act.wait_ge(drep_ready, counted(k + 1))
                        act.wait_ge(scan_ready, counted(k - 1) if g else counted(k))
                        nc.scalar.activation(dA[:, g % 2, :], drep_ps[g % 2][:, :], ACT.Exp,
                                             scale=a_col[:, g:g + 1]).then_inc(dA_ready, 1)
                    act.wait_ge(var_ready, counted(n + 1))
                    nc.scalar.activation(sm[:, 0, :], mom[:, :, 1], ACT.Ln, bias=consts["eps"]).then_inc(ea_ready, 1)
                    act.wait_ge(ea_ready, counted(n + 1))
                    nc.scalar.activation(sm[:, 1, :], sm[:, 0, :], ACT.Exp, scale=-0.5).then_inc(guess_ready, 1)
                    act.wait_ge(ln_ready, counted(n + 1))
                    nc.scalar.activation(mg[:, :, :], mm[:, 0, :, :], ACT.Gelu).then_inc(gelu_ready, 1)
                    act.wait_ge(mT_ps, counted(n + 1))
                    nc.scalar.copy(mT[:, :], g_ps[1][0:R, :]).then_inc(mT_ready, 1)

                pipelined(act, first, rest, CHUNKS)

            @block.gpsimd
            def _(pool):
                pool.sem_inc(hc_ready, 1)
                pool.sem_inc(du_ready, 1)

                def first(n, u):
                    pool.wait_ge(delta_ready, counted(n + 1))
                    nc.gpsimd.tensor_tensor(du[:, u, :], delta[:, u, :], u_sb[:, u, :], ALU.mult).then_inc(du_ready, 1)

                def rest(n, u, nxt):
                    for g in range(G):
                        if g == G // 2 + 1:
                            nxt()
                        k = n * G + g
                        pool.wait_ge(scan_ready, counted(k + 1))
                        pool.wait_ge(hc_used, counted(k - 1) if g else counted(k))
                        nc.gpsimd.tensor_tensor(hc[:, g % 2, :], hs[:, g % 2, :], bc[:, u, 1, :],
                                                ALU.mult).then_inc(hc_ready, 1)

                pipelined(pool, first, rest, CHUNKS)

            @block.vector
            def _(dve):
                for s in (front_sb, conv_ready, delta_ready, dBu_ready, scan_ready, y_gated, var_ready, ln_ready,
                          x_added):
                    dve.sem_inc(s, 1)
                dve.wait_ge(setup, 1)
                nc.vector.tensor_scalar(a_col[:, :], a_col[:, :], -1.0, None, ALU.mult).then_inc(setup, 1)
                nc.vector.memset(xi[:, :, :], 0.0).then_inc(setup, 1)
                nc.vector.memset(one[:, :], 1.0)
                nc.vector.memset(state[:, :, :], 0.0).then_inc(setup, 1)
                dve.wait_ge(setup, 4)

                def first(n, u):
                    chain = Chain(dve, conv_chain, 1 + DC + 4 + len(ATANH), n)
                    chain.link(nc.vector.tensor_scalar(xi[:, u, 0:DC - 1], xi[:, 1 - u, CH:CH + DC - 1],
                                                       keep[0:DI, bass.ds(n, 1)], None, ALU.mult))
                    dve.wait_ge(act_front, counted(n * 7 + 2))
                    chain.link(nc.vector.tensor_scalar(conv[:, 0, :], xi[:, u, 0:CH], convw[:, 0:1], cols[:, 0:1],
                                                       ALU.mult, ALU.add))
                    for k in range(1, DC):
                        chain.link(nc.vector.scalar_tensor_tensor(out=conv[:, k % 2, :], in0=xi[:, u, k:k + CH],
                                                                  scalar=convw[:, k:k + 1], in1=conv[:, (k + 1) % 2, :],
                                                                  op0=ALU.mult, op1=ALU.add))
                    dve.sem_inc(conv_ready, 1)
                    dve.wait_ge(soft_ready, counted(n + 1))
                    v, a, wexp, s, q, acc = (sp_a[:, k, :] for k in range(6))
                    chain.link(nc.vector.tensor_scalar(a, wexp, 2.0, None, ALU.add))
                    chain.link(nc.vector.reciprocal(s, a))
                    chain.link(nc.vector.tensor_tensor(s, s, wexp, ALU.mult))
                    chain.link(nc.vector.tensor_tensor(q, s, s, ALU.mult))
                    chain.link(nc.vector.tensor_scalar(acc, q, ATANH[-1], None, ALU.mult))
                    for c in ATANH[-2:0:-1]:
                        chain.link(nc.vector.scalar_tensor_tensor(out=acc, in0=acc, scalar=c, in1=q, op0=ALU.add,
                                                                  op1=ALU.mult))
                    chain.link(nc.vector.scalar_tensor_tensor(out=acc, in0=acc, scalar=ATANH[0], in1=s, op0=ALU.add,
                                                              op1=ALU.mult))
                    nc.vector.scalar_tensor_tensor(out=delta[:, u, :], in0=v, scalar=0.0,
                                                   in1=acc, op0=ALU.max, op1=ALU.add).then_inc(delta_ready, 1)
                    chain.close()

                def rest(n, u, nxt):
                    chain = Chain(dve, tail_chain, G + 1 + 2 * CT + 1 + 6, n)
                    for g in range(G):
                        if g == G // 2:
                            nxt()
                        k = n * G + g
                        dve.wait_ge(urep_ready, counted(k + 1))
                        nc.vector.tensor_tensor(dBu[:, g % 2, :], urep_ps[g % 2][:, :], bc[:, u, 0, :],
                                                ALU.mult).then_inc(dBu_ready, 1)
                        chain.link(nc.vector.tensor_scalar(state[:, 0, g:g + 1], state[:, 0, g:g + 1],
                                                           keep[:, bass.ds(n, 1)], None, ALU.mult))
                        dve.wait_ge(dBu_ready, counted(k + 1))
                        dve.wait_ge(dA_ready, counted(k + 1))
                        dve.wait_ge(hc_ready, counted(k - 1) if g else counted(k))
                        nc.vector.tensor_tensor_scan(hs[:, g % 2, :], dA[:, g % 2, :], dBu[:, g % 2, :],
                                                     state[:, 0, g:g + 1], ALU.mult, ALU.add).then_inc(scan_ready, 1)
                        dve.wait_ge(scan_ready, counted(k + 1))
                        nc.vector.tensor_copy(state[:, 0, g:g + 1], hs[:, g % 2, CH - 1:CH]).then_inc(state_ready, 1)
                        dve.wait_ge(state_ready, counted(k + 1))
                    dve.wait_ge(hc_used, counted(n * G + G))
                    chain.link(nc.vector.scalar_tensor_tensor(out=yy[:, 0, :], in0=u_sb[:, u, :], scalar=cols[:, 2:3],
                                                              in1=y_ps[:, :], op0=ALU.mult, op1=ALU.add))
                    nc.vector.tensor_tensor(yy[:, 1, :], yy[:, 0, :], zs[:, u, :], ALU.mult).then_inc(y_gated, 1)
                    dve.wait_ge(m_ready, counted(n + 1))
                    m_ps = g_ps[0][:, 0:CT * R].rearrange("p (t r) -> p t r", t=CT)
                    for t in range(CT):
                        hold(dve, dve_held)
                        chain.link(nc.vector.bn_stats(bns[:, t, :], m_ps[:, t, :]))
                    for t in range(CT):
                        hold(dve, dve_held)
                        chain.link(nc.vector.bn_aggr(mom[:, t, :], bns[:, t, :]))
                    dve.sem_inc(var_ready, 1)
                    chain.link(nc.vector.tensor_tensor(mm[:, 0, :, :], m_ps,
                                                       mom[:, :, 0:1].broadcast_to([P, CT, R]), ALU.subtract))
                    dve.wait_ge(guess_ready, counted(n + 1))
                    y = sm[:, 1, :]
                    chain.link(nc.vector.tensor_tensor(sm[:, 2, :], y, y, ALU.mult))
                    chain.link(nc.vector.scalar_tensor_tensor(out=sm[:, 3, :], in0=mom[:, :, 1], scalar=EPS,
                                                              in1=sm[:, 2, :], op0=ALU.add, op1=ALU.mult))
                    chain.link(nc.vector.tensor_scalar(sm[:, 4, :], sm[:, 3, :], -0.5, 1.5, ALU.mult, ALU.add))
                    chain.link(nc.vector.tensor_tensor(sm[:, 5, :], sm[:, 4, :], y, ALU.mult))
                    chain.link(nc.vector.tensor_tensor(mm[:, 1, :, :], mm[:, 0, :, :],
                                                       sm[:, 5, :].unsqueeze(2).broadcast_to([P, CT, R]), ALU.mult))
                    chain.link(nc.vector.tensor_tensor(mm[:, 1, :, :], mm[:, 1, :, :],
                                                       ln_g[:, :].unsqueeze(1).broadcast_to([P, CT, R]), ALU.mult))
                    nc.vector.tensor_tensor(mm[:, 0, :, :], mm[:, 1, :, :],
                                            ln_b[:, :].unsqueeze(1).broadcast_to([P, CT, R]),
                                            ALU.add).then_inc(ln_ready, 1)
                    for k in range(2):
                        dve.wait_ge(up_ready, counted(n * 2 + (k + 1)))
                        xt = x_res[:, bass.ds(n * CT + 2 * k, 2), :]
                        u_ps = (g_ps[2], g_ps[0])[k]
                        nc.vector.tensor_tensor(xt, u_ps[:, 0:2 * C].rearrange("p (t c) -> p t c", t=2), xt,
                                                ALU.add).then_inc(x_added, 1)
                    chain.close()

                pipelined(dve, first, rest, CHUNKS)

            @block.tensor
            def _(pe):
                for s in (front_ps, drep_ready, urep_ready, hc_used, m_ready, mT_ps, up_ready):
                    pe.sem_inc(s, 1)
                pe.wait_ge(weights_in, len(loads) * 16)

                def first(n, u):
                    pe.wait_ge(xT_in, n * 16 + 16)
                    if isinstance(n, int) and n == 0:
                        pass
                    else:
                        pe.wait_ge(x_added, counted(n * 2 - 2))
                    for h in range(2):
                        ins = nc.tensor.matmul(g_ps[0][0:R, :], down[:, h, :], xT[:, u, h, :], start=h == 0, stop=h == 1)
                    ins.then_inc(front_ps, 1)
                    pe.wait_ge(act_front, counted(n * 7 + 1))
                    for k in range(2):
                        nc.tensor.matmul(g_ps[1 + k][0:DI, :], inp[:, k * DI:(k + 1) * DI], xsT[:, :], start=True,
                                         stop=True).then_inc(front_ps, 1)
                    pe.wait_ge(act_front, counted(n * 7 + 3))
                    pe.wait_ge(silu_ready, counted(n + 1))
                    nc.tensor.matmul(g_ps[0][0:DTR, :], xdt[:, :], u_sb[:, u, :], start=True,
                                     stop=True).then_inc(front_ps, 1)
                    for k in range(2):
                        nc.tensor.matmul(g_ps[1 + k][:, :], xb[:, k, :, :], u_sb[:, u, :], start=True,
                                         stop=True).then_inc(front_ps, 1)
                    pe.wait_ge(act_front, counted(n * 7 + 4))
                    nc.tensor.matmul(g_ps[0][0:DI, :], dtw[:, :], dt_sb[:, :], start=True,
                                     stop=True).then_inc(front_ps, 1)

                def rest(n, u, nxt):
                    pe.wait_ge(delta_ready, counted(n + 1))
                    pe.wait_ge(du_ready, counted(n + 1))
                    pe.wait_ge(y_gated, counted(n))

                    def add_states(g):
                        pe.wait_ge(hc_ready, counted(n * G + (g + 1)))
                        nc.tensor.matmul(y_ps[:, :], selT[:, g, :], hc[:, g % 2, :], start=g == 0,
                                         stop=g == G - 1).then_inc(hc_used, 1)

                    for g in range(G):
                        if g == G // 2 + 1:
                            nxt()
                        k = n * G + g
                        pe.wait_ge(dA_ready, counted(k - 1) if g else counted(k))
                        nc.tensor.matmul(drep_ps[g % 2][:, :], sel[:, g, :], delta[:, u, :], start=True,
                                         stop=True).then_inc(drep_ready, 1)
                        pe.wait_ge(dBu_ready, counted(k - 1) if g else counted(k))
                        nc.tensor.matmul(urep_ps[g % 2][:, :], sel[:, g, :], du[:, u, :], start=True,
                                         stop=True).then_inc(urep_ready, 1)
                        if g:
                            add_states(g - 1)
                    add_states(G - 1)
                    pe.wait_ge(act_front, counted(n * 7 + 14) if not (isinstance(n, int) and n == CHUNKS - 1)
                               else counted(CHUNKS * 7))
                    pe.wait_ge(y_gated, counted(n + 1))
                    for t in range(CT):
                        ins = nc.tensor.matmul(g_ps[0][:, t * R:(t + 1) * R], yy[:, 1, t * P:(t + 1) * P], outp[:, :],
                                               start=True, stop=True)
                    ins.then_inc(m_ready, 1)
                    pe.wait_ge(gelu_ready, counted(n + 1))
                    hold(pe, pe_held)
                    for t in range(CT):
                        ins = nc.tensor.transpose(g_ps[1][0:R, t * P:(t + 1) * P], mg[:, t, :], consts["ident"])
                    ins.then_inc(mT_ps, 1)
                    pe.wait_ge(mT_ready, counted(n + 1))
                    for k in range(2):
                        for t in range(2):
                            at = 2 * k + t
                            ins = nc.tensor.matmul((g_ps[2], g_ps[0])[k][:, t * C:(t + 1) * C],
                                                   mT[:, at * P:(at + 1) * P], up[:, :], start=True, stop=True)
                        ins.then_inc(up_ready, 1)

                pipelined(pe, first, rest, CHUNKS)
        m.clear()


HEADS, HS, SLOTS = 12, 16, 8
FEAT = 2 * HS + 2
EXT = 12
PAIRS = HEADS // 2
STEPS = 2 * PAIRS
BIG, HUGE = 1.0e38, 3.4e38


def wrapped(ap, shift, depth):
    dims = [list(x) for x in ap.ap]
    step = dims[-1][0]
    return bass.AP(tensor=ap.tensor, offset=ap.offset + shift * step, ap=dims[:-1] + [[step, depth], [step, 8]])


def dpp_attention_phase(nc, x_res, moments, consts, w):
    RD = 4
    GRAMS = (RD - 1) * SLOTS + SLOTS // 2
    NCOMB = (1 + RD) * SLOTS
    with ExitStack() as ctx:
        m = Mem(nc, ctx, "l2a")
        wqk = m.sb("wqk", [HC, 2, 8, HC])
        wtok = m.sb("wtok", [HC, 2, 3 * C])
        bqk = m.sb("bqk", [HC, 8])
        btok = m.sb("btok", [1, 3 * C])
        wp = m.sb("wp", [HC, 2, C])
        bp = m.sb("bp", [P, C])
        thr = m.sb("thr", [P, 2 * P])
        ident_bf = m.sb("ident_bf", [P, P], BF16)
        mask_bf = m.sb("mask_bf", [P, P], BF16)
        tri_bf = m.sb("tri_bf", [P, P], BF16)
        ones_bf = m.sb("ones_bf", [P, P], BF16)
        ones_row = m.sb("ones_row", [1, P])
        weight_of = m.sb("weight_of", [P, 2, NCOMB])
        rstd = m.sb("rstd", [P, TILES])
        shift = m.sb("shift", [P, TILES])
        xn = m.sb("xn", [P, 2, C])
        tT = m.sb("tT", [HC, 2, T])
        qkT = m.sb("qkT", [HC, 2, 8, T])
        q_tok = m.sb("q_tok", [P, 2, 2, 2, C])
        feat = m.sb("feat", [P, 2, 2, HEADS, FEAT])
        rest_buf = m.sb("rest_f", [P, 2 * HEADS * FEAT])
        rest_f = rest_buf[:, :].rearrange("p (t h f) -> p t h f", t=2, h=HEADS)
        feat3 = m.sb("feat3", [P, 2, 2, 3, HEADS, FEAT], BF16)
        square = rest_buf[:, 0:4 * HEADS * HS].rearrange("p (k t h d) -> p k t h d", k=2, t=2, h=HEADS)
        own = m.sb("own", [P, 2, 2, HEADS])
        top8 = m.sb("top8", [P, 2, 2, 8])
        marked = m.sb("marked", [P, 2, 2 * P])
        chosen = m.sb("chosen", [P, 2, 2, 2 * P], BF16)
        chosenT = m.sb("chosenT", [P, 2, 2, 2, P], BF16)
        code = m.sb("code", [P, 2, 2, 2, P], BF16)
        onehot = m.sb("onehot", [P, SLOTS, 2, 2, P], BF16)
        keys = m.sb("keys", [P, 2, HEADS, EXT, HS])
        values = m.sb("values", [P, 2, HEADS, SLOTS, HS])
        facts = m.sb("facts", [P, 2, HEADS, EXT, 2])
        prod = m.sb("prod", [P, 2, 2, GRAMS + 2 * SLOTS, HS])
        dots = m.sb("dots", [P, 2, HEADS, RD * SLOTS + 2 * EXT])
        sv = m.sb("sv", [P, 3, HEADS, EXT])
        det = m.sb("det", [P, HEADS, 1 + RD, SLOTS])
        sc = m.sb("sc", [P, HEADS, 1 + RD, SLOTS])
        veto = m.sb("veto", [P, HEADS, 1 + RD, SLOTS])
        mx = m.sb("mx", [P, HEADS, 1 + RD, SLOTS])
        ex = m.sb("ex", [P, 3, HEADS, 1 + RD, SLOTS])
        shared = m.sb("shared", [P, HEADS * SLOTS * HS])
        pw = shared[:, 0:3 * HEADS * RD * SLOTS].rearrange("p (k h d a) -> p k h d a", k=3, h=HEADS, d=RD)
        z = shared[:, 0:3 * HEADS * NCOMB].rearrange("p (k h d a) -> p k h d a", k=3, h=HEADS, d=1 + RD)
        pv = shared[:, :].rearrange("p (h a d) -> p h a d", h=HEADS, a=SLOTS)
        guess = shared[:, 0:4 * TILES].rearrange("p (k t) -> p k t", k=4)
        hd = m.sb("hd", [P, 6, HEADS])
        alpha = m.sb("alpha", [P, HEADS, SLOTS])
        spread = m.sb("spread", [P, HEADS, EXT])
        kept = m.sb("kept", [P, 2, C])
        y = m.sb("y", [P, 2, C])
        yT = m.sb("yT", [HC, 2, P])

        s_ps = [m.ps(f"s{k}", [P, 512]) for k in range(2)]
        mt_ps = m.ps("mt", [P, 2, 2, P])
        code_psum = m.ps("code_psum", [P, 2, 2, P])
        g_ps = [m.ps(f"g{k}", [P, 512]) for k in range(2)]
        a_ps = [m.ps(f"a{k}", [P, 512]) for k in range(2)]

        names = """weights_in half_log dve_chain0 rstd_ready const_ready xn_ready a_psum a_sb
            rest_ready mid_ready split_ready square_ready own_ready scores_ready marked_ready chosen_ready
            chosenT_psum chosenT_ready code_in_psum code_ready onehot_ready gathered kv_ready prod_ready products
            dots_ready det_ready log_ready shifted probs_ready diff_ready exp_ready denom_ready inv_ready
            alpha_ready pv_ready kept_ready y_ready yT_psum yT_ready proj_ready x_added act_chain max_chain
            det_chain diff_chain log_chain inv_chain alpha_chain y_chain dve_held act_held pe_held pool_held""".split()
        S = {name: m.sem(name) for name in names}
        loads = ((wqk[:, :, :, :], w["wqk"]), (wtok[:, :, :], w["wtok"]), (bqk[:, :], w["bqk"]),
                 (btok[:, :], w["btok"].unsqueeze(0)), (wp[:, :, :], w["wp"]),
                 (bp[:, :], w["bp"].partition_broadcast(P)), (y[:, 0, 0:P], w["mask"]), (thr[:, :], w["thr"]),
                 (y[:, 1, 0:P], w["tri"]), (weight_of[:, :, :], w["comb"].partition_broadcast(P)))
        LOADED = len(loads) * 16

        def first_head(i):
            return 6 * (i % PAIRS // 3) + i % 3

        def keys_of(t):
            return (t + 1) * P

        def steps(eng, body):
            def image(n, u, first=False, last=False):
                for i in range(STEPS):
                    def back(lag, i=i):
                        if i >= lag:
                            return n, u, i - lag
                        return None if first else (n - 1, 1 - u, i - lag + STEPS)
                    body(n, u, i, back, last)
            image(0, 0, first=True)
            with eng.Fori(0, B // 2 - 1) as it:
                image(it * 2 + 1, 1)
                image(it * 2 + 2, 0)
            image(B - 1, 1, last=True)
            for i in range(STEPS, 2 * STEPS + 1):
                def back(lag, i=i):
                    return (B - 1, 1, i - lag) if 0 <= i - lag < STEPS else None
                body(B, 0, i - STEPS, back, True)

        DET, DIFF, LOG, INV, ALPHA, VALUE, OUT = range(7)
        FRONT, SQUARE, OWN, SPLIT = 5, 9, 10, 11

        def stage(back, k):
            s = back(4 + k)
            return (s[0], s[1], s[2] // PAIRS) if s and s[2] % PAIRS == PAIRS - 1 else None

        def next_image(n, u, last):
            return None if last or (isinstance(n, int) and n == B) else (n + 1, 1 - u)

        H = HEADS
        det2, cross2 = sv[:, 0, :, :], sv[:, 1, :, :]
        flat = lambda x: x.rearrange("p h d a -> p (h d a)")
        per_head = lambda x, k: x.rearrange("p h d a -> p h (d a)")
        over = lambda x, k: x.unsqueeze(2).broadcast_to([P, H, k])
        A = lambda x: x[:, :, 0:SLOTS].unsqueeze(2).broadcast_to([P, H, RD, SLOTS])
        Bx = lambda x: wrapped(x, 1, RD)
        zf = lambda k: flat(z[:, k, :, :, :])
        ef = lambda k: flat(ex[:, k, :, :, :])
        scp = per_head(sc[:, :, :, :], 0)

        def count_of(step):
            n, u, i = step
            return n * STEPS + i

        with nc.Block() as block:
            @block.sync
            def _(sp):
                for dst, src in loads:
                    sp.dma_start(dst, src).then_inc(S["weights_in"], 16)

            @block.scalar
            def _(act):
                for name in ("xn_ready a_sb mid_ready chosenT_ready code_ready kv_ready log_ready "
                             "probs_ready exp_ready inv_ready yT_ready").split():
                    act.sem_inc(S[name], 1)
                rstd_steps_act(nc, act, None, S["half_log"], moments, guess, consts["eps"])
                act.wait_ge(S["weights_in"], LOADED)
                act.wait_ge(S["const_ready"], 1)
                act.wait_ge(S["rstd_ready"], 1)
                hold(act, S["act_held"])

                def front(n, u, k):
                    if k == 0:
                        normalise(nc, xn[:, :, :], x_res, rstd, shift, n * 2).then_inc(S["xn_ready"], 1)
                    if k == 1 and not (isinstance(n, int) and n == 0):
                        act.wait_ge(S["prod_ready"], counted(n * STEPS - STEPS))
                    if k == 5 and not (isinstance(n, int) and n == 0):
                        act.wait_ge(S["diff_ready"], counted(n * 2 - 2))
                        act.wait_ge(S["kept_ready"], counted(n * 2 - 2))
                        hold(act, S["act_held"])
                    act.wait_ge(S["a_psum"], counted(n * 8 + (k + 1)))
                    b = a_ps[k % 2]
                    if k == 0:
                        ins = nc.scalar.copy(tT[:, :, :], b[0:HC, :].rearrange("p (h t) -> p h t", h=2))
                    elif k <= 4:
                        for j in range(2):
                            c = 2 * (k - 1) + j
                            ins = nc.scalar.activation(qkT[:, u, c, :], b[0:HC, j * T:(j + 1) * T],
                                                       ACT.Identity, bias=bqk[:, c:c + 1])
                    elif k == 6:
                        for tt in range(2):
                            ins = nc.scalar.copy(feat[:, u, tt, :, HS:2 * HS],
                                                 b[:, tt * C:(tt + 1) * C].rearrange("p (h d) -> p h d", h=HEADS))
                    else:
                        t = (k - 5) // 2
                        nc.scalar.copy(q_tok[:, u, t, :, :], b[:, 0:2 * C].rearrange("p (k c) -> p k c", k=2))
                        ins = nc.scalar.copy(feat[:, u, t, :, 0:HS],
                                             b[:, C:2 * C].rearrange("p (h d) -> p h d", h=HEADS))
                    ins.then_inc(S["a_sb"], 1)

                def split_high(n, u):
                    act.wait_ge(S["own_ready"], counted(n + 1))
                    nc.scalar.copy(feat3[:, u, :, 0, :, :], feat[:, u, :, :, :]).then_inc(S["mid_ready"], 1)

                def split_middle(n, u):
                    act.wait_ge(S["rest_ready"], counted(n + 1))
                    nc.scalar.copy(feat3[:, u, :, 1, :, :], rest_f[:, :, :, :]).then_inc(S["mid_ready"], 1)

                def logs(n, u, t):
                    act.wait_ge(S["det_ready"], counted(n * 2 + t + 1))
                    nc.scalar.activation(sc[:, :, :, :], det[:, :, :, :], ACT.Ln,
                                         bias=consts["eps6"]).then_inc(S["log_ready"], 1)

                def terms(n, u, t):
                    act.wait_ge(S["diff_ready"], counted(n * 2 + t + 1))
                    nc.scalar.activation(ex[:, :, :, :, :], ex[:, :, :, :, :], ACT.Exp,
                                         scale=0.25).then_inc(S["exp_ready"], 1)

                def inverses(n, u, t):
                    r = n * 2 + t
                    act.wait_ge(S["denom_ready"], counted(r + 1))
                    nc.scalar.activation(z[:, 1, :, :, :], z[:, 0, :, :, :], ACT.Ln).then_inc(S["act_chain"], 1)
                    act.wait_ge(S["act_chain"], r + 1)
                    nc.scalar.activation(z[:, 1, :, :, :], z[:, 1, :, :, :], ACT.Exp,
                                         scale=-1.0).then_inc(S["inv_ready"], 1)
                    act.wait_ge(S["shifted"], counted(r + 1))
                    nc.scalar.activation(sc[:, :, :, :], sc[:, :, :, :], ACT.Exp).then_inc(S["probs_ready"], 1)

                def out(n, u, t):
                    act.wait_ge(S["yT_psum"], counted(n * 2 + (t + 1)))
                    nc.scalar.copy(yT[:, :, :], a_ps[0][0:HC, 0:2 * P].rearrange("p (h t) -> p h t", h=2)
                                   ).then_inc(S["yT_ready"], 1)

                def body(n, u, i, back, last):
                    s = back(1)
                    if s:
                        q, t = count_of(s), s[2] // PAIRS
                        act.wait_ge(S["chosenT_psum"], counted(q + 1))
                        act.wait_ge(S["code_in_psum"], counted(q - 1) if not (isinstance(q, int) and q < 2) else 1)
                        nc.scalar.copy(chosenT[:, s[2] % 2, 0:t + 1, :, :],
                                       mt_ps[:, 0:t + 1, :, :]).then_inc(S["chosenT_ready"], 1)
                    s = back(3)
                    if s:
                        q, t = count_of(s), s[2] // PAIRS
                        if s[2] % PAIRS == 0:
                            act.wait_ge(S["y_ready"], counted(s[0] * 2 + t - 1) if not (isinstance(s[0], int) and s[0] == 0)
                                        else 1)
                        for j in range(2):
                            act.wait_ge(S["gathered"], counted(q * 2 + (j + 1)))
                            src = g_ps[j][:, 0:SLOTS * FEAT].rearrange("p (a f) -> p a f", a=SLOTS)
                            h = first_head(s[2]) + 3 * j
                            nc.scalar.copy(keys[:, t, h, 0:SLOTS, :], src[:, :, 0:HS])
                            nc.scalar.copy(keys[:, t, h, SLOTS:EXT, :], src[:, 0:EXT - SLOTS, 0:HS])
                            nc.scalar.copy(values[:, t, h, :, :], src[:, :, HS:2 * HS])
                            nc.scalar.copy(facts[:, t, h, 0:SLOTS, :], src[:, :, 2 * HS:])
                            ins = nc.scalar.copy(facts[:, t, h, SLOTS:EXT, :], src[:, 0:EXT - SLOTS, 2 * HS:])
                        ins.then_inc(S["kv_ready"], 1)
                    s = back(1)
                    if s:
                        q, t = count_of(s), s[2] // PAIRS
                        act.wait_ge(S["code_in_psum"], counted(q + 1))
                        act.wait_ge(S["onehot_ready"], counted(q - 1) if not (isinstance(q, int) and q < 2) else 1)
                        nc.scalar.copy(code[:, s[2] % 2, 0:t + 1, :, :],
                                       code_psum[:, 0:t + 1, :, :]).then_inc(S["code_ready"], 1)
                    for k, do in ((DIFF, logs), (LOG, terms), (INV, inverses), (OUT, out)):
                        if stage(back, k):
                            do(*stage(back, k))
                    nxt = next_image(n, u, last)
                    if nxt and FRONT <= i < FRONT + 4:
                        front(*nxt, 2 * (i - FRONT))
                        front(*nxt, 2 * (i - FRONT) + 1)
                    if nxt and i == SPLIT:
                        split_high(*nxt)
                    if i == 0 and not (isinstance(n, int) and n == B):
                        split_middle(n, u)

                for k in range(8):
                    front(0, 0, k)
                split_high(0, 0)
                steps(act, body)

            @block.gpsimd
            def _(pool):
                for name in ("rest_ready split_ready square_ready prod_ready pv_ready kept_ready").split():
                    pool.sem_inc(S[name], 1)

                def squares(n, u):
                    pool.wait_ge(S["a_sb"], counted(n * 8 + 8))
                    key = feat[:, u, :, :, 0:HS]
                    nc.gpsimd.tensor_tensor(square[:, 0, :, :, :], key, key, ALU.mult)
                    for t in range(2):
                        ins = nc.gpsimd.tensor_tensor(square[:, 1, t, :, :], feat[:, u, t, :, 0:HS],
                                                      q_tok[:, u, t, 0, :].rearrange("p (h d) -> p h d", h=HEADS),
                                                      ALU.mult)
                    ins.then_inc(S["square_ready"], 1)

                def split_rest(n, u):
                    pool.wait_ge(S["mid_ready"], counted(n * 2 + 1))
                    nc.gpsimd.tensor_tensor(rest_f[:, :, :, :], feat[:, u, :, :, :], feat3[:, u, :, 0, :, :],
                                            ALU.subtract).then_inc(S["rest_ready"], 1)

                def split_low(n, u):
                    pool.wait_ge(S["mid_ready"], counted(n * 2 + 2))
                    nc.gpsimd.tensor_tensor(feat3[:, u, :, 2, :, :], rest_f[:, :, :, :], feat3[:, u, :, 1, :, :],
                                            ALU.subtract).then_inc(S["split_ready"], 1)

                def keep(n, u, t):
                    if not (isinstance(n, int) and n == 0):
                        pool.wait_ge(S["y_ready"], counted(n * 2 + t - 1))
                        hold(pool, S["pool_held"])
                    nc.gpsimd.tensor_copy(kept[:, t, :].rearrange("p (h d) -> p h d", h=HEADS),
                                          feat[:, u, t, :, HS:2 * HS]).then_inc(S["kept_ready"], 1)

                def weigh(n, u, t):
                    r = n * 2 + t
                    pool.wait_ge(S["alpha_ready"], counted(r + 1))
                    for h in range(0, HEADS, 4):
                        ins = nc.gpsimd.tensor_tensor(pv[:, h:h + 4, :, :], values[:, t, h:h + 4, :, :],
                                                      alpha[:, h:h + 4, :].unsqueeze(3).broadcast_to([P, 4, SLOTS, HS]),
                                                      ALU.mult)
                    ins.then_inc(S["pv_ready"], 1)

                def body(n, u, i, back, last):
                    if stage(back, VALUE):
                        weigh(*stage(back, VALUE))
                    s = back(3)
                    if s:
                        q, t = count_of(s), s[2] // PAIRS
                        pool.wait_ge(S["kv_ready"], counted(q + 1))
                        pool.wait_ge(S["dots_ready"], counted(q - 1) if not (isinstance(q, int) and q < 2) else 1)
                        made = prod[:, s[2] % 2, :, :, :]
                        near = (RD - 1) * SLOTS
                        for j in range(2):
                            h = first_head(s[2]) + 3 * j
                            key = keys[:, t, h, :, :]
                            lo = key[:, 0:SLOTS, :].unsqueeze(1).broadcast_to([P, RD - 1, SLOTS, HS])
                            dims = [list(x) for x in key.ap]
                            hi = bass.AP(tensor=key.tensor, offset=key.offset + HS,
                                         ap=[dims[0], [HS, RD - 1], [HS, SLOTS], [1, HS]])
                            nc.gpsimd.tensor_tensor(made[:, j, 0:near, :].rearrange("p (d a) f -> p d a f", d=RD - 1),
                                                    lo, hi, ALU.mult)
                            mine = q_tok[:, s[1], t, :, h * HS:(h + 1) * HS]
                            nc.gpsimd.tensor_tensor(
                                made[:, j, GRAMS:, :].rearrange("p (k a) f -> p k a f", k=2),
                                key[:, 0:SLOTS, :].unsqueeze(1).broadcast_to([P, 2, SLOTS, HS]),
                                mine.unsqueeze(2).broadcast_to([P, 2, SLOTS, HS]), ALU.mult)
                        h = first_head(s[2])
                        nc.gpsimd.tensor_tensor(made[:, :, near:GRAMS, :], keys[:, t, h:h + 4:3, 0:SLOTS // 2, :],
                                                keys[:, t, h:h + 4:3, SLOTS // 2:SLOTS, :], ALU.mult
                                                ).then_inc(S["products"], 1)
                        pool.wait_ge(S["products"], q + 1)
                        every = made.rearrange("p j k f -> p (j k) f")
                        ins = nc.gpsimd.tensor_tensor(every[:, :, 0:HS // 2], every[:, :, 0:HS // 2],
                                                      every[:, :, HS // 2:], ALU.add)
                        ins.then_inc(S["prod_ready"], 1)
                    if stage(back, DIFF):
                        keep(*stage(back, DIFF))
                    nxt = next_image(n, u, last)
                    if nxt and i == SQUARE:
                        squares(*nxt)
                    if nxt and i == SPLIT:
                        split_rest(*nxt)
                    if i == 0 and not (isinstance(n, int) and n == B):
                        split_low(n, u)

                squares(0, 0)
                split_rest(0, 0)
                steps(pool, body)

            @block.vector
            def _(dve):
                for name in ("own_ready chosen_ready marked_ready onehot_ready dots_ready det_ready shifted diff_ready "
                             "denom_ready alpha_ready y_ready x_added").split():
                    dve.sem_inc(S[name], 1)
                chain0 = Chain(dve, S["dve_chain0"])
                rstd_steps_dve(nc, dve, chain0, S["half_log"], moments, guess, rstd, shift).then_inc(S["rstd_ready"], 1)
                dve.wait_ge(S["weights_in"], LOADED)
                nc.vector.tensor_copy(ident_bf[:, :], consts["ident"])
                nc.vector.tensor_copy(mask_bf[:, :], y[:, 0, 0:P])
                nc.vector.tensor_copy(tri_bf[:, :], y[:, 1, 0:P])
                nc.vector.memset(ones_bf[:, :], 1.0)
                nc.vector.memset(ones_row[:, :], 1.0)
                nc.vector.memset(feat[:, :, :, :, 2 * HS:2 * HS + 1], 1.0)
                nc.vector.memset(sv[:, :, :, :], 0.0).then_inc(S["const_ready"], 1)
                dve.wait_ge(S["const_ready"], 1)

                def own_facts(n, u):
                    dve.wait_ge(S["square_ready"], counted(n + 1))
                    nc.vector.tensor_reduce(feat[:, u, :, :, 2 * HS + 1], square[:, 0, :, :, :], AX.X, ALU.add)
                    nc.vector.tensor_reduce(own[:, u, :, :], square[:, 1, :, :, :], AX.X, ALU.add
                                            ).then_inc(S["own_ready"], 1)

                def chained(name, count, r):
                    chain = Chain(dve, S[name], count, r)
                    return (chain, chain.link, chain.send,
                            lambda out, a, b, op: chain.link(nc.vector.tensor_tensor(out, a, b, op)))

                def det_stage(n, u, t):
                    r = n * 2 + t
                    chain, link, send, tt = chained("det_chain", 13, r)
                    gram = dots[:, t, :, 0:RD * SLOTS]
                    cross = dots[:, t, :, RD * SLOTS + EXT:]
                    norm = facts[:, t, :, :, 1]
                    mine = feat[:, u, t, :, 2 * HS + 1]
                    w0, w1, w2 = (pw[:, k, :, :, :] for k in range(3))
                    mult = lambda out, a, b: nc.vector.tensor_tensor(out, a, b, ALU.mult)
                    dve.wait_ge(S["dots_ready"], counted(n * STEPS + (t + 1) * PAIRS))
                    send(nc.vector.tensor_copy(gram[:, :, GRAMS:], gram[:, :, (RD - 1) * SLOTS:GRAMS]))
                    both = dots[:, t, :, RD * SLOTS:].rearrange("p h (k a) -> p h k a", k=2)
                    link(nc.vector.tensor_copy(both[:, :, :, SLOTS:], both[:, :, :, 0:EXT - SLOTS]))
                    send(mult(sv[:, 2, :, :], norm, over(mine, EXT)))
                    send(mult(cross2, cross, cross))
                    send(mult(w0, A(cross), Bx(cross)))
                    link(mult(per_head(w1, 0), gram, over(mine, RD * SLOTS)))
                    send(nc.vector.tensor_tensor(det2, sv[:, 2, :, :], cross2, ALU.subtract))
                    link(nc.vector.scalar_tensor_tensor(out=flat(w2), in0=flat(w0), scalar=2.0, in1=flat(w1),
                                                        op0=ALU.mult, op1=ALU.subtract))
                    send(nc.vector.tensor_copy(det[:, :, 0, :], det2[:, :, 0:SLOTS]))
                    send(mult(per_head(w0, 0), per_head(w2, 0), gram))
                    link(mult(w1, A(det2), Bx(norm)))
                    send(nc.vector.tensor_tensor(flat(w0), flat(w0), flat(w1), ALU.add))
                    link(mult(w2, A(norm), Bx(cross2)))
                    nc.vector.tensor_tensor(det[:, :, 1:, :], w0, w2, ALU.subtract).then_inc(S["det_ready"], 1)
                    chain.close()

                def diff_stage(n, u, t):
                    r = n * 2 + t
                    chain, link, send, tt = chained("diff_chain", 10, r)
                    sim = dots[:, t, :, RD * SLOTS:RD * SLOTS + EXT]
                    there = facts[:, t, :, :, 0]
                    self_sim = own[:, u, t, :]
                    both = pw[:, 1, :, :, :]
                    send(nc.vector.tensor_tensor(both, A(there), Bx(there), ALU.mult))
                    send(nc.vector.tensor_tensor(mx[:, :, 1:, :], A(sim), Bx(sim), ALU.max))
                    link(nc.vector.tensor_copy(mx[:, :, 0, :], sim[:, :, 0:SLOTS]))
                    send(nc.vector.tensor_scalar(veto[:, :, 1:, :], both, 1e30, -1e30, ALU.mult, ALU.add))
                    send(nc.vector.tensor_scalar(veto[:, :, 0, :], there[:, :, 0:SLOTS], 1e30, -1e30, ALU.mult, ALU.add))
                    tt(per_head(mx[:, :, :, :], 0), per_head(mx[:, :, :, :], 0), over(self_sim, NCOMB), ALU.max)
                    send(nc.vector.tensor_tensor(per_head(ex[:, 0, :, :, :], 0), over(self_sim, NCOMB),
                                                 per_head(mx[:, :, :, :], 0), ALU.subtract))
                    send(nc.vector.tensor_tensor(ex[:, 1, :, :, :],
                                                 sim[:, :, 0:SLOTS].unsqueeze(2).broadcast_to([P, H, 1 + RD, SLOTS]),
                                                 mx[:, :, :, :], ALU.subtract))
                    send(nc.vector.tensor_tensor(ex[:, 2, :, 1:, :], Bx(sim), mx[:, :, 1:, :], ALU.subtract))
                    link(nc.vector.memset(ex[:, 2, :, 0, :], -1e30))
                    dve.sem_inc(S["diff_ready"], 1)
                    chain.close()

                def log_stage(n, u, t):
                    r = n * 2 + t
                    chain, link, send, tt = chained("log_chain", 7, r)
                    cw = weight_of[:, 0, :].unsqueeze(1).broadcast_to([P, H, NCOMB])
                    cn = weight_of[:, 1, :].unsqueeze(1).broadcast_to([P, H, NCOMB])
                    dve.wait_ge(S["log_ready"], counted(r + 1))
                    send(nc.vector.tensor_tensor(scp, scp, cw, ALU.mult))
                    dve.wait_ge(S["exp_ready"], counted(r + 1))
                    tt(zf(0), ef(0), ef(1), ALU.add)
                    nc.vector.tensor_tensor(zf(0), zf(0), ef(2), ALU.add).then_inc(S["denom_ready"], 1)
                    tt(flat(sc[:, :, :, :]), flat(sc[:, :, :, :]), flat(veto[:, :, :, :]), ALU.add)
                    tt(scp, scp, cn, ALU.add)
                    link(nc.vector.tensor_reduce(hd[:, 0, :], scp, AX.X, ALU.max))
                    tt(scp, scp, over(hd[:, 0, :], NCOMB), ALU.subtract)
                    link(nc.vector.memset(spread[:, :, :], 0.0))
                    dve.sem_inc(S["shifted"], 1)
                    chain.close()

                def inv_stage(n, u, t):
                    r = n * 2 + t
                    chain, link, send, tt = chained("inv_chain", 8, r)
                    dve.wait_ge(S["inv_ready"], counted(r + 1))
                    dve.wait_ge(S["probs_ready"], counted(r + 1))
                    send(nc.vector.tensor_reduce(hd[:, 1, :], scp, AX.X, ALU.add))
                    tt(zf(2), zf(0), zf(1), ALU.mult)
                    send(nc.vector.reciprocal(hd[:, 2, :], hd[:, 1, :]))
                    link(nc.vector.scalar_tensor_tensor(out=zf(2), in0=zf(2), scalar=2.0, in1=zf(1),
                                                        op0=ALU.subtract, op1=ALU.mult))
                    tt(zf(2), zf(2), flat(sc[:, :, :, :]), ALU.mult)
                    for k in range(2):
                        send(nc.vector.tensor_tensor(ef(k), ef(k), zf(2), ALU.mult))
                    tt(ef(2), ef(2), zf(2), ALU.mult)
                    chain.close()

                def alpha_stage(n, u, t):
                    r = n * 2 + t
                    chain, link, send, tt = chained("alpha_chain", 12, r)
                    there = facts[:, t, :, :, 0]

                    def spread_out(dd):
                        tt(spread[:, :, dd:dd + SLOTS], spread[:, :, dd:dd + SLOTS], ex[:, 2, :, dd, :], ALU.add)

                    send(nc.vector.tensor_reduce(hd[:, 3, :], per_head(ex[:, 0, :, :, :], 0), AX.X, ALU.add))
                    send(nc.vector.tensor_reduce(alpha[:, :, :], ex[:, 1, :, :, :].rearrange("p h d a -> p h a d"),
                                                 AX.X, ALU.add))
                    spread_out(1)
                    send(nc.vector.scalar_tensor_tensor(out=hd[:, 4, :], in0=hd[:, 3, :], scalar=-1.0, in1=hd[:, 2, :],
                                                        op0=ALU.mult, op1=ALU.mult))
                    spread_out(2)
                    send(nc.vector.tensor_scalar(hd[:, 2, :], hd[:, 2, :], -1.0, None, ALU.mult))
                    spread_out(3)
                    send(nc.vector.scalar_tensor_tensor(out=hd[:, 5, :], in0=hd[:, 4, :], scalar=1.0,
                                                        in1=there[:, :, 0], op0=ALU.subtract, op1=ALU.mult))
                    spread_out(4)
                    send(nc.vector.tensor_scalar(hd[:, 5, :], hd[:, 5, :], 1.0, None, ALU.add))
                    tt(alpha[:, :, :], alpha[:, :, :], spread[:, :, 0:SLOTS], ALU.add)
                    tt(alpha[:, :, 0:EXT - SLOTS], alpha[:, :, 0:EXT - SLOTS], spread[:, :, SLOTS:], ALU.add)
                    nc.vector.tensor_tensor(alpha[:, :, :], alpha[:, :, :], over(hd[:, 2, :], SLOTS),
                                            ALU.mult).then_inc(S["alpha_ready"], 1)
                    chain.close()

                def y_stage(n, u, t):
                    r = n * 2 + t
                    chain, link, send, tt = chained("y_chain", 2, r)
                    y3 = y[:, t, :].rearrange("p (h d) -> p h d", h=H)
                    own_value = kept[:, t, :].rearrange("p (h d) -> p h d", h=H)
                    dve.wait_ge(S["kept_ready"], counted(r + 1))
                    send(nc.vector.tensor_tensor(own_value, own_value, over(hd[:, 5, :], HS), ALU.mult))
                    dve.wait_ge(S["pv_ready"], counted(r + 1))
                    link(nc.vector.tensor_reduce(y3, pv[:, :, :, :].rearrange("p h a d -> p h d a"), AX.X, ALU.add))
                    nc.vector.tensor_tensor(y3, y3, own_value, ALU.add).then_inc(S["y_ready"], 1)
                    chain.close()

                def out(n, u, t):
                    r = n * 2 + t
                    dve.wait_ge(S["proj_ready"], counted(r + 1))
                    xt = tile_of(x_res, n, t)
                    nc.vector.tensor_tensor(xt, a_ps[1][:, 0:C], xt, ALU.add).then_inc(S["x_added"], 1)
                    dve.wait_ge(S["x_added"], counted(r * 2 + 1))
                    nc.vector.tensor_tensor(xt, xt, bp[:, :], ALU.add).then_inc(S["x_added"], 1)

                def body(n, u, i, back, last):
                    if not (isinstance(n, int) and n == B):
                        q, t = count_of((n, u, i)), i // PAIRS
                        nk = keys_of(t)
                        dve.wait_ge(S["scores_ready"], counted(q + 1))
                        hold(dve, S["dve_held"])
                        for j in range(2):
                            ins = nc.vector.max(top8[:, i % 2, j, :], s_ps[i % 2][:, j * nk:(j + 1) * nk])
                            ins.then_inc(S["max_chain"], 1)
                        for j in range(2):
                            dve.wait_ge(S["max_chain"], q * 2 + (j + 1))
                            hold(dve, S["dve_held"])
                            ins = nc.vector.match_replace(marked[:, j, 0:nk], top8[:, i % 2, j, :],
                                                          s_ps[i % 2][:, j * nk:(j + 1) * nk], HUGE * 0.9)
                        ins.then_inc(S["marked_ready"], 1)
                        dve.wait_ge(S["marked_ready"], counted(q + 1))
                        dve.wait_ge(S["chosenT_psum"], counted(q - 1) if not (isinstance(q, int) and q < 2) else 1)
                        nc.vector.tensor_tensor(chosen[:, i % 2, :, 0:nk], marked[:, :, 0:nk],
                                                thr[:, 2 * P - nk:2 * P].unsqueeze(1).broadcast_to([P, 2, nk]),
                                                ALU.is_ge).then_inc(S["chosen_ready"], 1)
                    s = back(2)
                    if s:
                        q, t = count_of(s), s[2] // PAIRS
                        dve.wait_ge(S["code_ready"], counted(q + 1))
                        dve.wait_ge(S["gathered"], counted(q * 2))
                        for a in range(SLOTS):
                            ins = nc.vector.tensor_scalar(onehot[:, a, 0:t + 1, :, :],
                                                          code[:, s[2] % 2, 0:t + 1, :, :], float(64 + 1 + a), None,
                                                          ALU.is_equal)
                        ins.then_inc(S["onehot_ready"], 1)
                    s = back(4)
                    if s:
                        q, t = count_of(s), s[2] // PAIRS
                        dve.wait_ge(S["prod_ready"], counted(q + 1))
                        h = first_head(s[2])
                        at = 0
                        for place, size in ((0, GRAMS), (RD * SLOTS, SLOTS), (RD * SLOTS + EXT, SLOTS)):
                            ins = nc.vector.tensor_reduce(dots[:, t, h:h + 4:3, place:place + size],
                                                          prod[:, s[2] % 2, :, at:at + size, 0:HS // 2], AX.X, ALU.add)
                            at += size
                        ins.then_inc(S["dots_ready"], 1)
                    for k, do in ((DET, det_stage), (DIFF, diff_stage), (LOG, log_stage), (INV, inv_stage),
                                  (ALPHA, alpha_stage), (VALUE, y_stage), (OUT + 1, out)):
                        if stage(back, k):
                            do(*stage(back, k))
                    nxt = next_image(n, u, last)
                    if nxt and i == OWN:
                        own_facts(*nxt)

                own_facts(0, 0)
                steps(dve, body)

            @block.tensor
            def _(pe):
                for name in ("a_psum scores_ready chosenT_psum code_in_psum gathered yT_psum proj_ready").split():
                    pe.sem_inc(S[name], 1)
                pe.wait_ge(S["weights_in"], LOADED)
                pe.wait_ge(S["const_ready"], 1)

                def front(n, u, k):
                    o = a_ps[k % 2]
                    if k == 0:
                        pe.wait_ge(S["xn_ready"], counted(n + 1))
                    if k < 2 and not (isinstance(n, int) and n < 2):
                        pe.wait_ge(S["yT_ready"], counted(n * 2 - 3))
                        pe.wait_ge(S["x_added"], counted(n * 4 - 6))
                    pe.wait_ge(S["a_sb"], counted(n * 8 + (1 if k == 1 else max(k - 1, 0))))
                    if k == 0:
                        for h in range(2):
                            for t in range(2):
                                ins = nc.tensor.transpose(o[0:HC, (2 * h + t) * P:(2 * h + t + 1) * P],
                                                          xn[:, t, h * HC:(h + 1) * HC], consts["ident"])
                    elif k <= 4:
                        for j in range(2):
                            for h in range(2):
                                ins = nc.tensor.matmul(o[0:HC, j * T:(j + 1) * T], wqk[:, h, 2 * (k - 1) + j, :],
                                                       tT[:, h, :], start=h == 0, stop=h == 1)
                    else:
                        for at, t, c0, c1 in {5: [(0, 0, 0, 2 * C)],
                                              6: [(0, 0, 2 * C, 3 * C), (C, 1, 2 * C, 3 * C)],
                                              7: [(0, 1, 0, 2 * C)]}[k]:
                            part = o[:, at:at + c1 - c0]
                            for h in range(2):
                                nc.tensor.matmul(part, tT[:, h, t * P:(t + 1) * P], wtok[:, h, c0:c1], start=h == 0,
                                                 stop=False)
                            ins = nc.tensor.matmul(part, ones_row[:, :], btok[:, c0:c1], start=False, stop=True)
                    ins.then_inc(S["a_psum"], 1)

                def turn_output(n, u, t):
                    pe.wait_ge(S["y_ready"], counted(n * 2 + t + 1))
                    if isinstance(n, int) and n + 1 + t >= B:
                        pe.wait_ge(S["a_sb"], counted(B * 8))
                    else:
                        pe.wait_ge(S["a_sb"], counted(n * 8 + 16 + 8 * t))
                    hold(pe, S["pe_held"])
                    for h in range(2):
                        ins = nc.tensor.transpose(a_ps[0][0:HC, h * P:(h + 1) * P], y[:, t, h * HC:(h + 1) * HC],
                                                  consts["ident"])
                    ins.then_inc(S["yT_psum"], 1)

                def project(n, u, t):
                    r = n * 2 + t
                    pe.wait_ge(S["yT_ready"], counted(r + 1))
                    pe.wait_ge(S["x_added"], counted(r * 2))
                    for h in range(2):
                        ins = nc.tensor.matmul(a_ps[1][:, 0:C], yT[:, h, :], wp[:, h, :], start=h == 0, stop=h == 1)
                    ins.then_inc(S["proj_ready"], 1)

                def body(n, u, i, back, last):
                    if stage(back, OUT + 1):
                        project(*stage(back, OUT + 1))
                    if not (isinstance(n, int) and n == B):
                        q, t = count_of((n, u, i)), i // PAIRS
                        nk = keys_of(t)
                        if i == 0:
                            pe.wait_ge(S["a_sb"], counted(n * 8 + 5))
                        pe.wait_ge(S["marked_ready"], counted(q - 1) if not (isinstance(q, int) and q < 2) else 1)
                        for j in range(2):
                            h = first_head(i) + 3 * j
                            rows = slice(32 * (h % 3), 32 * (h % 3) + 32)
                            o = s_ps[i % 2][:, j * nk:(j + 1) * nk]
                            nc.tensor.matmul(o, qkT[rows, u, h // 3, t * P:(t + 1) * P], qkT[rows, u, 4 + h // 3, 0:nk],
                                             start=True, stop=False, skip_group_check=True)
                            ins = nc.tensor.matmul(o[:, nk - P:nk], ident_bf[:, :], mask_bf[:, :], start=False,
                                                   stop=True, skip_group_check=True)
                        ins.then_inc(S["scores_ready"], 1)
                    s = back(1)
                    if s:
                        q, t = count_of(s), s[2] // PAIRS
                        pe.wait_ge(S["chosen_ready"], counted(q + 1))
                        pe.wait_ge(S["chosenT_ready"], counted(q))
                        for kt in range(t + 1):
                            for j in range(2):
                                ins = nc.tensor.matmul(mt_ps[:, kt, j, :], chosen[:, s[2] % 2, j, kt * P:(kt + 1) * P],
                                                       ident_bf[:, :], start=True, stop=True)
                        ins.then_inc(S["chosenT_psum"], 1)
                    s = back(3)
                    if s:
                        q, t = count_of(s), s[2] // PAIRS
                        if s[2] == 0:
                            pe.wait_ge(S["split_ready"], counted(s[0] + 1))
                        pe.wait_ge(S["onehot_ready"], counted(q + 1))
                        pe.wait_ge(S["kv_ready"], counted(q))
                        for j in range(2):
                            h = first_head(s[2]) + 3 * j
                            for a in range(SLOTS):
                                for kt in range(t + 1):
                                    for part in range(3):
                                        ins = nc.tensor.matmul(g_ps[j][:, a * FEAT:(a + 1) * FEAT],
                                                               onehot[:, a, kt, j, :],
                                                               feat3[:, s[1], kt, part, h, :],
                                                               start=kt == 0 and part == 0, stop=kt == t and part == 2)
                            ins.then_inc(S["gathered"], 1)
                    s = back(1)
                    if s:
                        q, t = count_of(s), s[2] // PAIRS
                        pe.wait_ge(S["chosenT_ready"], counted(q + 1))
                        pe.wait_ge(S["code_ready"], counted(q))
                        for kt in range(t + 1):
                            o = code_psum[:, kt, :, :]
                            ins = nc.tensor.matmul(o, tri_bf[:, :], chosenT[:, s[2] % 2, kt, :, :], start=True,
                                                   stop=kt == 0)
                            if kt:
                                ins = nc.tensor.matmul(o, ones_bf[:, :], chosenT[:, s[2] % 2, 0, :, :], start=False,
                                                       stop=True)
                        ins.then_inc(S["code_in_psum"], 1)
                    if stage(back, OUT):
                        turn_output(*stage(back, OUT))
                    nxt = next_image(n, u, last)
                    if nxt and FRONT <= i < FRONT + 4:
                        front(*nxt, 2 * (i - FRONT))
                        front(*nxt, 2 * (i - FRONT) + 1)

                for k in range(8):
                    front(0, 0, k)
                steps(pe, body)
        m.clear()


def host_layouts(inputs):
    a = {k: np.asarray(v) for k, v in inputs.items()}
    lay = {}

    def halves(m):
        return np.ascontiguousarray(m.reshape(2, HC, -1).transpose(1, 0, 2))

    lay["x"] = np.ascontiguousarray(a["x"].reshape(TILES, P, C).transpose(1, 0, 2))
    lay["l3f_wr"] = halves(a["L3_ffn_Wg"])
    lay["l3f_w1"] = np.ascontiguousarray(a["L3_ffn_W1"].reshape(E, 2, HC, 768).transpose(2, 1, 0, 3))
    lay["l3f_w2"] = np.ascontiguousarray(a["L3_ffn_W2"].reshape(E, 6, P, C).transpose(2, 1, 0, 3))
    lay["l3f_b1"] = np.ascontiguousarray(a["L3_ffn_b1"].reshape(E, 6, P).transpose(2, 0, 1))
    lay["l0_xT"] = np.ascontiguousarray(a["x"].reshape(TOK, 2, HC).transpose(2, 1, 0))
    lay["l0_down"] = halves(a["L0_conv_down_w"].T)
    lay["l0_inp"] = np.ascontiguousarray(a["L0_conv_in_proj_w"].T)
    lay["l0_convw"] = a["L0_conv_conv_w"]
    lay["l0_cols"] = np.ascontiguousarray(np.stack([a["L0_conv_conv_b"], a["L0_conv_dt_proj_b"],
                                                    a["L0_conv_D_ssm"]], axis=1))
    xp = a["L0_conv_x_proj_w"]
    lay["l0_xdt"] = np.ascontiguousarray(xp[0:12].T)
    lay["l0_xb"] = np.ascontiguousarray(np.broadcast_to(xp[12:44].T.reshape(96, 2, 1, 16), (96, 2, 8, 16)))
    lay["l0_dtw"] = np.ascontiguousarray(a["L0_conv_dt_proj_w"].T)
    lay["l0_alog"] = np.ascontiguousarray(a["L0_conv_A_log"].reshape(12, P).T)
    sel = np.zeros((96, 12, P), np.float32)
    for row in range(96):
        sel[row, row // 8, (row % 8) * 16:(row % 8 + 1) * 16] = 1.0
    lay["l0_sel"] = sel
    lay["l0_selT"] = np.ascontiguousarray(sel.transpose(2, 1, 0))
    lay["l0_outp"] = np.ascontiguousarray(a["L0_conv_out_proj_w"].T)
    lay["l0_up"] = np.ascontiguousarray(a["L0_conv_up_w"].T)
    lay["l0_lng"] = a["L0_conv_ln_g"]
    lay["l0_lnb"] = a["L0_conv_ln_b"]
    keep = np.ones(16, np.float32)
    keep[0] = keep[8] = 0.0
    lay["l0_keep"] = keep
    wa, ba = a["L2_attn_W_attn"], a["L2_attn_b_attn"]
    wqk, bqk = np.zeros((HC, 2, 8, 3, 32), np.float32), np.zeros((HC, 8), np.float32)
    for part in range(2):
        wpart = wa[part * C:(part + 1) * C].reshape(4, 3, 16, 2, HC)
        wqk[:, :, 4 * part:4 * part + 4, :, 0:16] = wpart.transpose(4, 3, 0, 1, 2)
        bqk.reshape(3, 32, 8)[:, 0:16, 4 * part:4 * part + 4] = \
            ba[part * C:(part + 1) * C].reshape(4, 3, 16).transpose(1, 2, 0)
    lay["l2a_wqk"] = wqk.reshape(HC, 2, 8, HC)
    lay["l2a_bqk"] = bqk
    lay["l2a_wtok"] = halves(wa.T)
    lay["l2a_btok"] = ba
    lay["l2a_wp"] = halves(a["L2_attn_W_proj"].T)
    lay["l2a_bp"] = a["L2_attn_b_proj"]
    row, col = np.arange(P)[:, None], np.arange(P)[None, :]
    lay["l2a_mask"] = np.where(col > row, -1e30, 0.0).astype(np.float32)
    lay["l2a_thr"] = np.concatenate([np.full((P, P), BIG), np.where(col < row, BIG, HUGE)], axis=1).astype(np.float32)
    lay["l2a_tri"] = (np.where(row <= col, 1.0, 0.0) + 64.0 * (row == col)).astype(np.float32)
    comb = np.zeros((2, 5, SLOTS), np.float32)
    comb[0, 0], comb[0, 1:] = 1.0 / 2.0, 1.0 / 3.0
    comb[1, 4, 4:] = -1e30
    lay["l2a_comb"] = comb.reshape(2, 5 * SLOTS)
    ky, kx = np.meshgrid(np.arange(HH), np.arange(WW // 2 + 1), indexing="ij")
    yy, xx = np.meshgrid(np.arange(HH), np.arange(WW), indexing="ij")
    turn = 2 * np.pi * (np.outer(yy.ravel(), ky.ravel()) + np.outer(xx.ravel(), kx.ravel())) / HH
    dft = np.concatenate([np.cos(turn), -np.sin(turn)], axis=1) / HH
    lay["l1_dft"] = np.ascontiguousarray(dft.reshape(2, P, 288).transpose(1, 0, 2)).astype(np.float32)
    twice = np.where((kx.ravel() == 0) | (kx.ravel() == WW // 2), 1.0, 2.0)[:, None]
    idft = np.stack([np.cos(turn).T * twice, -np.sin(turn).T * twice], axis=0) / HH
    lay["l1_idft"] = np.ascontiguousarray(idft.reshape(2, 2, 72, T).transpose(2, 1, 0, 3)).astype(np.float32)
    for name in ("w1", "w2"):
        full = np.zeros((HC, 2, 2, HC), np.float32)
        for blk in range(8):
            at = slice((blk % 4) * 24, (blk % 4 + 1) * 24)
            full[at, :, blk // 4, at] = a["L1_conv_" + name][:, blk].transpose(1, 0, 2)
        lay["l1_" + name] = full
    lay["l1_w2"] = np.ascontiguousarray(lay["l1_w2"].transpose(0, 2, 1, 3))
    lay["l1_b1"] = np.ascontiguousarray(a["L1_conv_b1"].reshape(2, 2, HC).transpose(2, 1, 0))
    lay["l1_b2"] = np.ascontiguousarray(a["L1_conv_b2"].reshape(2, 2, HC).transpose(1, 0, 2))
    for name in ("q", "k", "v", "o"):
        lay["l3a_w" + name] = halves(a["L3_attn_W" + name])
    lay["l3a_memT"] = halves(a["L3_attn_memory"].T)
    lay["l3a_bq"] = np.ascontiguousarray(a["L3_attn_bq"].reshape(2, HC).T)
    lay["l3a_bk"] = np.ascontiguousarray(a["L3_attn_bk"].reshape(2, HC).T)
    lay["l3a_bv"] = a["L3_attn_bv"]
    lay["l3a_bo"] = a["L3_attn_bo"]
    lay["l2f_wr"] = halves(a["L2_ffn_Wr"])
    lay["l2f_br"] = a["L2_ffn_br"]
    lay["l2f_wgu"] = np.ascontiguousarray(a["L2_ffn_Wgu"].reshape(E, 2, HC, 2 * C).transpose(2, 1, 0, 3))
    lay["l2f_wd"] = np.ascontiguousarray(a["L2_ffn_Wd"].reshape(E, 2, HC, C).transpose(2, 1, 0, 3))
    lay["l2f_bgu"] = np.ascontiguousarray(a["L2_ffn_bgu"].reshape(E, 4, HC).transpose(2, 0, 1))
    lay["l2f_bd"] = a["L2_ffn_bd"]
    lay["l3f_b2"] = a["L3_ffn_b2"]
    row_of = np.tile(np.arange(P)[:, None], (1, P))
    lay["moe_tri"] = (row_of < row_of.T).astype(np.float32)
    lay["moe_rev"] = np.arange(E, 0, -1).astype(np.float32)
    lay["moe_floor"] = (np.arange(TOK // ETOK) * ETOK).astype(np.float32)
    lay["moe_index"] = np.arange(ETILES).astype(np.float32)
    lay["ident"] = np.eye(P, dtype=np.float32)
    return lay


def moments_phase(nc, x_res, moments, tag):
    with ExitStack() as ctx:
        m = Mem(nc, ctx, tag + "_mom")
        stats = m.sb("stats", [P, TILES, 6])
        stats_ready = m.sem("stats_ready")
        with nc.Block() as block:
            @block.vector
            def _(dve):
                for t in range(TILES):
                    nc.vector.bn_stats(stats[:, t, :], x_res[:, t, :]).then_inc(stats_ready, 1)
                for t in range(TILES):
                    dve.wait_ge(stats_ready, t + 1)
                    nc.vector.bn_aggr(moments[:, t, :], stats[:, t, :])
        m.clear()


def build(nc, d, out, phases=("l0", "l1", "l2a", "l2f", "l3a", "l3f")):
    with ExitStack() as ctx:
        m = Mem(nc, ctx, "main")
        x_res = m.sb("x_res", [P, TILES, C])
        moments = m.sb("moments", [P, TILES, 2])
        ident = m.sb("ident", [P, P])
        ones8 = m.sb("ones8", [P, E])
        eps = m.sb("eps", [P, 1])
        eps6 = m.sb("eps6", [P, 1])
        x_in = m.sem("x_in")
        const_in = m.sem("const_in")
        x_out = m.sem("x_out")
        zeros = m.sb("zeros", [P, C])
        rows_in = nc.dram_tensor("rows_in", (ETILES * ETOK, C), F32).ap()
        rows_out = nc.dram_tensor("rows_out", (ETILES * ETOK, C), F32).ap()
        zeroed = m.sem("zeroed")
        zeros_ready = m.sem("zeros_ready")
        consts = {"ident": ident[:, :], "ones8": ones8[:, :], "eps": eps[:, :], "eps6": eps6[:, :],
                  "moe": [d[f"moe_{name}"] for name in ("tri", "rev", "floor", "index")],
                  "rows_in": rows_in, "rows_out": rows_out, "zeroed": zeroed}
        with nc.Block() as block:
            @block.sync
            def _(sp):
                sp.dma_start(ident[:, :], d["ident"]).then_inc(const_in, 16)
                sp.dma_start(x_res[:, :, :], d["x"]).then_inc(x_in, 16)
                sp.wait_ge(zeros_ready, 1)
                sp.dma_start(rows_in.rearrange("(k p) c -> p k c", p=P),
                             zeros[:, :].unsqueeze(1).broadcast_to([P, ETILES * ETOK // P, C])).then_inc(zeroed, 16)
                sp.wait_ge(const_in, 16)
                sp.wait_ge(x_in, 16)

            @block.vector
            def _(dve):
                nc.vector.memset(zeros[:, :], 0.0).then_inc(zeros_ready, 1)
                nc.vector.memset(ones8[:, :], 1.0)
                nc.vector.memset(eps[:, :], EPS)
                nc.vector.memset(eps6[:, :], 1e-6)
        w = {}
        for k, v in d.items():
            if "_" in k:
                tag, name = k.split("_", 1)
                w.setdefault(tag, {})[name] = v
        PH = {"l2a": lambda: dpp_attention_phase(nc, x_res, moments, consts, w["l2a"]),
              "l1": lambda: fourier_phase(nc, x_res, moments, consts, w["l1"]),
              "l0": lambda: mamba_phase(nc, x_res, moments, consts, w["l0"]),
              "l3a": lambda: memory_attention_phase(nc, x_res, moments, consts, w["l3a"]),
              "l2f": lambda: moe_glu_phase(nc, x_res, moments, consts, w["l2f"]),
              "l3f": lambda: moe_relu_phase(nc, x_res, moments, consts, w["l3f"])}
        for ph in phases:
            if ph not in ("l0", "l1"):
                moments_phase(nc, x_res, moments, ph)
            PH[ph]()
        with nc.Block() as block:
            @block.sync
            def _(sp):
                sp.dma_start(out, x_res[:, :, :]).then_inc(x_out, 16)
                sp.wait_ge(x_out, 16)


def kernel(**inputs):
    import concourse.bacc as _bacc
    from concourse.bass_utils import run_bass_kernel_spmd as _run

    nc = _bacc.Bacc("TRN2", target_bir_lowering=False, num_devices=1)
    arrays, d = {}, {}
    for name, a in host_layouts(inputs).items():
        arrays[f"in_{name}"] = a
        d[name] = nc.dram_tensor(f"in_{name}", a.shape, mybir.dt.from_np(a.dtype), kind="ExternalInput").ap()
    out = nc.dram_tensor("out_x", (P, TILES, C), F32, kind="ExternalOutput").ap()
    build(nc, d, out)
    r = _run(nc, [arrays], core_ids=[0])
    got = r.results[0]["out_x"]
    return np.ascontiguousarray(got.transpose(1, 0, 2)).reshape(B, HH, WW, C)
```

```python
import numpy as np
import concourse.bass as bass
from concourse import mybir
from contextlib import ExitStack

F32 = mybir.dt.float32
BF16 = mybir.dt.bfloat16
F32R = mybir.dt.float32r
U32 = mybir.dt.uint32
I32 = mybir.dt.int32
ALU = mybir.AluOpType
ACT = mybir.ActivationFunctionType
AX = mybir.AxisListType

P = 128
B, HH, WW, C = 32, 16, 16, 192
T = HH * WW
TOK = B * T
TILES = TOK // P
HC = C // 2
EPS = 1e-5
E = 8
ETOK = 2 * P
ETILES = 2 * TOK // ETOK + E


def counted(n):
    return n + 1


class Chain:

    def __init__(self, eng, sem, per=0, it=None):
        self.eng, self.sem, self.n, self.base = eng, sem, 0, (it * per if it is not None else 0)
        self.per = per

    def link(self, ins):
        self.n += 1
        ins.then_inc(self.sem, 1)
        self.eng.wait_ge(self.sem, self.base + self.n)

    def send(self, ins):
        self.n += 1
        ins.then_inc(self.sem, 1)

    def close(self):
        assert not self.per or self.n == self.per, (self.n, self.per)


class Mem:

    def __init__(self, nc, ctx, tag):
        self.nc, self.ctx, self.tag, self.sems = nc, ctx, tag, []

    def sb(self, name, shape, dt=F32):
        return self.ctx.enter_context(self.nc.sbuf_tensor(f"{self.tag}_{name}", shape, dt))

    def ps(self, name, shape, dt=F32):
        return self.ctx.enter_context(self.nc.psum_tensor(f"{self.tag}_{name}", shape, dt))

    def sem(self, name):
        self.sems.append(self.ctx.enter_context(self.nc.semaphore(f"{self.tag}_{name}")))
        return self.sems[-1]

    def clear(self):
        with self.nc.Block() as block:
            @block.gpsimd
            def _(pool):
                for s in self.sems:
                    pool.sem_clear(s)


def moment_steps(nc, dve, stats, stats_ready, moments_ready, x_res, moments):
    for t in range(TILES):
        nc.vector.bn_stats(stats[:, t, :], x_res[:, t, :]).then_inc(stats_ready, 1)
    for t in range(TILES):
        dve.wait_ge(stats_ready, t + 1)
        nc.vector.bn_aggr(moments[:, t, :], stats[:, t, :]).then_inc(moments_ready, 1)


def rstd_steps_act(nc, act, moments_ready, half_log, moments, y0, eps_col):
    act.wait_ge(moments_ready, TILES)
    nc.scalar.activation(y0[:, 0, :], moments[:, :, 1], ACT.Ln, bias=eps_col).then_inc(half_log, 1)
    act.wait_ge(half_log, 1)
    nc.scalar.activation(y0[:, 1, :], y0[:, 0, :], ACT.Exp, scale=-0.5).then_inc(half_log, 1)


def rstd_steps_dve(nc, dve, chain, half_log, moments, y0, rstd, shift):
    dve.wait_ge(half_log, 2)
    chain.link(nc.vector.tensor_tensor(y0[:, 2, :], y0[:, 1, :], y0[:, 1, :], ALU.mult))
    chain.link(nc.vector.scalar_tensor_tensor(out=y0[:, 3, :], in0=moments[:, :, 1], scalar=EPS,
                                              in1=y0[:, 2, :], op0=ALU.add, op1=ALU.mult))
    chain.link(nc.vector.tensor_scalar(y0[:, 2, :], y0[:, 3, :], -0.5, 1.5, ALU.mult, ALU.add))
    chain.link(nc.vector.tensor_tensor(rstd[:, :], y0[:, 2, :], y0[:, 1, :], ALU.mult))
    return nc.vector.scalar_tensor_tensor(out=shift[:, :], in0=moments[:, :, 0], scalar=-1.0, in1=rstd[:, :],
                                          op0=ALU.mult, op1=ALU.mult)


def normalise(nc, xn, x_res, rstd, shift, tile):
    for t in range(2):
        at = bass.ds(tile + t, 1)
        ins = nc.scalar.activation(xn[:, t, :], x_res[:, at, :].rearrange("p a c -> p (a c)"), ACT.Identity,
                                   bias=shift[:, at], scale=rstd[:, at])
    return ins


def hold(eng, held):
    eng.sem_inc(held, 1)


def pipelined(eng, first, rest, count=B):
    first(0, 0)
    with eng.Fori(0, count // 2 - 1) as it:
        rest(it * 2, 0, lambda: first(it * 2 + 1, 1))
        rest(it * 2 + 1, 1, lambda: first(it * 2 + 2, 0))
    rest(count - 2, 0, lambda: first(count - 1, 1))
    rest(count - 1, 1, lambda: None)


def pipelined_late(eng, first, rest, late, firsts=((),), lates=((),), count=B):
    for part in firsts:
        first(0, 0, *part)
    rest(0, 0, lambda *part: first(1, 1, *part), lambda *part: None)
    with eng.Fori(0, count // 2 - 1) as it:
        rest(it * 2 + 1, 1, lambda *part: first(it * 2 + 2, 0, *part), lambda *part: late(it * 2, 0, *part))
        rest(it * 2 + 2, 0, lambda *part: first(it * 2 + 3, 1, *part), lambda *part: late(it * 2 + 1, 1, *part))
    rest(count - 1, 1, lambda *part: None, lambda *part: late(count - 2, 0, *part))
    for part in lates:
        late(count - 1, 1, *part)


def tile_of(x_res, n, t):
    return x_res[:, bass.ds(n * 2 + t, 1), :].rearrange("p a c -> p (a c)")


def rounds(eng, tile):
    tile(0, 0)
    tile(0, 1)
    with eng.Fori(1, ETILES // 2) as r:
        for u in range(2):
            tile(r, u)


def ring_rounds(eng, ring, tile):
    for k in range(ring):
        tile(0, k)
    with eng.Fori(1, TILES // ring) as r:
        for k in range(ring):
            tile(r, k)


def first_round(r):
    return isinstance(r, int) and r == 0


def route(nc, x_res, moments, consts, w, norm, plan, tag, from_probabilities):
    with ExitStack() as ctx:
        m = Mem(nc, ctx, tag + "_route")
        wr = m.sb("wr", [HC, 2, E])
        br = m.sb("br", [P, E])
        y0 = m.sb("guess", [P, 4, TILES])
        stats = m.sb("stats", [P, TILES, 6])
        xn = m.sb("xn", [P, 2, 2, C])
        tT = m.sb("tT", [HC, 2, 2, T])
        val = m.sb("val", [P, TILES, E])
        soft = m.sb("soft", [P, TILES, E])
        key = m.sb("key", [P, TILES, E])
        one_hot = m.sb("one_hot", [P, 2, TILES, E])
        sel = m.sb("sel", [P, TILES, E])
        col = m.sb("col", [P, 4, TILES])
        tot = m.sb("tot", [P, E, TILES])
        incl = m.sb("incl", [P, E, TILES])
        over = m.sb("over", [P, E, TOK // ETOK])
        counts = m.sb("counts", [P, 4, E])
        after = m.sb("after", [P, ETILES, E])
        row_f = m.sb("row_f", [P, 2, TILES])
        owner = m.sb("owner", [P, ETILES])
        ones = m.sb("ones", [P, P])[:, :]
        tri = m.sb("tri", [P, P])[:, :]
        rev = m.sb("rev", [P, E])[:, :]
        floor = m.sb("floor", [P, TOK // ETOK])[:, :]
        index = m.sb("index", [P, ETILES])[:, :]
        tp = [m.ps(f"tp{k}", [P, 512]) for k in range(2)]
        lg = m.ps("lg", [P, TILES, E])
        before = m.ps("before", [P, TILES, E])
        total = m.ps("total", [P, TILES, E])

        router_in = m.sem("router_in")
        tables_in = m.sem("tables_in")
        ones_ready = m.sem("ones_ready")
        stats_ready = m.sem("stats_ready")
        moments_ready = m.sem("moments_ready")
        half_log = m.sem("half_log")
        steps = m.sem("steps")
        norm_ready = m.sem("norm_ready")
        xn_ready = m.sem("xn_ready")
        tp_ready = m.sem("tp_ready")
        tT_ready = m.sem("tT_ready")
        logits_ready = m.sem("logits_ready")
        soft_in = m.sem("soft_in")
        soft_ready = m.sem("soft_ready")
        sel_ready = m.sem("sel_ready")
        counted_ready = m.sem("counted_ready")
        act_held = m.sem("act_held")

        with nc.Block() as block:
            @block.sync
            def _(sp):
                sp.dma_start(wr[:, :, :], w["wr"]).then_inc(router_in, 16)
                if not from_probabilities:
                    sp.dma_start(br[:, :], w["br"].partition_broadcast(P)).then_inc(router_in, 16)
                sp.dma_start(tri, consts["moe"][0]).then_inc(tables_in, 16)
                for place, source in zip((rev, floor, index), consts["moe"][1:]):
                    sp.dma_start(place, source.partition_broadcast(P)).then_inc(tables_in, 16)
                sp.wait_ge(consts["zeroed"], 16)
                for place, source in norm["weights"]:
                    sp.dma_start(place, source).then_inc(norm["weights_in"], 16)

            @block.scalar
            def _(act):
                act.sem_inc(xn_ready, 1)
                rstd_steps_act(nc, act, moments_ready, half_log, moments, y0, consts["eps"])
                act.wait_ge(norm_ready, 1)
                hold(act, act_held)

                def image(n, u):
                    act.wait_ge(tp_ready, counted(n))
                    normalise(nc, xn[:, u, :, :], x_res, norm["rstd"], norm["shift"], n * 2).then_inc(xn_ready, 1)

                with act.Fori(0, B // 2) as it:
                    image(it * 2, 0)
                    image(it * 2 + 1, 1)
                act.wait_ge(soft_in, 1)
                nc.scalar.activation(soft[:, :, :] if from_probabilities else col[:, 2, :],
                                     soft[:, :, :] if from_probabilities else col[:, 2, :],
                                     ACT.Exp if from_probabilities else ACT.Sigmoid).then_inc(soft_ready, 1)

            @block.tensor
            def _(pe):
                pe.sem_inc(tp_ready, 2)
                pe.sem_inc(logits_ready, 1)
                pe.wait_ge(router_in, 16 if from_probabilities else 32)

                def first(n, u):
                    pe.wait_ge(xn_ready, counted(n + 1))
                    pe.wait_ge(tT_ready, counted(n))
                    for h in range(2):
                        for t in range(2):
                            ins = nc.tensor.transpose(tp[u][0:HC, (2 * h + t) * P:(2 * h + t + 1) * P],
                                                      xn[:, u, t, h * HC:(h + 1) * HC], consts["ident"])
                    ins.then_inc(tp_ready, 1)

                def rest(n, u, nxt):
                    nxt()
                    pe.wait_ge(tT_ready, counted(n + 2))
                    for t in range(2):
                        for h in range(2):
                            ins = nc.tensor.matmul(lg[:, bass.ds(n * 2 + t, 1), :].rearrange("p a e -> p (a e)"),
                                                   tT[:, u, h, t * P:(t + 1) * P], wr[:, h, :],
                                                   start=h == 0, stop=h == 1)
                    ins.then_inc(logits_ready, 1)

                pipelined(pe, first, rest)
                pe.wait_ge(sel_ready, 1)
                pe.wait_ge(tables_in, 64)
                pe.wait_ge(ones_ready, 1)
                chosen = sel[:, :, :].rearrange("p t e -> p (t e)")
                nc.tensor.matmul(before[:, :, :].rearrange("p t e -> p (t e)"), tri, chosen, start=True, stop=True)
                nc.tensor.matmul(total[:, :, :].rearrange("p t e -> p (t e)"), ones, chosen,
                                 start=True, stop=True).then_inc(counted_ready, 1)

            @block.vector
            def _(dve):
                chain = Chain(dve, steps)
                link = chain.link
                dve.sem_inc(tT_ready, 2)
                nc.vector.memset(ones, 1.0).then_inc(ones_ready, 1)
                dve.wait_ge(ones_ready, 1)
                dve.wait_ge(tables_in, 64)
                moment_steps(nc, dve, stats, stats_ready, moments_ready, x_res, moments)
                rstd_steps_dve(nc, dve, chain, half_log, moments, y0, norm["rstd"],
                               norm["shift"]).then_inc(norm_ready, 1)

                def image(n, u):
                    dve.wait_ge(tp_ready, counted(n + 2))
                    dve.wait_ge(logits_ready, counted(n - 1) if not (isinstance(n, int) and n < 2) else 1)
                    nc.vector.tensor_copy(tT[:, u, :, :].rearrange("p h t -> p (h t)"),
                                          tp[u][0:HC, :]).then_inc(tT_ready, 1)

                image(0, 0)
                image(1, 1)
                with dve.Fori(0, B // 2 - 1) as it:
                    image(it * 2 + 2, 0)
                    image(it * 2 + 3, 1)
                dve.wait_ge(logits_ready, counted(B))

                def over_experts(c):
                    return c.unsqueeze(2).broadcast_to([P, TILES, E])

                def of_expert(r):
                    return r.unsqueeze(1).broadcast_to([P, TILES, E])

                if from_probabilities:
                    link(nc.vector.tensor_reduce(col[:, 0, :], lg[:, :, :], AX.X, ALU.max))
                    nc.vector.tensor_tensor(soft[:, :, :], lg[:, :, :], over_experts(col[:, 0, :]),
                                            ALU.subtract).then_inc(soft_in, 1)
                    dve.wait_ge(soft_ready, 1)
                    link(nc.vector.tensor_reduce(col[:, 1, :], soft[:, :, :], AX.X, ALU.add))
                    link(nc.vector.reciprocal(col[:, 2, :], col[:, 1, :]))
                    link(nc.vector.tensor_tensor(val[:, :, :], soft[:, :, :], over_experts(col[:, 2, :]), ALU.mult))
                    best = [plan["gates"][:, k, :] for k in range(2)]
                else:
                    dve.wait_ge(router_in, 32)
                    link(nc.vector.tensor_tensor(val[:, :, :], lg[:, :, :], of_expert(br[:, :]), ALU.add))
                    best = [col[:, k, :] for k in range(2)]
                for k in range(2):
                    hot = one_hot[:, k, :, :]
                    link(nc.vector.tensor_reduce(best[k], val[:, :, :], AX.X, ALU.max))
                    link(nc.vector.tensor_tensor(key[:, :, :], val[:, :, :], over_experts(best[k]), ALU.is_equal))
                    link(nc.vector.tensor_tensor(key[:, :, :], key[:, :, :], of_expert(rev), ALU.mult))
                    link(nc.vector.tensor_reduce(col[:, 3, :], key[:, :, :], AX.X, ALU.max))
                    link(nc.vector.tensor_tensor(hot, key[:, :, :], over_experts(col[:, 3, :]), ALU.is_equal))
                    if k == 0:
                        link(nc.vector.scalar_tensor_tensor(
                            out=val[:, :, :].rearrange("p t e -> p (t e)"), in0=hot.rearrange("p t e -> p (t e)"),
                            scalar=-1e30, in1=val[:, :, :].rearrange("p t e -> p (t e)"), op0=ALU.mult, op1=ALU.add))
                nc.vector.tensor_tensor(sel[:, :, :], one_hot[:, 0, :, :], one_hot[:, 1, :, :],
                                        ALU.add).then_inc(sel_ready, 1)
                if not from_probabilities:
                    nc.vector.tensor_tensor(col[:, 2, :], best[0], best[1], ALU.subtract).then_inc(soft_in, 1)
                    dve.wait_ge(soft_ready, 1)
                    link(nc.vector.tensor_copy(plan["gates"][:, 0, :], col[:, 2, :]))
                    link(nc.vector.tensor_scalar(plan["gates"][:, 1, :], col[:, 2, :], -1.0, 1.0, ALU.mult, ALU.add))
                dve.wait_ge(counted_ready, 1)
                link(nc.vector.tensor_copy(tot[:, :, :], total[:, :, :].rearrange("p t e -> p e t")))
                for e in range(E):
                    ins = nc.vector.tensor_tensor_scan(incl[:, e, :], ones[:, 0:TILES], tot[:, e, :], 0.0,
                                                       ALU.mult, ALU.add)
                link(ins)
                shape = [P, E, TOK // ETOK]
                link(nc.vector.tensor_tensor(over[:, :, :], incl[:, :, TILES - 1:TILES].broadcast_to(shape),
                                             floor.unsqueeze(1).broadcast_to(shape), ALU.is_gt))
                link(nc.vector.tensor_reduce(counts[:, 0, :], over[:, :, :], AX.X, ALU.add))
                link(nc.vector.tensor_tensor_scan(counts[:, 1, :], ones[:, 0:E], counts[:, 0, :], 0.0,
                                                  ALU.mult, ALU.add))
                link(nc.vector.tensor_tensor(after[:, :, :],
                                             index.unsqueeze(2).broadcast_to([P, ETILES, E]),
                                             counts[:, 1, :].unsqueeze(1).broadcast_to([P, ETILES, E]), ALU.is_ge))
                link(nc.vector.tensor_reduce(owner[:, :], after[:, :, :], AX.X, ALU.add))
                link(nc.vector.tensor_scalar(plan["expert"][:, :], owner[:, :], float(E - 1), None, ALU.min))
                link(nc.vector.tensor_tensor(counts[:, 2, :], counts[:, 1, :], counts[:, 0, :], ALU.subtract))
                link(nc.vector.tensor_scalar(counts[:, 3, :], counts[:, 2, :], float(ETOK), None, ALU.mult))
                link(nc.vector.tensor_tensor(incl[:, :, :], incl[:, :, :], tot[:, :, :], ALU.subtract))
                link(nc.vector.tensor_tensor(incl[:, :, :], incl[:, :, :],
                                             counts[:, 3, :].unsqueeze(2).broadcast_to([P, E, TILES]), ALU.add))
                link(nc.vector.tensor_tensor(val[:, :, :], before[:, :, :],
                                             incl[:, :, :].rearrange("p e t -> p t e"), ALU.add))
                for k in range(2):
                    link(nc.vector.tensor_tensor(key[:, :, :], val[:, :, :], one_hot[:, k, :, :], ALU.mult))
                    link(nc.vector.tensor_reduce(row_f[:, k, :], key[:, :, :], AX.X, ALU.add))
                link(nc.vector.tensor_copy(plan["rows"][:, :, :], row_f[:, :, :]))
        m.clear()


def dispatch(nc, x_res, norm, plan, rows_dram, tag):
    RING = 4
    with ExitStack() as ctx:
        m = Mem(nc, ctx, tag + "_dispatch")
        xn = m.sb("xn", [P, RING, C])
        at = m.sb("at", [P, RING, 2], U32)
        xn_ready = m.sem("xn_ready")
        at_ready = m.sem("at_ready")
        act_held = m.sem("act_held")
        pool_held = m.sem("pool_held")
        written = [m.sem(f"written{k}") for k in range(RING)]
        with nc.Block() as block:
            @block.scalar
            def _(act):
                def tile(r, k):
                    if not first_round(r):
                        act.wait_ge(written[k], r * 32)
                        hold(act, act_held)
                    at_tile = bass.ds(r * RING + k, 1)
                    nc.scalar.activation(xn[:, k, :], x_res[:, at_tile, :].rearrange("p a c -> p (a c)"),
                                         ACT.Identity, bias=norm["shift"][:, at_tile],
                                         scale=norm["rstd"][:, at_tile]).then_inc(xn_ready, 1)

                ring_rounds(act, RING, tile)

            @block.vector
            def _(dve):
                def tile(r, k):
                    if not first_round(r):
                        dve.wait_ge(written[k], r * 32)
                    nc.vector.tensor_copy(at[:, k, :], plan["rows"][:, :, bass.ds(r * RING + k, 1)]
                                          .rearrange("p c a -> p (c a)")).then_inc(at_ready, 1)

                ring_rounds(dve, RING, tile)

            @block.gpsimd
            def _(pool):
                def tile(r, k):
                    pool.wait_ge(xn_ready, r * RING + k + 1)
                    pool.wait_ge(at_ready, r * RING + k + 1)
                    hold(pool, pool_held)
                    for c in range(2):
                        pool.indirect_dma_start(rows_dram, bass.IndirectOffsetOnAxis(ap=at[:, k, c:c + 1], axis=0),
                                                xn[:, k, :], None).then_inc(written[k], 16)

                ring_rounds(pool, RING, tile)
                for k in range(RING):
                    pool.wait_ge(written[k], TILES // RING * 32)
        m.clear()


def combine(nc, x_res, plan, rows_dram, tag, out=None):
    RING = 4
    with ExitStack() as ctx:
        m = Mem(nc, ctx, tag + "_combine")
        y = m.sb("y", [P, RING, 2, C])
        at = m.sb("at", [P, RING, 2], U32)
        at_ready = m.sem("at_ready")
        half = m.sem("half")
        stored = m.sem("stored")
        added = m.sem("added")
        pool_held = m.sem("pool_held")
        gathered = [m.sem(f"gathered{k}") for k in range(RING)]
        with nc.Block() as block:
            if out is not None:
                @block.sync
                def _(sp):
                    part = TILES // 4
                    for k in range(4):
                        sp.wait_ge(added, (k + 1) * part)
                        sp.dma_start(out[:, k * part:(k + 1) * part, :],
                                     x_res[:, k * part:(k + 1) * part, :]).then_inc(stored, 16)
                    sp.wait_ge(stored, 64)

            @block.gpsimd
            def _(pool):
                def tile(r, k):
                    n = r * RING + k
                    if not first_round(r):
                        pool.wait_ge(added, n - RING + 1)
                    pool.wait_ge(at_ready, n + 1)
                    hold(pool, pool_held)
                    for c in range(2):
                        pool.indirect_dma_start(y[:, k, c, :], None, rows_dram,
                                                bass.IndirectOffsetOnAxis(ap=at[:, k, c:c + 1], axis=0)
                                                ).then_inc(gathered[k], 16)

                ring_rounds(pool, RING, tile)

            @block.vector
            def _(dve):
                def indices(r, k):
                    nc.vector.tensor_copy(at[:, k, :], plan["rows"][:, :, bass.ds(r * RING + k, 1)]
                                          .rearrange("p c a -> p (c a)")).then_inc(at_ready, 1)

                def add_up(r, k):
                    n = r * RING + k
                    xt = x_res[:, bass.ds(n, 1), :].rearrange("p a c -> p (a c)")
                    dve.wait_ge(gathered[k], r * 32 + 32)
                    nc.vector.scalar_tensor_tensor(out=xt, in0=y[:, k, 0, :],
                                                   scalar=plan["gates"][:, 0, bass.ds(n, 1)],
                                                   in1=xt, op0=ALU.mult, op1=ALU.add).then_inc(half, 1)
                    dve.wait_ge(half, n + 1)
                    nc.vector.scalar_tensor_tensor(out=xt, in0=y[:, k, 1, :],
                                                   scalar=plan["gates"][:, 1, bass.ds(n, 1)],
                                                   in1=xt, op0=ALU.mult, op1=ALU.add).then_inc(added, 1)

                last = TILES // RING - 1
                for k in range(RING):
                    indices(0, k)
                with dve.Fori(0, last) as r:
                    for k in range(RING):
                        add_up(r, k)
                        indices(r + 1, k)
                for k in range(RING):
                    add_up(last, k)
        m.clear()


def moe_buffers(nc, m):
    norm = {"rstd": m.sb("rstd", [P, TILES])[:, :], "shift": m.sb("shift", [P, TILES])[:, :]}
    plan = {"gates": m.sb("gates", [P, 2, TILES]), "rows": m.sb("rows", [P, 2, TILES], U32),
            "expert": m.sb("expert", [P, ETILES], I32)}
    return norm, plan


def owner_of(eng, plan, j):
    return eng.value_load(plan["expert"][0:1, bass.ds(j, 1)], min_val=0, max_val=E - 1)


def rows_of(rows, r, u):
    return rows.rearrange("(j t p) c -> p (j t) c", p=P, t=2)[:, bass.ds((r * 2 + u) * 2, 2), :]


def load_rows(sp, rows_in, xg, xg_in, tp_ready):
    for u in range(2):
        sp.dma_start(xg[:, u, :, :], rows_of(rows_in, 0, u)).then_inc(xg_in[u], 16)
    with sp.Fori(1, ETILES // 2) as r:
        for u in range(2):
            sp.wait_ge(tp_ready, r * 2 + u - 1)
            sp.dma_start(xg[:, u, :, :], rows_of(rows_in, r, u)).then_inc(xg_in[u], 16)


def store_rows(pool, held, rows_out, ys, ys_out, ys_ready, r, u):
    pool.wait_ge(ys_ready, r * 2 + u + 1)
    hold(pool, held)
    pool.dma_start(rows_of(rows_out, r, u), ys[:, u, :, :]).then_inc(ys_out[u], 16)


def turn_rows(nc, tp, rows, ident):
    for h in range(2):
        for t in range(2):
            ins = nc.tensor.transpose(tp[0:HC, (2 * h + t) * P:(2 * h + t + 1) * P],
                                      rows[:, t, h * HC:(h + 1) * HC], ident)
    return ins


def expert_order(pe, turn, first_layer, second_layer):
    last = ETILES // 2 - 1
    turn(0, 0)
    first_layer(0, 0)
    turn(0, 1)
    first_layer(0, 1)
    turn(1, 0)
    second_layer(0, 0)
    with pe.Fori(1, last) as r:
        first_layer(r, 0)
        turn(r, 1)
        second_layer(r - 1, 1)
        first_layer(r, 1)
        turn(r + 1, 0)
        second_layer(r, 0)
    first_layer(last, 0)
    turn(last, 1)
    second_layer(last - 1, 1)
    first_layer(last, 1)
    second_layer(last, 0)
    second_layer(last, 1)


def moe_relu_phase(nc, x_res, moments, consts, w):
    H = 768
    MC = H // P
    HB = MC // 2
    rows_in, rows_out = consts["rows_in"], consts["rows_out"]
    with ExitStack() as ctx:
        m = Mem(nc, ctx, "l3f")
        w1 = m.sb("w1", [HC, 2, E, H])
        w2 = m.sb("w2", [P, MC, E, C])
        b1 = m.sb("b1", [P, E, MC])
        b2 = m.sb("b2", [P, E, C])
        norm, plan = moe_buffers(nc, m)
        weights_in = m.sem("weights_in")
        norm["weights_in"] = weights_in
        norm["weights"] = [(b1[:, :, :], w["b1"]), (b2[:, :, :], w["b2"].partition_broadcast(P)),
                           (w1[:, :, :, :], w["w1"]), (w2[:, :, :, :], w["w2"])]
        route(nc, x_res, moments, consts, w, norm, plan, "l3f", True)
        dispatch(nc, x_res, norm, plan, rows_in, "l3f")

        xg = m.sb("xg", [P, 2, 2, C])
        tT = m.sb("tT", [HC, 2, 2, 2, ETOK], F32R)
        w1_own = m.sb("w1_own", [HC, 2, 2, 2, H], F32R)
        hT = m.sb("hT", [P, 2, MC, ETOK])
        ys = m.sb("ys", [P, 2, 2, C])
        pctx = ctx.enter_context(ExitStack())
        pm = Mem(nc, pctx, "l3f_expert")
        h_ps = [pm.ps(f"h{k}", [P, 2, ETOK]) for k in range(HB)]
        y_ps = [pm.ps(f"y{k}", [P, 512]) for k in range(2)]
        tp = [pm.ps(f"tp{k}", [P, 512]) for k in range(2)]
        xg_in = [m.sem(f"xg_in{k}") for k in range(2)]
        ys_out = [m.sem(f"ys_out{k}") for k in range(2)]
        tp_ready = m.sem("tp_ready")
        tT_high = m.sem("tT_high")
        tT_ready = m.sem("tT_ready")
        w1_high = m.sem("w1_high")
        w1_ready = m.sem("w1_ready")
        h_ready = m.sem("h_ready")
        relu_done = m.sem("relu_done")
        y_ready = m.sem("y_ready")
        ys_ready = m.sem("ys_ready")
        act_held = m.sem("act_held")
        pool_held = m.sem("pool_held")
        dve_held = m.sem("dve_held")
        LAST = ETILES // 2 - 1

        with nc.Block() as block:
            @block.sync
            def _(sp):
                load_rows(sp, rows_in, xg, xg_in, tp_ready)

            @block.gpsimd
            def _(pool):
                pool.wait_ge(weights_in, 64)

                def low_weights(r, u):
                    e = owner_of(pool, plan, r * 2 + u)
                    pool.wait_ge(w1_high, r * 2 + u + 1)
                    hold(pool, pool_held)
                    nc.gpsimd.tensor_tensor(w1_own[:, u, 1, :, :],
                                            w1[:, :, bass.ds(e, 1), :].rearrange("p h a f -> p h (a f)"),
                                            w1_own[:, u, 0, :, :].bitcast(F32), ALU.subtract).then_inc(w1_ready, 1)

                def store(r, u):
                    store_rows(pool, pool_held, rows_out, ys, ys_out, ys_ready, r, u)

                low_weights(0, 0)
                low_weights(0, 1)
                low_weights(1, 0)
                low_weights(1, 1)
                store(0, 0)
                with pool.Fori(1, LAST) as r:
                    low_weights(r + 1, 0)
                    store(r - 1, 1)
                    low_weights(r + 1, 1)
                    store(r, 0)
                store(LAST - 1, 1)
                store(LAST, 0)
                store(LAST, 1)
                for u in range(2):
                    pool.wait_ge(ys_out[u], ETILES // 2 * 16)

            @block.tensor
            def _(pe):
                pe.wait_ge(weights_in, 64)

                def turn(r, u):
                    pe.wait_ge(xg_in[u], r * 16 + 16)
                    turn_rows(nc, tp[u], xg[:, u, :, :], consts["ident"]).then_inc(tp_ready, 1)

                def first_layer(r, u):
                    j = r * 2 + u
                    pe.wait_ge(tT_ready, j + 1)
                    pe.wait_ge(w1_ready, j + 1)
                    for b in range(HB):
                        if not (u == 0 and first_round(r)):
                            pe.wait_ge(relu_done, j * HB - HB + b + 1)
                        for c in (2 * b, 2 * b + 1):
                            for h in range(2):
                                for wp, tp_ in ((0, 0), (0, 1), (1, 0)):
                                    ins = nc.tensor.matmul(h_ps[b][:, c % 2, :],
                                                           w1_own[:, u, wp, h, c * P:(c + 1) * P],
                                                           tT[:, u, tp_, h, :], start=h == 0 and wp == tp_,
                                                           stop=h == 1 and wp == 1)
                        ins.then_inc(h_ready, 1)

                def second_layer(r, u):
                    j = r * 2 + u
                    e = owner_of(pe, plan, j)
                    pe.wait_ge(relu_done, j * HB + HB)
                    if not first_round(r):
                        pe.wait_ge(ys_ready, j - 1)
                    for t in range(2):
                        for c in range(MC):
                            ins = nc.tensor.matmul(y_ps[u][:, t * C:(t + 1) * C], hT[:, u, c, t * P:(t + 1) * P],
                                                   w2[:, c, bass.ds(e, 1), :].rearrange("p a c -> p (a c)"),
                                                   start=c == 0, stop=c == MC - 1)
                    ins.then_inc(y_ready, 1)

                expert_order(pe, turn, first_layer, second_layer)

            @block.scalar
            def _(act):
                def tile(r, u):
                    j = r * 2 + u
                    e = owner_of(act, plan, j)
                    if not first_round(r):
                        act.wait_ge(h_ready, j * HB - HB)
                    act.wait_ge(tp_ready, j + 1)
                    nc.scalar.copy(tT[:, u, 0, :, :].rearrange("p h t -> p (h t)"), tp[u][0:HC, :]
                                   ).then_inc(tT_high, 1)
                    if not first_round(r):
                        act.wait_ge(y_ready, j - 1)
                    for c in range(MC):
                        if c % 2 == 0:
                            act.wait_ge(h_ready, j * HB + c // 2 + 1)
                            hold(act, act_held)
                        ins = nc.scalar.activation(hT[:, u, c, :], h_ps[c // 2][:, c % 2, :], ACT.Relu,
                                                   bias=b1[:, bass.ds(e, 1), c:c + 1].rearrange("p a c -> p (a c)"))
                        if c % 2:
                            ins.then_inc(relu_done, 1)

                rounds(act, tile)

            @block.vector
            def _(dve):
                dve.wait_ge(weights_in, 64)

                def own_weights(r, u):
                    j = r * 2 + u
                    e = owner_of(dve, plan, j)
                    if not first_round(r):
                        dve.wait_ge(h_ready, j * HB - HB)
                        hold(dve, dve_held)
                    nc.vector.tensor_copy(w1_own[:, u, 0, :, :],
                                          w1[:, :, bass.ds(e, 1), :].rearrange("p h a f -> p h (a f)")
                                          ).then_inc(w1_high, 1)

                def low_rows(r, u):
                    dve.wait_ge(tT_high, r * 2 + u + 1)
                    nc.vector.tensor_tensor(tT[:, u, 1, :, :].rearrange("p h t -> p (h t)"), tp[u][0:HC, :],
                                            tT[:, u, 0, :, :].rearrange("p h t -> p (h t)").bitcast(F32),
                                            ALU.subtract).then_inc(tT_ready, 1)

                def finish(r, u):
                    j = r * 2 + u
                    e = owner_of(dve, plan, j)
                    if not first_round(r):
                        dve.wait_ge(ys_out[u], r * 16)
                    dve.wait_ge(y_ready, j + 1)
                    nc.vector.tensor_tensor(ys[:, u, :, :], y_ps[u][:, 0:2 * C].rearrange("p (t c) -> p t c", t=2),
                                            b2[:, bass.ds(e, 1), :].broadcast_to([P, 2, C]),
                                            ALU.add).then_inc(ys_ready, 1)

                low_rows(0, 0)
                own_weights(0, 0)
                own_weights(0, 1)
                low_rows(0, 1)
                own_weights(1, 0)
                low_rows(1, 0)
                own_weights(1, 1)
                finish(0, 0)
                with dve.Fori(1, LAST) as r:
                    low_rows(r, 1)
                    own_weights(r + 1, 0)
                    finish(r - 1, 1)
                    low_rows(r + 1, 0)
                    own_weights(r + 1, 1)
                    finish(r, 0)
                low_rows(LAST, 1)
                finish(LAST - 1, 1)
                finish(LAST, 0)
                finish(LAST, 1)
        pctx.close()
        combine(nc, x_res, plan, rows_out, "l3f", consts["out"])
        m.clear()


def moe_glu_phase(nc, x_res, moments, consts, w):
    LIMIT = 7.0
    ALPHA = 1.702
    rows_in, rows_out = consts["rows_in"], consts["rows_out"]
    with ExitStack() as ctx:
        m = Mem(nc, ctx, "l2f")
        wgu = m.sb("wgu", [HC, 2, E, 4 * HC])
        wd = m.sb("wd", [HC, 2, E, C])
        bgu = m.sb("bgu", [HC, E, 4])
        bd = m.sb("bd", [P, E, C])
        norm, plan = moe_buffers(nc, m)
        weights_in = m.sem("weights_in")
        norm["weights_in"] = weights_in
        norm["weights"] = [(bgu[:, :, :], w["bgu"]), (bd[:, :, :], w["bd"].partition_broadcast(P)),
                           (wgu[:, :, :, :], w["wgu"]), (wd[:, :, :, :], w["wd"])]
        route(nc, x_res, moments, consts, w, norm, plan, "l2f", False)
        dispatch(nc, x_res, norm, plan, rows_in, "l2f")

        xg = m.sb("xg", [P, 2, 2, C])
        tT = m.sb("tT", [HC, 2, 2, ETOK])
        wgu_own = m.sb("wgu_own", [HC, 2, 2, 4 * HC])
        gate_in = m.sb("gate_in", [HC, 2, 2, ETOK])
        up_in = m.sb("up_in", [HC, 2, 2, ETOK])
        silu = m.sb("silu", [HC, 2, 2, ETOK])
        aT = m.sb("aT", [HC, 2, 2, ETOK])
        ys = m.sb("ys", [P, 2, 2, C])
        pctx = ctx.enter_context(ExitStack())
        pm = Mem(nc, pctx, "l2f_expert")
        gate_ps = [pm.ps(f"gate{k}", [HC, 2, ETOK]) for k in range(2)]
        up_ps = [pm.ps(f"up{k}", [HC, 2, ETOK]) for k in range(2)]
        y_ps = [pm.ps(f"y{k}", [P, 512]) for k in range(2)]
        tp = [pm.ps(f"tp{k}", [P, 512]) for k in range(2)]
        xg_in = [m.sem(f"xg_in{k}") for k in range(2)]
        ys_out = [m.sem(f"ys_out{k}") for k in range(2)]
        tp_ready = m.sem("tp_ready")
        tT_ready = m.sem("tT_ready")
        own_ready = m.sem("own_ready")
        gate_ready = m.sem("gate_ready")
        up_ready = m.sem("up_ready")
        gate_clipped = m.sem("gate_clipped")
        up_half = m.sem("up_half")
        up_clipped = m.sem("up_clipped")
        silu_ready = m.sem("silu_ready")
        aT_ready = m.sem("aT_ready")
        y_ready = m.sem("y_ready")
        ys_ready = m.sem("ys_ready")
        pool_held = m.sem("pool_held")
        LAST = ETILES // 2 - 1

        with nc.Block() as block:
            @block.sync
            def _(sp):
                load_rows(sp, rows_in, xg, xg_in, tp_ready)

            @block.tensor
            def _(pe):
                pe.wait_ge(weights_in, 64)

                def turn(r, u):
                    pe.wait_ge(xg_in[u], r * 16 + 16)
                    turn_rows(nc, tp[u], xg[:, u, :, :], consts["ident"]).then_inc(tp_ready, 1)

                def first_layer(r, u):
                    j = r * 2 + u
                    pe.wait_ge(tT_ready, j + 1)
                    pe.wait_ge(own_ready, j + 1)
                    for ps, free, ready, c0 in ((gate_ps, gate_clipped, gate_ready, 0),
                                                (up_ps, up_half, up_ready, 2)):
                        if not first_round(r):
                            pe.wait_ge(free, j - 1)
                        for c in range(2):
                            for h in range(2):
                                ins = nc.tensor.matmul(ps[u][:, c, :],
                                                       wgu_own[:, u, h, (c0 + c) * HC:(c0 + c + 1) * HC],
                                                       tT[:, u, h, :], start=h == 0, stop=h == 1)
                        ins.then_inc(ready, 1)

                def second_layer(r, u):
                    j = r * 2 + u
                    e = owner_of(pe, plan, j)
                    pe.wait_ge(aT_ready, j + 1)
                    if not first_round(r):
                        pe.wait_ge(ys_ready, j - 1)
                    for t in range(2):
                        for h in range(2):
                            ins = nc.tensor.matmul(y_ps[u][:, t * C:(t + 1) * C], aT[:, u, h, t * P:(t + 1) * P],
                                                   wd[:, h, bass.ds(e, 1), :].rearrange("p a c -> p (a c)"),
                                                   start=h == 0, stop=h == 1)
                    ins.then_inc(y_ready, 1)

                expert_order(pe, turn, first_layer, second_layer)

            @block.scalar
            def _(act):
                def turned(r, u):
                    j = r * 2 + u
                    if not first_round(r):
                        act.wait_ge(up_ready, j - 1)
                    act.wait_ge(tp_ready, j + 1)
                    nc.scalar.copy(tT[:, u, :, :].rearrange("p h t -> p (h t)"), tp[u][0:HC, :]).then_inc(tT_ready, 1)

                def silu_of(r, u):
                    j = r * 2 + u
                    if not first_round(r):
                        act.wait_ge(aT_ready, j - 1)
                    act.wait_ge(gate_clipped, j + 1)
                    nc.scalar.activation(silu[:, u, :, :], gate_in[:, u, :, :], ACT.Silu,
                                         scale=ALPHA).then_inc(silu_ready, 1)

                turned(0, 0)
                turned(0, 1)
                silu_of(0, 0)
                with act.Fori(1, LAST + 1) as r:
                    turned(r, 0)
                    silu_of(r - 1, 1)
                    turned(r, 1)
                    silu_of(r, 0)
                silu_of(LAST, 1)

            @block.gpsimd
            def _(pool):
                def own_weights(r, u):
                    e = owner_of(pool, plan, r * 2 + u)
                    if not first_round(r):
                        pool.wait_ge(up_ready, r * 2 + u - 1)
                        hold(pool, pool_held)
                    nc.gpsimd.tensor_copy(wgu_own[:, u, :, :],
                                          wgu[:, :, bass.ds(e, 1), :].rearrange("p h a f -> p h (a f)")
                                          ).then_inc(own_ready, 1)

                def store(r, u):
                    store_rows(pool, pool_held, rows_out, ys, ys_out, ys_ready, r, u)

                pool.wait_ge(weights_in, 64)
                own_weights(0, 0)
                own_weights(0, 1)
                own_weights(1, 0)
                own_weights(1, 1)
                store(0, 0)
                with pool.Fori(1, LAST) as r:
                    own_weights(r + 1, 0)
                    store(r - 1, 1)
                    own_weights(r + 1, 1)
                    store(r, 0)
                store(LAST - 1, 1)
                store(LAST, 0)
                store(LAST, 1)
                for u in range(2):
                    pool.wait_ge(ys_out[u], ETILES // 2 * 16)

            @block.vector
            def _(dve):
                dve.wait_ge(weights_in, 64)

                def clip(r, u):
                    j = r * 2 + u
                    e = owner_of(dve, plan, j)
                    if not first_round(r):
                        dve.wait_ge(silu_ready, j - 1)
                        dve.wait_ge(aT_ready, j - 1)
                    dve.wait_ge(gate_ready, j + 1)
                    for c in range(2):
                        ins = nc.vector.tensor_scalar(gate_in[:, u, c, :], gate_ps[u][:, c, :],
                                                      bgu[:, bass.ds(e, 1), c:c + 1].rearrange("p a c -> p (a c)"),
                                                      LIMIT, ALU.add, ALU.min)
                    ins.then_inc(gate_clipped, 1)
                    dve.wait_ge(up_ready, j + 1)
                    for c in range(2):
                        ins = nc.vector.tensor_scalar(up_in[:, u, c, :], up_ps[u][:, c, :],
                                                      bgu[:, bass.ds(e, 1), 2 + c:3 + c].rearrange("p a c -> p (a c)"),
                                                      LIMIT, ALU.add, ALU.min)
                    ins.then_inc(up_half, 1)
                    dve.wait_ge(up_half, j + 1)
                    nc.vector.tensor_scalar(up_in[:, u, :, :], up_in[:, u, :, :], -LIMIT, 1.0,
                                            ALU.max, ALU.add).then_inc(up_clipped, 1)

                    dve.wait_ge(silu_ready, j + 1)
                    dve.wait_ge(up_clipped, j + 1)
                    if not first_round(r):
                        dve.wait_ge(y_ready, j - 1)
                    nc.vector.scalar_tensor_tensor(out=aT[:, u, :, :], in0=silu[:, u, :, :], scalar=1.0 / ALPHA,
                                                   in1=up_in[:, u, :, :], op0=ALU.mult,
                                                   op1=ALU.mult).then_inc(aT_ready, 1)

                def finish(r, u):
                    j = r * 2 + u
                    e = owner_of(dve, plan, j)
                    if not first_round(r):
                        dve.wait_ge(ys_out[u], r * 16)
                    dve.wait_ge(y_ready, j + 1)
                    nc.vector.tensor_tensor(ys[:, u, :, :], y_ps[u][:, 0:2 * C].rearrange("p (t c) -> p t c", t=2),
                                            bd[:, bass.ds(e, 1), :].broadcast_to([P, 2, C]),
                                            ALU.add).then_inc(ys_ready, 1)

                clip(0, 0)
                clip(0, 1)
                finish(0, 0)
                with dve.Fori(1, LAST + 1) as r:
                    clip(r, 0)
                    finish(r - 1, 1)
                    clip(r, 1)
                    finish(r, 0)
                finish(LAST, 1)
        pctx.close()
        combine(nc, x_res, plan, rows_out, "l2f")
        m.clear()


def memory_attention_phase(nc, x_res, moments, consts, w):
    M = 8
    SCALE = float(C) ** -0.5
    with ExitStack() as ctx:
        m = Mem(nc, ctx, "l3a")
        wq = m.sb("wq", [HC, 2, C])
        wk = m.sb("wk", [HC, 2, C])
        wv = m.sb("wv", [HC, 2, C])
        wo = m.sb("wo", [HC, 2, C])
        memT = m.sb("memT", [HC, 2, M])
        bq = m.sb("bq", [HC, 2])
        bk = m.sb("bk", [HC, 2])
        bv = m.sb("bv", [P, C])
        bo = m.sb("bo", [P, C])
        rstd = m.sb("rstd", [P, TILES])
        shift = m.sb("shift", [P, TILES])
        y0 = m.sb("guess", [P, 4, TILES])
        stats = m.sb("stats", [P, TILES, 6])
        xn = m.sb("xn", [P, 2, 2, C])
        tT = m.sb("tT", [HC, 2, 2, T])
        qT = m.sb("qT", [HC, 2, 2, T])
        kT = [m.sb(f"kT{k}", [HC, 2, T + M]) for k in range(2)]
        v = m.sb("v", [P, 2, 2, C])
        vm = m.sb("vm", [M, C])
        top = m.sb("top", [P, 2, 2])
        sums = m.sb("sums", [P, 2, 2, 2])
        probs = m.sb("probs", [P, 2, T + M])
        pT = m.sb("pT", [P, 2, T])
        pmT = m.sb("pmT", [M, T])
        oT = m.sb("oT", [HC, 2, T])
        tp = m.ps("tp", [P, 512])
        q_ps = m.ps("q", [HC, 2, T])
        k_ps = m.ps("k", [HC, 2, T])
        v_ps = m.ps("v_ps", [P, 512])
        s_ps = [m.ps(f"s{t}", [P, 512]) for t in range(2)]
        pT_ps = m.ps("pT_ps", [P, 2, T])
        pmT_ps = m.ps("pmT_ps", [P, 512])
        tp_ps = tp[0:HC, :].rearrange("p (h t) -> p h t", h=2)
        o_ps = q_ps
        y_ps = pmT_ps

        weights_in = m.sem("weights_in")
        stats_ready = m.sem("stats_ready")
        moments_ready = m.sem("moments_ready")
        half_log = m.sem("half_log")
        dve_chain0 = m.sem("dve_chain0")
        rstd_ready = m.sem("rstd_ready")
        xn_ready = m.sem("xn_ready")
        tp_ready = m.sem("tp_ready")
        tT_ready = m.sem("tT_ready")
        mem_ps = m.sem("mem_ps")
        mem_ready = m.sem("mem_ready")
        q_ready = m.sem("q_ready")
        k_ready = m.sem("k_ready")
        v_ready = m.sem("v_ready")
        qT_ready = m.sem("qT_ready")
        kT_ready = m.sem("kT_ready")
        vb_ready = m.sem("vb_ready")
        scores_ready = m.sem("scores_ready")
        max_ready = m.sem("max_ready")
        probs_ready = m.sem("probs_ready")
        pT_psum = m.sem("pT_psum")
        pT_ready = m.sem("pT_ready")
        pmT_ready = m.sem("pmT_ready")
        o_ready = m.sem("o_ready")
        oT_ready = m.sem("oT_ready")
        y_ready = m.sem("y_ready")
        y_used = m.sem("y_used")
        dve_chain = m.sem("dve_chain")
        sum_chain = m.sem("sum_chain")
        act_held = m.sem("act_held")

        with nc.Block() as block:
            @block.sync
            def _(sp):
                for dst, src in ((memT[:, :, :], w["memT"]), (wk[:, :, :], w["wk"]), (wv[:, :, :], w["wv"]),
                                 (wq[:, :, :], w["wq"]), (wo[:, :, :], w["wo"]), (bq[:, :], w["bq"]),
                                 (bk[:, :], w["bk"]), (bv[:, :], w["bv"].partition_broadcast(P)),
                                 (bo[:, :], w["bo"].partition_broadcast(P))):
                    sp.dma_start(dst, src).then_inc(weights_in, 16)

            @block.scalar
            def _(act):
                for s in (xn_ready, tT_ready, qT_ready, kT_ready, probs_ready, oT_ready):
                    act.sem_inc(s, 1)
                rstd_steps_act(nc, act, moments_ready, half_log, moments, y0, consts["eps"])
                act.wait_ge(weights_in, 9 * 16)
                act.wait_ge(mem_ps, 1)
                for k in range(2):
                    for h in range(2):
                        nc.scalar.activation(kT[k][:, h, T:T + M], k_ps[:, h, 0:M], ACT.Identity,
                                             bias=bk[:, h:h + 1]).then_inc(mem_ready, 1)
                act.wait_ge(rstd_ready, 1)
                hold(act, act_held)

                def normal(n, u):
                    if not (isinstance(n, int) and n < 2):
                        act.wait_ge(tp_ready, counted(n - 1))
                        hold(act, act_held)
                    normalise(nc, xn[:, u, :, :], x_res, rstd, shift, n * 2).then_inc(xn_ready, 1)

                def first(n, u):
                    act.wait_ge(tp_ready, counted(n + 1))
                    nc.scalar.copy(tT[:, u, :, :], tp_ps).then_inc(tT_ready, 1)
                    act.wait_ge(k_ready, counted(n + 1))
                    for h in range(2):
                        ins = nc.scalar.activation(kT[u][:, h, 0:T], k_ps[:, h, :], ACT.Identity, bias=bk[:, h:h + 1])
                    ins.then_inc(kT_ready, 1)
                    act.wait_ge(q_ready, counted(n + 1))
                    for h in range(2):
                        ins = nc.scalar.activation(qT[:, u, h, :], q_ps[:, h, :], ACT.Identity, bias=bq[:, h:h + 1])
                    ins.then_inc(qT_ready, 1)

                def rest(n, u, nxt, before):
                    if not (isinstance(n, int) and n == B - 1):
                        normal(n + 1, 1 - u)
                    for t in range(2):
                        act.wait_ge(max_ready, counted(n * 2 + (t + 1)))
                        nc.scalar.activation(probs[:, t, :], s_ps[t][:, 0:T + M], ACT.Exp, bias=top[:, t, 1:2],
                                             scale=SCALE, accum_out=sums[:, u, t, 0:1]).then_inc(probs_ready, 1)
                    before()
                    nxt()

                def late(n, u):
                    act.wait_ge(o_ready, counted(n + 1))
                    nc.scalar.copy(oT[:, :, :], o_ps[:, :, :]).then_inc(oT_ready, 1)

                normal(0, 0)
                pipelined_late(act, first, rest, late)

            @block.vector
            def _(dve):
                moment_steps(nc, dve, stats, stats_ready, moments_ready, x_res, moments)
                chain0 = Chain(dve, dve_chain0)
                rstd_steps_dve(nc, dve, chain0, half_log, moments, y0, rstd, shift).then_inc(rstd_ready, 1)
                for s in (vb_ready, max_ready, pT_ready, pmT_ready, y_used):
                    dve.sem_inc(s, 1)
                dve.wait_ge(weights_in, 9 * 16)
                dve.wait_ge(mem_ps, 2)
                nc.vector.tensor_tensor(vm[:, :], v_ps[0:M, 0:C], bv[0:M, :], ALU.add).then_inc(mem_ready, 1)

                def first(n, u):
                    dve.wait_ge(v_ready, counted(n + 1))
                    nc.vector.tensor_tensor(v[:, u, :, :], v_ps[:, 0:2 * C].rearrange("p (t c) -> p t c", t=2),
                                            bv[:, :].unsqueeze(1).broadcast_to([P, 2, C]), ALU.add).then_inc(vb_ready, 1)

                def rest(n, u, nxt, before):
                    chain = Chain(dve, dve_chain, 2, n)
                    for t in range(2):
                        dve.wait_ge(scores_ready, counted(n * 2 + (t + 1)))
                        chain.link(nc.vector.tensor_reduce(top[:, t, 0:1], s_ps[t][:, 0:T + M], AX.X, ALU.max))
                        nc.vector.tensor_scalar(top[:, t, 1:2], top[:, t, 0:1], -SCALE, None,
                                                ALU.mult).then_inc(max_ready, 1)
                    chain.close()
                    before()
                    nxt()
                    dve.wait_ge(pT_psum, counted(n + 1))
                    nc.vector.tensor_copy(pT[:, :, :], pT_ps[:, :, :]).then_inc(pT_ready, 1)
                    nc.vector.tensor_copy(pmT[:, :], pmT_ps[0:M, 0:T]).then_inc(pmT_ready, 1)

                def late(n, u):
                    chain = Chain(dve, sum_chain, 1 + 3, n)
                    chain.link(nc.vector.reciprocal(sums[:, u, :, 1], sums[:, u, :, 0]))
                    dve.wait_ge(y_ready, counted(n + 1))
                    for t in range(2):
                        xt = tile_of(x_res, n, t)
                        chain.send(nc.vector.scalar_tensor_tensor(out=xt, in0=y_ps[:, t * C:(t + 1) * C],
                                                                  scalar=sums[:, u, t, 1:2], in1=xt,
                                                                  op0=ALU.mult, op1=ALU.add))
                    dve.wait_ge(sum_chain, n * 4 + 3)
                    dve.sem_inc(y_used, 1)
                    xt = x_res[:, bass.ds(n * 2, 2), :]
                    chain.link(nc.vector.tensor_tensor(xt, xt, bo[:, :].unsqueeze(1).broadcast_to([P, 2, C]), ALU.add))
                    chain.close()

                pipelined_late(dve, first, rest, late)

            @block.tensor
            def _(pe):
                for s in (tp_ready, q_ready, k_ready, v_ready, scores_ready, pT_psum, o_ready, y_ready):
                    pe.sem_inc(s, 1)
                pe.wait_ge(weights_in, 9 * 16)
                for ho in range(2):
                    for h in range(2):
                        ins = nc.tensor.matmul(k_ps[:, ho, 0:M], wk[:, h, ho * HC:(ho + 1) * HC], memT[:, h, :],
                                               start=h == 0, stop=h == 1)
                ins.then_inc(mem_ps, 1)
                for h in range(2):
                    ins = nc.tensor.matmul(v_ps[0:M, 0:C], memT[:, h, :], wv[:, h, :], start=h == 0, stop=h == 1)
                ins.then_inc(mem_ps, 1)
                pe.wait_ge(mem_ready, 5)

                def first(n, u, part):
                    if part == "turn":
                        pe.wait_ge(xn_ready, counted(n + 1))
                        pe.wait_ge(tT_ready, counted(n))
                        for h in range(2):
                            for t in range(2):
                                ins = nc.tensor.transpose(tp_ps[:, h, t * P:(t + 1) * P],
                                                          xn[:, u, t, h * HC:(h + 1) * HC], consts["ident"])
                        ins.then_inc(tp_ready, 1)
                        return
                    pe.wait_ge(tT_ready, counted(n + 1))

                    def project(ps, wx):
                        for ho in range(2):
                            for h in range(2):
                                ins = nc.tensor.matmul(ps[:, ho, :], wx[:, h, ho * HC:(ho + 1) * HC], tT[:, u, h, :],
                                                       start=h == 0, stop=h == 1)
                        return ins

                    pe.wait_ge(kT_ready, counted(n))
                    project(k_ps, wk).then_inc(k_ready, 1)
                    pe.wait_ge(vb_ready, counted(n))
                    for t in range(2):
                        for h in range(2):
                            ins = nc.tensor.matmul(v_ps[:, t * C:(t + 1) * C], tT[:, u, h, t * P:(t + 1) * P],
                                                   wv[:, h, :], start=h == 0, stop=h == 1)
                    ins.then_inc(v_ready, 1)
                    pe.wait_ge(qT_ready, counted(n))
                    pe.wait_ge(oT_ready, counted(0) if isinstance(n, int) and n < 2 else counted(n - 1))
                    project(q_ps, wq).then_inc(q_ready, 1)

                def rest(n, u, nxt, before):
                    pe.wait_ge(qT_ready, counted(n + 1))
                    pe.wait_ge(kT_ready, counted(n + 1))
                    for t in range(2):
                        pe.wait_ge(probs_ready, counted(n * 2))
                        for h in range(2):
                            ins = nc.tensor.matmul(s_ps[t][:, 0:T + M], qT[:, u, h, t * P:(t + 1) * P], kT[u][:, h, :],
                                                   start=h == 0, stop=h == 1)
                        ins.then_inc(scores_ready, 1)
                    before("values")
                    nxt("turn")
                    before("project")
                    nxt("project")
                    pe.wait_ge(pT_ready, counted(n))
                    pe.wait_ge(y_used, counted(n))
                    for t in range(2):
                        pe.wait_ge(probs_ready, counted(n * 2 + (t + 1)))
                        for j in range(2):
                            nc.tensor.transpose(pT_ps[:, j, t * P:(t + 1) * P], probs[:, t, j * P:(j + 1) * P],
                                                consts["ident"])
                        ins = nc.tensor.transpose(pmT_ps[0:M, t * P:(t + 1) * P], probs[:, t, T:T + M], consts["ident"])
                    ins.then_inc(pT_psum, 1)

                def late(n, u, part):
                    if part == "project":
                        pe.wait_ge(oT_ready, counted(n + 1))
                        for t in range(2):
                            for h in range(2):
                                ins = nc.tensor.matmul(y_ps[:, t * C:(t + 1) * C], oT[:, h, t * P:(t + 1) * P],
                                                       wo[:, h, :], start=h == 0, stop=h == 1)
                        ins.then_inc(y_ready, 1)
                        return
                    pe.wait_ge(pT_ready, counted(n + 1))
                    pe.wait_ge(pmT_ready, counted(n + 1))
                    pe.wait_ge(vb_ready, counted(n + 1))
                    for h in range(2):
                        for j in range(2):
                            nc.tensor.matmul(o_ps[:, h, :], v[:, u, j, h * HC:(h + 1) * HC], pT[:, j, :],
                                             start=j == 0, stop=False)
                        ins = nc.tensor.matmul(o_ps[:, h, :], vm[:, h * HC:(h + 1) * HC], pmT[:, :],
                                               start=False, stop=True)
                    ins.then_inc(o_ready, 1)

                pipelined_late(pe, first, rest, late, (("turn",), ("project",)), (("values",), ("project",)))
        m.clear()


def fourier_phase(nc, x_res, moments, consts, w):
    MODES = HH * (WW // 2 + 1)
    MH = MODES // 2
    LAMBDA = 0.01
    with ExitStack() as ctx:
        m = Mem(nc, ctx, "l1")
        dft = m.sb("dft", [P, 2, 2 * MODES])
        idft = m.sb("idft", [MH, 2, 2, T])
        w1 = m.sb("w1", [HC, 3, 2, HC])
        w2 = m.sb("w2", [HC, 2, 3, HC])
        b1 = m.sb("b1", [HC, 2, 2])
        b2 = m.sb("b2", [MH, 2, 2, HC])
        xs = m.sb("xs", [P, 2, 2, C])
        spec = m.sb("spec", [HC, 2, 2, 2 * MODES])
        o1 = m.sb("o1", [HC, 2, 2 * MODES])
        o2 = m.sb("o2", [MH, 2, 2, 2, HC])
        clip = m.sb("clip", [MH, 2, 2, 2, HC])
        o3 = m.sb("o3", [MH, 2, 2, 2, HC])
        spec_ps = [m.ps(f"spec{h}", [P, 512]) for h in range(2)]
        o1_ps = [m.ps(f"o1_{h}", [P, 512]) for h in range(2)]
        o2_ps = [m.ps(f"o2_{h}", [P, 512]) for h in range(2)]
        y_ps = m.ps("y", [P, 512])

        weights_in = m.sem("weights_in")
        negated = m.sem("negated")
        xs_ready = m.sem("xs_ready")
        spec_psum = m.sem("spec_psum")
        spec_ready = m.sem("spec_ready")
        o1_psum = m.sem("o1_psum")
        o1_ready = m.sem("o1_ready")
        o2_psum = m.sem("o2_psum")
        biased = m.sem("biased")
        clipped = m.sem("clipped")
        o3_ready = m.sem("o3_ready")
        y_ready = m.sem("y_ready")
        y_used = m.sem("y_used")

        with nc.Block() as block:
            @block.sync
            def _(sp):
                for dst, src in ((dft[:, :, :], w["dft"]), (w1[:, 0:2, :, :], w["w1"]), (w2[:, :, 1:3, :], w["w2"]),
                                 (b1[:, :, :], w["b1"]), (b2[:, :, :, :], w["b2"].partition_broadcast(MH)),
                                 (idft[:, :, :, :], w["idft"])):
                    sp.dma_start(dst, src).then_inc(weights_in, 16)

            @block.scalar
            def _(act):
                for s in (xs_ready, spec_ready, o1_ready):
                    act.sem_inc(s, 1)
                act.wait_ge(weights_in, 6 * 16)

                def first(n, u):
                    nc.scalar.copy(xs[:, u, :, :], x_res[:, bass.ds(n * 2, 2), :]).then_inc(xs_ready, 1)
                    for h in range(2):
                        act.wait_ge(spec_psum, counted(n * 2 + (h + 1)))
                        nc.scalar.copy(spec[:, u, h, :], spec_ps[h][0:HC, 0:2 * MODES]).then_inc(spec_ready, 1)

                def rest(n, u, nxt):
                    for h in range(2):
                        act.wait_ge(o1_psum, counted(n * 2 + (h + 1)))
                        for ri in range(2):
                            at = slice(ri * MODES, (ri + 1) * MODES)
                            ins = nc.scalar.activation(o1[:, h, at], o1_ps[h][0:HC, at], ACT.Relu,
                                                       bias=b1[:, h, ri:ri + 1])
                        ins.then_inc(o1_ready, 1)
                    nxt()

                pipelined(act, first, rest)

            @block.gpsimd
            def _(pool):
                pool.sem_inc(o3_ready, 1)
                with pool.Fori(0, B) as n:
                    pool.wait_ge(clipped, counted(n * 2 + 2))
                    pool.wait_ge(y_ready, counted(n))
                    nc.gpsimd.tensor_tensor(o3[:, :, :, :, :], o2[:, :, :, :, :], clip[:, :, :, :, :],
                                            ALU.subtract).then_inc(o3_ready, 1)

            @block.vector
            def _(dve):
                for s in (biased, clipped, y_used):
                    dve.sem_inc(s, 1)
                dve.wait_ge(weights_in, 6 * 16)
                nc.vector.tensor_scalar(w1[:, 2, :, :], w1[:, 1, :, :], -1.0, None, ALU.mult).then_inc(negated, 1)
                nc.vector.tensor_scalar(w2[:, :, 0, :], w2[:, :, 2, :], -1.0, None, ALU.mult).then_inc(negated, 1)

                def late(n, u):
                    dve.wait_ge(y_ready, counted(n + 1))
                    xt = x_res[:, bass.ds(n * 2, 2), :]
                    nc.vector.tensor_tensor(xt, y_ps[:, 0:2 * C].rearrange("p (t c) -> p t c", t=2), xt,
                                            ALU.add).then_inc(y_used, 1)

                def rest(n, u, nxt, before):
                    before()
                    dve.wait_ge(o3_ready, counted(n))
                    for q in range(2):
                        dve.wait_ge(o2_psum, counted(n * 2 + (q + 1)))
                        nc.vector.tensor_tensor(o2[:, q, :, :, :],
                                                o2_ps[q][0:MH, 0:2 * C].rearrange("p (h r c) -> p h r c", h=2, r=2),
                                                b2[:, :, :, :], ALU.add).then_inc(biased, 1)
                        dve.wait_ge(biased, counted(n * 2 + (q + 1)))
                        nc.vector.tensor_scalar(clip[:, q, :, :, :], o2[:, q, :, :, :], LAMBDA, -LAMBDA,
                                                ALU.min, ALU.max).then_inc(clipped, 1)

                pipelined_late(dve, lambda n, u: None, rest, late)

            @block.tensor
            def _(pe):
                for s in (spec_psum, o1_psum, o2_psum, y_ready):
                    pe.sem_inc(s, 1)
                pe.wait_ge(weights_in, 6 * 16)
                pe.wait_ge(negated, 2)

                def first(n, u):
                    pe.wait_ge(xs_ready, counted(n + 1))
                    for h in range(2):
                        pe.wait_ge(spec_ready, counted(n * 2 + (h + 1) - 2) if h else counted(n * 2))
                        for t in range(2):
                            ins = nc.tensor.matmul(spec_ps[h][0:HC, 0:2 * MODES], xs[:, u, t, h * HC:(h + 1) * HC],
                                                   dft[:, t, :], start=t == 0, stop=t == 1)
                        ins.then_inc(spec_psum, 1)

                def rest(n, u, nxt, before):
                    re, im = slice(0, MODES), slice(MODES, 2 * MODES)
                    for h in range(2):
                        pe.wait_ge(spec_ready, counted(n * 2 + (h + 1)))
                        pe.wait_ge(o1_ready, counted(n * 2))
                        o = o1_ps[h][0:HC, :]
                        s = spec[:, u, h, :]
                        nc.tensor.matmul(o[:, 0:2 * MODES], w1[:, 0, h, :], s, start=True, stop=False,
                                         skip_group_check=True)
                        nc.tensor.matmul(o[:, re], w1[:, 2, h, :], s[:, im], start=False, stop=False,
                                         skip_group_check=True)
                        nc.tensor.matmul(o[:, im], w1[:, 1, h, :], s[:, re], start=False, stop=True,
                                         skip_group_check=True).then_inc(o1_psum, 1)
                    before()
                    nxt()
                    pe.wait_ge(o1_ready, counted(n * 2 + 2))
                    for q in range(2):
                        pe.wait_ge(biased, counted(n * 2))
                        for h in range(2):
                            o = o2_ps[q][0:MH, h * C:(h + 1) * C]
                            for ri in range(2):
                                rhs = w2[:, h, 1:3, :] if ri == 0 else w2[:, h, 0:2, :]
                                lhs = o1[:, h, ri * MODES + q * MH:ri * MODES + (q + 1) * MH]
                                ins = nc.tensor.matmul(o, lhs, rhs, start=ri == 0, stop=ri == 1)
                        ins.then_inc(o2_psum, 1)

                def late(n, u):
                    pe.wait_ge(o3_ready, counted(n + 1))
                    pe.wait_ge(y_used, counted(n))
                    for t in range(2):
                        for k in range(4):
                            q, ri = k // 2, k % 2
                            ins = nc.tensor.matmul(y_ps[:, t * C:(t + 1) * C], idft[:, q, ri, t * P:(t + 1) * P],
                                                   o3[:, q, :, ri, :], start=k == 0, stop=k == 3)
                    ins.then_inc(y_ready, 1)

                pipelined_late(pe, first, rest, late)
        m.clear()


def mamba_phase(nc, x_res, moments, consts, w):
    R, DI, NS, DC, DTR = 48, 96, 16, 4, 12
    CH = 512
    CHUNKS = TOK // CH
    CT = CH // P
    ATANH = [2.0 / (2 * k + 1) for k in range(8)]
    DG = P // NS
    G = DI // DG
    with ExitStack() as ctx:
        m = Mem(nc, ctx, "l0")
        down = m.sb("down", [HC, 2, R])
        inp = m.sb("inp", [R, 2 * DI])
        convw = m.sb("convw", [DI, DC])
        cols = m.sb("cols", [DI, 3])
        xdt = m.sb("xdt", [DI, DTR])
        xb = m.sb("xb", [DI, 2, DG, NS])
        dtw = m.sb("dtw", [DTR, DI])
        a_col = m.sb("a_col", [P, G])
        sel = m.sb("sel", [DI, G, P])
        selT = m.sb("selT", [P, G, DI])
        outp = m.sb("outp", [DI, R])
        up = m.sb("up", [R, C])
        ln_g = m.sb("ln_g", [P, R])
        ln_b = m.sb("ln_b", [P, R])
        keep = m.sb("keep", [P, CHUNKS])
        xT = m.sb("xT", [HC, 2, 2, CH])
        xsT = m.sb("xsT", [R, CH])
        xi = m.sb("xi", [DI, 2, DC - 1 + CH])
        conv = m.sb("conv", [DI, 2, CH])
        u_sb = m.sb("u", [DI, 2, CH])
        zs = m.sb("zs", [DI, 2, CH])
        dt_sb = m.sb("dt", [DTR, CH])
        bc = m.sb("bc", [P, 2, 2, CH])
        sp_a = m.sb("sp_a", [DI, 6, CH])
        delta = m.sb("delta", [DI, 2, CH])
        du = m.sb("du", [DI, 2, CH])
        sel_r = m.sb("sel_r", [DI, G, P], F32R)
        delta_r = m.sb("delta_r", [DI, 2, 2, CH], F32R)
        du_r = m.sb("du_r", [DI, 2, 2, CH], F32R)
        dA = m.sb("dA", [P, 2, CH])
        dBu = m.sb("dBu", [P, 2, CH])
        hs = m.sb("hs", [P, 2, CH])
        hc = m.sb("hc", [P, 2, CH])
        state = m.sb("state", [P, 1, G])
        yy = m.sb("yy", [DI, 2, CH])
        mm = m.sb("mm", [P, 2, CT, R])
        mg = m.sb("mg", [P, CT, R])
        mT = m.sb("mT", [R, CH])
        bns = m.sb("bns", [P, CT, 6])
        mom = m.sb("mom", [P, CT, 2])
        sm = m.sb("sm", [P, 6, CT])
        one = m.sb("one", [P, 1])
        drep_ps = [m.ps(f"drep{k}", [P, CH]) for k in range(2)]
        urep_ps = [m.ps(f"urep{k}", [P, CH]) for k in range(2)]
        y_ps = m.ps("y", [DI, CH])
        g_ps = [m.ps(f"g{k}", [P, CH]) for k in range(2)]
        t_ps = m.ps("t", [P, CH])

        weights_in = m.sem("weights_in")
        setup = m.sem("setup")
        sel_ready = m.sem("sel_ready")
        xT_in = m.sem("xT_in")
        front_ps = m.sem("front_ps")
        front_sb = m.sem("front_sb")
        act_front = m.sem("act_front")
        conv_ready = m.sem("conv_ready")
        silu_ready = m.sem("silu_ready")
        ea_ready = m.sem("ea_ready")
        soft_ready = m.sem("soft_ready")
        delta_ready = m.sem("delta_ready")
        du_ready = m.sem("du_ready")
        delta_high = m.sem("delta_high")
        du_high = m.sem("du_high")
        delta_split = m.sem("delta_split")
        du_split = m.sem("du_split")
        drep_ready = m.sem("drep_ready")
        urep_ready = m.sem("urep_ready")
        dA_ready = m.sem("dA_ready")
        dBu_ready = m.sem("dBu_ready")
        scan_ready = m.sem("scan_ready")
        state_ready = m.sem("state_ready")
        hc_ready = m.sem("hc_ready")
        hc_used = m.sem("hc_used")
        y_gated = m.sem("y_gated")
        m_ready = m.sem("m_ready")
        var_ready = m.sem("var_ready")
        guess_ready = m.sem("guess_ready")
        ln_ready = m.sem("ln_ready")
        gelu_ready = m.sem("gelu_ready")
        mT_ps = m.sem("mT_ps")
        mT_ready = m.sem("mT_ready")
        up_ready = m.sem("up_ready")
        x_added = m.sem("x_added")
        conv_chain = m.sem("conv_chain")
        log_chain = m.sem("log_chain")
        state_chain = m.sem("state_chain")
        norm_chain = m.sem("norm_chain")
        tail_chain = m.sem("tail_chain")
        act_chain = m.sem("act_chain")
        act_held = m.sem("act_held")
        dve_held = m.sem("dve_held")
        pe_held = m.sem("pe_held")
        sp_held = m.sem("sp_held")

        loads = ((down[:, :, :], w["down"]), (inp[:, :], w["inp"]), (convw[:, :], w["convw"]), (cols[:, :], w["cols"]),
                 (xdt[:, :], w["xdt"]), (xb[:, :, :, :], w["xb"]), (dtw[:, :], w["dtw"]), (a_col[:, :], w["alog"]),
                 (sel[:, :, :], w["sel"]), (selT[:, :, :], w["selT"]), (outp[:, :], w["outp"]), (up[:, :], w["up"]),
                 (ln_g[:, :], w["lng"].partition_broadcast(P)), (ln_b[:, :], w["lnb"].partition_broadcast(P)),
                 (keep[:, :], w["keep"].partition_broadcast(P)))

        def chunks(eng, groups, front, tail, stages):
            def chunk(n, u, first=False, last=False):
                for g in range(-1, G):
                    if g >= 0:
                        groups(n, u, g)
                    for part in stages.get(g, ()):
                        if part[0] == "front" and not last:
                            front(n + 1, 1 - u, *part[1:])
                        if part[0] == "tail" and not first:
                            tail(n - 1, 1 - u, *part[1:])

            for g in range(-1, G):
                for part in stages.get(g, ()):
                    if part[0] == "front":
                        front(0, 0, *part[1:])
            chunk(0, 0, first=True)
            with eng.Fori(0, CHUNKS // 2 - 1) as it:
                chunk(it * 2 + 1, 1)
                chunk(it * 2 + 2, 0)
            chunk(CHUNKS - 1, 1, last=True)
            for g in range(-1, G):
                for part in stages.get(g, ()):
                    if part[0] == "tail":
                        tail(CHUNKS - 1, 1, *part[1:])

        with nc.Block() as block:
            @block.sync
            def _(sp):
                for dst, src in loads:
                    sp.dma_start(dst, src).then_inc(weights_in, 16)

                def load(n, u):
                    sp.dma_start(xT[:, u, :, :], w["xT"][:, :, bass.ds(n * CH, CH)]).then_inc(xT_in, 16)

                load(0, 0)
                sp.wait_ge(xT_in, 16)
                load(1, 1)
                sp.wait_ge(xT_in, 32)
                consts["load_x"](sp)
                with sp.Fori(0, CHUNKS // 2 - 1) as it:
                    for u in range(2):
                        sp.wait_ge(front_ps, counted(it * 14 + (7 * u + 1)))
                        hold(sp, sp_held)
                        load(it * 2 + (2 + u), u)
                        sp.wait_ge(xT_in, it * 32 + (48 + 16 * u))
                        hold(sp, sp_held)

            @block.scalar
            def _(act):
                act.wait_ge(weights_in, len(loads) * 16)
                nc.scalar.activation(a_col[:, :], a_col[:, :], ACT.Exp).then_inc(setup, 1)
                for s in (delta_high, du_high, act_front, silu_ready, ea_ready, soft_ready, dA_ready, guess_ready,
                          gelu_ready, mT_ready,
                          state_ready):
                    act.sem_inc(s, 1)
                act.wait_ge(setup, 4)
                hold(act, act_held)

                def front(n, u, part):
                    def bank(k):
                        act.wait_ge(front_ps, counted(n * 7 + (k + 1)))
                        return g_ps[k % 2]
                    if part == "xs":
                        nc.scalar.copy(xsT[:, :], bank(0)[0:R, :]).then_inc(act_front, 1)
                    if part == "xi":
                        nc.scalar.copy(xi[:, u, DC - 1:], bank(1)[0:DI, :]).then_inc(act_front, 1)
                    if part == "z":
                        if not (isinstance(n, int) and n < 2):
                            act.wait_ge(y_gated, counted(n - 1))
                            hold(act, act_held)
                        nc.scalar.activation(zs[:, u, :], bank(2)[0:DI, :], ACT.Silu).then_inc(act_front, 1)
                    if part == "u":
                        act.wait_ge(conv_ready, counted(n + 1))
                        nc.scalar.activation(u_sb[:, u, :], conv[:, 1, :], ACT.Silu).then_inc(silu_ready, 1)
                    if part == "dt":
                        nc.scalar.copy(dt_sb[:, :], bank(3)[0:DTR, :]).then_inc(act_front, 1)
                    if part in ("B", "C"):
                        k = "BC".index(part)
                        nc.scalar.copy(bc[:, u, k, :], bank(4 + k)[:, :]).then_inc(act_front, 1)
                    if part == "soft":
                        chain = Chain(act, act_chain, 2, n)
                        nc.scalar.activation(sp_a[:, 0, :], bank(6)[0:DI, :], ACT.Identity,
                                             bias=cols[:, 1:2]).then_inc(act_front, 1)
                        act.wait_ge(act_front, counted(n * 7 + 7))
                        chain.link(nc.scalar.activation(sp_a[:, 1, :], sp_a[:, 0, :], ACT.Abs))
                        chain.link(nc.scalar.activation(sp_a[:, 2, :], sp_a[:, 1, :], ACT.Exp, scale=-1.0))
                        act.sem_inc(soft_ready, 1)
                        chain.close()

                    if part == "delta":
                        act.wait_ge(delta_ready, counted(n + 1))
                        nc.scalar.copy(delta_r[:, u, 0, :], delta[:, u, :]).then_inc(delta_high, 1)
                    if part == "du":
                        act.wait_ge(du_ready, counted(n + 1))
                        nc.scalar.copy(du_r[:, u, 0, :], du[:, u, :]).then_inc(du_high, 1)

                def groups(n, u, g):
                    k = n * G + g
                    act.wait_ge(drep_ready, counted(k + 1))
                    act.wait_ge(scan_ready, counted(k - 1) if g else counted(k))
                    nc.scalar.activation(dA[:, g % 2, :], drep_ps[g % 2][:, :], ACT.Exp,
                                         scale=a_col[:, g:g + 1]).then_inc(dA_ready, 1)

                def tail(n, u, part):
                    if part == "guess":
                        act.wait_ge(var_ready, counted(n + 1))
                        nc.scalar.activation(sm[:, 0, :], mom[:, :, 1], ACT.Ln, bias=consts["eps"]).then_inc(ea_ready, 1)
                        act.wait_ge(ea_ready, counted(n + 1))
                        nc.scalar.activation(sm[:, 1, :], sm[:, 0, :], ACT.Exp, scale=-0.5).then_inc(guess_ready, 1)
                    if part == "gelu":
                        act.wait_ge(ln_ready, counted(n + 1))
                        nc.scalar.activation(mg[:, :, :], mm[:, 0, :, :], ACT.Gelu).then_inc(gelu_ready, 1)
                    if part == "turned":
                        act.wait_ge(mT_ps, counted(n + 1))
                        nc.scalar.copy(mT[:, :], t_ps[0:R, :]).then_inc(mT_ready, 1)

                chunks(act, groups, front, tail,
                       {0: [("front", "xs")],
                        1: [("front", "xi")],
                        2: [("front", "z"), ("tail", "guess")],
                        3: [("front", "u")],
                        4: [("front", "dt"), ("front", "B"), ("tail", "gelu")],
                        5: [("front", "C")],
                        6: [("front", "soft"), ("tail", "turned")],
                        9: [("front", "delta")],
                        10: [("front", "du")]})

            @block.gpsimd
            def _(pool):
                pool.sem_inc(hc_ready, 1)
                for s in (du_ready, delta_split, du_split):
                    pool.sem_inc(s, 1)

                def front(n, u, part):
                    if part == "du":
                        pool.wait_ge(delta_ready, counted(n + 1))
                        nc.gpsimd.tensor_tensor(du[:, u, :], delta[:, u, :], u_sb[:, u, :],
                                                ALU.mult).then_inc(du_ready, 1)
                    if part == "low":
                        for high, whole, parts, split in ((delta_high, delta, delta_r, delta_split),
                                                          (du_high, du, du_r, du_split)):
                            pool.wait_ge(high, counted(n + 1))
                            nc.gpsimd.tensor_tensor(parts[:, u, 1, :], whole[:, u, :], parts[:, u, 0, :].bitcast(F32),
                                                    ALU.subtract).then_inc(split, 1)

                def groups(n, u, g):
                    k = n * G + g
                    pool.wait_ge(scan_ready, counted(k + 1))
                    pool.wait_ge(hc_used, counted(k - 1) if g else counted(k))
                    nc.gpsimd.tensor_tensor(hc[:, g % 2, :], hs[:, g % 2, :], bc[:, u, 1, :],
                                            ALU.mult).then_inc(hc_ready, 1)

                chunks(pool, groups, front, None, {9: [("front", "du")], 10: [("front", "low")]})

            @block.vector
            def _(dve):
                for s in (front_sb, conv_ready, delta_ready, dBu_ready, scan_ready, y_gated, var_ready, ln_ready,
                          x_added):
                    dve.sem_inc(s, 1)
                dve.wait_ge(setup, 1)
                nc.vector.tensor_scalar(a_col[:, :], a_col[:, :], -1.0, None, ALU.mult).then_inc(setup, 1)
                nc.vector.memset(xi[:, :, :], 0.0).then_inc(setup, 1)
                nc.vector.tensor_copy(sel_r[:, :, :], sel[:, :, :]).then_inc(sel_ready, 1)
                nc.vector.memset(one[:, :], 1.0)
                nc.vector.memset(state[:, :, :], 0.0).then_inc(setup, 1)
                dve.wait_ge(setup, 4)

                def front(n, u, part):
                    if part == "conv":
                        chain = Chain(dve, conv_chain, 1 + DC, n)
                        chain.link(nc.vector.tensor_scalar(xi[:, u, 0:DC - 1], xi[:, 1 - u, CH:CH + DC - 1],
                                                           keep[0:DI, bass.ds(n, 1)], None, ALU.mult))
                        dve.wait_ge(act_front, counted(n * 7 + 2))
                        chain.link(nc.vector.tensor_scalar(conv[:, 0, :], xi[:, u, 0:CH], convw[:, 0:1], cols[:, 0:1],
                                                           ALU.mult, ALU.add))
                        for k in range(1, DC):
                            chain.link(nc.vector.scalar_tensor_tensor(
                                out=conv[:, k % 2, :], in0=xi[:, u, k:k + CH], scalar=convw[:, k:k + 1],
                                in1=conv[:, (k + 1) % 2, :], op0=ALU.mult, op1=ALU.add))
                        dve.sem_inc(conv_ready, 1)
                        chain.close()
                        return
                    v, a, wexp, s, q, acc = (sp_a[:, k, :] for k in range(6))
                    if part == "ratio":
                        dve.wait_ge(soft_ready, counted(n + 1))
                        front.log = Chain(dve, log_chain, 4 + len(ATANH), n)
                        link = front.log.link
                        link(nc.vector.tensor_scalar(a, wexp, 2.0, None, ALU.add))
                        link(nc.vector.reciprocal(s, a))
                        link(nc.vector.tensor_tensor(s, s, wexp, ALU.mult))
                    if part == "series":
                        link = front.log.link
                        link(nc.vector.tensor_tensor(q, s, s, ALU.mult))
                        link(nc.vector.tensor_scalar(acc, q, ATANH[-1], None, ALU.mult))
                        for c in ATANH[-2:3:-1]:
                            link(nc.vector.scalar_tensor_tensor(out=acc, in0=acc, scalar=c, in1=q, op0=ALU.add,
                                                                op1=ALU.mult))
                    if part == "delta":
                        link = front.log.link
                        for c in ATANH[3:0:-1]:
                            link(nc.vector.scalar_tensor_tensor(out=acc, in0=acc, scalar=c, in1=q, op0=ALU.add,
                                                                op1=ALU.mult))
                        link(nc.vector.scalar_tensor_tensor(out=acc, in0=acc, scalar=ATANH[0], in1=s, op0=ALU.add,
                                                            op1=ALU.mult))
                        nc.vector.scalar_tensor_tensor(out=delta[:, u, :], in0=v, scalar=0.0,
                                                       in1=acc, op0=ALU.max, op1=ALU.add).then_inc(delta_ready, 1)
                        front.log.close()

                def groups(n, u, g):
                    k = n * G + g
                    dve.wait_ge(urep_ready, counted(k + 1))
                    nc.vector.tensor_tensor(dBu[:, g % 2, :], urep_ps[g % 2][:, :], bc[:, u, 0, :],
                                            ALU.mult).then_inc(dBu_ready, 1)
                    nc.vector.tensor_scalar(state[:, 0, g:g + 1], state[:, 0, g:g + 1],
                                            keep[:, bass.ds(n, 1)], None, ALU.mult).then_inc(state_chain, 1)
                    dve.wait_ge(state_chain, k + 1)
                    dve.wait_ge(dBu_ready, counted(k + 1))
                    dve.wait_ge(dA_ready, counted(k + 1))
                    dve.wait_ge(hc_ready, counted(k - 1) if g else counted(k))
                    nc.vector.tensor_tensor_scan(hs[:, g % 2, :], dA[:, g % 2, :], dBu[:, g % 2, :],
                                                 state[:, 0, g:g + 1], ALU.mult, ALU.add).then_inc(scan_ready, 1)
                    dve.wait_ge(scan_ready, counted(k + 1))
                    nc.vector.tensor_copy(state[:, 0, g:g + 1], hs[:, g % 2, CH - 1:CH]).then_inc(state_ready, 1)
                    dve.wait_ge(state_ready, counted(k + 1))

                def tail(n, u, part):
                    m_ps = t_ps[:, 0:CT * R].rearrange("p (t r) -> p t r", t=CT)
                    if part == "gate":
                        dve.wait_ge(hc_used, counted(n * G + G))
                        chain = Chain(dve, tail_chain, 2 + 2 * CT, n)
                        chain.link(nc.vector.scalar_tensor_tensor(out=yy[:, 0, :], in0=u_sb[:, u, :],
                                                                  scalar=cols[:, 2:3], in1=y_ps[:, :],
                                                                  op0=ALU.mult, op1=ALU.add))
                        nc.vector.tensor_tensor(yy[:, 1, :], yy[:, 0, :], zs[:, u, :], ALU.mult).then_inc(y_gated, 1)
                        tail.chain = chain
                    if part == "moments":
                        chain = tail.chain
                        dve.wait_ge(m_ready, counted(n + 1))
                        for t in range(CT):
                            hold(dve, dve_held)
                            chain.send(nc.vector.bn_stats(bns[:, t, :], m_ps[:, t, :]))
                        dve.wait_ge(tail_chain, n * (2 + 2 * CT) + chain.n)
                        for t in range(CT):
                            hold(dve, dve_held)
                            chain.send(nc.vector.bn_aggr(mom[:, t, :], bns[:, t, :]))
                        dve.wait_ge(tail_chain, n * (2 + 2 * CT) + chain.n)
                        dve.sem_inc(var_ready, 1)
                        chain.link(nc.vector.tensor_tensor(mm[:, 0, :, :], m_ps,
                                                           mom[:, :, 0:1].broadcast_to([P, CT, R]), ALU.subtract))
                        chain.close()
                    if part == "norm":
                        chain = Chain(dve, norm_chain, 6, n)
                        dve.wait_ge(guess_ready, counted(n + 1))
                        y = sm[:, 1, :]
                        chain.link(nc.vector.tensor_tensor(sm[:, 2, :], y, y, ALU.mult))
                        chain.link(nc.vector.scalar_tensor_tensor(out=sm[:, 3, :], in0=mom[:, :, 1], scalar=EPS,
                                                                  in1=sm[:, 2, :], op0=ALU.add, op1=ALU.mult))
                        chain.link(nc.vector.tensor_scalar(sm[:, 4, :], sm[:, 3, :], -0.5, 1.5, ALU.mult, ALU.add))
                        chain.link(nc.vector.tensor_tensor(sm[:, 5, :], sm[:, 4, :], y, ALU.mult))
                        chain.link(nc.vector.tensor_tensor(mm[:, 1, :, :], mm[:, 0, :, :],
                                                           sm[:, 5, :].unsqueeze(2).broadcast_to([P, CT, R]), ALU.mult))
                        chain.link(nc.vector.tensor_tensor(mm[:, 1, :, :], mm[:, 1, :, :],
                                                           ln_g[:, :].unsqueeze(1).broadcast_to([P, CT, R]), ALU.mult))
                        nc.vector.tensor_tensor(mm[:, 0, :, :], mm[:, 1, :, :],
                                                ln_b[:, :].unsqueeze(1).broadcast_to([P, CT, R]),
                                                ALU.add).then_inc(ln_ready, 1)
                        chain.close()
                    if part in (0, 1):
                        dve.wait_ge(consts["x_in"], 16)
                        dve.wait_ge(up_ready, counted(n * 2 + (part + 1)))
                        xt = x_res[:, bass.ds(n * CT + 2 * part, 2), :]
                        nc.vector.tensor_tensor(xt, t_ps[:, 0:2 * C].rearrange("p (t c) -> p t c", t=2), xt,
                                                ALU.add).then_inc(x_added, 1)

                chunks(dve, groups, front, tail,
                       {-1: [("tail", "gate")],
                        0: [("tail", "moments")],
                        2: [("front", "conv")],
                        3: [("tail", "norm")],
                        6: [("front", "ratio")],
                        7: [("front", "series"), ("tail", 0)],
                        8: [("front", "delta"), ("tail", 1)]})

            @block.tensor
            def _(pe):
                for s in (front_ps, drep_ready, urep_ready, hc_used, m_ready, mT_ps, up_ready):
                    pe.sem_inc(s, 1)
                pe.wait_ge(weights_in, len(loads) * 16)
                pe.wait_ge(sel_ready, 1)

                def front(n, u, part):
                    k = ("xs", "xi", "z", "dt", "B", "C", "delta").index(part)
                    o = g_ps[k % 2]
                    if part == "xs":
                        pe.wait_ge(xT_in, n * 16 + 16)
                    if part == "dt":
                        pe.wait_ge(silu_ready, counted(n + 1))
                    pe.wait_ge(act_front, counted(n * 7 + (1 if k == 1 else max(k - 1, 0))))
                    if part == "xs":
                        for h in range(2):
                            ins = nc.tensor.matmul(o[0:R, :], down[:, h, :], xT[:, u, h, :], start=h == 0, stop=h == 1)
                    elif part in ("xi", "z"):
                        ins = nc.tensor.matmul(o[0:DI, :], inp[:, (k - 1) * DI:k * DI], xsT[:, :], start=True, stop=True)
                    elif part == "dt":
                        ins = nc.tensor.matmul(o[0:DTR, :], xdt[:, :], u_sb[:, u, :], start=True, stop=True)
                    elif part in ("B", "C"):
                        ins = nc.tensor.matmul(o[:, :], xb[:, k - 4, :, :], u_sb[:, u, :], start=True, stop=True)
                    else:
                        ins = nc.tensor.matmul(o[0:DI, :], dtw[:, :], dt_sb[:, :], start=True, stop=True)
                    ins.then_inc(front_ps, 1)

                def add_states(n, u, g):
                    pe.wait_ge(hc_ready, counted(n * G + (g + 1)))
                    nc.tensor.matmul(y_ps[:, :], selT[:, g, :], hc[:, g % 2, :], start=g == 0,
                                     stop=g == G - 1).then_inc(hc_used, 1)

                def groups(n, u, g):
                    k = n * G + g
                    if g == 0:
                        pe.wait_ge(delta_split, counted(n + 1))
                    pe.wait_ge(dA_ready, counted(k - 1) if g else counted(k))
                    for part in range(2):
                        ins = nc.tensor.matmul(drep_ps[g % 2][:, :], sel_r[:, g, :], delta_r[:, u, part, :],
                                               start=part == 0, stop=part == 1)
                    ins.then_inc(drep_ready, 1)
                    if g == 0:
                        pe.wait_ge(du_split, counted(n + 1))
                    pe.wait_ge(dBu_ready, counted(k - 1) if g else counted(k))
                    for part in range(2):
                        ins = nc.tensor.matmul(urep_ps[g % 2][:, :], sel_r[:, g, :], du_r[:, u, part, :],
                                               start=part == 0, stop=part == 1)
                    ins.then_inc(urep_ready, 1)
                    if g == 1:
                        pe.wait_ge(y_gated, counted(n))
                    if g:
                        add_states(n, u, g - 1)
                    if g == G - 1:
                        add_states(n, u, g)

                def tail(n, u, part):
                    if part == "m":
                        pe.wait_ge(y_gated, counted(n + 1))
                        pe.wait_ge(x_added, counted(n * 2))
                        for t in range(CT):
                            ins = nc.tensor.matmul(t_ps[:, t * R:(t + 1) * R], yy[:, 1, t * P:(t + 1) * P], outp[:, :],
                                                   start=True, stop=True)
                        ins.then_inc(m_ready, 1)
                    if part == "turn":
                        pe.wait_ge(gelu_ready, counted(n + 1))
                        hold(pe, pe_held)
                        for t in range(CT):
                            ins = nc.tensor.transpose(t_ps[0:R, t * P:(t + 1) * P], mg[:, t, :], consts["ident"])
                        ins.then_inc(mT_ps, 1)
                    if part in (0, 1):
                        pe.wait_ge(mT_ready, counted(n + 1))
                        pe.wait_ge(x_added, counted(n * 2 + part))
                        for t in range(2):
                            at = 2 * part + t
                            ins = nc.tensor.matmul(t_ps[:, t * C:(t + 1) * C], mT[:, at * P:(at + 1) * P], up[:, :],
                                                   start=True, stop=True)
                        ins.then_inc(up_ready, 1)

                chunks(pe, groups, front, tail,
                       {0: [("front", "xs"), ("tail", "m")],
                        1: [("front", "xi"), ("front", "z")],
                        4: [("front", "dt"), ("front", "B")],
                        5: [("front", "C"), ("front", "delta"), ("tail", "turn")],
                        7: [("tail", 0)],
                        8: [("tail", 1)]})
        m.clear()


HEADS, HS, SLOTS = 12, 16, 8
FEAT = 2 * HS + 2
EXT = 12
PAIRS = HEADS // 2
STEPS = 2 * PAIRS
BIG, HUGE = 1.0e38, 3.4e38


def wrapped(ap, shift, depth):
    dims = [list(x) for x in ap.ap]
    step = dims[-1][0]
    return bass.AP(tensor=ap.tensor, offset=ap.offset + shift * step, ap=dims[:-1] + [[step, depth], [step, 8]])


def dpp_attention_phase(nc, x_res, moments, consts, w):
    RD = 4
    GRAMS = (RD - 1) * SLOTS + SLOTS // 2
    NCOMB = (1 + RD) * SLOTS
    with ExitStack() as ctx:
        m = Mem(nc, ctx, "l2a")
        wqk = m.sb("wqk", [HC, 2, 8, HC])
        wtok = m.sb("wtok", [HC, 2, 3 * C])
        bqk = m.sb("bqk", [HC, 8])
        btok = m.sb("btok", [1, 3 * C])
        wp = m.sb("wp", [HC, 2, C])
        bp = m.sb("bp", [P, C])
        thr = m.sb("thr", [P, 2 * P])
        ident_bf = m.sb("ident_bf", [P, P], BF16)
        mask_bf = m.sb("mask_bf", [P, P], BF16)
        tri_bf = m.sb("tri_bf", [P, P], BF16)
        ones_bf = m.sb("ones_bf", [P, P], BF16)
        ones_row = m.sb("ones_row", [1, P])
        weight_of = m.sb("weight_of", [P, 2, NCOMB])
        rstd = m.sb("rstd", [P, TILES])
        shift = m.sb("shift", [P, TILES])
        xn = m.sb("xn", [P, 2, C])
        tT = m.sb("tT", [HC, 2, T])
        qkT = m.sb("qkT", [HC, 2, 8, T])
        q_tok = m.sb("q_tok", [P, 2, 2, 2, C])
        feat = m.sb("feat", [P, 2, 2, HEADS, FEAT])
        rest_buf = m.sb("rest_f", [P, 2 * HEADS * FEAT])
        rest_f = rest_buf[:, :].rearrange("p (t h f) -> p t h f", t=2, h=HEADS)
        feat3 = m.sb("feat3", [P, 2, 2, 3, HEADS, FEAT], BF16)
        square = rest_buf[:, 0:4 * HEADS * HS].rearrange("p (k t h d) -> p k t h d", k=2, t=2, h=HEADS)
        own = m.sb("own", [P, 2, 2, HEADS])
        top8 = m.sb("top8", [P, 2, 2, 8])
        marked = m.sb("marked", [P, 2, 2 * P])
        chosen = m.sb("chosen", [P, 2, 2, 2 * P], BF16)
        chosenT = m.sb("chosenT", [P, 2, 2, 2, P], BF16)
        code = m.sb("code", [P, 2, 2, 2, P], BF16)
        onehot = m.sb("onehot", [P, SLOTS, 2, 2, P], BF16)
        keys = m.sb("keys", [P, 2, HEADS, EXT, HS])
        values = m.sb("values", [P, 2, HEADS, SLOTS, HS])
        facts = m.sb("facts", [P, 2, HEADS, EXT, 2])
        prod = m.sb("prod", [P, 2, 2, GRAMS + 2 * SLOTS, HS])
        dots = m.sb("dots", [P, 2, HEADS, RD * SLOTS + 2 * EXT])
        sv = m.sb("sv", [P, 3, HEADS, EXT])
        det = m.sb("det", [P, HEADS, 1 + RD, SLOTS])
        sc = m.sb("sc", [P, HEADS, 1 + RD, SLOTS])
        veto = m.sb("veto", [P, HEADS, 1 + RD, SLOTS])
        mx = m.sb("mx", [P, HEADS, 1 + RD, SLOTS])
        ex = m.sb("ex", [P, 3, HEADS, 1 + RD, SLOTS])
        shared = m.sb("shared", [P, HEADS * SLOTS * HS])
        pw = shared[:, 0:3 * HEADS * RD * SLOTS].rearrange("p (k h d a) -> p k h d a", k=3, h=HEADS, d=RD)
        z = shared[:, 0:3 * HEADS * NCOMB].rearrange("p (k h d a) -> p k h d a", k=3, h=HEADS, d=1 + RD)
        pv = shared[:, :].rearrange("p (h a d) -> p h a d", h=HEADS, a=SLOTS)
        guess = shared[:, 0:4 * TILES].rearrange("p (k t) -> p k t", k=4)
        stats = shared[:, 4 * TILES:10 * TILES].rearrange("p (t k) -> p t k", t=TILES)
        hd = m.sb("hd", [P, 6, HEADS])
        alpha = m.sb("alpha", [P, HEADS, SLOTS])
        spread = m.sb("spread", [P, HEADS, EXT])
        kept = m.sb("kept", [P, 2, C])
        y = m.sb("y", [P, 2, C])
        yT = m.sb("yT", [HC, 2, P])

        s_ps = [m.ps(f"s{k}", [P, 512]) for k in range(2)]
        mt_ps = m.ps("mt", [P, 2, 2, P])
        code_psum = m.ps("code_psum", [P, 2, 2, P])
        g_ps = [m.ps(f"g{k}", [P, 512]) for k in range(2)]
        a_ps = [m.ps(f"a{k}", [P, 512]) for k in range(2)]

        names = """weights_in stats_ready moments_ready half_log dve_chain0 rstd_ready const_ready xn_ready a_psum a_sb
            rest_ready mid_ready split_ready square_ready own_ready scores_ready marked_ready chosen_ready
            chosenT_psum chosenT_ready code_in_psum code_ready onehot_ready gathered kv_ready prod_ready products
            dots_ready det_ready log_ready shifted probs_ready diff_ready exp_ready denom_ready inv_ready
            alpha_ready pv_ready kept_ready y_ready yT_psum yT_ready proj_ready x_added act_chain max_chain
            det_chain diff_chain log_chain inv_chain alpha_chain y_chain dve_held act_held pe_held pool_held""".split()
        S = {name: m.sem(name) for name in names}
        loads = ((wqk[:, :, :, :], w["wqk"]), (wtok[:, :, :], w["wtok"]), (bqk[:, :], w["bqk"]),
                 (btok[:, :], w["btok"].unsqueeze(0)), (wp[:, :, :], w["wp"]),
                 (bp[:, :], w["bp"].partition_broadcast(P)), (y[:, 0, 0:P], w["mask"]), (thr[:, :], w["thr"]),
                 (y[:, 1, 0:P], w["tri"]), (weight_of[:, :, :], w["comb"].partition_broadcast(P)))
        LOADED = len(loads) * 16

        def first_head(i):
            return 6 * (i % PAIRS // 3) + i % 3

        def keys_of(t):
            return (t + 1) * P

        def steps(eng, body):
            def image(n, u, first=False, last=False):
                for i in range(STEPS):
                    def back(lag, i=i):
                        if i >= lag:
                            return n, u, i - lag
                        return None if first else (n - 1, 1 - u, i - lag + STEPS)
                    body(n, u, i, back, last)
            image(0, 0, first=True)
            with eng.Fori(0, B // 2 - 1) as it:
                image(it * 2 + 1, 1)
                image(it * 2 + 2, 0)
            image(B - 1, 1, last=True)
            for i in range(STEPS, 2 * STEPS + 1):
                def back(lag, i=i):
                    return (B - 1, 1, i - lag) if 0 <= i - lag < STEPS else None
                body(B, 0, i - STEPS, back, True)

        DET, DIFF, LOG, INV, ALPHA, VALUE, OUT = range(7)
        FRONT, SQUARE, OWN, SPLIT = 5, 9, 10, 11

        def stage(back, k):
            s = back(4 + k)
            return (s[0], s[1], s[2] // PAIRS) if s and s[2] % PAIRS == PAIRS - 1 else None

        def next_image(n, u, last):
            return None if last or (isinstance(n, int) and n == B) else (n + 1, 1 - u)

        H = HEADS
        det2, cross2 = sv[:, 0, :, :], sv[:, 1, :, :]
        flat = lambda x: x.rearrange("p h d a -> p (h d a)")
        per_head = lambda x, k: x.rearrange("p h d a -> p h (d a)")
        over = lambda x, k: x.unsqueeze(2).broadcast_to([P, H, k])
        A = lambda x: x[:, :, 0:SLOTS].unsqueeze(2).broadcast_to([P, H, RD, SLOTS])
        Bx = lambda x: wrapped(x, 1, RD)
        zf = lambda k: flat(z[:, k, :, :, :])
        ef = lambda k: flat(ex[:, k, :, :, :])
        scp = per_head(sc[:, :, :, :], 0)

        def count_of(step):
            n, u, i = step
            return n * STEPS + i

        with nc.Block() as block:
            @block.sync
            def _(sp):
                for dst, src in loads:
                    sp.dma_start(dst, src).then_inc(S["weights_in"], 16)

            @block.scalar
            def _(act):
                for name in ("xn_ready a_sb mid_ready chosenT_ready code_ready kv_ready log_ready "
                             "probs_ready exp_ready inv_ready yT_ready").split():
                    act.sem_inc(S[name], 1)
                rstd_steps_act(nc, act, S["moments_ready"], S["half_log"], moments, guess, consts["eps"])
                act.wait_ge(S["weights_in"], LOADED)
                act.wait_ge(S["const_ready"], 1)
                act.wait_ge(S["rstd_ready"], 1)
                hold(act, S["act_held"])

                def front(n, u, k):
                    if k == 0:
                        normalise(nc, xn[:, :, :], x_res, rstd, shift, n * 2).then_inc(S["xn_ready"], 1)
                    if k == 1 and not (isinstance(n, int) and n == 0):
                        act.wait_ge(S["prod_ready"], counted(n * STEPS - STEPS))
                    if k == 5 and not (isinstance(n, int) and n == 0):
                        act.wait_ge(S["diff_ready"], counted(n * 2 - 2))
                        act.wait_ge(S["kept_ready"], counted(n * 2 - 2))
                        hold(act, S["act_held"])
                    act.wait_ge(S["a_psum"], counted(n * 8 + (k + 1)))
                    b = a_ps[k % 2]
                    if k == 0:
                        ins = nc.scalar.copy(tT[:, :, :], b[0:HC, :].rearrange("p (h t) -> p h t", h=2))
                    elif k <= 4:
                        for j in range(2):
                            c = 2 * (k - 1) + j
                            ins = nc.scalar.activation(qkT[:, u, c, :], b[0:HC, j * T:(j + 1) * T],
                                                       ACT.Identity, bias=bqk[:, c:c + 1])
                    elif k == 6:
                        for tt in range(2):
                            ins = nc.scalar.copy(feat[:, u, tt, :, HS:2 * HS],
                                                 b[:, tt * C:(tt + 1) * C].rearrange("p (h d) -> p h d", h=HEADS))
                    else:
                        t = (k - 5) // 2
                        nc.scalar.copy(q_tok[:, u, t, :, :], b[:, 0:2 * C].rearrange("p (k c) -> p k c", k=2))
                        ins = nc.scalar.copy(feat[:, u, t, :, 0:HS],
                                             b[:, C:2 * C].rearrange("p (h d) -> p h d", h=HEADS))
                    ins.then_inc(S["a_sb"], 1)

                def split_high(n, u):
                    act.wait_ge(S["own_ready"], counted(n + 1))
                    nc.scalar.copy(feat3[:, u, :, 0, :, :], feat[:, u, :, :, :]).then_inc(S["mid_ready"], 1)

                def split_middle(n, u):
                    act.wait_ge(S["rest_ready"], counted(n + 1))
                    nc.scalar.copy(feat3[:, u, :, 1, :, :], rest_f[:, :, :, :]).then_inc(S["mid_ready"], 1)

                def logs(n, u, t):
                    act.wait_ge(S["det_ready"], counted(n * 2 + t + 1))
                    nc.scalar.activation(sc[:, :, :, :], det[:, :, :, :], ACT.Ln,
                                         bias=consts["eps6"]).then_inc(S["log_ready"], 1)

                def terms(n, u, t):
                    act.wait_ge(S["diff_ready"], counted(n * 2 + t + 1))
                    nc.scalar.activation(ex[:, :, :, :, :], ex[:, :, :, :, :], ACT.Exp,
                                         scale=0.25).then_inc(S["exp_ready"], 1)

                def inverses(n, u, t):
                    r = n * 2 + t
                    act.wait_ge(S["denom_ready"], counted(r + 1))
                    nc.scalar.activation(z[:, 1, :, :, :], z[:, 0, :, :, :], ACT.Ln).then_inc(S["act_chain"], 1)
                    act.wait_ge(S["act_chain"], r + 1)
                    nc.scalar.activation(z[:, 1, :, :, :], z[:, 1, :, :, :], ACT.Exp,
                                         scale=-1.0).then_inc(S["inv_ready"], 1)
                    act.wait_ge(S["shifted"], counted(r + 1))
                    nc.scalar.activation(sc[:, :, :, :], sc[:, :, :, :], ACT.Exp).then_inc(S["probs_ready"], 1)

                def out(n, u, t):
                    act.wait_ge(S["yT_psum"], counted(n * 2 + (t + 1)))
                    nc.scalar.copy(yT[:, :, :], a_ps[0][0:HC, 0:2 * P].rearrange("p (h t) -> p h t", h=2)
                                   ).then_inc(S["yT_ready"], 1)

                def body(n, u, i, back, last):
                    s = back(1)
                    if s:
                        q, t = count_of(s), s[2] // PAIRS
                        act.wait_ge(S["chosenT_psum"], counted(q + 1))
                        act.wait_ge(S["code_in_psum"], counted(q - 1) if not (isinstance(q, int) and q < 2) else 1)
                        nc.scalar.copy(chosenT[:, s[2] % 2, 0:t + 1, :, :],
                                       mt_ps[:, 0:t + 1, :, :]).then_inc(S["chosenT_ready"], 1)
                    for k, do in ((DIFF, logs), (LOG, terms), (INV, inverses), (OUT, out)):
                        if stage(back, k):
                            do(*stage(back, k))
                    s = back(3)
                    if s:
                        q, t = count_of(s), s[2] // PAIRS
                        if s[2] % PAIRS == 0:
                            act.wait_ge(S["y_ready"], counted(s[0] * 2 + t - 1) if not (isinstance(s[0], int) and s[0] == 0)
                                        else 1)
                        for j in range(2):
                            act.wait_ge(S["gathered"], counted(q * 2 + (j + 1)))
                            src = g_ps[j][:, 0:SLOTS * FEAT].rearrange("p (a f) -> p a f", a=SLOTS)
                            h = first_head(s[2]) + 3 * j
                            nc.scalar.copy(keys[:, t, h, 0:SLOTS, :], src[:, :, 0:HS])
                            nc.scalar.copy(keys[:, t, h, SLOTS:EXT, :], src[:, 0:EXT - SLOTS, 0:HS])
                            nc.scalar.copy(values[:, t, h, :, :], src[:, :, HS:2 * HS])
                            nc.scalar.copy(facts[:, t, h, 0:SLOTS, :], src[:, :, 2 * HS:])
                            ins = nc.scalar.copy(facts[:, t, h, SLOTS:EXT, :], src[:, 0:EXT - SLOTS, 2 * HS:])
                        ins.then_inc(S["kv_ready"], 1)
                    s = back(1)
                    if s:
                        q, t = count_of(s), s[2] // PAIRS
                        act.wait_ge(S["code_in_psum"], counted(q + 1))
                        act.wait_ge(S["onehot_ready"], counted(q - 1) if not (isinstance(q, int) and q < 2) else 1)
                        nc.scalar.copy(code[:, s[2] % 2, 0:t + 1, :, :],
                                       code_psum[:, 0:t + 1, :, :]).then_inc(S["code_ready"], 1)
                    nxt = next_image(n, u, last)
                    if nxt and FRONT <= i < FRONT + 4:
                        front(*nxt, 2 * (i - FRONT))
                        front(*nxt, 2 * (i - FRONT) + 1)
                    if nxt and i == SPLIT:
                        split_high(*nxt)
                    if i == 0 and not (isinstance(n, int) and n == B):
                        split_middle(n, u)

                for k in range(8):
                    front(0, 0, k)
                split_high(0, 0)
                steps(act, body)

            @block.gpsimd
            def _(pool):
                for name in ("rest_ready split_ready square_ready prod_ready pv_ready kept_ready").split():
                    pool.sem_inc(S[name], 1)

                def squares(n, u):
                    pool.wait_ge(S["a_sb"], counted(n * 8 + 8))
                    key = feat[:, u, :, :, 0:HS]
                    nc.gpsimd.tensor_tensor(square[:, 0, :, :, :], key, key, ALU.mult)
                    for t in range(2):
                        ins = nc.gpsimd.tensor_tensor(square[:, 1, t, :, :], feat[:, u, t, :, 0:HS],
                                                      q_tok[:, u, t, 0, :].rearrange("p (h d) -> p h d", h=HEADS),
                                                      ALU.mult)
                    ins.then_inc(S["square_ready"], 1)

                def split_rest(n, u):
                    pool.wait_ge(S["mid_ready"], counted(n * 2 + 1))
                    nc.gpsimd.tensor_tensor(rest_f[:, :, :, :], feat[:, u, :, :, :], feat3[:, u, :, 0, :, :],
                                            ALU.subtract).then_inc(S["rest_ready"], 1)

                def split_low(n, u):
                    pool.wait_ge(S["mid_ready"], counted(n * 2 + 2))
                    nc.gpsimd.tensor_tensor(feat3[:, u, :, 2, :, :], rest_f[:, :, :, :], feat3[:, u, :, 1, :, :],
                                            ALU.subtract).then_inc(S["split_ready"], 1)

                def keep(n, u, t):
                    if not (isinstance(n, int) and n == 0):
                        pool.wait_ge(S["y_ready"], counted(n * 2 + t - 1))
                        hold(pool, S["pool_held"])
                    nc.gpsimd.tensor_copy(kept[:, t, :].rearrange("p (h d) -> p h d", h=HEADS),
                                          feat[:, u, t, :, HS:2 * HS]).then_inc(S["kept_ready"], 1)

                def weigh(n, u, t):
                    r = n * 2 + t
                    pool.wait_ge(S["alpha_ready"], counted(r + 1))
                    for h in range(0, HEADS, 4):
                        ins = nc.gpsimd.tensor_tensor(pv[:, h:h + 4, :, :], values[:, t, h:h + 4, :, :],
                                                      alpha[:, h:h + 4, :].unsqueeze(3).broadcast_to([P, 4, SLOTS, HS]),
                                                      ALU.mult)
                    ins.then_inc(S["pv_ready"], 1)

                def body(n, u, i, back, last):
                    if stage(back, VALUE):
                        weigh(*stage(back, VALUE))
                    s = back(3)
                    if s:
                        q, t = count_of(s), s[2] // PAIRS
                        pool.wait_ge(S["kv_ready"], counted(q + 1))
                        pool.wait_ge(S["dots_ready"], counted(q - 1) if not (isinstance(q, int) and q < 2) else 1)
                        made = prod[:, s[2] % 2, :, :, :]
                        near = (RD - 1) * SLOTS
                        for j in range(2):
                            h = first_head(s[2]) + 3 * j
                            key = keys[:, t, h, :, :]
                            lo = key[:, 0:SLOTS, :].unsqueeze(1).broadcast_to([P, RD - 1, SLOTS, HS])
                            dims = [list(x) for x in key.ap]
                            hi = bass.AP(tensor=key.tensor, offset=key.offset + HS,
                                         ap=[dims[0], [HS, RD - 1], [HS, SLOTS], [1, HS]])
                            nc.gpsimd.tensor_tensor(made[:, j, 0:near, :].rearrange("p (d a) f -> p d a f", d=RD - 1),
                                                    lo, hi, ALU.mult)
                            mine = q_tok[:, s[1], t, :, h * HS:(h + 1) * HS]
                            nc.gpsimd.tensor_tensor(
                                made[:, j, GRAMS:, :].rearrange("p (k a) f -> p k a f", k=2),
                                key[:, 0:SLOTS, :].unsqueeze(1).broadcast_to([P, 2, SLOTS, HS]),
                                mine.unsqueeze(2).broadcast_to([P, 2, SLOTS, HS]), ALU.mult)
                        h = first_head(s[2])
                        nc.gpsimd.tensor_tensor(made[:, :, near:GRAMS, :], keys[:, t, h:h + 4:3, 0:SLOTS // 2, :],
                                                keys[:, t, h:h + 4:3, SLOTS // 2:SLOTS, :], ALU.mult
                                                ).then_inc(S["products"], 1)
                        pool.wait_ge(S["products"], q + 1)
                        every = made.rearrange("p j k f -> p (j k) f")
                        ins = nc.gpsimd.tensor_tensor(every[:, :, 0:HS // 2], every[:, :, 0:HS // 2],
                                                      every[:, :, HS // 2:], ALU.add)
                        ins.then_inc(S["prod_ready"], 1)
                    if stage(back, DIFF):
                        keep(*stage(back, DIFF))
                    nxt = next_image(n, u, last)
                    if nxt and i == SQUARE:
                        squares(*nxt)
                    if nxt and i == SPLIT:
                        split_rest(*nxt)
                    if i == 0 and not (isinstance(n, int) and n == B):
                        split_low(n, u)

                squares(0, 0)
                split_rest(0, 0)
                steps(pool, body)

            @block.vector
            def _(dve):
                for name in ("own_ready chosen_ready marked_ready onehot_ready dots_ready det_ready shifted diff_ready "
                             "denom_ready alpha_ready y_ready x_added").split():
                    dve.sem_inc(S[name], 1)
                moment_steps(nc, dve, stats, S["stats_ready"], S["moments_ready"], x_res, moments)
                chain0 = Chain(dve, S["dve_chain0"])
                rstd_steps_dve(nc, dve, chain0, S["half_log"], moments, guess, rstd, shift).then_inc(S["rstd_ready"], 1)
                dve.wait_ge(S["weights_in"], LOADED)
                nc.vector.tensor_copy(ident_bf[:, :], consts["ident"])
                nc.vector.tensor_copy(mask_bf[:, :], y[:, 0, 0:P])
                nc.vector.tensor_copy(tri_bf[:, :], y[:, 1, 0:P])
                nc.vector.memset(ones_bf[:, :], 1.0)
                nc.vector.memset(ones_row[:, :], 1.0)
                nc.vector.memset(feat[:, :, :, :, 2 * HS:2 * HS + 1], 1.0)
                nc.vector.memset(sv[:, :, :, :], 0.0).then_inc(S["const_ready"], 1)
                dve.wait_ge(S["const_ready"], 1)

                def own_facts(n, u):
                    dve.wait_ge(S["square_ready"], counted(n + 1))
                    nc.vector.tensor_reduce(feat[:, u, :, :, 2 * HS + 1], square[:, 0, :, :, :], AX.X, ALU.add)
                    nc.vector.tensor_reduce(own[:, u, :, :], square[:, 1, :, :, :], AX.X, ALU.add
                                            ).then_inc(S["own_ready"], 1)

                def chained(name, count, r):
                    chain = Chain(dve, S[name], count, r)
                    return (chain, chain.link, chain.send,
                            lambda out, a, b, op: chain.link(nc.vector.tensor_tensor(out, a, b, op)))

                def det_stage(n, u, t):
                    r = n * 2 + t
                    chain, link, send, tt = chained("det_chain", 13, r)
                    gram = dots[:, t, :, 0:RD * SLOTS]
                    cross = dots[:, t, :, RD * SLOTS + EXT:]
                    norm = facts[:, t, :, :, 1]
                    mine = feat[:, u, t, :, 2 * HS + 1]
                    w0, w1, w2 = (pw[:, k, :, :, :] for k in range(3))
                    mult = lambda out, a, b: nc.vector.tensor_tensor(out, a, b, ALU.mult)
                    dve.wait_ge(S["dots_ready"], counted(n * STEPS + (t + 1) * PAIRS))
                    send(nc.vector.tensor_copy(gram[:, :, GRAMS:], gram[:, :, (RD - 1) * SLOTS:GRAMS]))
                    both = dots[:, t, :, RD * SLOTS:].rearrange("p h (k a) -> p h k a", k=2)
                    link(nc.vector.tensor_copy(both[:, :, :, SLOTS:], both[:, :, :, 0:EXT - SLOTS]))
                    send(mult(sv[:, 2, :, :], norm, over(mine, EXT)))
                    send(mult(cross2, cross, cross))
                    send(mult(w0, A(cross), Bx(cross)))
                    link(mult(per_head(w1, 0), gram, over(mine, RD * SLOTS)))
                    send(nc.vector.tensor_tensor(det2, sv[:, 2, :, :], cross2, ALU.subtract))
                    link(nc.vector.scalar_tensor_tensor(out=flat(w2), in0=flat(w0), scalar=2.0, in1=flat(w1),
                                                        op0=ALU.mult, op1=ALU.subtract))
                    send(nc.vector.tensor_copy(det[:, :, 0, :], det2[:, :, 0:SLOTS]))
                    send(mult(per_head(w0, 0), per_head(w2, 0), gram))
                    link(mult(w1, A(det2), Bx(norm)))
                    send(nc.vector.tensor_tensor(flat(w0), flat(w0), flat(w1), ALU.add))
                    link(mult(w2, A(norm), Bx(cross2)))
                    nc.vector.tensor_tensor(det[:, :, 1:, :], w0, w2, ALU.subtract).then_inc(S["det_ready"], 1)
                    chain.close()

                def diff_stage(n, u, t):
                    r = n * 2 + t
                    chain, link, send, tt = chained("diff_chain", 10, r)
                    sim = dots[:, t, :, RD * SLOTS:RD * SLOTS + EXT]
                    there = facts[:, t, :, :, 0]
                    self_sim = own[:, u, t, :]
                    both = pw[:, 1, :, :, :]
                    send(nc.vector.tensor_tensor(both, A(there), Bx(there), ALU.mult))
                    send(nc.vector.tensor_tensor(mx[:, :, 1:, :], A(sim), Bx(sim), ALU.max))
                    link(nc.vector.tensor_copy(mx[:, :, 0, :], sim[:, :, 0:SLOTS]))
                    send(nc.vector.tensor_scalar(veto[:, :, 1:, :], both, 1e30, -1e30, ALU.mult, ALU.add))
                    send(nc.vector.tensor_scalar(veto[:, :, 0, :], there[:, :, 0:SLOTS], 1e30, -1e30, ALU.mult, ALU.add))
                    tt(per_head(mx[:, :, :, :], 0), per_head(mx[:, :, :, :], 0), over(self_sim, NCOMB), ALU.max)
                    send(nc.vector.tensor_tensor(per_head(ex[:, 0, :, :, :], 0), over(self_sim, NCOMB),
                                                 per_head(mx[:, :, :, :], 0), ALU.subtract))
                    send(nc.vector.tensor_tensor(ex[:, 1, :, :, :],
                                                 sim[:, :, 0:SLOTS].unsqueeze(2).broadcast_to([P, H, 1 + RD, SLOTS]),
                                                 mx[:, :, :, :], ALU.subtract))
                    send(nc.vector.tensor_tensor(ex[:, 2, :, 1:, :], Bx(sim), mx[:, :, 1:, :], ALU.subtract))
                    link(nc.vector.memset(ex[:, 2, :, 0, :], -1e30))
                    dve.sem_inc(S["diff_ready"], 1)
                    chain.close()

                def log_stage(n, u, t):
                    r = n * 2 + t
                    chain, link, send, tt = chained("log_chain", 7, r)
                    cw = weight_of[:, 0, :].unsqueeze(1).broadcast_to([P, H, NCOMB])
                    cn = weight_of[:, 1, :].unsqueeze(1).broadcast_to([P, H, NCOMB])
                    dve.wait_ge(S["log_ready"], counted(r + 1))
                    send(nc.vector.tensor_tensor(scp, scp, cw, ALU.mult))
                    dve.wait_ge(S["exp_ready"], counted(r + 1))
                    tt(zf(0), ef(0), ef(1), ALU.add)
                    nc.vector.tensor_tensor(zf(0), zf(0), ef(2), ALU.add).then_inc(S["denom_ready"], 1)
                    tt(flat(sc[:, :, :, :]), flat(sc[:, :, :, :]), flat(veto[:, :, :, :]), ALU.add)
                    tt(scp, scp, cn, ALU.add)
                    link(nc.vector.tensor_reduce(hd[:, 0, :], scp, AX.X, ALU.max))
                    tt(scp, scp, over(hd[:, 0, :], NCOMB), ALU.subtract)
                    link(nc.vector.memset(spread[:, :, :], 0.0))
                    dve.sem_inc(S["shifted"], 1)
                    chain.close()

                def inv_stage(n, u, t):
                    r = n * 2 + t
                    chain, link, send, tt = chained("inv_chain", 8, r)
                    dve.wait_ge(S["inv_ready"], counted(r + 1))
                    dve.wait_ge(S["probs_ready"], counted(r + 1))
                    send(nc.vector.tensor_reduce(hd[:, 1, :], scp, AX.X, ALU.add))
                    tt(zf(2), zf(0), zf(1), ALU.mult)
                    send(nc.vector.reciprocal(hd[:, 2, :], hd[:, 1, :]))
                    link(nc.vector.scalar_tensor_tensor(out=zf(2), in0=zf(2), scalar=2.0, in1=zf(1),
                                                        op0=ALU.subtract, op1=ALU.mult))
                    tt(zf(2), zf(2), flat(sc[:, :, :, :]), ALU.mult)
                    for k in range(2):
                        send(nc.vector.tensor_tensor(ef(k), ef(k), zf(2), ALU.mult))
                    tt(ef(2), ef(2), zf(2), ALU.mult)
                    chain.close()

                def alpha_stage(n, u, t):
                    r = n * 2 + t
                    chain, link, send, tt = chained("alpha_chain", 12, r)
                    there = facts[:, t, :, :, 0]

                    def spread_out(dd):
                        tt(spread[:, :, dd:dd + SLOTS], spread[:, :, dd:dd + SLOTS], ex[:, 2, :, dd, :], ALU.add)

                    send(nc.vector.tensor_reduce(hd[:, 3, :], per_head(ex[:, 0, :, :, :], 0), AX.X, ALU.add))
                    send(nc.vector.tensor_reduce(alpha[:, :, :], ex[:, 1, :, :, :].rearrange("p h d a -> p h a d"),
                                                 AX.X, ALU.add))
                    spread_out(1)
                    send(nc.vector.scalar_tensor_tensor(out=hd[:, 4, :], in0=hd[:, 3, :], scalar=-1.0, in1=hd[:, 2, :],
                                                        op0=ALU.mult, op1=ALU.mult))
                    spread_out(2)
                    send(nc.vector.tensor_scalar(hd[:, 2, :], hd[:, 2, :], -1.0, None, ALU.mult))
                    spread_out(3)
                    send(nc.vector.scalar_tensor_tensor(out=hd[:, 5, :], in0=hd[:, 4, :], scalar=1.0,
                                                        in1=there[:, :, 0], op0=ALU.subtract, op1=ALU.mult))
                    spread_out(4)
                    send(nc.vector.tensor_scalar(hd[:, 5, :], hd[:, 5, :], 1.0, None, ALU.add))
                    tt(alpha[:, :, :], alpha[:, :, :], spread[:, :, 0:SLOTS], ALU.add)
                    tt(alpha[:, :, 0:EXT - SLOTS], alpha[:, :, 0:EXT - SLOTS], spread[:, :, SLOTS:], ALU.add)
                    nc.vector.tensor_tensor(alpha[:, :, :], alpha[:, :, :], over(hd[:, 2, :], SLOTS),
                                            ALU.mult).then_inc(S["alpha_ready"], 1)
                    chain.close()

                def y_stage(n, u, t):
                    r = n * 2 + t
                    chain, link, send, tt = chained("y_chain", 2, r)
                    y3 = y[:, t, :].rearrange("p (h d) -> p h d", h=H)
                    own_value = kept[:, t, :].rearrange("p (h d) -> p h d", h=H)
                    dve.wait_ge(S["kept_ready"], counted(r + 1))
                    send(nc.vector.tensor_tensor(own_value, own_value, over(hd[:, 5, :], HS), ALU.mult))
                    dve.wait_ge(S["pv_ready"], counted(r + 1))
                    link(nc.vector.tensor_reduce(y3, pv[:, :, :, :].rearrange("p h a d -> p h d a"), AX.X, ALU.add))
                    nc.vector.tensor_tensor(y3, y3, own_value, ALU.add).then_inc(S["y_ready"], 1)
                    chain.close()

                def out(n, u, t):
                    r = n * 2 + t
                    dve.wait_ge(S["proj_ready"], counted(r + 1))
                    xt = tile_of(x_res, n, t)
                    nc.vector.tensor_tensor(xt, a_ps[1][:, 0:C], xt, ALU.add).then_inc(S["x_added"], 1)
                    dve.wait_ge(S["x_added"], counted(r * 2 + 1))
                    nc.vector.tensor_tensor(xt, xt, bp[:, :], ALU.add).then_inc(S["x_added"], 1)

                def body(n, u, i, back, last):
                    if not (isinstance(n, int) and n == B):
                        q, t = count_of((n, u, i)), i // PAIRS
                        nk = keys_of(t)
                        dve.wait_ge(S["scores_ready"], counted(q + 1))
                        hold(dve, S["dve_held"])
                        for j in range(2):
                            ins = nc.vector.max(top8[:, i % 2, j, :], s_ps[i % 2][:, j * nk:(j + 1) * nk])
                            ins.then_inc(S["max_chain"], 1)
                        for j in range(2):
                            dve.wait_ge(S["max_chain"], q * 2 + (j + 1))
                            hold(dve, S["dve_held"])
                            ins = nc.vector.match_replace(marked[:, j, 0:nk], top8[:, i % 2, j, :],
                                                          s_ps[i % 2][:, j * nk:(j + 1) * nk], HUGE * 0.9)
                        ins.then_inc(S["marked_ready"], 1)
                        dve.wait_ge(S["marked_ready"], counted(q + 1))
                        dve.wait_ge(S["chosenT_psum"], counted(q - 1) if not (isinstance(q, int) and q < 2) else 1)
                        nc.vector.tensor_tensor(chosen[:, i % 2, :, 0:nk], marked[:, :, 0:nk],
                                                thr[:, 2 * P - nk:2 * P].unsqueeze(1).broadcast_to([P, 2, nk]),
                                                ALU.is_ge).then_inc(S["chosen_ready"], 1)
                    s = back(2)
                    if s:
                        q, t = count_of(s), s[2] // PAIRS
                        dve.wait_ge(S["code_ready"], counted(q + 1))
                        dve.wait_ge(S["gathered"], counted(q * 2))
                        for a in range(SLOTS):
                            ins = nc.vector.tensor_scalar(onehot[:, a, 0:t + 1, :, :],
                                                          code[:, s[2] % 2, 0:t + 1, :, :], float(64 + 1 + a), None,
                                                          ALU.is_equal)
                        ins.then_inc(S["onehot_ready"], 1)
                    s = back(4)
                    if s:
                        q, t = count_of(s), s[2] // PAIRS
                        dve.wait_ge(S["prod_ready"], counted(q + 1))
                        h = first_head(s[2])
                        at = 0
                        for place, size in ((0, GRAMS), (RD * SLOTS, SLOTS), (RD * SLOTS + EXT, SLOTS)):
                            ins = nc.vector.tensor_reduce(dots[:, t, h:h + 4:3, place:place + size],
                                                          prod[:, s[2] % 2, :, at:at + size, 0:HS // 2], AX.X, ALU.add)
                            at += size
                        ins.then_inc(S["dots_ready"], 1)
                    for k, do in ((DET, det_stage), (DIFF, diff_stage), (LOG, log_stage), (INV, inv_stage),
                                  (ALPHA, alpha_stage), (VALUE, y_stage), (OUT + 1, out)):
                        if stage(back, k):
                            do(*stage(back, k))
                    nxt = next_image(n, u, last)
                    if nxt and i == OWN:
                        own_facts(*nxt)

                own_facts(0, 0)
                steps(dve, body)

            @block.tensor
            def _(pe):
                for name in ("a_psum scores_ready chosenT_psum code_in_psum gathered yT_psum proj_ready").split():
                    pe.sem_inc(S[name], 1)
                pe.wait_ge(S["weights_in"], LOADED)
                pe.wait_ge(S["const_ready"], 1)

                def front(n, u, k):
                    o = a_ps[k % 2]
                    if k == 0:
                        pe.wait_ge(S["xn_ready"], counted(n + 1))
                    if k < 2 and not (isinstance(n, int) and n < 2):
                        pe.wait_ge(S["yT_ready"], counted(n * 2 - 3))
                        pe.wait_ge(S["x_added"], counted(n * 4 - 6))
                    pe.wait_ge(S["a_sb"], counted(n * 8 + (1 if k == 1 else max(k - 1, 0))))
                    if k == 0:
                        for h in range(2):
                            for t in range(2):
                                ins = nc.tensor.transpose(o[0:HC, (2 * h + t) * P:(2 * h + t + 1) * P],
                                                          xn[:, t, h * HC:(h + 1) * HC], consts["ident"])
                    elif k <= 4:
                        for j in range(2):
                            for h in range(2):
                                ins = nc.tensor.matmul(o[0:HC, j * T:(j + 1) * T], wqk[:, h, 2 * (k - 1) + j, :],
                                                       tT[:, h, :], start=h == 0, stop=h == 1)
                    else:
                        for at, t, c0, c1 in {5: [(0, 0, 0, 2 * C)],
                                              6: [(0, 0, 2 * C, 3 * C), (C, 1, 2 * C, 3 * C)],
                                              7: [(0, 1, 0, 2 * C)]}[k]:
                            part = o[:, at:at + c1 - c0]
                            for h in range(2):
                                nc.tensor.matmul(part, tT[:, h, t * P:(t + 1) * P], wtok[:, h, c0:c1], start=h == 0,
                                                 stop=False)
                            ins = nc.tensor.matmul(part, ones_row[:, :], btok[:, c0:c1], start=False, stop=True)
                    ins.then_inc(S["a_psum"], 1)

                def turn_output(n, u, t):
                    pe.wait_ge(S["y_ready"], counted(n * 2 + t + 1))
                    if isinstance(n, int) and n + 1 + t >= B:
                        pe.wait_ge(S["a_sb"], counted(B * 8))
                    else:
                        pe.wait_ge(S["a_sb"], counted(n * 8 + 16 + 8 * t))
                    hold(pe, S["pe_held"])
                    for h in range(2):
                        ins = nc.tensor.transpose(a_ps[0][0:HC, h * P:(h + 1) * P], y[:, t, h * HC:(h + 1) * HC],
                                                  consts["ident"])
                    ins.then_inc(S["yT_psum"], 1)

                def project(n, u, t):
                    r = n * 2 + t
                    pe.wait_ge(S["yT_ready"], counted(r + 1))
                    pe.wait_ge(S["x_added"], counted(r * 2))
                    for h in range(2):
                        ins = nc.tensor.matmul(a_ps[1][:, 0:C], yT[:, h, :], wp[:, h, :], start=h == 0, stop=h == 1)
                    ins.then_inc(S["proj_ready"], 1)

                def body(n, u, i, back, last):
                    if stage(back, OUT + 1):
                        project(*stage(back, OUT + 1))
                    if not (isinstance(n, int) and n == B):
                        q, t = count_of((n, u, i)), i // PAIRS
                        nk = keys_of(t)
                        if i == 0:
                            pe.wait_ge(S["a_sb"], counted(n * 8 + 5))
                        pe.wait_ge(S["marked_ready"], counted(q - 1) if not (isinstance(q, int) and q < 2) else 1)
                        for j in range(2):
                            h = first_head(i) + 3 * j
                            rows = slice(32 * (h % 3), 32 * (h % 3) + 32)
                            o = s_ps[i % 2][:, j * nk:(j + 1) * nk]
                            nc.tensor.matmul(o, qkT[rows, u, h // 3, t * P:(t + 1) * P], qkT[rows, u, 4 + h // 3, 0:nk],
                                             start=True, stop=False, skip_group_check=True)
                            ins = nc.tensor.matmul(o[:, nk - P:nk], ident_bf[:, :], mask_bf[:, :], start=False,
                                                   stop=True, skip_group_check=True)
                        ins.then_inc(S["scores_ready"], 1)
                    s = back(1)
                    if s:
                        q, t = count_of(s), s[2] // PAIRS
                        pe.wait_ge(S["chosen_ready"], counted(q + 1))
                        pe.wait_ge(S["chosenT_ready"], counted(q))
                        for kt in range(t + 1):
                            for j in range(2):
                                ins = nc.tensor.matmul(mt_ps[:, kt, j, :], chosen[:, s[2] % 2, j, kt * P:(kt + 1) * P],
                                                       ident_bf[:, :], start=True, stop=True)
                        ins.then_inc(S["chosenT_psum"], 1)
                    s = back(3)
                    if s:
                        q, t = count_of(s), s[2] // PAIRS
                        if s[2] == 0:
                            pe.wait_ge(S["split_ready"], counted(s[0] + 1))
                        pe.wait_ge(S["onehot_ready"], counted(q + 1))
                        pe.wait_ge(S["kv_ready"], counted(q))
                        for j in range(2):
                            h = first_head(s[2]) + 3 * j
                            for a in range(SLOTS):
                                for kt in range(t + 1):
                                    for part in range(3):
                                        ins = nc.tensor.matmul(g_ps[j][:, a * FEAT:(a + 1) * FEAT],
                                                               onehot[:, a, kt, j, :],
                                                               feat3[:, s[1], kt, part, h, :],
                                                               start=kt == 0 and part == 0, stop=kt == t and part == 2)
                            ins.then_inc(S["gathered"], 1)
                    s = back(1)
                    if s:
                        q, t = count_of(s), s[2] // PAIRS
                        pe.wait_ge(S["chosenT_ready"], counted(q + 1))
                        pe.wait_ge(S["code_ready"], counted(q))
                        for kt in range(t + 1):
                            o = code_psum[:, kt, :, :]
                            ins = nc.tensor.matmul(o, tri_bf[:, :], chosenT[:, s[2] % 2, kt, :, :], start=True,
                                                   stop=kt == 0)
                            if kt:
                                ins = nc.tensor.matmul(o, ones_bf[:, :], chosenT[:, s[2] % 2, 0, :, :], start=False,
                                                       stop=True)
                        ins.then_inc(S["code_in_psum"], 1)
                    if stage(back, OUT):
                        turn_output(*stage(back, OUT))
                    nxt = next_image(n, u, last)
                    if nxt and FRONT <= i < FRONT + 4:
                        front(*nxt, 2 * (i - FRONT))
                        front(*nxt, 2 * (i - FRONT) + 1)

                for k in range(8):
                    front(0, 0, k)
                steps(pe, body)
        m.clear()


def host_layouts(inputs):
    a = {k: np.asarray(v) for k, v in inputs.items()}
    lay = {}

    def halves(m):
        return np.ascontiguousarray(m.reshape(2, HC, -1).transpose(1, 0, 2))

    lay["x"] = np.ascontiguousarray(a["x"].reshape(TILES, P, C).transpose(1, 0, 2))
    lay["l3f_wr"] = halves(a["L3_ffn_Wg"])
    lay["l3f_w1"] = np.ascontiguousarray(a["L3_ffn_W1"].reshape(E, 2, HC, 768).transpose(2, 1, 0, 3))
    lay["l3f_w2"] = np.ascontiguousarray(a["L3_ffn_W2"].reshape(E, 6, P, C).transpose(2, 1, 0, 3))
    lay["l3f_b1"] = np.ascontiguousarray(a["L3_ffn_b1"].reshape(E, 6, P).transpose(2, 0, 1))
    lay["l0_xT"] = np.ascontiguousarray(a["x"].reshape(TOK, 2, HC).transpose(2, 1, 0))
    lay["l0_down"] = halves(a["L0_conv_down_w"].T)
    lay["l0_inp"] = np.ascontiguousarray(a["L0_conv_in_proj_w"].T)
    lay["l0_convw"] = a["L0_conv_conv_w"]
    lay["l0_cols"] = np.ascontiguousarray(np.stack([a["L0_conv_conv_b"], a["L0_conv_dt_proj_b"],
                                                    a["L0_conv_D_ssm"]], axis=1))
    xp = a["L0_conv_x_proj_w"]
    lay["l0_xdt"] = np.ascontiguousarray(xp[0:12].T)
    lay["l0_xb"] = np.ascontiguousarray(np.broadcast_to(xp[12:44].T.reshape(96, 2, 1, 16), (96, 2, 8, 16)))
    lay["l0_dtw"] = np.ascontiguousarray(a["L0_conv_dt_proj_w"].T)
    lay["l0_alog"] = np.ascontiguousarray(a["L0_conv_A_log"].reshape(12, P).T)
    sel = np.zeros((96, 12, P), np.float32)
    for row in range(96):
        sel[row, row // 8, (row % 8) * 16:(row % 8 + 1) * 16] = 1.0
    lay["l0_sel"] = sel
    lay["l0_selT"] = np.ascontiguousarray(sel.transpose(2, 1, 0))
    lay["l0_outp"] = np.ascontiguousarray(a["L0_conv_out_proj_w"].T)
    lay["l0_up"] = np.ascontiguousarray(a["L0_conv_up_w"].T)
    lay["l0_lng"] = a["L0_conv_ln_g"]
    lay["l0_lnb"] = a["L0_conv_ln_b"]
    keep = np.ones(16, np.float32)
    keep[0] = keep[8] = 0.0
    lay["l0_keep"] = keep
    wa, ba = a["L2_attn_W_attn"], a["L2_attn_b_attn"]
    wqk, bqk = np.zeros((HC, 2, 8, 3, 32), np.float32), np.zeros((HC, 8), np.float32)
    for part in range(2):
        wpart = wa[part * C:(part + 1) * C].reshape(4, 3, 16, 2, HC)
        wqk[:, :, 4 * part:4 * part + 4, :, 0:16] = wpart.transpose(4, 3, 0, 1, 2)
        bqk.reshape(3, 32, 8)[:, 0:16, 4 * part:4 * part + 4] = \
            ba[part * C:(part + 1) * C].reshape(4, 3, 16).transpose(1, 2, 0)
    lay["l2a_wqk"] = wqk.reshape(HC, 2, 8, HC)
    lay["l2a_bqk"] = bqk
    lay["l2a_wtok"] = halves(wa.T)
    lay["l2a_btok"] = ba
    lay["l2a_wp"] = halves(a["L2_attn_W_proj"].T)
    lay["l2a_bp"] = a["L2_attn_b_proj"]
    row, col = np.arange(P)[:, None], np.arange(P)[None, :]
    lay["l2a_mask"] = np.where(col > row, -1e30, 0.0).astype(np.float32)
    lay["l2a_thr"] = np.concatenate([np.full((P, P), BIG), np.where(col < row, BIG, HUGE)], axis=1).astype(np.float32)
    lay["l2a_tri"] = (np.where(row <= col, 1.0, 0.0) + 64.0 * (row == col)).astype(np.float32)
    comb = np.zeros((2, 5, SLOTS), np.float32)
    comb[0, 0], comb[0, 1:] = 1.0 / 2.0, 1.0 / 3.0
    comb[1, 4, 4:] = -1e30
    lay["l2a_comb"] = comb.reshape(2, 5 * SLOTS)
    ky, kx = np.meshgrid(np.arange(HH), np.arange(WW // 2 + 1), indexing="ij")
    yy, xx = np.meshgrid(np.arange(HH), np.arange(WW), indexing="ij")
    turn = 2 * np.pi * (np.outer(yy.ravel(), ky.ravel()) + np.outer(xx.ravel(), kx.ravel())) / HH
    dft = np.concatenate([np.cos(turn), -np.sin(turn)], axis=1) / HH
    lay["l1_dft"] = np.ascontiguousarray(dft.reshape(2, P, 288).transpose(1, 0, 2)).astype(np.float32)
    twice = np.where((kx.ravel() == 0) | (kx.ravel() == WW // 2), 1.0, 2.0)[:, None]
    idft = np.stack([np.cos(turn).T * twice, -np.sin(turn).T * twice], axis=0) / HH
    lay["l1_idft"] = np.ascontiguousarray(idft.reshape(2, 2, 72, T).transpose(2, 1, 0, 3)).astype(np.float32)
    for name in ("w1", "w2"):
        full = np.zeros((HC, 2, 2, HC), np.float32)
        for blk in range(8):
            at = slice((blk % 4) * 24, (blk % 4 + 1) * 24)
            full[at, :, blk // 4, at] = a["L1_conv_" + name][:, blk].transpose(1, 0, 2)
        lay["l1_" + name] = full
    lay["l1_w2"] = np.ascontiguousarray(lay["l1_w2"].transpose(0, 2, 1, 3))
    lay["l1_b1"] = np.ascontiguousarray(a["L1_conv_b1"].reshape(2, 2, HC).transpose(2, 1, 0))
    lay["l1_b2"] = np.ascontiguousarray(a["L1_conv_b2"].reshape(2, 2, HC).transpose(1, 0, 2))
    for name in ("q", "k", "v", "o"):
        lay["l3a_w" + name] = halves(a["L3_attn_W" + name])
    lay["l3a_memT"] = halves(a["L3_attn_memory"].T)
    lay["l3a_bq"] = np.ascontiguousarray(a["L3_attn_bq"].reshape(2, HC).T)
    lay["l3a_bk"] = np.ascontiguousarray(a["L3_attn_bk"].reshape(2, HC).T)
    lay["l3a_bv"] = a["L3_attn_bv"]
    lay["l3a_bo"] = a["L3_attn_bo"]
    lay["l2f_wr"] = halves(a["L2_ffn_Wr"])
    lay["l2f_br"] = a["L2_ffn_br"]
    lay["l2f_wgu"] = np.ascontiguousarray(a["L2_ffn_Wgu"].reshape(E, 2, HC, 2 * C).transpose(2, 1, 0, 3))
    lay["l2f_wd"] = np.ascontiguousarray(a["L2_ffn_Wd"].reshape(E, 2, HC, C).transpose(2, 1, 0, 3))
    lay["l2f_bgu"] = np.ascontiguousarray(a["L2_ffn_bgu"].reshape(E, 4, HC).transpose(2, 0, 1))
    lay["l2f_bd"] = a["L2_ffn_bd"]
    lay["l3f_b2"] = a["L3_ffn_b2"]
    row_of = np.tile(np.arange(P)[:, None], (1, P))
    lay["moe_tri"] = (row_of < row_of.T).astype(np.float32)
    lay["moe_rev"] = np.arange(E, 0, -1).astype(np.float32)
    lay["moe_floor"] = (np.arange(TOK // ETOK) * ETOK).astype(np.float32)
    lay["moe_index"] = np.arange(ETILES).astype(np.float32)
    lay["ident"] = np.eye(P, dtype=np.float32)
    return lay


def build(nc, d, out, phases=("l0", "l1", "l2a", "l2f", "l3a", "l3f")):
    with ExitStack() as ctx:
        m = Mem(nc, ctx, "main")
        x_res = m.sb("x_res", [P, TILES, C])
        moments = m.sb("moments", [P, TILES, 2])
        ident = m.sb("ident", [P, P])
        eps = m.sb("eps", [P, 1])
        eps6 = m.sb("eps6", [P, 1])
        x_in = m.sem("x_in")
        const_in = m.sem("const_in")
        x_out = m.sem("x_out")
        zeros = m.sb("zeros", [P, C])
        rows_in = nc.dram_tensor("rows_in", (ETILES * ETOK, C), F32).ap()
        rows_out = nc.dram_tensor("rows_out", (ETILES * ETOK, C), F32).ap()
        zeroed = m.sem("zeroed")
        zeros_ready = m.sem("zeros_ready")
        consts = {"ident": ident[:, :], "eps": eps[:, :], "eps6": eps6[:, :],
                  "moe": [d[f"moe_{name}"] for name in ("tri", "rev", "floor", "index")],
                  "rows_in": rows_in, "rows_out": rows_out, "zeroed": zeroed}

        def load_x(sp):
            sp.dma_start(x_res[:, :, :], d["x"]).then_inc(x_in, 16)
            sp.wait_ge(zeros_ready, 1)
            sp.dma_start(rows_in.rearrange("(k p) c -> p k c", p=P),
                         zeros[:, :].unsqueeze(1).broadcast_to([P, ETILES * ETOK // P, C])).then_inc(zeroed, 16)

        consts["load_x"], consts["x_in"], consts["out"] = load_x, x_in, out
        with nc.Block() as block:
            @block.sync
            def _(sp):
                sp.dma_start(ident[:, :], d["ident"]).then_inc(const_in, 16)
                sp.wait_ge(const_in, 16)
                if phases[0] != "l0":
                    load_x(sp)
                    sp.wait_ge(x_in, 16)

            @block.vector
            def _(dve):
                nc.vector.memset(zeros[:, :], 0.0).then_inc(zeros_ready, 1)
                nc.vector.memset(eps[:, :], EPS)
                nc.vector.memset(eps6[:, :], 1e-6)
        w = {}
        for k, v in d.items():
            if "_" in k:
                tag, name = k.split("_", 1)
                w.setdefault(tag, {})[name] = v
        PH = {"l2a": lambda: dpp_attention_phase(nc, x_res, moments, consts, w["l2a"]),
              "l1": lambda: fourier_phase(nc, x_res, moments, consts, w["l1"]),
              "l0": lambda: mamba_phase(nc, x_res, moments, consts, w["l0"]),
              "l3a": lambda: memory_attention_phase(nc, x_res, moments, consts, w["l3a"]),
              "l2f": lambda: moe_glu_phase(nc, x_res, moments, consts, w["l2f"]),
              "l3f": lambda: moe_relu_phase(nc, x_res, moments, consts, w["l3f"])}
        for ph in phases:
            PH[ph]()
        if phases[-1] != "l3f":
            with nc.Block() as block:
                @block.sync
                def _(sp):
                    sp.dma_start(out, x_res[:, :, :]).then_inc(x_out, 16)
                    sp.wait_ge(x_out, 16)


def kernel(**inputs):
    import concourse.bacc as _bacc
    from concourse.bass_utils import run_bass_kernel_spmd as _run

    nc = _bacc.Bacc("TRN2", target_bir_lowering=False, num_devices=1)
    arrays, d = {}, {}
    for name, a in host_layouts(inputs).items():
        arrays[f"in_{name}"] = a
        d[name] = nc.dram_tensor(f"in_{name}", a.shape, mybir.dt.from_np(a.dtype), kind="ExternalInput").ap()
    out = nc.dram_tensor("out_x", (P, TILES, C), F32, kind="ExternalOutput").ap()
    build(nc, d, out)
    r = _run(nc, [arrays], core_ids=[0])
    got = r.results[0]["out_x"]
    return np.ascontiguousarray(got.transpose(1, 0, 2)).reshape(B, HH, WW, C)
```
